# Optimizing a Trainium2 kernel written in Bass

```python
import numpy as np
import jax
import jax.numpy as jnp

def _softmax(x, axis=-1):
    return jax.nn.softmax(x, axis=axis)

def _gelu(x):
    return jax.nn.gelu(x, approximate=True)

def _silu(x):
    return jax.nn.silu(x)

def _sigmoid(x):
    return jax.nn.sigmoid(x)

def _layernorm(x, axis=-1, eps=1e-05):
    m = jnp.mean(x, axis=axis, keepdims=True)
    v = jnp.var(x, axis=axis, keepdims=True)
    return (x - m) / jnp.sqrt(v + eps)

def _scatter_add(tgt, idx, src, axis=0):
    return tgt.at[idx].add(src)

def _segment_sum(src, seg, n):
    return jax.ops.segment_sum(src, seg, n)
kernel_name = 'mk_perceiver_d4_seqx_r4_e7b688'

def setup_inputs(seed: int=0):
    np.random.seed(seed)
    _w = jnp.asarray

    def _rec_inputs():
        import jax
        import jax.numpy as jnp
        _rk = jax.random.key(seed)
        x = -0.0003929 + 0.9999 * jax.random.normal(jax.random.fold_in(_rk, 1), (32, 32, 256), jnp.float32)
        _lenS = 32 - jax.random.randint(jax.random.fold_in(_rk, 7), (32,), 0, max(1, 32 // 4) + 1, jnp.int32)
        _lenS2 = 257 - jax.random.randint(jax.random.fold_in(_rk, 8), (32,), 0, max(1, 257 // 4) + 1, jnp.int32)
        _ctx_1024P = jax.random.normal(jax.random.fold_in(_rk, 11), (32, 16, 256), jnp.float32)
        _ctx_1024c = jax.random.dirichlet(jax.random.fold_in(_rk, 511), 0.3 * jnp.ones((16,), jnp.float32), (32, 257))
        _ctx_1024t = jnp.einsum('bsk,bkd->bsd', _ctx_1024c, _ctx_1024P)
        _ctx_1024t = _ctx_1024t * jax.lax.rsqrt(jnp.mean(jnp.square(_ctx_1024t)) + 1e-12) * 0.953939
        ctx_1024 = 2.81802e-05 + 1.00001 * (_ctx_1024t + 0.3 * jax.random.normal(jax.random.fold_in(_rk, 611), (32, 257, 256), jnp.float32))
        _validS = jnp.arange(32)[None, :] < _lenS[:, None]
        _validS2 = jnp.arange(257)[None, :] < _lenS2[:, None]
        _causal = jnp.tril(jnp.ones((32, 32), dtype=bool))
        mask_BxS2_ff1 = jnp.where(jnp.ones((32, 257), dtype=bool), 1.0, 0.0).astype(jnp.float32)
        return (x, ctx_1024, mask_BxS2_ff1)
    x, ctx_1024, mask_BxS2_ff1 = _rec_inputs()

    def _L0_xattn_setup():
        import jax, jax.numpy as jnp
        import numpy as np
        D_MODEL = 256
        HEADS = 16
        DEPTH = D_MODEL // HEADS
        B, S = (4, 1024)
        EPS_K = 1e-06
        EPS_LN = 1e-06

        def _layernorm(x, g, b):
            m = jnp.mean(x, axis=-1, keepdims=True)
            var = jnp.var(x, axis=-1, keepdims=True)
            return (x - m) * jax.lax.rsqrt(var + EPS_LN) * g + b

        def _split_heads(x):
            bsz, sl, _ = x.shape
            return x.reshape(bsz, sl, HEADS, DEPTH).transpose(0, 2, 1, 3)
        key = jax.random.key(seed)
        ks = jax.random.split(key, 8)
        lecun = 1.0 / np.sqrt(D_MODEL)
        glorot = np.sqrt(2.0 / (D_MODEL + D_MODEL))
        return {'q': jax.random.normal(ks[0], (B, S, D_MODEL), jnp.float32), 'k': jax.random.normal(ks[1], (B, S, D_MODEL), jnp.float32), 'v': jax.random.normal(ks[2], (B, S, D_MODEL), jnp.float32), 'mask': jnp.ones((B, S), jnp.float32), 'wq': jax.random.normal(ks[3], (D_MODEL, D_MODEL), jnp.float32) * lecun, 'wk': jax.random.normal(ks[4], (D_MODEL, D_MODEL), jnp.float32) * lecun, 'wv': jax.random.normal(ks[5], (D_MODEL, D_MODEL), jnp.float32) * lecun, 'ln_gamma': jnp.ones((D_MODEL,), jnp.float32), 'ln_beta': jnp.zeros((D_MODEL,), jnp.float32), 'dense_w': jax.random.normal(ks[6], (D_MODEL, D_MODEL), jnp.float32) * glorot, 'dense_b': jnp.zeros((D_MODEL,), jnp.float32)}
    _L0_xattn_all = _L0_xattn_setup()
    _L0_xattn_in = {k: v for k, v in _L0_xattn_all.items() if k in ('wq', 'wk', 'wv', 'ln_gamma', 'ln_beta', 'dense_w', 'dense_b')}
    del _L0_xattn_all

    def _L0_attn_setup():
        import jax, jax.numpy as jnp
        import numpy as np
        NUM_HEADS = 16
        THETA = 10000.0

        def _rope(x, theta):
            S, d_k = (x.shape[1], x.shape[-1])
            k = jnp.arange(d_k // 2, dtype=jnp.float32)
            inv_freq = theta ** (-2.0 * k / d_k)
            ang = jnp.arange(S, dtype=jnp.float32)[:, None] * inv_freq
            cos = jnp.cos(ang)[None, :, None, :]
            sin = jnp.sin(ang)[None, :, None, :]
            x_even = x[..., 0::2]
            x_odd = x[..., 1::2]
            y_even = cos * x_even - sin * x_odd
            y_odd = sin * x_even + cos * x_odd
            y = jnp.stack([y_even, y_odd], axis=-1)
            return y.reshape(x.shape)
        key = jax.random.key(seed)
        ks = jax.random.split(key, 5)
        B, S, D = (2, 512, 256)
        std = 1.0 / np.sqrt(D)
        return {'in_features': jax.random.normal(ks[0], (B, S, D), dtype=jnp.float32), 'W_Q': jax.random.normal(ks[1], (D, D), dtype=jnp.float32) * std, 'W_K': jax.random.normal(ks[2], (D, D), dtype=jnp.float32) * std, 'W_V': jax.random.normal(ks[3], (D, D), dtype=jnp.float32) * std, 'W_O': jax.random.normal(ks[4], (D, D), dtype=jnp.float32) * std}
    _L0_attn_all = _L0_attn_setup()
    _L0_attn_in = {k: v for k, v in _L0_attn_all.items() if k in ('W_Q', 'W_K', 'W_V', 'W_O')}
    del _L0_attn_all

    def _L0_ffn_setup():
        import jax, jax.numpy as jnp
        import numpy as np
        EPS = 1e-06
        N_EXPERTS = 8

        def _rms_norm(x, scale, eps=EPS):
            mean_sq = jnp.mean(x.astype(jnp.float32) ** 2, axis=-1, keepdims=True)
            s = scale.astype(jnp.float32) * jax.lax.rsqrt(mean_sq + eps)
            return x * s.astype(x.dtype)

        def _dist2(x, y):
            nx = jnp.sum(x ** 2, axis=-1)[..., :, None]
            ny = jnp.sum(y ** 2, axis=-1)[..., None, :]
            return nx + ny - 2.0 * (x @ y.T)
        key = jax.random.key(seed)
        ks = jax.random.split(key, 5)
        dim, hidden, E = (256, 512, N_EXPERTS)
        x = jax.random.normal(ks[0], (4, 512, dim), dtype=jnp.float32)
        scale = jnp.ones((dim,), dtype=jnp.float32)
        centroids = jax.random.normal(ks[1], (E, dim), dtype=jnp.float32)
        up_w = jax.random.normal(ks[2], (E, dim, hidden * 2), dtype=jnp.float32) * dim ** (-0.5)
        down_w = jax.random.normal(ks[3], (E, hidden, dim), dtype=jnp.float32) * hidden ** (-0.5)
        return {'x': x, 'scale': scale, 'centroids': centroids, 'up_w': up_w, 'down_w': down_w}
    _L0_ffn_all = _L0_ffn_setup()
    _L0_ffn_in = {k: v for k, v in _L0_ffn_all.items() if k in ('scale', 'centroids', 'up_w', 'down_w')}
    del _L0_ffn_all

    def _L1_xattn_setup():
        import jax, jax.numpy as jnp
        import numpy as np
        DIM = 256
        CTX_DIM = 256
        HEADS = 16
        DIM_HEAD = 64
        INNER = HEADS * DIM_HEAD
        FF_INNER = 4 * DIM
        EPS = 1e-05

        def layer_norm(x, g, b):
            mu = jnp.mean(x, axis=-1, keepdims=True)
            var = jnp.var(x, axis=-1, keepdims=True)
            return (x - mu) * jax.lax.rsqrt(var + EPS) * g + b
        key = jax.random.key(seed)
        ks = jax.random.split(key, 9)
        b, n, j = (4, 512, 256)
        inp = {'x': jax.random.normal(ks[0], (b, n, DIM), dtype=jnp.float32), 'context': jax.random.normal(ks[1], (b, j, CTX_DIM), dtype=jnp.float32), 'ln_g': jnp.ones((DIM,), jnp.float32), 'ln_b': jnp.zeros((DIM,), jnp.float32), 'cln_g': jnp.ones((CTX_DIM,), jnp.float32), 'cln_b': jnp.zeros((CTX_DIM,), jnp.float32), 'Wq': jax.random.normal(ks[2], (DIM, INNER), dtype=jnp.float32) * DIM ** (-0.5), 'Wkv': jax.random.normal(ks[3], (CTX_DIM, 2 * DIM_HEAD), dtype=jnp.float32) * CTX_DIM ** (-0.5), 'Wo': jax.random.normal(ks[4], (INNER, DIM), dtype=jnp.float32) * INNER ** (-0.5), 'Wff1': jax.random.normal(ks[5], (DIM, 2 * FF_INNER), dtype=jnp.float32) * DIM ** (-0.5), 'Wff2': jax.random.normal(ks[6], (FF_INNER, DIM), dtype=jnp.float32) * FF_INNER ** (-0.5)}
        return inp
    _L1_xattn_all = _L1_xattn_setup()
    _L1_xattn_in = {k: v for k, v in _L1_xattn_all.items() if k in ('ln_g', 'ln_b', 'cln_g', 'cln_b', 'Wq', 'Wkv', 'Wo', 'Wff1', 'Wff2')}
    del _L1_xattn_all

    def _L1_attn_setup():
        import math
        import jax, jax.numpy as jnp
        import numpy as np
        N_EMBD = 256
        N_HEAD = 16
        N_QUERY_SETS = 4
        B, T = (8, 256)
        key = jax.random.key(seed)
        kx, kw1, kw2 = jax.random.split(key, 3)
        C = N_EMBD
        x = jax.random.normal(kx, (B, T, C), dtype=jnp.float32)
        W_attn = jax.random.normal(kw1, ((N_QUERY_SETS + 2) * C, C), dtype=jnp.float32) * (1.0 / math.sqrt(C))
        W_proj = jax.random.normal(kw2, (C, N_QUERY_SETS * C), dtype=jnp.float32) * (1.0 / math.sqrt(N_QUERY_SETS * C))
        return {'x': x, 'W_attn': W_attn, 'W_proj': W_proj}
    _L1_attn_all = _L1_attn_setup()
    _L1_attn_in = {k: v for k, v in _L1_attn_all.items() if k in ('W_attn', 'W_proj')}
    del _L1_attn_all

    def _L1_ffn_setup():
        import jax, jax.numpy as jnp
        import numpy as np
        ALPHA = 1.702
        LIMIT = 7.0
        TOPK = 2
        D, I, E = (256, 512, 8)
        B, S = (2, 512)

        def swiglu(x):
            g = x[..., ::2]
            l = x[..., 1::2]
            g = jnp.minimum(g, LIMIT)
            l = jnp.clip(l, -LIMIT, LIMIT)
            return g * jax.nn.sigmoid(ALPHA * g) * (l + 1.0)
        key = jax.random.key(seed)
        ks = jax.random.split(key, 16)
        sc = 0.02
        n = lambda k, shape, s=sc: jax.random.normal(k, shape, dtype=jnp.float32) * s
        return {'x': jax.random.normal(ks[0], (B, S, D), dtype=jnp.float32), 'gate_w': n(ks[1], (E, D)), 'gate_b': n(ks[2], (E,)), 'w1': n(ks[3], (E, D, 2 * I)), 'b1': n(ks[4], (E, 2 * I)), 'w3': n(ks[5], (E, D, 2 * I)), 'b3': n(ks[6], (E, 2 * I)), 'w2': n(ks[7], (E, I, D)), 'b2': n(ks[8], (E, D)), 'sw1': n(ks[9], (D, 2 * I)), 'sb1': n(ks[10], (2 * I,)), 'sw3': n(ks[11], (D, 2 * I)), 'sb3': n(ks[12], (2 * I,)), 'sw2': n(ks[13], (I, D)), 'sb2': n(ks[14], (D,))}
    _L1_ffn_all = _L1_ffn_setup()
    _L1_ffn_in = {k: v for k, v in _L1_ffn_all.items() if k in ('gate_w', 'gate_b', 'w1', 'b1', 'w3', 'b3', 'w2', 'b2', 'sw1', 'sb1', 'sw3', 'sb3', 'sw2', 'sb2')}
    del _L1_ffn_all

    def _L2_xattn_setup():
        import jax, jax.numpy as jnp
        import numpy as np
        D_MODEL = 256
        NUM_HEAD = 16
        HEAD_DIM = D_MODEL // NUM_HEAD
        D_OUT = 256
        B, S = (2, 512)
        key = jax.random.key(seed)
        ks = jax.random.split(key, 11)
        s = 0.02
        return {'Q': jax.random.normal(ks[0], (B, S, D_MODEL), jnp.float32), 'K': jax.random.normal(ks[1], (B, S, D_MODEL), jnp.float32), 'V': jax.random.normal(ks[2], (B, S, D_MODEL), jnp.float32), 'Wq': jax.random.normal(ks[3], (D_MODEL, D_MODEL), jnp.float32) * s, 'bq': jnp.zeros((D_MODEL,), jnp.float32), 'Wk': jax.random.normal(ks[4], (D_MODEL, D_MODEL), jnp.float32) * s, 'bk': jnp.zeros((D_MODEL,), jnp.float32), 'Wv': jax.random.normal(ks[5], (D_MODEL, D_MODEL), jnp.float32) * s, 'bv': jnp.zeros((D_MODEL,), jnp.float32), 'Wo': jax.random.normal(ks[6], (D_MODEL, D_OUT), jnp.float32) * s, 'bo': jnp.zeros((D_OUT,), jnp.float32)}
    _L2_xattn_all = _L2_xattn_setup()
    _L2_xattn_in = {k: v for k, v in _L2_xattn_all.items() if k in ('Wq', 'bq', 'Wk', 'bk', 'Wv', 'bv', 'Wo', 'bo')}
    del _L2_xattn_all

    def _L2_attn_setup():
        import jax, jax.numpy as jnp
        import numpy as np
        D_MODEL = 256
        N_HEADS = 16
        N_KV = 4
        HEAD_DIM = D_MODEL // N_HEADS
        SEQ = 512
        BATCH = 2
        CAP = 50.0
        EPS = 1e-05
        THETA = 10000.0

        def _rms_norm(x, eps=EPS):
            return x * jax.lax.rsqrt(jnp.mean(jnp.square(x), axis=-1, keepdims=True) + eps)

        def _rope_cos_sin(seq_len, head_dim, theta=THETA):
            inv_freq = 1.0 / theta ** (jnp.arange(0, head_dim, 2, dtype=jnp.float32) / head_dim)
            freqs = jnp.arange(seq_len, dtype=jnp.float32)[:, None] * inv_freq[None, :]
            return (jnp.cos(freqs)[None, :, None, :], jnp.sin(freqs)[None, :, None, :])

        def _apply_rope(x, cos, sin):
            d = x.shape[-1] // 2
            x1, x2 = (x[..., :d], x[..., d:])
            return jnp.concatenate([x1 * cos - x2 * sin, x2 * cos + x1 * sin], axis=-1).astype(x.dtype)
        key = jax.random.key(seed)
        ks = jax.random.split(key, 5)
        s = 0.02
        return {'x': jax.random.normal(ks[0], (BATCH, SEQ, D_MODEL), dtype=jnp.float32), 'w_q': jax.random.normal(ks[1], (D_MODEL, N_HEADS * HEAD_DIM), dtype=jnp.float32) * s, 'w_k': jax.random.normal(ks[2], (D_MODEL, N_KV * HEAD_DIM), dtype=jnp.float32) * s, 'w_v': jax.random.normal(ks[3], (D_MODEL, N_KV * HEAD_DIM), dtype=jnp.float32) * s, 'w_o': jax.random.normal(ks[4], (N_HEADS * HEAD_DIM, D_MODEL), dtype=jnp.float32) * s}
    _L2_attn_all = _L2_attn_setup()
    _L2_attn_in = {k: v for k, v in _L2_attn_all.items() if k in ('w_q', 'w_k', 'w_v', 'w_o')}
    del _L2_attn_all

    def _L2_ffn_setup():
        import jax, jax.numpy as jnp
        import numpy as np
        B, S, H, E = (2, 2048, 256, 8)
        SCALE = 0.5
        key = jax.random.key(seed)
        k1, k2 = jax.random.split(key)
        x = jax.random.normal(k1, (B, S, H), dtype=jnp.float32)
        gate_w = jax.random.normal(k2, (E, H), dtype=jnp.float32) * 0.02
        coeff = SCALE * (1.0 + 0.05 * jnp.arange(E, dtype=jnp.float32))
        expert_w = coeff[:, None, None] * jnp.eye(H, dtype=jnp.float32)
        return {'x': x, 'gate_w': gate_w, 'expert_w': expert_w}
    _L2_ffn_all = _L2_ffn_setup()
    _L2_ffn_in = {k: v for k, v in _L2_ffn_all.items() if k in ('gate_w', 'expert_w')}
    del _L2_ffn_all

    def _L3_xattn_setup():
        import jax, jax.numpy as jnp
        import numpy as np
        D_MODEL = 256
        D_HEAD = 64
        NHEADS = 8
        IN_DIM = D_HEAD * NHEADS
        EPS = 1e-05

        def layernorm(x, g, b):
            mu = jnp.mean(x, axis=-1, keepdims=True)
            var = jnp.var(x, axis=-1, keepdims=True)
            return (x - mu) * jax.lax.rsqrt(var + EPS) * g + b
        key = jax.random.key(seed)
        ks = jax.random.split(key, 8)
        B, M, L = (4, 2048, 64)
        x = jax.random.normal(ks[0], (B, M, D_MODEL), dtype=jnp.float32)
        latents = jax.random.normal(ks[1], (B, L, D_MODEL), dtype=jnp.float32)
        s = 1.0 / np.sqrt(D_MODEL)
        Wq = jax.random.normal(ks[2], (D_MODEL, IN_DIM), dtype=jnp.float32) * s
        Wkv = jax.random.normal(ks[3], (D_MODEL, 2 * IN_DIM), dtype=jnp.float32) * s
        Wout = jax.random.normal(ks[4], (IN_DIM, D_MODEL), dtype=jnp.float32) * (1.0 / np.sqrt(IN_DIM))
        gm = jnp.ones((D_MODEL,), jnp.float32)
        bm = jnp.zeros((D_MODEL,), jnp.float32)
        gl = jnp.ones((D_MODEL,), jnp.float32)
        bl = jnp.zeros((D_MODEL,), jnp.float32)
        return {'x': x, 'latents': latents, 'Wq': Wq, 'Wkv': Wkv, 'Wout': Wout, 'gm': gm, 'bm': bm, 'gl': gl, 'bl': bl}
    _L3_xattn_all = _L3_xattn_setup()
    _L3_xattn_in = {k: v for k, v in _L3_xattn_all.items() if k in ('Wq', 'Wkv', 'Wout', 'gm', 'bm', 'gl', 'bl')}
    del _L3_xattn_all

    def _L3_attn_setup():
        import jax, jax.numpy as jnp
        import numpy as np
        DIM = 256
        HEADS = 16
        HEAD_DIM = DIM // HEADS
        THRESH = 0.29514
        SHARP = 15.0
        LN_EPS = 1e-05
        NORM_EPS = 1e-12

        def _l2norm(t):
            n = jnp.sqrt(jnp.sum(t * t, axis=-1, keepdims=True))
            return t / jnp.maximum(n, NORM_EPS)
        key = jax.random.key(seed)
        ks = jax.random.split(key, 8)
        s = 1.0 / np.sqrt(DIM)
        sg = 1.0 / np.sqrt(HEAD_DIM)
        return {'x': jax.random.normal(ks[0], (2, 512, DIM), dtype=jnp.float32), 'Wq': jax.random.uniform(ks[1], (DIM, DIM), jnp.float32, -s, s), 'Wk': jax.random.uniform(ks[2], (DIM, DIM), jnp.float32, -s, s), 'Wv': jax.random.uniform(ks[3], (DIM, DIM), jnp.float32, -s, s), 'gq': jax.random.uniform(ks[4], (HEAD_DIM,), jnp.float32, -sg, sg), 'gk': jax.random.uniform(ks[5], (HEAD_DIM,), jnp.float32, -sg, sg), 'Wo': jax.random.uniform(ks[6], (DIM, DIM), jnp.float32, -s, s), 'bo': jax.random.uniform(ks[7], (DIM,), jnp.float32, -s, s), 'ln_w': jnp.ones((DIM,), jnp.float32), 'ln_b': jnp.zeros((DIM,), jnp.float32)}
    _L3_attn_all = _L3_attn_setup()
    _L3_attn_in = {k: v for k, v in _L3_attn_all.items() if k in ('Wq', 'Wk', 'Wv', 'gq', 'gk', 'Wo', 'bo', 'ln_w', 'ln_b')}
    del _L3_attn_all

    def _L3_ffn_setup():
        import jax, jax.numpy as jnp
        import numpy as np
        DIM = 256
        NUM_EXPERTS = 6
        TOP_K = 2
        HIDDEN = DIM * 2
        key = jax.random.key(seed)
        ks = jax.random.split(key, 7)
        s_in = 1.0 / np.sqrt(DIM)
        s_h = 1.0 / np.sqrt(HIDDEN)
        x = jax.random.normal(ks[0], (4, 512, DIM), dtype=jnp.float32)
        Wg = jax.random.uniform(ks[1], (DIM, NUM_EXPERTS), jnp.float32, -s_in, s_in)
        bg = jax.random.uniform(ks[2], (NUM_EXPERTS,), jnp.float32, -s_in, s_in)
        W1 = jax.random.uniform(ks[3], (NUM_EXPERTS, DIM, HIDDEN), jnp.float32, -s_in, s_in)
        b1 = jax.random.uniform(ks[4], (NUM_EXPERTS, HIDDEN), jnp.float32, -s_in, s_in)
        W2 = jax.random.uniform(ks[5], (NUM_EXPERTS, HIDDEN, DIM), jnp.float32, -s_h, s_h)
        b2 = jax.random.uniform(ks[6], (NUM_EXPERTS, DIM), jnp.float32, -s_h, s_h)
        return {'x': x, 'Wg': Wg, 'bg': bg, 'W1': W1, 'b1': b1, 'W2': W2, 'b2': b2}
    _L3_ffn_all = _L3_ffn_setup()
    _L3_ffn_in = {k: v for k, v in _L3_ffn_all.items() if k in ('Wg', 'bg', 'W1', 'b1', 'W2', 'b2')}
    del _L3_ffn_all
    return {'x': x, 'ctx_1024': ctx_1024, 'mask_BxS2_ff1': mask_BxS2_ff1, 'L0_xattn_wq': _L0_xattn_in['wq'], 'L0_xattn_wk': _L0_xattn_in['wk'], 'L0_xattn_wv': _L0_xattn_in['wv'], 'L0_xattn_ln_gamma': _L0_xattn_in['ln_gamma'], 'L0_xattn_ln_beta': _L0_xattn_in['ln_beta'], 'L0_xattn_dense_w': _L0_xattn_in['dense_w'], 'L0_xattn_dense_b': _L0_xattn_in['dense_b'], 'L0_attn_W_Q': _L0_attn_in['W_Q'], 'L0_attn_W_K': _L0_attn_in['W_K'], 'L0_attn_W_V': _L0_attn_in['W_V'], 'L0_attn_W_O': _L0_attn_in['W_O'], 'L0_ffn_scale': _L0_ffn_in['scale'], 'L0_ffn_centroids': _L0_ffn_in['centroids'], 'L0_ffn_up_w': _L0_ffn_in['up_w'], 'L0_ffn_down_w': _L0_ffn_in['down_w'], 'L1_xattn_ln_g': _L1_xattn_in['ln_g'], 'L1_xattn_ln_b': _L1_xattn_in['ln_b'], 'L1_xattn_cln_g': _L1_xattn_in['cln_g'], 'L1_xattn_cln_b': _L1_xattn_in['cln_b'], 'L1_xattn_Wq': _L1_xattn_in['Wq'], 'L1_xattn_Wkv': _L1_xattn_in['Wkv'], 'L1_xattn_Wo': _L1_xattn_in['Wo'], 'L1_xattn_Wff1': _L1_xattn_in['Wff1'], 'L1_xattn_Wff2': _L1_xattn_in['Wff2'], 'L1_attn_W_attn': _L1_attn_in['W_attn'], 'L1_attn_W_proj': _L1_attn_in['W_proj'], 'L1_ffn_gate_w': _L1_ffn_in['gate_w'], 'L1_ffn_gate_b': _L1_ffn_in['gate_b'], 'L1_ffn_w1': _L1_ffn_in['w1'], 'L1_ffn_b1': _L1_ffn_in['b1'], 'L1_ffn_w3': _L1_ffn_in['w3'], 'L1_ffn_b3': _L1_ffn_in['b3'], 'L1_ffn_w2': _L1_ffn_in['w2'], 'L1_ffn_b2': _L1_ffn_in['b2'], 'L1_ffn_sw1': _L1_ffn_in['sw1'], 'L1_ffn_sb1': _L1_ffn_in['sb1'], 'L1_ffn_sw3': _L1_ffn_in['sw3'], 'L1_ffn_sb3': _L1_ffn_in['sb3'], 'L1_ffn_sw2': _L1_ffn_in['sw2'], 'L1_ffn_sb2': _L1_ffn_in['sb2'], 'L2_xattn_Wq': _L2_xattn_in['Wq'], 'L2_xattn_bq': _L2_xattn_in['bq'], 'L2_xattn_Wk': _L2_xattn_in['Wk'], 'L2_xattn_bk': _L2_xattn_in['bk'], 'L2_xattn_Wv': _L2_xattn_in['Wv'], 'L2_xattn_bv': _L2_xattn_in['bv'], 'L2_xattn_Wo': _L2_xattn_in['Wo'], 'L2_xattn_bo': _L2_xattn_in['bo'], 'L2_attn_w_q': _L2_attn_in['w_q'], 'L2_attn_w_k': _L2_attn_in['w_k'], 'L2_attn_w_v': _L2_attn_in['w_v'], 'L2_attn_w_o': _L2_attn_in['w_o'], 'L2_ffn_gate_w': _L2_ffn_in['gate_w'], 'L2_ffn_expert_w': _L2_ffn_in['expert_w'], 'L3_xattn_Wq': _L3_xattn_in['Wq'], 'L3_xattn_Wkv': _L3_xattn_in['Wkv'], 'L3_xattn_Wout': _L3_xattn_in['Wout'], 'L3_xattn_gm': _L3_xattn_in['gm'], 'L3_xattn_bm': _L3_xattn_in['bm'], 'L3_xattn_gl': _L3_xattn_in['gl'], 'L3_xattn_bl': _L3_xattn_in['bl'], 'L3_attn_Wq': _L3_attn_in['Wq'], 'L3_attn_Wk': _L3_attn_in['Wk'], 'L3_attn_Wv': _L3_attn_in['Wv'], 'L3_attn_gq': _L3_attn_in['gq'], 'L3_attn_gk': _L3_attn_in['gk'], 'L3_attn_Wo': _L3_attn_in['Wo'], 'L3_attn_bo': _L3_attn_in['bo'], 'L3_attn_ln_w': _L3_attn_in['ln_w'], 'L3_attn_ln_b': _L3_attn_in['ln_b'], 'L3_ffn_Wg': _L3_ffn_in['Wg'], 'L3_ffn_bg': _L3_ffn_in['bg'], 'L3_ffn_W1': _L3_ffn_in['W1'], 'L3_ffn_b1': _L3_ffn_in['b1'], 'L3_ffn_W2': _L3_ffn_in['W2'], 'L3_ffn_b2': _L3_ffn_in['b2']}

def reference(x, ctx_1024, mask_BxS2_ff1, L0_xattn_wq, L0_xattn_wk, L0_xattn_wv, L0_xattn_ln_gamma, L0_xattn_ln_beta, L0_xattn_dense_w, L0_xattn_dense_b, L0_attn_W_Q, L0_attn_W_K, L0_attn_W_V, L0_attn_W_O, L0_ffn_scale, L0_ffn_centroids, L0_ffn_up_w, L0_ffn_down_w, L1_xattn_ln_g, L1_xattn_ln_b, L1_xattn_cln_g, L1_xattn_cln_b, L1_xattn_Wq, L1_xattn_Wkv, L1_xattn_Wo, L1_xattn_Wff1, L1_xattn_Wff2, L1_attn_W_attn, L1_attn_W_proj, L1_ffn_gate_w, L1_ffn_gate_b, L1_ffn_w1, L1_ffn_b1, L1_ffn_w3, L1_ffn_b3, L1_ffn_w2, L1_ffn_b2, L1_ffn_sw1, L1_ffn_sb1, L1_ffn_sw3, L1_ffn_sb3, L1_ffn_sw2, L1_ffn_sb2, L2_xattn_Wq, L2_xattn_bq, L2_xattn_Wk, L2_xattn_bk, L2_xattn_Wv, L2_xattn_bv, L2_xattn_Wo, L2_xattn_bo, L2_attn_w_q, L2_attn_w_k, L2_attn_w_v, L2_attn_w_o, L2_ffn_gate_w, L2_ffn_expert_w, L3_xattn_Wq, L3_xattn_Wkv, L3_xattn_Wout, L3_xattn_gm, L3_xattn_bm, L3_xattn_gl, L3_xattn_bl, L3_attn_Wq, L3_attn_Wk, L3_attn_Wv, L3_attn_gq, L3_attn_gk, L3_attn_Wo, L3_attn_bo, L3_attn_ln_w, L3_attn_ln_b, L3_ffn_Wg, L3_ffn_bg, L3_ffn_W1, L3_ffn_b1, L3_ffn_W2, L3_ffn_b2):
    import jax
    import jax.numpy as jnp

    def _L0_xattn_ref(q, k, v, mask, wq, wk, wv, ln_gamma, ln_beta, dense_w, dense_b):
        import jax, jax.numpy as jnp
        import numpy as np
        D_MODEL = 256
        HEADS = 16
        DEPTH = D_MODEL // HEADS
        B, S = (4, 1024)
        EPS_K = 1e-06
        EPS_LN = 1e-06

        def _layernorm(x, g, b):
            m = jnp.mean(x, axis=-1, keepdims=True)
            var = jnp.var(x, axis=-1, keepdims=True)
            return (x - m) * jax.lax.rsqrt(var + EPS_LN) * g + b

        def _split_heads(x):
            bsz, sl, _ = x.shape
            return x.reshape(bsz, sl, HEADS, DEPTH).transpose(0, 2, 1, 3)
        bsz = q.shape[0]
        em = mask[:, None, :, None]
        qh = _split_heads(_layernorm(q @ wq, ln_gamma, ln_beta))
        kh = _split_heads(_layernorm(k @ wk, ln_gamma, ln_beta))
        vh = _split_heads(_layernorm(v @ wv, ln_gamma, ln_beta))
        q_prime = jax.nn.relu(qh) + EPS_K
        k_prime = (jax.nn.relu(kh) + EPS_K) * em
        vh = vh * em
        kv = jnp.einsum('bhnd,bhne->bhde', k_prime, vh)
        z = 1.0 / (jnp.einsum('bhnd,bhd->bhn', q_prime, k_prime.sum(axis=-2)) + EPS_K)
        att = jnp.einsum('bhnd,bhde,bhn->bhne', q_prime, kv, z)
        att = att.reshape(bsz, -1, D_MODEL)
        out = att @ dense_w + dense_b
        return _layernorm(out, ln_gamma, ln_beta)

    def _L0_attn_ref(in_features, W_Q, W_K, W_V, W_O):
        import jax, jax.numpy as jnp
        import numpy as np
        NUM_HEADS = 16
        THETA = 10000.0

        def _rope(x, theta):
            S, d_k = (x.shape[1], x.shape[-1])
            k = jnp.arange(d_k // 2, dtype=jnp.float32)
            inv_freq = theta ** (-2.0 * k / d_k)
            ang = jnp.arange(S, dtype=jnp.float32)[:, None] * inv_freq
            cos = jnp.cos(ang)[None, :, None, :]
            sin = jnp.sin(ang)[None, :, None, :]
            x_even = x[..., 0::2]
            x_odd = x[..., 1::2]
            y_even = cos * x_even - sin * x_odd
            y_odd = sin * x_even + cos * x_odd
            y = jnp.stack([y_even, y_odd], axis=-1)
            return y.reshape(x.shape)
        B, S, D = in_features.shape
        H = NUM_HEADS
        d_k = D // H
        scale = 1.0 / np.sqrt(np.float32(d_k))
        q = jnp.einsum('kd,bsd->bsk', W_Q, in_features).reshape(B, S, H, d_k)
        k = jnp.einsum('kd,bsd->bsk', W_K, in_features).reshape(B, S, H, d_k)
        v = jnp.einsum('vd,bsd->bsv', W_V, in_features).reshape(B, S, H, d_k)
        q = _rope(q, THETA)
        k = _rope(k, THETA)
        q = q.transpose(0, 2, 1, 3)
        k = k.transpose(0, 2, 1, 3)
        v = v.transpose(0, 2, 1, 3)
        scores = jnp.einsum('bhqd,bhkd->bhqk', q, k) * scale
        causal = jnp.tril(jnp.ones((S, S), dtype=bool))
        scores = jnp.where(causal[None, None], scores, -jnp.inf)
        attn = jax.nn.softmax(scores, axis=-1)
        out = jnp.einsum('bhqk,bhkd->bhqd', attn, v)
        out = out.transpose(0, 2, 1, 3).reshape(B, S, D)
        return jnp.einsum('dv,bsv->bsd', W_O, out)

    def _L0_ffn_ref(x, scale, centroids, up_w, down_w):
        import jax, jax.numpy as jnp
        import numpy as np
        EPS = 1e-06
        N_EXPERTS = 8

        def _rms_norm(x, scale, eps=EPS):
            mean_sq = jnp.mean(x.astype(jnp.float32) ** 2, axis=-1, keepdims=True)
            s = scale.astype(jnp.float32) * jax.lax.rsqrt(mean_sq + eps)
            return x * s.astype(x.dtype)

        def _dist2(x, y):
            nx = jnp.sum(x ** 2, axis=-1)[..., :, None]
            ny = jnp.sum(y ** 2, axis=-1)[..., None, :]
            return nx + ny - 2.0 * (x @ y.T)
        skip = x
        xn = _rms_norm(x, scale)
        ids = jnp.argmin(_dist2(xn, centroids), axis=-1)
        out = jnp.zeros_like(x)
        for e in range(N_EXPERTS):
            h = jnp.einsum('bsd,dh->bsh', xn, up_w[e])
            a, g = jnp.split(h, 2, axis=-1)
            y = jnp.einsum('bsh,hd->bsd', a * jax.nn.silu(g), down_w[e])
            out = jnp.where((ids == e)[..., None], y, out)
        return out + skip

    def _L1_xattn_ref(x, context, ln_g, ln_b, cln_g, cln_b, Wq, Wkv, Wo, Wff1, Wff2):
        import jax, jax.numpy as jnp
        import numpy as np
        DIM = 256
        CTX_DIM = 256
        HEADS = 16
        DIM_HEAD = 64
        INNER = HEADS * DIM_HEAD
        FF_INNER = 4 * DIM
        EPS = 1e-05

        def layer_norm(x, g, b):
            mu = jnp.mean(x, axis=-1, keepdims=True)
            var = jnp.var(x, axis=-1, keepdims=True)
            return (x - mu) * jax.lax.rsqrt(var + EPS) * g + b
        scale = DIM_HEAD ** (-0.5)
        xn = layer_norm(x, ln_g, ln_b)
        cn = layer_norm(context, cln_g, cln_b)
        b, n, _ = xn.shape
        q = (xn @ Wq).reshape(b, n, HEADS, DIM_HEAD).transpose(0, 2, 1, 3) * scale
        kv = cn @ Wkv
        k, v = (kv[..., :DIM_HEAD], kv[..., DIM_HEAD:])
        sim = jnp.einsum('bhid,bjd->bhij', q, k)
        attn = jax.nn.softmax(sim, axis=-1)
        out = jnp.einsum('bhij,bjd->bhid', attn, v)
        out = out.transpose(0, 2, 1, 3).reshape(b, n, INNER) @ Wo
        ff = xn @ Wff1
        h, gate = (ff[..., :FF_INNER], ff[..., FF_INNER:])
        out = out + jax.nn.silu(gate) * h @ Wff2
        return out

    def _L1_attn_ref(x, W_attn, W_proj):
        import math
        import jax, jax.numpy as jnp
        import numpy as np
        N_EMBD = 256
        N_HEAD = 16
        N_QUERY_SETS = 4
        B, T = (8, 256)
        Bz, Tz, C = x.shape
        hd = C // N_HEAD
        scale = 1.0 / math.sqrt(hd)
        qkv = x @ W_attn.T
        parts = jnp.split(qkv, N_QUERY_SETS + 2, axis=-1)
        k = parts[-2].reshape(Bz, Tz, N_HEAD, hd).transpose(0, 2, 1, 3)
        v = parts[-1].reshape(Bz, Tz, N_HEAD, hd).transpose(0, 2, 1, 3)
        causal = jnp.tril(jnp.ones((Tz, Tz), dtype=bool))
        outs = []
        for g in range(N_QUERY_SETS):
            q = parts[g].reshape(Bz, Tz, N_HEAD, hd).transpose(0, 2, 1, 3)
            att = jnp.einsum('bhqd,bhkd->bhqk', q, k) * scale
            att = jnp.where(causal, att, -jnp.inf)
            att = jax.nn.softmax(att, axis=-1)
            y = jnp.einsum('bhqk,bhkd->bhqd', att, v)
            outs.append(y.transpose(0, 2, 1, 3).reshape(Bz, Tz, C))
        combined = jnp.concatenate(outs, axis=-1)
        return combined @ W_proj.T

    def _L1_ffn_ref(x, gate_w, gate_b, w1, b1, w3, b3, w2, b2, sw1, sb1, sw3, sb3, sw2, sb2):
        import jax, jax.numpy as jnp
        import numpy as np
        ALPHA = 1.702
        LIMIT = 7.0
        TOPK = 2
        D, I, E = (256, 512, 8)
        B, S = (2, 512)

        def swiglu(x):
            g = x[..., ::2]
            l = x[..., 1::2]
            g = jnp.minimum(g, LIMIT)
            l = jnp.clip(l, -LIMIT, LIMIT)
            return g * jax.nn.sigmoid(ALPHA * g) * (l + 1.0)
        b, s, d = x.shape
        xt = x.reshape(-1, d)
        scores = jax.nn.softmax(xt @ gate_w.T, axis=-1)
        biased = scores + gate_b
        _, idx = jax.lax.top_k(biased, TOPK)
        weights = jnp.take_along_axis(scores, idx, axis=-1)
        comb = (weights[..., None] * jax.nn.one_hot(idx, E, dtype=xt.dtype)).sum(1)

        def body(acc, p):
            ew1, eb1, ew3, eb3, ew2, eb2, ce = p
            h = swiglu((xt @ ew1 + eb1) * (xt @ ew3 + eb3))
            return (acc + ce[:, None] * (h @ ew2 + eb2), None)
        routed, _ = jax.lax.scan(body, jnp.zeros_like(xt), (w1, b1, w3, b3, w2, b2, comb.T))
        shared = swiglu((xt @ sw1 + sb1) * (xt @ sw3 + sb3)) @ sw2 + sb2
        return (routed + shared).reshape(b, s, d)

    def _L2_xattn_ref(Q, K, V, Wq, bq, Wk, bk, Wv, bv, Wo, bo):
        import jax, jax.numpy as jnp
        import numpy as np
        D_MODEL = 256
        NUM_HEAD = 16
        HEAD_DIM = D_MODEL // NUM_HEAD
        D_OUT = 256
        B, S = (2, 512)
        T = jnp.asarray(HEAD_DIM, Q.dtype) ** 0.5
        b = Q.shape[0]
        q = (Q @ Wq + bq) / T
        k = K @ Wk + bk
        v = V @ Wv + bv
        q = q.reshape(b, -1, NUM_HEAD, HEAD_DIM)
        k = k.reshape(b, -1, NUM_HEAD, HEAD_DIM)
        v = v.reshape(b, -1, NUM_HEAD, HEAD_DIM)
        scores = jnp.einsum('bqhd,bkhd->bhqk', q, k)
        attn = jax.nn.softmax(scores, axis=-1)
        out = jnp.einsum('bhqk,bkhd->bqhd', attn, v).reshape(b, -1, D_MODEL)
        return out @ Wo + bo

    def _L2_attn_ref(x, w_q, w_k, w_v, w_o):
        import jax, jax.numpy as jnp
        import numpy as np
        D_MODEL = 256
        N_HEADS = 16
        N_KV = 4
        HEAD_DIM = D_MODEL // N_HEADS
        SEQ = 512
        BATCH = 2
        CAP = 50.0
        EPS = 1e-05
        THETA = 10000.0

        def _rms_norm(x, eps=EPS):
            return x * jax.lax.rsqrt(jnp.mean(jnp.square(x), axis=-1, keepdims=True) + eps)

        def _rope_cos_sin(seq_len, head_dim, theta=THETA):
            inv_freq = 1.0 / theta ** (jnp.arange(0, head_dim, 2, dtype=jnp.float32) / head_dim)
            freqs = jnp.arange(seq_len, dtype=jnp.float32)[:, None] * inv_freq[None, :]
            return (jnp.cos(freqs)[None, :, None, :], jnp.sin(freqs)[None, :, None, :])

        def _apply_rope(x, cos, sin):
            d = x.shape[-1] // 2
            x1, x2 = (x[..., :d], x[..., d:])
            return jnp.concatenate([x1 * cos - x2 * sin, x2 * cos + x1 * sin], axis=-1).astype(x.dtype)
        B, S, _ = x.shape
        q = (x @ w_q).reshape(B, S, N_HEADS, HEAD_DIM)
        k = (x @ w_k).reshape(B, S, N_KV, HEAD_DIM)
        v = (x @ w_v).reshape(B, S, N_KV, HEAD_DIM)
        q = _rms_norm(q)
        k = _rms_norm(k)
        cos, sin = _rope_cos_sin(S, HEAD_DIM)
        q = _apply_rope(q, cos, sin)
        k = _apply_rope(k, cos, sin)
        rep = N_HEADS // N_KV
        k = jnp.repeat(k, rep, axis=2)
        v = jnp.repeat(v, rep, axis=2)
        scores = jnp.einsum('bqhd,bkhd->bhqk', q, k) / np.sqrt(HEAD_DIM).astype(np.float32)
        scores = jnp.tanh(scores.astype(jnp.float32) / CAP) * CAP
        causal = jnp.tril(jnp.ones((S, S), dtype=bool))
        scores = jnp.where(causal[None, None], scores, -jnp.inf)
        probs = jax.nn.softmax(scores, axis=-1)
        y = jnp.einsum('bhqk,bkhd->bqhd', probs, v).reshape(B, S, N_HEADS * HEAD_DIM)
        return y @ w_o

    def _L2_ffn_ref(x, gate_w, expert_w):
        import jax, jax.numpy as jnp
        import numpy as np
        B, S, H, E = (2, 2048, 256, 8)
        SCALE = 0.5
        scores = jnp.einsum('bsh,eh->bse', x, gate_w)
        chosen = jnp.argmax(scores, axis=-1)
        onehot = jax.nn.one_hot(chosen, gate_w.shape[0], dtype=x.dtype)
        expert_out = jnp.einsum('bsh,efh->bsef', x, expert_w)
        return x + jnp.einsum('bsef,bse->bsf', expert_out, onehot)

    def _L3_xattn_ref(x, latents, Wq, Wkv, Wout, gm, bm, gl, bl):
        import jax, jax.numpy as jnp
        import numpy as np
        D_MODEL = 256
        D_HEAD = 64
        NHEADS = 8
        IN_DIM = D_HEAD * NHEADS
        EPS = 1e-05

        def layernorm(x, g, b):
            mu = jnp.mean(x, axis=-1, keepdims=True)
            var = jnp.var(x, axis=-1, keepdims=True)
            return (x - mu) * jax.lax.rsqrt(var + EPS) * g + b
        scale = D_HEAD ** (-0.5)
        xn = layernorm(x, gm, bm)
        ln = layernorm(latents, gl, bl)
        q = ln @ Wq
        kv_input = jnp.concatenate([xn, ln], axis=-2)
        kv = kv_input @ Wkv
        k, v = jnp.split(kv, 2, axis=-1)

        def heads(t):
            B, S, _ = t.shape
            return t.reshape(B, S, NHEADS, D_HEAD).transpose(0, 2, 1, 3)
        q, k, v = (heads(q), heads(k), heads(v))
        q = q / scale
        sim = jnp.einsum('bhid,bhjd->bhij', q, k)
        sim = sim - jax.lax.stop_gradient(jnp.max(sim, axis=-1, keepdims=True))
        attn = jax.nn.softmax(sim, axis=-1)
        out = jnp.einsum('bhij,bhjd->bhid', attn, v)
        B, H, L, dh = out.shape
        out = out.transpose(0, 2, 1, 3).reshape(B, L, H * dh)
        return out @ Wout

    def _L3_attn_ref(x, Wq, Wk, Wv, gq, gk, Wo, bo, ln_w, ln_b):
        import jax, jax.numpy as jnp
        import numpy as np
        DIM = 256
        HEADS = 16
        HEAD_DIM = DIM // HEADS
        THRESH = 0.29514
        SHARP = 15.0
        LN_EPS = 1e-05
        NORM_EPS = 1e-12

        def _l2norm(t):
            n = jnp.sqrt(jnp.sum(t * t, axis=-1, keepdims=True))
            return t / jnp.maximum(n, NORM_EPS)
        B, T, D = x.shape
        mu = jnp.mean(x, axis=-1, keepdims=True)
        var = jnp.mean((x - mu) ** 2, axis=-1, keepdims=True)
        x_norm = (x - mu) / jnp.sqrt(var + LN_EPS) * ln_w + ln_b

        def split_heads(t):
            return t.reshape(B, T, HEADS, HEAD_DIM).transpose(0, 2, 1, 3)
        q = _l2norm(split_heads(x_norm @ Wq))
        k = _l2norm(split_heads(x_norm @ Wk))
        v = split_heads(x @ Wv)
        align = jnp.einsum('bhtd,bhsd->bhts', q, k)
        resonance = jax.nn.sigmoid((align - THRESH) * SHARP)
        gate_q = jnp.einsum('bhtd,d->bht', q, gq)
        gate_k = jnp.einsum('bhsd,d->bhs', k, gk)
        modulation = resonance * gate_q[..., :, None] * gate_k[..., None, :]
        collapse = jnp.einsum('bhts,bhsd->bhtd', modulation, v)
        collapse = collapse.transpose(0, 2, 1, 3).reshape(B, T, D)
        return collapse @ Wo + bo

    def _L3_ffn_ref(x, Wg, bg, W1, b1, W2, b2):
        import jax, jax.numpy as jnp
        import numpy as np
        DIM = 256
        NUM_EXPERTS = 6
        TOP_K = 2
        HIDDEN = DIM * 2
        gate_logits = jnp.einsum('bsd,de->bse', x, Wg) + bg
        topk_w, topk_idx = jax.lax.top_k(gate_logits, TOP_K)
        topk_w = jax.nn.softmax(topk_w, axis=-1)
        combine = jnp.sum(jax.nn.one_hot(topk_idx, NUM_EXPERTS, dtype=x.dtype) * topk_w[..., None], axis=-2)
        h = jnp.einsum('bsd,edh->ebsh', x, W1) + b1[:, None, None, :]
        h = jax.nn.gelu(h, approximate=False)
        y = jnp.einsum('ebsh,ehd->ebsd', h, W2) + b2[:, None, None, :]
        out = jnp.einsum('ebsd,bse->bsd', y, combine)
        return out
    x = x + _L0_xattn_ref(_layernorm(x, axis=-1), ctx_1024, ctx_1024, mask_BxS2_ff1, L0_xattn_wq, L0_xattn_wk, L0_xattn_wv, L0_xattn_ln_gamma, L0_xattn_ln_beta, L0_xattn_dense_w, L0_xattn_dense_b)
    x = x + _L0_attn_ref(_layernorm(x, axis=-1), L0_attn_W_Q, L0_attn_W_K, L0_attn_W_V, L0_attn_W_O)
    x = x + _L0_ffn_ref(_layernorm(x, axis=-1), L0_ffn_scale, L0_ffn_centroids, L0_ffn_up_w, L0_ffn_down_w)
    x = x + _L1_xattn_ref(_layernorm(x, axis=-1), ctx_1024, L1_xattn_ln_g, L1_xattn_ln_b, L1_xattn_cln_g, L1_xattn_cln_b, L1_xattn_Wq, L1_xattn_Wkv, L1_xattn_Wo, L1_xattn_Wff1, L1_xattn_Wff2)
    x = x + _L1_attn_ref(_layernorm(x, axis=-1), L1_attn_W_attn, L1_attn_W_proj)
    x = x + _L1_ffn_ref(_layernorm(x, axis=-1), L1_ffn_gate_w, L1_ffn_gate_b, L1_ffn_w1, L1_ffn_b1, L1_ffn_w3, L1_ffn_b3, L1_ffn_w2, L1_ffn_b2, L1_ffn_sw1, L1_ffn_sb1, L1_ffn_sw3, L1_ffn_sb3, L1_ffn_sw2, L1_ffn_sb2)
    x = x + _L2_xattn_ref(_layernorm(x, axis=-1), ctx_1024, ctx_1024, L2_xattn_Wq, L2_xattn_bq, L2_xattn_Wk, L2_xattn_bk, L2_xattn_Wv, L2_xattn_bv, L2_xattn_Wo, L2_xattn_bo)
    x = x + _L2_attn_ref(_layernorm(x, axis=-1), L2_attn_w_q, L2_attn_w_k, L2_attn_w_v, L2_attn_w_o)
    x = x + _L2_ffn_ref(_layernorm(x, axis=-1), L2_ffn_gate_w, L2_ffn_expert_w)
    x = x + _L3_xattn_ref(ctx_1024, _layernorm(x, axis=-1), L3_xattn_Wq, L3_xattn_Wkv, L3_xattn_Wout, L3_xattn_gm, L3_xattn_bm, L3_xattn_gl, L3_xattn_bl)
    x = x + _L3_attn_ref(_layernorm(x, axis=-1), L3_attn_Wq, L3_attn_Wk, L3_attn_Wv, L3_attn_gq, L3_attn_gk, L3_attn_Wo, L3_attn_bo, L3_attn_ln_w, L3_attn_ln_b)
    x = x + _L3_ffn_ref(_layernorm(x, axis=-1), L3_ffn_Wg, L3_ffn_bg, L3_ffn_W1, L3_ffn_b1, L3_ffn_W2, L3_ffn_b2)
    return x

_drawn_inputs = setup_inputs


def setup_inputs(seed=0):
    import zlib

    import numpy as np

    out = dict(_drawn_inputs(seed))
    spreads = {'L0_xattn_ln_gamma': (1.0, 0.2),
     'L0_xattn_ln_beta': (0.0, 0.1),
     'L0_xattn_dense_b': (0.0, 0.1),
     'L0_ffn_scale': (1.0, 0.2),
     'L1_xattn_ln_g': (1.0, 0.2),
     'L1_xattn_ln_b': (0.0, 0.1),
     'L1_xattn_cln_g': (1.0, 0.2),
     'L1_xattn_cln_b': (0.0, 0.1),
     'L2_xattn_bq': (0.0, 2.0),
     'L2_xattn_bk': (0.0, 2.0),
     'L2_xattn_bv': (0.0, 2.0),
     'L2_xattn_bo': (0.0, 0.8),
     'L3_xattn_gm': (1.0, 0.2),
     'L3_xattn_bm': (0.0, 0.477),
     'L3_xattn_gl': (1.0, 0.2),
     'L3_xattn_bl': (0.0, 0.1),
     'L3_attn_ln_w': (1.0, 0.6),
     'L3_attn_ln_b': (0.0, 0.8)}
    factors = {'L1_ffn_gate_w': 8.0,
     'L1_ffn_gate_b': 8.0,
     'L1_ffn_w1': 8.0,
     'L1_ffn_b1': 8.0,
     'L1_ffn_w3': 8.0,
     'L1_ffn_b3': 8.0,
     'L1_ffn_w2': 8.0,
     'L1_ffn_b2': 57.026,
     'L1_ffn_sw1': 3.436,
     'L1_ffn_sb1': 8.0,
     'L1_ffn_sw3': 3.403,
     'L1_ffn_sb3': 8.0,
     'L1_ffn_sw2': 3.4,
     'L1_ffn_sb2': 29.56,
     'L2_xattn_Wq': 57.841,
     'L2_xattn_Wk': 56.46,
     'L2_attn_w_q': 26.096,
     'L2_attn_w_k': 25.752,
     'L2_ffn_gate_w': 200.0,
     'L3_attn_Wq': 8.0,
     'L3_attn_Wk': 8.0,
     'L3_attn_Wv': 8.0,
     'L3_attn_gq': 8.0,
     'L3_attn_gk': 8.0,
     'L3_attn_Wo': 8.0,
     'L3_attn_bo': 54.048,
     'L3_ffn_bg': 64.0,
     'L3_ffn_b1': 64.0,
     'L3_ffn_b2': 174.957,
     'L2_xattn_Wv': 5.756,
     'L2_xattn_Wo': 3.785,
     'L2_attn_w_v': 8.0,
     'L2_attn_w_o': 8.0,
     'L3_ffn_Wg': 8.0,
     'L3_ffn_W1': 8.0,
     'L3_ffn_W2': 8.0}
    for name, (base, spread) in spreads.items():
        noise = np.random.default_rng([zlib.crc32(name.encode()), seed]).standard_normal(out[name].shape)
        drawn = base * np.exp(spread * noise) if base else spread * noise
        out[name] = jnp.asarray(drawn.astype(out[name].dtype))
    for name, factor in factors.items():
        out[name] = (out[name] * factor).astype(out[name].dtype)
    return out
```

```python
from contextlib import ExitStack

import concourse.bass as bass
import numpy as np
from concourse import mybir

F32 = mybir.dt.float32
ALU = mybir.AluOpType
ACT = mybir.ActivationFunctionType
AX = mybir.AxisListType

P = 128
B, S, D = 32, 32, 256
CTX = 257
NT = B * S // P
C = D // P
TB = P // S
NEG = -1e30
LAYERS = list(range(12))
EXPERTS = {2: (8, 3072), 5: (9, 5136), 11: (6, 2052)}


class Core:

    def __init__(self, nc, es, dram):
        self.nc, self.es, self.dram = nc, es, dram
        self.sems = []
        self.X = self.sb("X", [P, NT, D])
        self.H = self.sb("H", [P, NT, D])
        self.HT = self.sb("HT", [P, C, NT * P])
        self.weights = [self.sb("weights0", [P, 6400]), self.sb("weights1", [P, 10880])]
        self.ident = self.sb("ident", [P, P])
        self.eps = self.sb("eps", [P, 2])
        self.zero = self.sb("zero", [P, 1])
        self.dve_step = Steps(self, "dve_step")
        self.act_step = Steps(self, "act_step")
        self.pool_step = Steps(self, "pool_step")
        self.stats = self.sb("stats", [P, NT, 6])
        self.moments = self.sb("moments", [P, NT, 2])
        self.std = self.sb("std", [P, NT])
        self.rstd = self.sb("rstd", [P, NT])
        self.PS = es.enter_context(nc.psum_tensor("PS", [P, 8, 512], F32))
        self.consts_in = self.sem("consts_in")
        self.eps_set = self.sem("eps_set")
        self.weights_in = [self.sem(f"weights_in{i}") for i in range(12)]
        self.eps5, self.eps6 = self.eps[:, 0:1], self.eps[:, 1:2]
        self.x_in = self.sem("x_in")
        self.expert_in = {k: [self.sem(f"expert_in{k}_{i}") for i in range(2)] for k in EXPERTS}
        self.norm = Norm(self)
        self.flip = Flip(self)
        self.ctx_norm = ContextNorm(self)
        self.sems = []

    def sb(self, name, shape, es=None):
        return (es or self.es).enter_context(self.nc.sbuf_tensor(name, shape, F32))

    def sem(self, name):
        self.sems.append(self.nc.alloc_semaphore(name=name))
        return self.sems[-1]

    def free_sems(self):
        self.nc.clear_and_free_semaphores(self.sems)
        self.sems = []
        self.nc.all_engine_barrier()

    def arena(self, layer):
        return Arena(self, layer)


class Arena:

    def __init__(self, core, layer):
        self.mem, self.at = core.weights[layer % 2], 2 * EXPERTS[layer][1] if layer in EXPERTS else 0

    def take(self, *shape):
        n = 1
        for s in shape:
            n *= s
        out = self.mem[:, self.at:self.at + n]
        self.at += n
        assert self.at <= self.mem.shape[1], self.at
        if len(shape) == 2:
            out = out.rearrange("p (a b) -> p a b", b=shape[1])
        elif len(shape) == 3:
            out = out.rearrange("p (a b c) -> p a b c", b=shape[1], c=shape[2])
        return out


def load_weights(core, sp, layer):
    w, mem = core.dram[f"pack{layer}"], core.weights[layer % 2]
    at = 0
    if layer in EXPERTS:
        width = EXPERTS[layer][1]
        at = 2 * width
    sp.dma_start(mem[:, at:at + w.shape[1]], w).then_inc(core.weights_in[layer], 16)
    if layer in EXPERTS:
        for s in range(2):
            sp.dma_start(mem[:, s * width:(s + 1) * width], core.dram[f"experts{layer}"][s]).then_inc(core.expert_in[layer][s], 16)


class Steps:

    def __init__(self, core, name):
        self.sem, self.n, self.i = core.sem(name), 0, None

    def enter(self, i, per):
        self.i, self.per, self.k = i, per, 0

    def leave(self, trips):
        assert self.k == self.per, (self.k, self.per)
        self.n, self.i = self.n + trips * self.per, None

    def __call__(self, eng, instruction):
        instruction.then_inc(self.sem, 1)
        if self.i is None:
            self.n += 1
            eng.wait_ge(self.sem, self.n)
        else:
            self.k += 1
            eng.wait_ge(self.sem, self.i * self.per + (self.n + self.k))


class Norm:

    def __init__(self, core):
        self.core = core
        self.moments_done = core.sem("norm_moments_done")
        self.std_done = core.sem("norm_std_done")
        self.uses_dve = self.uses_act = 0

    def vector(self, dve, src, dst, rows_done):
        c, nc, dve_step = self.core, self.core.nc, self.core.dve_step
        self.uses_dve += 1
        for t in range(NT):
            done = nc.vector.bn_stats(c.stats[:, t, :], src[:, t, :])
        dve_step(dve, done)
        for t in range(NT):
            done = nc.vector.bn_aggr(c.moments[:, t, :], c.stats[:, t, :])
        done.then_inc(self.moments_done, 1)
        dve.wait_ge(self.std_done, self.uses_dve)
        dve_step(dve, nc.vector.reciprocal(c.rstd[:], c.std[:]))
        for t in range(NT):
            nc.vector.tensor_scalar(dst[:, t, :], src[:, t, :], c.moments[:, t, 0:1], c.rstd[:, t:t + 1],
                                    ALU.subtract, ALU.mult).then_inc(rows_done, 1)

    def scalar(self, act, eps):
        c, nc = self.core, self.core.nc
        self.uses_act += 1
        act.wait_ge(self.moments_done, self.uses_act)
        nc.scalar.activation(c.std[:], c.moments[:, :, 1], ACT.Sqrt, bias=eps).then_inc(self.std_done, 1)


class Flip:

    def __init__(self, core):
        self.core = core
        self.flipped = core.sem("flipped")
        self.copied_act = core.sem("flip_copied_act")
        self.copied_dve = core.sem("flip_copied_dve")
        self.uses = {"pe": 0, "act": 0, "dve": 0}

    def tensor(self, pe, src, rows_done, before):
        c, nc = self.core, self.core.nc
        if self.uses["pe"]:
            self.ready(pe, "pe")
        self.uses["pe"] += 1
        for half in range(2):
            for ch in range(C):
                for t in range(4 * half, 4 * half + 4):
                    pe.wait_ge(rows_done, before + t + 1)
                    last = nc.tensor.transpose(c.PS[:, 2 * half + ch, (t % 4) * P:(t % 4 + 1) * P],
                                               src[:, t, ch * P:(ch + 1) * P], c.ident[:])
                last.then_inc(self.flipped, 1)

    def scalar(self, act, dst, scale=None, bias=None):
        c, nc, n = self.core, self.core.nc, self.uses["act"]
        self.uses["act"] += 1
        for half in range(2):
            act.wait_ge(self.flipped, 4 * n + 2 * half + 1)
            bank, to = c.PS[:, 2 * half, :], dst[:, 0, half * 512:(half + 1) * 512]
            if scale is None:
                last = nc.scalar.copy(to, bank)
            elif bias is None:
                last = nc.scalar.activation(to, bank, ACT.Copy, scale=scale[:, 0:1])
            else:
                last = nc.scalar.activation(to, bank, ACT.Identity, bias=bias[:, 0:1], scale=scale[:, 0:1])
            last.then_inc(self.copied_act, 1)

    def vector(self, dve, dst, scale=None, bias=None):
        c, nc, n = self.core, self.core.nc, self.uses["dve"]
        self.uses["dve"] += 1
        for half in range(2):
            dve.wait_ge(self.flipped, 4 * n + 2 * half + 2)
            bank, to = c.PS[:, 2 * half + 1, :], dst[:, 1, half * 512:(half + 1) * 512]
            if scale is None:
                last = nc.vector.tensor_copy(to, bank)
            elif bias is None:
                last = nc.vector.tensor_scalar(to, bank, scale[:, 1:2], None, ALU.mult)
            else:
                last = nc.vector.tensor_scalar(to, bank, scale[:, 1:2], bias[:, 1:2], ALU.mult, ALU.add)
            last.then_inc(self.copied_dve, 1)

    def ready(self, eng, key):
        eng.wait_ge(self.copied_act, 2 * self.uses[key])
        eng.wait_ge(self.copied_dve, 2 * self.uses[key])


def bcast(ap, axis, n):
    shape = list(ap.shape)
    shape.insert(axis, n)
    return ap.unsqueeze(axis).to_broadcast(shape)


class SelfAttention:

    def __init__(self, core, es, name, kind, scale):
        self.core, self.name, self.kind, self.scale = core, name, kind, scale
        sb = lambda n, shape: core.sb(f"{name}_{n}", shape, es)
        sem = lambda n: core.sem(f"{name}_{n}")
        self.Q, self.K, self.V = (sb(n, [P, NT, D]) for n in "QKV")
        self.QT, self.KT = (sb(n, [P, C, NT * P]) for n in ("QT", "KT"))
        self.spread = [sb(f"spread{i}", [P, C, TB, 8, S]) for i in range(2)]
        self.scores = [sb(f"scores{i}", [P, 16, S]) for i in range(2)]
        self.probs = [sb(f"probs{i}", [P, 16, S]) for i in range(2)]
        self.probsT = [sb(f"probsT{i}", [P, 16, S]) for i in range(2)]
        self.top = [sb(f"top{i}", [P, 16]) for i in range(2)]
        self.factor = sb("factor", [P, NT, 16])
        self.qk_done, self.v_done = sem("qk_done"), sem("v_done")
        self.qk_copied, self.v_copied = sem("qk_copied"), sem("v_copied")
        self.q_rows, self.k_rows = sem("q_rows"), sem("k_rows")
        self.spread_done, self.scores_done = sem("spread_done"), sem("scores_done")
        self.scores_read = sem("scores_read")
        self.shifted, self.probs_done = sem("shifted"), sem("probs_done")
        self.probsT_done, self.out_done, self.out_rows = sem("probsT_done"), sem("out_done"), sem("out_rows")
        self.proj_done = sem("proj_done")


    def project(self, pe, xT, xT_v, wqk, wv):
        nc, PS = self.core.nc, self.core.PS
        for t in range(NT):
            if t >= 2:
                pe.wait_ge(self.qk_copied, t - 1)
            for c in range(C):
                last = nc.tensor.matmul(PS[:, 4 + t % 2, :], xT[:, c, t * P:(t + 1) * P], wqk[:, c, :], start=(c == 0), stop=(c == 1))
            last.then_inc(self.qk_done, 1)
            if t >= 2:
                pe.wait_ge(self.v_copied, t - 1)
            for c in range(C):
                last = nc.tensor.matmul(PS[:, 6 + t % 2, 0:D], xT_v[:, c, t * P:(t + 1) * P], wv[:, c, :], start=(c == 0), stop=(c == 1))
            last.then_inc(self.v_done, 1)

    def copy_qk(self, act):
        nc, PS = self.core.nc, self.core.PS
        for t in range(NT):
            act.wait_ge(self.qk_done, t + 1)
            nc.scalar.copy(self.Q[:, t, :], PS[:, 4 + t % 2, 0:D])
            nc.scalar.copy(self.K[:, t, :], PS[:, 4 + t % 2, D:2 * D]).then_inc(self.qk_copied, 1)

    def copy_v(self, dve):
        nc, PS = self.core.nc, self.core.PS
        for t in range(NT):
            dve.wait_ge(self.v_done, t + 1)
            nc.vector.tensor_copy(self.V[:, t, :], PS[:, 6 + t % 2, 0:D]).then_inc(self.v_copied, 1)

    def flip_tensor(self, pe):
        self.core.flip.tensor(pe, self.Q, self.q_rows, 0)
        self.core.flip.tensor(pe, self.K, self.k_rows, 0)


    def spread_keys(self, pool, head_of):
        nc, flip = self.core.nc, self.core.flip
        for t in range(NT):
            if t >= 2:
                pool.wait_ge(self.scores_done, t - 1)
            for c in range(C):
                last = nc.gpsimd.tensor_tensor(self.spread[t % 2][:, c],
                                               bcast(self.KT[:, c, t * P:(t + 1) * P].rearrange("p (b k) -> p b k", k=S), 2, 8),
                                               bcast(bcast(head_of, 1, TB), 3, S), ALU.mult)
            last.then_inc(self.spread_done, 1)

    def attend_tensor(self, pe):
        nc, PS = self.core.nc, self.core.PS
        for t in range(NT + 1):
            if t < NT:
                pe.wait_ge(self.spread_done, t + 1)
                if t >= 2:
                    pe.wait_ge(self.scores_read, t - 1)
                for c in range(C):
                    for b in range(TB):
                        last = nc.tensor.matmul(PS[b * S:(b + 1) * S, 4 + t % 2, c * 256:(c + 1) * 256],
                                                self.QT[:, c, t * P + b * S:t * P + (b + 1) * S],
                                                self.spread[t % 2][:, c, b].rearrange("p h k -> p (h k)"), start=True, stop=True)
                last.then_inc(self.scores_done, 1)
            if t >= 1:
                u = t - 1
                pe.wait_ge(self.probsT_done, u + 1)
                if u >= 2:
                    pe.wait_ge(self.out_rows, u - 1)
                for h in range(16):
                    for b in range(TB):
                        rows = slice(b * S, (b + 1) * S)
                        last = nc.tensor.matmul(PS[rows, 6 + u % 2, h * 16:(h + 1) * 16], self.probsT[u % 2][rows, h, :],
                                                self.V[rows, u, h * 16:(h + 1) * 16], start=True, stop=True)
                last.then_inc(self.out_done, 1)

    def attend_scalar(self, act):
        nc, PS = self.core.nc, self.core.PS
        for t in range(NT):
            i = t % 2
            bank = PS[:, 4 + i, :].rearrange("p (h k) -> p h k", k=S)
            if self.kind == "resonance":
                act.wait_ge(self.scores_done, t + 1)
                if t >= 2:
                    act.wait_ge(self.probsT_done, t - 1)
                nc.scalar.activation(self.probs[i][:], bank, ACT.Sigmoid, scale=self.scale,
                                     bias=self.resonance_bias).then_inc(self.scores_read, 1)
                continue
            if self.kind == "capped":
                act.wait_ge(self.scores_done, t + 1)
                if t >= 2:
                    act.wait_ge(self.probs_done, t - 1)
                nc.scalar.activation(self.scores[i][:], bank, ACT.Tanh, scale=self.tanh_scale).then_inc(self.scores_read, 1)
            act.wait_ge(self.shifted, t + 1)
            if t >= 2:
                act.wait_ge(self.probsT_done, t - 1)
            nc.scalar.activation(self.probs[i][:], self.scores[i][:], ACT.Exp, scale=self.scale).then_inc(self.probs_done, 1)

    def attend_vector(self, dve, causal):
        nc, PS, step = self.core.nc, self.core.PS, self.core.dve_step
        for t in range(NT + 2):
            if t < NT and self.kind != "resonance":
                s = self.scores[t % 2]
                if self.kind == "capped":
                    dve.wait_ge(self.scores_read, t + 1)
                    step(dve, nc.vector.tensor_tensor(s[:], s[:], bcast(causal, 1, 16), ALU.add))
                else:
                    dve.wait_ge(self.scores_done, t + 1)
                    if t >= 2:
                        dve.wait_ge(self.probs_done, t - 1)
                    last = nc.vector.tensor_tensor(s[:], PS[:, 4 + t % 2, :].rearrange("p (h k) -> p h k", k=S),
                                                   bcast(causal, 1, 16), ALU.add)
                    last.then_inc(self.scores_read, 1)
                    dve.wait_ge(self.scores_read, t + 1)
                step(dve, nc.vector.reduce_max(self.top[t % 2][:], s[:], AX.X))
                nc.vector.tensor_tensor(s[:], s[:], bcast(self.top[t % 2][:], 2, S), ALU.subtract).then_inc(self.shifted, 1)
            if 1 <= t <= NT:
                u = t - 1
                p = self.probs[u % 2]
                if u >= 2:
                    dve.wait_ge(self.out_done, u - 1)
                if self.kind == "resonance":
                    dve.wait_ge(self.scores_read, u + 1)
                else:
                    dve.wait_ge(self.probs_done, u + 1)
                    step(dve, nc.vector.reduce_sum(self.factor[:, u, :], p[:], AX.X))
                    step(dve, nc.vector.reciprocal(self.factor[:, u, :], self.factor[:, u, :]))
                nc.vector.transpose(self.probsT[u % 2][:].rearrange("p h k -> p (h k)"),
                                    p[:].rearrange("p h k -> p (h k)")).then_inc(self.probsT_done, 1)
            if t >= 2:
                u = t - 2
                dve.wait_ge(self.out_done, u + 1)
                nc.vector.tensor_tensor(self.core.H[:, u, :].rearrange("p (h d) -> p h d", d=16),
                                        PS[:, 6 + u % 2, 0:D].rearrange("p (h d) -> p h d", d=16),
                                        bcast(self.factor[:, u, :], 2, 16), ALU.mult).then_inc(self.out_rows, 1)


    def output_tensor(self, pe, wo):
        nc, PS = self.core.nc, self.core.PS
        self.core.flip.tensor(pe, self.core.H, self.out_rows, 0)
        self.core.flip.ready(pe, "pe")
        for t in range(NT):
            for c in range(C):
                last = nc.tensor.matmul(PS[:, 4 + t // 2, (t % 2) * D:(t % 2 + 1) * D], self.core.HT[:, c, t * P:(t + 1) * P],
                                        wo[:, c, :], start=(c == 0), stop=(c == 1))
            if t % 2:
                last.then_inc(self.proj_done, 1)

    def output_vector(self, dve, bias=None):
        nc, PS, X = self.core.nc, self.core.PS, self.core.X
        for j in range(NT // 2):
            x = X[:, 2 * j:2 * j + 2, :]
            if bias is not None:
                self.core.dve_step(dve, nc.vector.tensor_tensor(x, x, bcast(bias, 1, 2), ALU.add))
            dve.wait_ge(self.proj_done, j + 1)
            nc.vector.tensor_tensor(x, PS[:, 4 + j, :].rearrange("p (t d) -> p t d", t=2), x, ALU.add)


def rotate(core, dve, first, second, t1, t2, cos, sin, done):
    nc, step = core.nc, core.dve_step
    cos, sin = (bcast(bcast(x, 1, NT), 2, 16) for x in (cos, sin))
    nc.vector.tensor_tensor(t1, first, sin, ALU.mult)
    nc.vector.tensor_tensor(t2, second, sin, ALU.mult)
    nc.vector.tensor_tensor(first, first, cos, ALU.mult)
    step(dve, nc.vector.tensor_tensor(second, second, cos, ALU.mult))
    nc.vector.tensor_tensor(first, first, t2, ALU.subtract)
    last = nc.vector.tensor_tensor(second, second, t1, ALU.add)
    last.then_inc(done, NT)
    dve.wait_ge(done, NT)


def at_least(eng, sem, value):
    if not isinstance(value, int) or value > 0:
        eng.wait_ge(sem, value)


class Experts:

    def __init__(self, core, es, name, layer, kind, n, width):
        self.core, self.name, self.kind, self.n, self.layer, self.width = core, name, kind, n, layer, width
        sb = lambda x, shape: core.sb(f"{name}_{x}", shape, es)
        sem = lambda x: core.sem(f"{name}_{x}")
        self.pairs = 2 if kind == "swiglu" else 1
        self.per_half = 4 * self.pairs
        self.hidden = [sb(f"hidden{i}", [P, 4, 512]) for i in range(2)]
        self.side = [sb(f"side{i}", [P, 512]) for i in range(2)]
        if kind == "swiglu":
            self.product = [sb(f"product{i}", [P, 512]) for i in range(2)]
            self.gated = [sb(f"gated{i}", [P, 512]) for i in range(2)]
            self.sigmoid = [sb(f"sigmoid{i}", [P, 512]) for i in range(2)]
            self.gate_done, self.sigmoid_done = sem("gate_done"), sem("sigmoid_done")
        self.up_done, self.side_done = sem("up_done"), sem("side_done")
        self.hidden_done, self.down_done, self.summed = sem("hidden_done"), sem("down_done"), sem("summed")
        mem = core.weights[layer % 2]
        self.slots = []
        for s in range(2):
            at = s * width
            part = {}
            for key, shape in self.parts():
                m = int(np.prod(shape))
                part[key] = mem[:, at:at + m]
                if len(shape) == 2:
                    part[key] = part[key].rearrange("p (c n) -> p c n", c=shape[0])
                at += m
            assert at == (s + 1) * width, (at, width)
            self.slots.append(part)

    def parts(self):
        if self.kind == "glu":
            return [("up", (C, 1024)), ("down", (4, D))]
        if self.kind == "swiglu":
            return [("up1", (C, 1024)), ("up3", (C, 1024)), ("down", (4, D)), ("b1", (8,)), ("b3", (8,))]
        return [("up", (C, 512)), ("down", (4, D)), ("b1", (4,))]

    def each(self, eng, step, after):
        step(0, 0)
        pairs = (self.n - 1) // 2
        with eng.Fori(0, pairs) as i:
            after_loop = self.turn(eng, i, pairs)
            step(2 * i + 1, 1)
            step(2 * i + 2, 0)
            after_loop()
        if (self.n - 1) % 2:
            step(self.n - 1, 1)
        after()

    def turn(self, eng, i, trips):
        if eng is not self.core.nc.vector or not self.own_steps:
            return lambda: None
        self.core.dve_step.enter(i, 2 * self.own_steps)
        return lambda: self.core.dve_step.leave(trips)


    def load(self, sp):
        dram, mem, width = self.core.dram[f"experts{self.layer}"], self.core.weights[self.layer % 2], self.width
        pairs = (self.n - 1) // 2

        def reload(e, slot):
            sp.wait_ge(self.down_done, 8 * e - 8)
            sp.dma_start(mem[:, slot * width:(slot + 1) * width], dram[e]).then_inc(self.core.expert_in[self.layer][slot], 16)

        for e in range(2, min(self.n, 4)):
            reload(e, e % 2)
        if self.n > 4:
            left = self.n - 4
            with sp.Fori(0, left // 2) as i:
                for j in range(2):
                    reload(2 * i + (4 + j), j)
            if left % 2:
                reload(self.n - 1, 0)


    def tensor(self, pe, xT):
        self.pe, self.xT = pe, xT
        self.each(pe, self.step_tensor, lambda: self.down(self.n - 1, (self.n - 1) % 2, 1))

    def step_tensor(self, e, slot):
        self.pe.wait_ge(self.core.expert_in[self.layer][slot], 8 * e + (16 - 8 * slot))
        self.up(e, slot, 0)
        if not isinstance(e, int) or e > 0:
            self.down(e - 1, 1 - slot, 1)
        self.up(e, slot, 1)
        self.down(e, slot, 0)

    def up(self, e, slot, half):
        nc, PS, w = self.core.nc, self.core.PS, self.slots[slot]
        x = self.xT[:, :, half * 512:(half + 1) * 512]
        for u in range(self.per_half):
            n = e * (2 * self.per_half) + half * self.per_half + u
            at_least(self.pe, self.hidden_done, n - 1)
            bank = 2 * (u % 2)
            m, pair = u // self.pairs, u % self.pairs
            if self.kind == "glu":
                mats = [w["up"][:, :, m * P:(m + 1) * P], w["up"][:, :, 512 + m * P:512 + (m + 1) * P]]
            elif self.kind == "swiglu":
                cols = slice(512 * pair + m * P, 512 * pair + (m + 1) * P)
                mats = [w["up1"][:, :, cols], w["up3"][:, :, cols]]
            else:
                mats = [w["up"][:, :, m * P:(m + 1) * P]]
            for k, mat in enumerate(mats):
                for c in range(C):
                    last = nc.tensor.matmul(PS[:, bank + k, :], mat[:, c, :], x[:, c, :], start=(c == 0), stop=(c == 1))
            last.then_inc(self.up_done, 1)

    def down(self, e, slot, half):
        nc, PS = self.core.nc, self.core.PS
        self.pe.wait_ge(self.hidden_done, e * (2 * self.per_half) + (half + 1) * self.per_half)
        for t in range(4):
            d = e * 8 + (4 * half + t)
            at_least(self.pe, self.summed, d - 3)
            for m in range(4):
                last = nc.tensor.matmul(PS[:, 4 + t, 0:D], self.hidden[half][:, m, t * P:(t + 1) * P],
                                        self.slots[slot]["down"][:, m, :], start=(m == 0), stop=(m == 3))
            last.then_inc(self.down_done, 1)


    def scalar(self, act):
        self.act = act
        self.each(act, self.step_scalar, lambda: None)

    def step_scalar(self, e, slot):
        nc, PS, act, w = self.core.nc, self.core.PS, self.act, self.slots[slot]
        for u in range(2 * self.per_half):
            n = e * (2 * self.per_half) + u
            bank, half, m = 2 * (u % 2), u // self.per_half, u % self.per_half // self.pairs
            act.wait_ge(self.up_done, n + 1)
            if self.kind == "glu":
                at_least(act, self.hidden_done, n - 1)
                nc.scalar.activation(self.side[u % 2][:], PS[:, bank + 1, :], ACT.Silu).then_inc(self.side_done, 1)
            elif self.kind == "gelu":
                if u % self.per_half == 0:
                    at_least(act, self.down_done, e * 8 + (4 * half - 4))
                nc.scalar.activation(self.hidden[half][:, m, :], PS[:, bank, :], ACT.Gelu,
                                     bias=w["b1"][:, m:m + 1]).then_inc(self.hidden_done, 1)
            else:
                pair = u % 2
                at_least(act, self.hidden_done, n - 1)
                b = w["b1"][:, 4 * pair + m:4 * pair + m + 1]
                nc.scalar.activation(self.side[u % 2][:], PS[:, bank, :], ACT.Identity, bias=b).then_inc(self.side_done, 1)
                if pair == 0:
                    block = e * 8 + u // 2
                    act.wait_ge(self.gate_done, block + 1)
                    at_least(act, self.hidden_done, n - 2)
                    nc.scalar.activation(self.sigmoid[u // 2 % 2][:], self.gated[u // 2 % 2][:], ACT.Sigmoid,
                                         scale=1.702).then_inc(self.sigmoid_done, 1)


    def vector(self, dve, acc, gate):
        self.dve, self.acc, self.gate = dve, acc, gate
        self.own_steps = {"glu": 0, "gelu": 0, "swiglu": 4 * 8}[self.kind]
        self.each(dve, self.step_vector, lambda: self.add(self.n - 1, 1))
        dve.wait_ge(self.summed, 8 * self.n)

    def step_vector(self, e, slot):
        self.units(e, slot, 0)
        if not isinstance(e, int) or e > 0:
            self.add(e - 1, 1)
        self.units(e, slot, 1)
        self.add(e, 0)

    def units(self, e, slot, half):
        nc, PS, dve, w, step = self.core.nc, self.core.PS, self.dve, self.slots[slot], self.core.dve_step
        if self.kind == "gelu":
            return
        at_least(dve, self.down_done, e * 8 + (4 * half - 4))
        for u in range(self.per_half):
            n = e * (2 * self.per_half) + half * self.per_half + u
            bank, m, i = 2 * (u % 2), u // self.pairs, u % 2
            dve.wait_ge(self.side_done, n + 1)
            if self.kind == "glu":
                nc.vector.tensor_tensor(self.hidden[half][:, m, :], PS[:, bank, :], self.side[i][:], ALU.mult).then_inc(self.hidden_done, 1)
                continue
            block = e * 8 + (half * 4 + m)
            j = m % 2
            b = w["b3"][:, 4 * i + m:4 * i + m + 1]
            product = nc.vector.scalar_tensor_tensor(self.product[i][:], PS[:, bank + 1, :], b, self.side[i][:], ALU.add, ALU.mult)
            step(dve, product)
            if i == 0:
                at_least(dve, self.sigmoid_done, block - 1)
                nc.vector.tensor_scalar(self.gated[j][:], self.product[0][:], 7.0, None, ALU.min).then_inc(self.gate_done, 1)
                dve.wait_ge(self.gate_done, block + 1)
                dve.sem_inc(self.hidden_done, 1)
            else:
                step(dve, nc.vector.tensor_scalar(self.product[1][:], self.product[1][:], -7.0, 7.0, ALU.max, ALU.min))
                step(dve, nc.vector.scalar_tensor_tensor(self.product[1][:], self.product[1][:], 1.0, self.gated[j][:], ALU.add, ALU.mult))
                dve.wait_ge(self.sigmoid_done, block + 1)
                nc.vector.tensor_tensor(self.hidden[half][:, m, :], self.product[1][:], self.sigmoid[j][:], ALU.mult).then_inc(self.hidden_done, 1)

    def add(self, e, half):
        nc, PS, dve = self.core.nc, self.core.PS, self.dve
        at_least(dve, self.summed, e * 8 + (4 * half - 4))
        for t in range(4):
            d = e * 8 + (4 * half + t)
            tile = 4 * half + t
            dve.wait_ge(self.down_done, d + 1)
            e_col = slice(e, e + 1) if isinstance(e, int) else bass.ds(e, 1)
            nc.vector.scalar_tensor_tensor(self.acc[:, tile, :], PS[:, 4 + t, 0:D], self.gate[:, tile, e_col], self.acc[:, tile, :],
                                           ALU.mult, ALU.add).then_inc(self.summed, 1)


def first_best(core, dve, values, number, best, place, chosen):
    nc, step = core.nc, core.dve_step
    n = values.shape[2]
    step(dve, nc.vector.reduce_max(best[:], values[:], AX.X))
    step(dve, nc.vector.tensor_tensor(chosen[:], values[:], bcast(best[:], 2, n), ALU.is_equal))
    step(dve, nc.vector.tensor_tensor(chosen[:], chosen[:], bcast(number, 1, NT), ALU.mult))
    step(dve, nc.vector.tensor_reduce(place[:], chosen[:], AX.X, ALU.min))
    step(dve, nc.vector.tensor_tensor(chosen[:], bcast(number, 1, NT), bcast(place[:], 2, n), ALU.is_equal))


def router_tensor(core, pe, xT, wg, done):
    nc, PS, n = core.nc, core.PS, wg.shape[2]
    for t in range(NT):
        for c in range(C):
            last = nc.tensor.matmul(PS[:, 4, t * n:(t + 1) * n], xT[:, c, t * P:(t + 1) * P], wg[:, c, :], start=(c == 0), stop=(c == 1))
    last.then_inc(done, 1)


class OutputBias:

    def __init__(self, core, es, name, n):
        self.core, self.n = core, n
        self.gateT = core.sb(f"{name}_gateT", [n, NT * P], es)
        self.flipped, self.copied, self.done, self.added = (core.sem(f"{name}_bias_{x}") for x in ("flipped", "copied", "done", "added"))

    def tensor(self, pe, gate, gate_done, b2):
        nc, PS = self.core.nc, self.core.PS
        pe.wait_ge(gate_done, 1)
        for t in range(NT):
            last = nc.tensor.transpose(PS[0:self.n, 4 + t // 4, (t % 4) * P:(t % 4 + 1) * P], gate[:, t, :], self.core.ident[:])
        last.then_inc(self.flipped, 1)
        pe.wait_ge(self.copied, 1)
        for t in range(NT):
            last = nc.tensor.matmul(PS[:, 4 + t // 2, (t % 2) * D:(t % 2 + 1) * D], self.gateT[:, t * P:(t + 1) * P], b2[0:self.n, :],
                                    start=True, stop=True)
        last.then_inc(self.done, 1)
        pe.wait_ge(self.added, 1)

    def vector(self, dve):
        nc, PS, X = self.core.nc, self.core.PS, self.core.X
        dve.wait_ge(self.flipped, 1)
        nc.vector.tensor_copy(self.gateT[:], PS[0:self.n, 4:6, :].rearrange("e a n -> e (a n)")).then_inc(self.copied, 1)
        dve.wait_ge(self.done, 1)
        nc.vector.tensor_tensor(X[:], PS[:, 4:8, :].rearrange("p a (t d) -> p (a t) d", d=D), X[:], ALU.add).then_inc(self.added, 1)
        dve.wait_ge(self.added, 1)


def exists(b):
    return not isinstance(b, int) or b < B


def over_batches(eng, first, turn, last, enter=None, leave=None):
    first()
    trips = (B - 4) // 2
    with eng.Fori(0, trips) as i:
        if enter:
            enter(i)
        turn(2 * i, 0)
        turn(2 * i + 1, 1)
        if leave:
            leave(trips)
    for b in range(2 * trips, B - 1):
        turn(b, b % 2)
    last(B - 1, 1)


class ContextNorm:

    def __init__(self, core):
        self.core = core
        self.mean, self.rstd = core.sb("ctx_mean", [P, B, 2]), core.sb("ctx_rstd", [P, B, 2])
        self.shift = core.sb("ctx_shift", [P, B, 2])
        self.last, self.lastT = core.sb("ctx_last", [B, D]), core.sb("ctx_lastT", [P, C, B])
        self.slot_in = [core.sem("ctx_slot_in0"), core.sem("ctx_slot_in1")]
        self.last_in, self.stats_done = core.sem("ctx_last_in"), core.sem("ctx_stats_done")
        self.spread_done, self.std_done = core.sem("ctx_spread_done"), core.sem("ctx_std_done")
        self.ready, self.flipped, self.lastT_done = core.sem("ctx_ready"), core.sem("ctx_flipped"), core.sem("ctx_lastT_done")
        self.computed, self.loads = False, 0

    def allocate(self, es, name):
        self.stats = self.core.sb(name + "_ctx_stats", [P, B, 2, 6], es)
        self.stats_last, self.moments_last = self.core.sb(name + "_ctx_stats_last", [B, 6], es), self.core.sb(name + "_ctx_moments_last", [B, 2], es)
        self.std, self.std_last = self.core.sb(name + "_ctx_std", [P, B, 2], es), self.core.sb(name + "_ctx_std_last", [B, 1], es)
        self.gap = self.core.sb(name + "_ctx_gap", [P, B, 2], es)

    def load(self, sp, slots):
        ctx = self.core.dram["ctx"]
        tile = lambda b: ctx[b, 0:2 * P, :].rearrange("(h p) d -> p h d", p=P)
        sp.dma_start(self.last[:], ctx[:, CTX - 1, :]).then_inc(self.last_in, 16)
        for j in range(2):
            sp.dma_start(slots[j][:], tile(j)).then_inc(self.slot_in[j], 16)
        with sp.Fori(0, B // 2 - 1) as i:
            for j in range(2):
                sp.wait_ge(self.stats_done, 2 * i + (j + 1))
                sp.dma_start(slots[j][:], tile(2 * i + (j + 2))).then_inc(self.slot_in[j], 16)
        for j in range(2):
            sp.wait_ge(self.stats_done, B - 1 + j)
            sp.dma_start(slots[j][:], tile(j)).then_inc(self.slot_in[j], 16)

    def vector_stats(self, dve, slots):
        nc, step = self.core.nc, self.core.dve_step
        with dve.Fori(0, B // 2) as i:
            for j in range(2):
                dve.wait_ge(self.slot_in[j], 16 * i + 16)
                for h in range(2):
                    done = nc.vector.bn_stats(self.stats[:, 2 * i + j, h, :], slots[j][:, h, :])
                done.then_inc(self.stats_done, 1)
        dve.wait_ge(self.stats_done, B)
        dve.wait_ge(self.last_in, 16)
        step(dve, nc.vector.bn_stats(self.stats_last[:], self.last[:]))
        m0, s0, m1, s1 = (self.stats[:, :, :, n] for n in (1, 2, 4, 5))
        nc.vector.bn_aggr(self.moments_last[:], self.stats_last[:])
        nc.vector.tensor_tensor(self.gap[:], m0, m1, ALU.subtract)
        step(dve, nc.vector.tensor_tensor(self.mean[:], m0, m1, ALU.add))
        nc.vector.tensor_scalar(self.mean[:], self.mean[:], 0.5, None, ALU.mult)
        step(dve, nc.vector.tensor_tensor(self.std[:], s0, s1, ALU.add))
        step(dve, nc.vector.tensor_tensor(self.gap[:], self.gap[:], self.gap[:], ALU.mult))
        step(dve, nc.vector.tensor_scalar(self.gap[:], self.gap[:], 0.25, None, ALU.mult))
        nc.vector.scalar_tensor_tensor(self.std[:], self.std[:], 1.0 / D, self.gap[:], ALU.mult, ALU.add).then_inc(self.spread_done, 1)

    def vector_finish(self, dve):
        nc, step = self.core.nc, self.core.dve_step
        dve.wait_ge(self.std_done, 1)
        nc.vector.reciprocal(self.rstd[:], self.std[:])
        step(dve, nc.vector.reciprocal(self.std_last[:], self.std_last[:]))
        nc.vector.scalar_tensor_tensor(self.shift[:], self.mean[:], -1.0, self.rstd[:], ALU.mult, ALU.mult)
        nc.vector.tensor_scalar(self.last[:], self.last[:], self.moments_last[:, 0:1], self.std_last[:], ALU.subtract, ALU.mult).then_inc(self.ready, 1)
        dve.wait_ge(self.flipped, 1)
        nc.vector.tensor_copy(self.lastT[:], self.core.PS[:, 7, 0:C * B].rearrange("p (c b) -> p c b", c=C)).then_inc(self.lastT_done, 1)
        dve.wait_ge(self.lastT_done, 1)

    def scalar(self, act):
        nc = self.core.nc
        act.wait_ge(self.spread_done, 1)
        nc.scalar.activation(self.std_last[:], self.moments_last[:, 1:2], ACT.Sqrt, bias=self.core.eps5[0:B, :])
        nc.scalar.activation(self.std[:], self.std[:], ACT.Sqrt, bias=self.core.eps5).then_inc(self.std_done, 1)

    def tensor(self, pe):
        nc = self.core.nc
        pe.wait_ge(self.ready, 1)
        for c in range(C):
            done = nc.tensor.transpose(self.core.PS[:, 7, c * B:(c + 1) * B], self.last[:, c * P:(c + 1) * P], self.core.ident[0:B, 0:B])
        done.then_inc(self.flipped, 1)
        pe.wait_ge(self.lastT_done, 1)


def l0_cross(core, load_next):
    nc, PS, norm, flip, dve_step = core.nc, core.PS, core.norm, core.flip, core.dve_step
    KVW = P + 8
    RW = P + 2
    w = core.arena(0)
    wqkv = w.take(6, D)
    dense = w.take(C, D)
    gamma, beta, dense_b = w.take(D), w.take(D), w.take(D)
    head_of = w.take(8)
    same_head = w.take(P)
    em_in = w.take(B, 2)
    em_left_in = w.take(1)
    cleft = w.take(C, B)
    with ExitStack() as es:
        sb = lambda name, shape: core.sb("l0x_" + name, shape, es)
        ctxT = [sb(f"ctxT{i}", [P, C, CTX]) for i in range(2)]
        wsum, sq = sb("wsum", [P, 6]), sb("sq", [P, NT, D])
        em = sb("em", [P, B, 2, 2])
        eml = sb("eml", [B, 2])
        ss = [sb(f"ss{i}", [P, 4]) for i in range(2)]
        std = [sb(f"std{i}", [P, 4]) for i in range(2)]
        rstd = [sb(f"rstd{i}", [P, 4]) for i in range(2)]
        kp = [sb(f"kp{i}", [P, 2, D]) for i in range(2)]
        vr = [sb(f"vr{i}", [P, 2, C, RW]) for i in range(2)]
        kp_left, vr_left = sb("kp_left", [B, D]), sb("vr_left", [B, C, RW])
        vr_one = [sb(f"vr_one{i}", [B, C, RW]) for i in range(2)]
        kv_tmp = [sb(f"kv_tmp{i}", [P, C, P]) for i in range(2)]
        KV = sb("KV", [P, B, C, KVW])
        qss, qstd, qrstd = sb("qss", [P, NT]), sb("qstd", [P, NT]), sb("qrstd", [P, NT])
        z = [sb(f"z{i}", [P, C, 8]) for i in range(2)]

        ctx_in = [core.sem(f"l0x_ctx_in{i}") for i in range(2)]
        rows_done = core.sem("l0x_rows_done")
        centered = core.sem("l0x_centered")
        q_done = core.sem("l0x_q_done")
        q_squared = core.sem("l0x_q_squared")
        q_std = core.sem("l0x_q_std")
        proj_done = core.sem("l0x_proj_done")
        std_done = core.sem("l0x_std_done")
        kv_ready = core.sem("l0x_kv_ready")
        kv_done = core.sem("l0x_kv_done")
        kv_kept = core.sem("l0x_kv_kept")
        att_done = core.sem("l0x_att_done")
        att_rows = core.sem("l0x_att_rows")
        dense_done = core.sem("l0x_dense_done")

        att_stored = [core.sem(f"l0x_att_stored{i}") for i in range(2)]
        att_in = core.sem("l0x_att_in")
        att_dram = nc.dram_tensor("att_dram", (B, 16, S, 16), F32).ap()
        AR = sb("AR", [P, NT, D])

        block = es.enter_context(nc.Block())

        @block.sync
        def _(sp):
            for j in range(2):
                sp.dma_start(ctxT[j][:], core.dram["ctxT"][j]).then_inc(ctx_in[j], 16)
            load_next(sp)
            with sp.Fori(0, B // 2 - 1) as i:
                for j in range(2):
                    sp.wait_ge(proj_done, 2 * i + (j + 2))
                    sp.dma_start(ctxT[j][:], core.dram["ctxT"][2 * i + (j + 2)]).then_inc(ctx_in[j], 16)
            for t in range(NT):
                sp.wait_ge(att_rows, t + 1)
                for b in range(TB):
                    sp.dma_start(att_dram[TB * t + b].rearrange("h n e -> n h e"),
                                 core.H[b * S:(b + 1) * S, t, :].rearrange("n (h e) -> n h e", e=16)).then_inc(att_stored[t // 4], 16)
            for half in range(2):
                sp.wait_ge(att_stored[half], 16 * 16)
                sp.dma_start(AR[:, 4 * half:4 * half + 4, :],
                             att_dram[16 * half:16 * half + 16].rearrange("(t b) h n e -> (b h n e) t", b=TB)
                             .rearrange("(p d) t -> p t d", d=D)).then_inc(att_in, 16)

        @block.tensor
        def _(pe):
            pe.wait_ge(core.consts_in, 16)
            flip.tensor(pe, core.H, rows_done, 0)
            flip.ready(pe, "pe")
            pe.wait_ge(centered, 1)
            for t in range(NT):
                for c in range(C):
                    last = nc.tensor.matmul(PS[:, 4 + t // 2, (t % 2) * D:(t % 2 + 1) * D],
                                            core.HT[:, c, t * P:(t + 1) * P], wqkv[:, c, :], start=(c == 0), stop=(c == 1))
                last.then_inc(q_done, 1)
            kw = wqkv[:, 2:6, :].rearrange("p (c k) d -> p c (k d)", c=C)

            def proj(lhsT, bank, m):
                for c in range(C):
                    last = nc.tensor.matmul(PS[0:m, bank, :], lhsT[:, c, :], kw[:, c, :], start=(c == 0), stop=(c == 1))
                return last

            proj(cleft, 2, B).then_inc(proj_done, 1)

            def proj_batch(b, j):
                pe.wait_ge(ctx_in[j], 8 * b + (16 - 8 * j))
                for half in range(2):
                    last = proj(ctxT[j][:, :, half * P:(half + 1) * P], 2 * j + half, P)
                last.then_inc(proj_done, 1)

            def kv_batch(b, j):
                pe.wait_ge(kv_ready, b + 3)
                for c in range(C):
                    acc = PS[:, 4 + j, c * RW:(c + 1) * RW]
                    for half in range(2):
                        nc.tensor.matmul(acc, kp[j][:, half, c * P:(c + 1) * P], vr[j][:, half, c, :],
                                         start=(half == 0), stop=False)
                    last = nc.tensor.matmul(acc, kp_left[:, c * P:(c + 1) * P], vr_one[j][:, c, :], start=False, stop=True)
                last.then_inc(kv_done, 1)

            pe.wait_ge(kv_ready, 2)
            proj_batch(0, 0)
            with pe.Fori(0, B // 2 - 1) as i:
                pe.wait_ge(kv_ready, 2 * i + 2)
                proj_batch(2 * i + 1, 1)
                pe.wait_ge(kv_kept, 2 * i + 1)
                kv_batch(2 * i, 0)
                proj_batch(2 * i + 2, 0)
                pe.wait_ge(kv_kept, 2 * i + 2)
                kv_batch(2 * i + 1, 1)
            pe.wait_ge(kv_ready, B)
            proj_batch(B - 1, 1)
            pe.wait_ge(kv_kept, B - 1)
            kv_batch(B - 2, 0)
            pe.wait_ge(kv_kept, B)
            kv_batch(B - 1, 1)
            flip.tensor(pe, core.H, rows_done, NT)
            flip.ready(pe, "pe")
            pe.wait_ge(kv_kept, B + 2)
            for t in range(NT):
                if t >= 2:
                    pe.wait_ge(att_rows, t - 1)
                for b in range(TB * t, TB * t + TB):
                    r = S * (b % TB)
                    for c in range(C):
                        last = nc.tensor.matmul(PS[r:r + S, 6 + t % 2, c * KVW:(c + 1) * KVW],
                                                core.HT[:, c, b * S:(b + 1) * S], KV[:, b, c, :], start=True, stop=True)
                last.then_inc(att_done, 1)
            pe.wait_ge(att_in, 32)
            flip.tensor(pe, AR, att_rows, 0)
            flip.ready(pe, "pe")
            for t in range(NT):
                for c in range(C):
                    last = nc.tensor.matmul(PS[:, 4 + t // 2, (t % 2) * D:(t % 2 + 1) * D],
                                            core.HT[:, c, t * P:(t + 1) * P], dense[:, c, :], start=(c == 0), stop=(c == 1))
                last.then_inc(dense_done, 1)

        @block.scalar
        def _(act):
            act.wait_ge(core.eps_set, 1)
            norm.scalar(act, core.eps5)
            flip.scalar(act, core.HT)
            for t in range(NT):
                act.wait_ge(q_done, (t | 1) + 1)
                last = nc.scalar.activation(sq[:, t, :], PS[:, 4 + t // 2, (t % 2) * D:(t % 2 + 1) * D], ACT.Square,
                                            accum_out=qss[:, t:t + 1])
            core.act_step(act, last)
            nc.scalar.activation(qstd[:], qss[:], ACT.Sqrt, bias=core.eps6, scale=1.0 / D).then_inc(q_std, 1)
            act.wait_ge(proj_done, 1)
            for h in range(2):
                last = nc.scalar.activation(sq[0:B, h, :], PS[0:B, 2, h * D:(h + 1) * D], ACT.Square,
                                            accum_out=ss[1][0:B, h:h + 1])
            core.act_step(act, last)
            nc.scalar.activation(std[1][0:B, 0:2], ss[1][0:B, 0:2], ACT.Sqrt, bias=core.eps6[0:B, :], scale=1.0 / D).then_inc(std_done, 1)
            with act.Fori(0, B // 2) as i:
                core.act_step.enter(i, 2)
                for j in range(2):
                    act.wait_ge(proj_done, 2 * i + (j + 2))
                    for half in range(2):
                        for h in range(2):
                            last = nc.scalar.activation(sq[:, 4 * j + 2 * half + h, :], PS[:, 2 * j + half, h * D:(h + 1) * D], ACT.Square,
                                                        accum_out=ss[j][:, 2 * half + h:2 * half + h + 1])
                    core.act_step(act, last)
                    act.wait_ge(kv_ready, 2 * i + (j + 1))
                    nc.scalar.activation(std[j][:], ss[j][:], ACT.Sqrt, bias=core.eps6, scale=1.0 / D).then_inc(std_done, 1)
                core.act_step.leave(B // 2)
            flip.scalar(act, core.HT)
            flip.scalar(act, core.HT)
            norm.scalar(act, core.eps6)

        @block.vector
        def _(dve):
            nc.vector.memset(core.eps[:, 0:1], 1e-5)
            nc.vector.memset(core.eps[:, 1:2], 1e-6).then_inc(core.eps_set, 1)
            dve.wait_ge(core.x_in, 16)
            norm.vector(dve, core.X, core.H, rows_done)
            flip.vector(dve, core.HT)
            dve.wait_ge(core.weights_in[0], 16)
            dve_step(dve, nc.vector.reduce_sum(wsum[:], wqkv, AX.X))
            dve_step(dve, nc.vector.tensor_scalar(wsum[:], wsum[:], 1.0 / D, None, ALU.mult))
            nc.vector.tensor_tensor(wqkv, wqkv, bcast(wsum[:], 2, D), ALU.subtract).then_inc(centered, 1)
            nc.vector.tensor_copy(em[:, :, :, 0], em_in)
            nc.vector.tensor_tensor(em[:, :, :, 1], em_in, em_in, ALU.mult)
            nc.vector.tensor_copy(eml[:, 0:1], em_left_in[0:B])
            dve_step(dve, nc.vector.tensor_tensor(eml[:, 1:2], em_left_in[0:B], em_left_in[0:B], ALU.mult))
            dve.wait_ge(q_std, 1)
            dve.wait_ge(rows_done, NT)
            flip.ready(dve, "dve")
            dve_step(dve, nc.vector.reciprocal(qrstd[:], qstd[:]))
            for t in range(NT):
                last = nc.vector.scalar_tensor_tensor(core.H[:, t, :], PS[:, 4 + t // 2, (t % 2) * D:(t % 2 + 1) * D],
                                                      qrstd[:, t:t + 1], gamma, ALU.mult, ALU.mult)
            dve_step(dve, last)
            dve_step(dve, nc.vector.tensor_tensor(core.H[:], core.H[:], bcast(beta, 1, NT), ALU.add))
            for t in range(NT):
                nc.vector.tensor_scalar(core.H[:, t, :], core.H[:, t, :], 0.0, 1e-6, ALU.max, ALU.add).then_inc(rows_done, 1)

            def keys_values(k_rows, v_rows, psum, scale, em_cols):
                n = psum.shape[1]
                for h in range(n):
                    nc.vector.tensor_scalar(scale[:, 2 * h + 1:2 * h + 2], scale[:, 2 * h + 1:2 * h + 2],
                                            em_cols[:, h, 1:2], None, ALU.mult)
                    last = nc.vector.scalar_tensor_tensor(k_rows[:, h, :], psum[:, h, 0, :], scale[:, 2 * h:2 * h + 1],
                                                          gamma[0:psum.shape[0], :], ALU.mult, ALU.mult)
                dve_step(dve, last)
                for h in range(n):
                    nc.vector.scalar_tensor_tensor(v_rows[:, h, :, 0:P], psum[:, h, 1, :].rearrange("p (c d) -> p c d", c=C),
                                                   scale[:, 2 * h + 1:2 * h + 2],
                                                   gamma[0:psum.shape[0], :].rearrange("p (c d) -> p c d", c=C), ALU.mult, ALU.mult)
                    nc.vector.tensor_copy(v_rows[:, h, :, P:RW], bcast(em_cols[:, h, :], 1, C))
                dve_step(dve, nc.vector.tensor_tensor(k_rows, k_rows, bcast(beta[0:psum.shape[0], :], 1, n), ALU.add))
                return nc.vector.tensor_scalar(k_rows, k_rows, 0.0, 1e-6, ALU.max, ALU.add)

            def keep(b, j):
                dve.wait_ge(kv_done, b + 1)
                A = PS[:, 4 + j, 0:C * RW].rearrange("p (c r) -> p c r", c=C)
                for c in range(C):
                    last = nc.vector.scalar_tensor_tensor(kv_tmp[j][:, c, :], beta[:, c * P:(c + 1) * P], A[:, c, P + 1:P + 2],
                                                          A[:, c, 0:P], ALU.mult, ALU.add)
                    nc.vector.tensor_scalar(KV[:, b, c, P:KVW], head_of, A[:, c, P:P + 1], None, ALU.mult)
                dve_step(dve, last)
                nc.vector.tensor_tensor(KV[:, b, :, 0:P], kv_tmp[j][:], bcast(same_head, 1, C), ALU.mult).then_inc(kv_kept, 1)

            def prepare(b, j):
                dve.wait_ge(std_done, b + 2)
                dve_step(dve, nc.vector.reciprocal(rstd[j][:], std[j][:]))
                nc.vector.tensor_scalar(vr_one[j][:], vr_left[:], core.ident[0:B, bass.ds(b, 1)], None, ALU.mult)
                keys_values(kp[j][:], vr[j][:], PS[:, 2 * j:2 * j + 2, :].rearrange("p t (k d) -> p t k d", k=2), rstd[j][:],
                            em[:, b, :, :]).then_inc(kv_ready, 1)

            dve.wait_ge(std_done, 1)
            dve_step(dve, nc.vector.reciprocal(rstd[1][0:B, 0:2], std[1][0:B, 0:2]))
            keys_values(kp_left[:].unsqueeze(1), vr_left[:].unsqueeze(1), PS[0:B, 2:3, :].rearrange("p t (k d) -> p t k d", k=2),
                        rstd[1][0:B, 0:2], eml[:].unsqueeze(1)).then_inc(kv_ready, 2)
            dve.wait_ge(kv_ready, 2)
            dve.sem_inc(kv_kept, 2)
            prepare(0, 0)
            with dve.Fori(0, B // 2 - 1) as i:
                dve_step.enter(i, 8)
                prepare(2 * i + 1, 1)
                keep(2 * i, 0)
                prepare(2 * i + 2, 0)
                keep(2 * i + 1, 1)
                dve_step.leave(B // 2 - 1)
            prepare(B - 1, 1)
            keep(B - 2, 0)
            keep(B - 1, 1)
            flip.vector(dve, core.HT)
            flip.ready(dve, "dve")
            for t in range(NT):
                dve.wait_ge(att_done, t + 1)
                acc = PS[:, 6 + t % 2, 0:C * KVW].rearrange("p (c r) -> p c r", c=C)
                dve_step(dve, nc.vector.tensor_scalar(z[t % 2][:], acc[:, :, P:KVW], 1e-6, None, ALU.add))
                dve_step(dve, nc.vector.reciprocal(z[t % 2][:], z[t % 2][:]))
                nc.vector.tensor_tensor(core.H[:, t, :].rearrange("p (c h d) -> p c h d", c=C, h=8),
                                        acc[:, :, 0:P].rearrange("p c (h d) -> p c h d", h=8),
                                        bcast(z[t % 2][:], 3, 16), ALU.mult).then_inc(att_rows, 1)
            flip.vector(dve, core.HT)
            flip.ready(dve, "dve")
            for t in range(NT):
                dve.wait_ge(dense_done, (t | 1) + 1)
                last = nc.vector.tensor_tensor(core.H[:, t, :], PS[:, 4 + t // 2, (t % 2) * D:(t % 2 + 1) * D], dense_b, ALU.add)
            dve_step(dve, last)
            norm.vector(dve, core.H, core.H, rows_done)
            dve.wait_ge(rows_done, 3 * NT)
            dve_step(dve, nc.vector.tensor_tensor(core.H[:], core.H[:], bcast(gamma, 1, NT), ALU.mult))
            dve_step(dve, nc.vector.tensor_tensor(core.H[:], core.H[:], bcast(beta, 1, NT), ALU.add))
            dve_step(dve, nc.vector.tensor_tensor(core.X[:], core.X[:], core.H[:], ALU.add))


def l0_self(core, load_next):
    nc, norm, flip, dve_step = core.nc, core.norm, core.flip, core.dve_step
    w = core.arena(1)
    wqk, wv, wo = w.take(C, 2 * D), w.take(C, D), w.take(C, D)
    cos, sin, causal, head_of = w.take(8), w.take(8), w.take(S), w.take(8)
    with ExitStack() as es:
        at = SelfAttention(core, es, "l0a", "softmax", 16.0 ** -0.5)
        t1, t2 = (core.sb(f"l0a_t{i}", [P, NT, 16, 8], es) for i in range(2))
        rows_done = core.sem("l0a_rows_done")
        block = es.enter_context(nc.Block())

        @block.sync
        def _(sp):
            load_next(sp)

        @block.tensor
        def _(pe):
            pe.wait_ge(core.consts_in, 16)
            pe.wait_ge(core.weights_in[1], 16)
            flip.tensor(pe, core.H, rows_done, 0)
            flip.ready(pe, "pe")
            at.project(pe, core.HT, core.HT, wqk, wv)
            at.flip_tensor(pe)
            flip.ready(pe, "pe")
            at.attend_tensor(pe)
            at.output_tensor(pe, wo)

        @block.gpsimd
        def _(pool):
            pool.wait_ge(core.weights_in[1], 16)
            flip.uses["pool"] = flip.uses["pe"] - 1
            flip.ready(pool, "pool")
            at.spread_keys(pool, head_of)

        @block.scalar
        def _(act):
            act.wait_ge(core.eps_set, 1)
            norm.scalar(act, core.eps5)
            flip.scalar(act, core.HT)
            at.copy_qk(act)
            flip.scalar(act, at.QT)
            flip.scalar(act, at.KT)
            at.attend_scalar(act)
            flip.scalar(act, core.HT)

        @block.vector
        def _(dve):
            dve.wait_ge(core.x_in, 16)
            norm.vector(dve, core.X, core.H, rows_done)
            flip.vector(dve, core.HT)
            at.copy_v(dve)
            dve.wait_ge(core.weights_in[1], 16)
            dve.wait_ge(at.qk_copied, NT)
            for rows, done in ((at.Q, at.q_rows), (at.K, at.k_rows)):
                pairs = rows[:].rearrange("p t (h d two) -> p t h d two", h=16, two=2)
                rotate(core, dve, pairs[:, :, :, :, 0], pairs[:, :, :, :, 1], t1[:], t2[:], cos, sin, done)
            flip.vector(dve, at.QT)
            flip.vector(dve, at.KT)
            at.attend_vector(dve, causal)
            flip.vector(dve, core.HT)
            at.output_vector(dve)


def l0_feed_forward(core, load_next):
    nc, PS, norm, flip, dve_step = core.nc, core.PS, core.norm, core.flip, core.dve_step
    E = EXPERTS[2][0]
    w = core.arena(2)
    cent, scale, number = w.take(C, E), w.take(C), w.take(E)
    with ExitStack() as es:
        ex = Experts(core, es, "l0f", 2, "glu", *EXPERTS[2])
        sb = lambda n, shape: core.sb("l0f_" + n, shape, es)
        R, squares = sb("R", [P, NT, D]), sb("squares", [P, NT, D])
        XT, XT2 = sb("XT", [P, C, NT * P]), sb("XT2", [P, C, NT * P])
        size, least = sb("size", [P, NT]), sb("least", [P, NT])
        cent2, centm2, ones = sb("cent2", [P, C, E]), sb("centm2", [P, C, E]), sb("ones", [P, P])
        dist, gate = sb("dist", [P, NT, E]), sb("gate", [P, NT, E])
        rows_done, rms_rows = core.sem("l0f_rows_done"), core.sem("l0f_rms_rows")
        summed, rooted = core.sem("l0f_ms_summed"), core.sem("l0f_ms_rooted")
        dist_ready, dist_done = core.sem("l0f_dist_ready"), core.sem("l0f_dist_done")
        block = es.enter_context(nc.Block())

        @block.sync
        def _(sp):
            load_next(sp)
            ex.load(sp)

        @block.tensor
        def _(pe):
            pe.wait_ge(core.consts_in, 16)
            flip.tensor(pe, R, rms_rows, 0)
            pe.wait_ge(dist_ready, 1)
            flip.ready(pe, "pe")
            for t in range(NT):
                for c in range(C):
                    tok = slice(t * P, (t + 1) * P)
                    nc.tensor.matmul(PS[:, 4, t * E:(t + 1) * E], XT2[:, c, tok], ones[:, 0:E], start=(c == 0), stop=False)
                    nc.tensor.matmul(PS[:, 4, t * E:(t + 1) * E], ones[:], cent2[:, c, :], start=False, stop=False)
                    last = nc.tensor.matmul(PS[:, 4, t * E:(t + 1) * E], XT[:, c, tok], centm2[:, c, :], start=False, stop=(c == 1))
            last.then_inc(dist_done, 1)
            pe.wait_ge(dist_done, 1)
            ex.tensor(pe, XT)

        @block.scalar
        def _(act):
            act.wait_ge(core.eps_set, 1)
            norm.scalar(act, core.eps5)
            for t in range(NT):
                act.wait_ge(rows_done, t + 1)
                last = nc.scalar.activation(squares[:, t, :], core.H[:, t, :], ACT.Square, accum_out=size[:, t:t + 1])
            core.act_step(act, last)
            nc.scalar.activation(size[:], size[:], ACT.Sqrt, bias=core.eps6, scale=1.0 / D).then_inc(rooted, 1)
            act.wait_ge(core.weights_in[2], 16)
            flip.scalar(act, XT, scale)
            ex.scalar(act)

        @block.vector
        def _(dve):
            nc.vector.memset(ones[:], 1.0)
            dve.wait_ge(core.x_in, 16)
            norm.vector(dve, core.X, core.H, rows_done)
            dve.wait_ge(core.weights_in[2], 16)
            nc.vector.tensor_scalar(centm2[:], cent, -2.0, None, ALU.mult)
            nc.vector.tensor_tensor(cent2[:], cent, cent, ALU.mult)
            dve.wait_ge(rooted, 1)
            dve_step(dve, nc.vector.reciprocal(size[:], size[:]))
            for t in range(NT):
                nc.vector.tensor_scalar(R[:, t, :], core.H[:, t, :], size[:, t:t + 1], None, ALU.mult).then_inc(rms_rows, 1)
            dve_step(dve, nc.vector.tensor_tensor(core.X[:], core.X[:], core.H[:], ALU.add))
            flip.vector(dve, XT, scale)
            flip.ready(dve, "dve")
            nc.vector.tensor_tensor(XT2[:], XT[:], XT[:], ALU.mult).then_inc(dist_ready, 1)
            dve.wait_ge(dist_done, 1)
            dve_step(dve, nc.vector.tensor_copy(dist[:], PS[:, 4, 0:NT * E].rearrange("p (t e) -> p t e", e=E)))
            dve_step(dve, nc.vector.tensor_reduce(least[:], dist[:], AX.X, ALU.min))
            dve_step(dve, nc.vector.tensor_tensor(dist[:], dist[:], bcast(least[:], 2, E), ALU.is_equal))
            dve_step(dve, nc.vector.tensor_tensor(dist[:], dist[:], bcast(number, 1, NT), ALU.mult))
            dve_step(dve, nc.vector.tensor_reduce(least[:], dist[:], AX.X, ALU.min))
            dve_step(dve, nc.vector.tensor_tensor(gate[:], bcast(number, 1, NT), bcast(least[:], 2, E), ALU.is_equal))
            ex.vector(dve, core.X, gate)


def l1_cross(core, load_next):
    nc, PS, norm, flip, dve_step, cn = core.nc, core.PS, core.norm, core.flip, core.dve_step, core.ctx_norm
    HB = 8
    DH = 64
    w = core.arena(3)
    wq, wkv, wo = w.take(C, HB * P), w.take(C, 3 * DH), w.take(HB, D)
    ff1, ff2 = w.take(C, 2 * HB * P), w.take(HB, D)
    ln_g, ln_b, cln_g, cln_b = w.take(C), w.take(C), w.take(C), w.take(C)
    half_of = w.take(2)
    scale = DH ** -0.5
    U = 4
    with ExitStack() as es:
        sb = lambda n, shape: core.sb("l1x_" + n, shape, es)
        two = lambda n, shape: [sb(f"{n}{i}", shape) for i in range(2)]
        sem = lambda n: core.sem("l1x_" + n)
        QT = sb("QT", [P, HB, NT * P])
        hidden = AT = sb("AT", [P, HB, NT * P])
        side = [core.H[:, 2 * i:2 * i + 2, :].rearrange("p t d -> p (t d)") for i in range(2)]
        last_cols = sb("last_cols", [P, C, B])
        ctx, ctx_n, ctxT = two("ctx", [P, 2, D]), two("ctx_n", [P, 2, D]), two("ctxT", [P, C, CTX])
        queries, kT, V, V_last = two("queries", [P, 2, HB, S]), two("kT", [P, CTX]), two("V", [P, 2, DH]), two("V_last", [P, U, DH])
        last_rows, V_last_all = sb("last_rows", [B, DH]), sb("V_last_all", [U, B, DH])
        probs, probsT, probsT_last = two("probs", [P, U, CTX]), two("probsT", [P, 2, U * P]), two("probsT_last", [P, P])
        top, total = two("top", [P, U]), two("total", [P, U])
        cn.allocate(es, "l1x")
        rows_done, normed_done, q_done, q_copied = sem("rows_done"), sem("normed_done"), sem("q_done"), sem("q_copied")
        up_done, side_done, hidden_done, ff_done, ff_added = (sem(n) for n in ("up_done", "side_done", "hidden_done", "ff_done", "ff_added"))
        last_cols_done, ctx_normed, ctx_flipped, ctxT_copied = (sem(n) for n in ("last_cols_done", "ctx_normed", "ctx_flipped", "ctxT_copied"))
        last_v_done, last_rows_done, last_stored = sem("last_v_done"), sem("last_rows_done"), sem("last_stored")
        zeros_set, last_placed, V_last_done = sem("zeros_set"), sem("last_placed"), sem("V_last_done")
        last_v_dram = nc.dram_tensor("l1x_last_v_dram", (B, DH), F32).ap()
        queries_done, k_done, v_done, k_copied, v_copied = (sem(n) for n in ("queries_done", "k_done", "v_done", "k_copied", "v_copied"))
        sim_done, top_done, exps_done, probs_done = (sem(n) for n in ("sim_done", "top_done", "exps_done", "probs_done"))
        pt_done, pt_copied_act, pt_copied_dve = sem("pt_done"), sem("pt_copied_act"), sem("pt_copied_dve")
        pv_done, out_copied, out_done = sem("pv_done"), sem("out_copied"), sem("out_done")
        block = es.enter_context(nc.Block())

        @block.sync
        def _(sp):
            cn.load(sp, ctx)
            load_next(sp)
            sp.wait_ge(last_rows_done, 1)
            sp.dma_start(last_v_dram, last_rows[:]).then_inc(last_stored, 16)
            sp.wait_ge(last_stored, 16)
            for u in range(U):
                sp.dma_start(V_last_all[u:u + 1, :, :], last_v_dram.unsqueeze(0)).then_inc(last_placed, 16)
            with sp.Fori(0, B // 2 - 1) as i:
                for j in range(2):
                    sp.wait_ge(ctx_normed, 2 * i + (j + 1))
                    sp.dma_start(ctx[j][:], core.dram["ctx"][2 * i + (j + 2), 0:2 * P, :].rearrange("(h p) d -> p h d", p=P)).then_inc(cn.slot_in[j], 16)

        @block.gpsimd
        def _(pool):
            for j in range(2):
                nc.gpsimd.memset(V_last[j][:], 0.0).then_inc(zeros_set, 1)
                nc.gpsimd.memset(probsT_last[j][:], 0.0).then_inc(zeros_set, 1)
            pool.wait_ge(zeros_set, 4)
            pool.wait_ge(q_copied, 2 * HB)
            pool.wait_ge(last_cols_done, 1)
            pool.wait_ge(last_placed, 16 * U)
            pool.wait_ge(core.consts_in, 16)

            def prepare(b, j):
                at_least(pool, sim_done, 2 * b - 2)
                nc.gpsimd.tensor_copy(ctxT[j][:, :, 2 * P:CTX], last_cols[:, :, bass.ds(b, 1)])
                nc.gpsimd.tensor_tensor(queries[j][:], bcast(QT[:, :, bass.ds(b * S, S)], 1, 2), bcast(bcast(half_of, 2, HB), 3, S), ALU.mult).then_inc(queries_done, 1)
                at_least(pool, pv_done, b - 1)
                nc.gpsimd.tensor_tensor(V_last[j][0:U], V_last_all[:, bass.ds(b, 1), :].to_broadcast([U, U, DH]), bcast(core.ident[0:U, 0:U], 2, DH), ALU.mult).then_inc(V_last_done, 1)

            prepare(0, 0)
            prepare(1, 1)
            with pool.Fori(0, B // 2 - 1) as i:
                for j in range(2):
                    prepare(2 * i + (j + 2), j)

        @block.tensor
        def _(pe):
            pe.wait_ge(core.consts_in, 16)
            pe.wait_ge(core.weights_in[3], 16)
            flip.tensor(pe, core.H, normed_done, 0)
            flip.ready(pe, "pe")
            for n in range(2 * HB):
                o, half = n // 2, n % 2
                if n >= 4:
                    pe.wait_ge(q_copied, n - 3)
                for c in range(C):
                    done = nc.tensor.matmul(PS[:, 4 + n % 4, :], wq[:, c, o * P:(o + 1) * P], core.HT[:, c, half * 512:(half + 1) * 512],
                                            start=(c == 0), stop=(c == 1))
                done.then_inc(q_done, 1)
            for n in range(2 * HB):
                m, half = n // 2, n % 2
                if n >= 2:
                    pe.wait_ge(hidden_done, n - 1)
                for g in range(2):
                    for c in range(C):
                        done = nc.tensor.matmul(PS[:, 2 * (n % 2) + g, :], ff1[:, c, (g * HB + m) * P:(g * HB + m + 1) * P],
                                                core.HT[:, c, half * 512:(half + 1) * 512], start=(c == 0), stop=(c == 1))
                done.then_inc(up_done, 1)
            pe.wait_ge(hidden_done, 2 * HB)
            pe.wait_ge(q_copied, 2 * HB)
            for t in range(NT):
                if t >= 3:
                    pe.wait_ge(ff_added, t - 2)
                for m in range(HB):
                    done = nc.tensor.matmul(PS[:, 4 + t % 3, 0:D], hidden[:, m, t * P:(t + 1) * P], ff2[:, m, :], start=(m == 0), stop=(m == HB - 1))
                done.then_inc(ff_done, 1)
            if not cn.computed:
                cn.tensor(pe)

            pe.wait_ge(ff_added, NT)
            pe.wait_ge(last_cols_done, 1)
            for c in range(C):
                done = nc.tensor.matmul(PS[0:B, 6, 0:DH], last_cols[:, c, :], wkv[:, c, P:P + DH], start=(c == 0), stop=(c == 1))
            done.then_inc(last_v_done, 1)

            def flip_context(b, j):
                pe.wait_ge(ctx_normed, b + 1)
                for c in range(C):
                    for half in range(2):
                        done = nc.tensor.transpose(PS[:, 5, (2 * c + half) * P:(2 * c + half + 1) * P], ctx_n[j][:, half, c * P:(c + 1) * P], core.ident[:])
                done.then_inc(ctx_flipped, 1)

            def keys_values(b, j):
                pe.wait_ge(ctxT_copied, b + 1)
                pe.wait_ge(queries_done, b + 1)
                for half in range(2):
                    for c in range(C):
                        done = nc.tensor.matmul(PS[:, 6, half * DH:(half + 1) * DH], ctxT[j][:, c, half * P:(half + 1) * P], wkv[:, c, P:P + DH], start=(c == 0), stop=(c == 1))
                done.then_inc(v_done, 1)
                for c in range(C):
                    done = nc.tensor.matmul(PS[:, 4, 0:CTX], wkv[:, c, 0:P], ctxT[j][:, c, :], start=(c == 0), stop=(c == 1))
                done.then_inc(k_done, 1)

            def sim(b, j):
                pe.wait_ge(queries_done, b + 1)
                for u in range(U):
                    done = nc.tensor.matmul(PS[:, u, 0:CTX], queries[j][:, u // 2, 4 * (u % 2):4 * (u % 2) + 4, :].rearrange("p h q -> p (h q)"),
                                            kT[j][:], start=True, stop=True)
                    if u % 2:
                        done.then_inc(sim_done, 1)

            def flip_probs(b, j):
                pe.wait_ge(probs_done, b + 1)
                for half in (1, 0):
                    if not half and exists(b + 1):
                        pe.wait_ge(k_copied, b + 2)
                        pe.wait_ge(v_copied, b + 2)
                    elif half and exists(b + 2):
                        pe.wait_ge(ctxT_copied, b + 3)
                    for u in range(U):
                        nc.tensor.transpose(PS[:, 4 + half, u * P:(u + 1) * P], probs[j][:, u, half * P:(half + 1) * P], core.ident[:])
                nc.tensor.transpose(PS[0:U, 6, 3 * P:4 * P], probs[j][:, :, 2 * P], core.ident[:]).then_inc(pt_done, 1)

            def weigh(b, j):
                pe.wait_ge(pt_copied_act, b + 1)
                pe.wait_ge(pt_copied_dve, b + 1)
                pe.wait_ge(V_last_done, b + 1)
                pe.wait_ge(out_copied, b + 1)
                for n in range(2):
                    for key in range(3):
                        for par in range(2):
                            u = 2 * par + n
                            value, weight = ((V[j][:, key, :], probsT[j][:, key, u * P:(u + 1) * P]) if key < 2 else
                                             (V_last[j][:, u, :], probsT_last[j][:]))
                            done = nc.tensor.matmul(PS[DH * par:DH * (par + 1), 7, n * P:(n + 1) * P], value, weight, start=(key == 0), stop=(key == 2))
                done.then_inc(pv_done, 1)

            def first():
                flip_context(0, 0)
                pe.wait_ge(ctxT_copied, 1)
                flip_context(1, 1)
                pe.wait_ge(last_rows_done, 1)
                keys_values(0, 0)
                pe.wait_ge(ctxT_copied, 2)
                flip_context(2, 0)
                pe.wait_ge(v_copied, 1)
                pe.wait_ge(k_copied, 1)
                keys_values(1, 1)
                sim(0, 0)

            def turn(b, j):
                flip_probs(b, j)
                sim(b + 1, 1 - j)
                weigh(b, j)
                if exists(b + 3):
                    flip_context(b + 3, 1 - j)
                if exists(b + 2):
                    keys_values(b + 2, j)

            def last(b, j):
                flip_probs(b, j)
                weigh(b, j)

            over_batches(pe, first, turn, last)
            pe.wait_ge(out_copied, B + 1)
            for t in range(NT):
                for m in range(HB):
                    done = nc.tensor.matmul(PS[:, 4 + t // 2, (t % 2) * D:(t % 2 + 1) * D], AT[:, m, t * P:(t + 1) * P],
                                            wo[:, m, :], start=(m == 0), stop=(m == HB - 1))
                if t % 2:
                    done.then_inc(out_done, 1)

        @block.scalar
        def _(act):
            act.wait_ge(core.eps_set, 1)
            act.wait_ge(core.weights_in[3], 16)
            norm.scalar(act, core.eps5)
            norm.scalar(act, core.eps5)
            flip.scalar(act, core.HT, ln_g, ln_b)
            for n in range(2 * HB):
                o, half = n // 2, n % 2
                act.wait_ge(q_done, n + 1)
                nc.scalar.copy(QT[:, o, half * 512:(half + 1) * 512], PS[:, 4 + n % 4, :]).then_inc(q_copied, 1)
            for n in range(2 * HB):
                act.wait_ge(up_done, n + 1)
                if n >= 2:
                    act.wait_ge(hidden_done, n - 1)
                nc.scalar.activation(side[n % 2], PS[:, 2 * (n % 2) + 1, :], ACT.Silu).then_inc(side_done, 1)
            if not cn.computed:
                cn.scalar(act)

            def copy_context(b, j):
                act.wait_ge(ctx_flipped, b + 1)
                at_least(act, k_done, b - 1)
                for c in range(C):
                    done = nc.scalar.activation(ctxT[j][:, c, 0:2 * P], PS[:, 5, c * 2 * P:(c + 1) * 2 * P], ACT.Identity, bias=cln_b[:, c:c + 1], scale=cln_g[:, c:c + 1])
                done.then_inc(ctxT_copied, 1)

            def copy_keys(b, j):
                act.wait_ge(k_done, b + 1)
                nc.scalar.copy(kT[j][:], PS[:, 4, 0:CTX]).then_inc(k_copied, 1)

            def exps(b, j):
                for u in range(U):
                    if u % 2 == 0:
                        act.wait_ge(top_done, 2 * b + (u // 2 + 1))
                    done = nc.scalar.activation(probs[j][:, u, :], PS[:, u, 0:CTX], ACT.Exp, bias=top[j][:, u:u + 1], scale=scale,
                                                accum_out=total[j][:, u:u + 1])
                    if u % 2:
                        done.then_inc(exps_done, 1)

            def copy_probs(b, j):
                act.wait_ge(pt_done, b + 1)
                nc.scalar.copy(probsT[j][:, 0, :], PS[:, 4, :]).then_inc(pt_copied_act, 1)

            def copy_out(b, j):
                act.wait_ge(pv_done, b + 1)
                nc.scalar.copy(AT[:, :, bass.ds(b * S, S)], PS[:, 7, 0:2 * P].rearrange("p (m q) -> p m q", m=HB)).then_inc(out_copied, 1)

            def first():
                act.wait_ge(ff_done, NT)
                act.sem_inc(out_copied, 1)
                copy_context(0, 0)
                copy_context(1, 1)
                copy_keys(0, 0)
                copy_context(2, 0)
                copy_keys(1, 1)
                exps(0, 0)

            def turn(b, j):
                copy_probs(b, j)
                exps(b + 1, 1 - j)
                copy_out(b, j)
                if exists(b + 3):
                    copy_context(b + 3, 1 - j)
                if exists(b + 2):
                    copy_keys(b + 2, j)

            def last(b, j):
                copy_probs(b, j)
                copy_out(b, j)

            over_batches(act, first, turn, last)

        @block.vector
        def _(dve):
            dve.wait_ge(core.x_in, 16)
            norm.vector(dve, core.X, core.H, rows_done)
            dve.wait_ge(rows_done, NT)
            norm.vector(dve, core.H, core.H, normed_done)
            dve.wait_ge(core.weights_in[3], 16)
            flip.vector(dve, core.HT, ln_g, ln_b)
            if not cn.computed:
                cn.vector_stats(dve, ctx)
            for n in range(2 * HB):
                m, half = n // 2, n % 2
                dve.wait_ge(side_done, n + 1)
                nc.vector.tensor_tensor(hidden[:, m, half * 512:(half + 1) * 512], PS[:, 2 * (n % 2), :], side[n % 2], ALU.mult).then_inc(hidden_done, 1)
            for t in range(NT):
                dve.wait_ge(ff_done, t + 1)
                nc.vector.tensor_tensor(core.X[:, t, :], PS[:, 4 + t % 3, 0:D], core.X[:, t, :], ALU.add).then_inc(ff_added, 1)
            if not cn.computed:
                cn.vector_finish(dve)
            for c in range(C):
                done = nc.vector.tensor_scalar(last_cols[:, c, :], cn.lastT[:, c, :], cln_g[:, c:c + 1], cln_b[:, c:c + 1], ALU.mult, ALU.add)
            done.then_inc(last_cols_done, 1)
            dve.wait_ge(last_cols_done, 1)
            before = 16 * (cn.loads + (0 if cn.computed else B // 2))

            dve.wait_ge(zeros_set, 4)
            dve.wait_ge(last_v_done, 1)
            nc.vector.tensor_copy(last_rows[:], PS[0:B, 6, 0:DH]).then_inc(last_rows_done, 1)

            def norm_context(b, j):
                at_least(dve, ctx_flipped, b - 1)
                dve.wait_ge(cn.slot_in[j], 8 * b + (before + 16 - 8 * j))
                for h in range(2):
                    done = nc.vector.tensor_scalar(ctx_n[j][:, h, :], ctx[j][:, h, :], cn.rstd[:, b, h:h + 1], cn.shift[:, b, h:h + 1], ALU.mult, ALU.add)
                done.then_inc(ctx_normed, 1)

            def copy_values(b, j):
                dve.wait_ge(v_done, b + 1)
                at_least(dve, pv_done, b - 1)
                nc.vector.tensor_copy(V[j][:].rearrange("p h d -> p (h d)"), PS[:, 6, 0:2 * DH]).then_inc(v_copied, 1)

            def tops(b, j):
                for n in range(2):
                    dve.wait_ge(sim_done, 2 * b + (n + 1))
                    t = top[j][:, 2 * n:2 * n + 2]
                    dve_step(dve, nc.vector.reduce_max(t, PS[:, 2 * n:2 * n + 2, 0:CTX], AX.X))
                    nc.vector.tensor_scalar(t, t, -scale, None, ALU.mult).then_inc(top_done, 1)

            def weights(b, j):
                for n in range(2):
                    dve.wait_ge(exps_done, 2 * b + (n + 1))
                    t = total[j][:, 2 * n:2 * n + 2]
                    dve_step(dve, nc.vector.reciprocal(t, t))
                    for u in range(2 * n, 2 * n + 2):
                        done = nc.vector.tensor_scalar(probs[j][:, u, :], probs[j][:, u, :], total[j][:, u:u + 1], None, ALU.mult)
                done.then_inc(probs_done, 1)

            def copy_probs(b, j):
                dve.wait_ge(pt_done, b + 1)
                nc.vector.tensor_copy(probsT[j][:, 1, :], PS[:, 5, :])
                nc.vector.tensor_copy(probsT_last[j][0:U], PS[0:U, 6, 3 * P:4 * P]).then_inc(pt_copied_dve, 1)

            def first():
                norm_context(0, 0)
                norm_context(1, 1)
                norm_context(2, 0)
                copy_values(0, 0)
                copy_values(1, 1)
                tops(0, 0)
                weights(0, 0)

            def turn(b, j):
                copy_probs(b, j)
                if exists(b + 3):
                    norm_context(b + 3, 1 - j)
                tops(b + 1, 1 - j)
                weights(b + 1, 1 - j)
                if exists(b + 2):
                    copy_values(b + 2, j)

            def last(b, j):
                copy_probs(b, j)

            over_batches(dve, first, turn, last, lambda i: dve_step.enter(i, 8), dve_step.leave)
            for n in range(NT // 2):
                dve.wait_ge(out_done, n + 1)
                x = core.X[:, 2 * n:2 * n + 2, :]
                nc.vector.tensor_tensor(x, PS[:, 4 + n, :].rearrange("p (t d) -> p t d", t=2), x, ALU.add)

        cn.loads, cn.computed = cn.loads + B // 2 * (1 if cn.computed else 2), True


def l1_self(core, load_next):
    nc, PS, norm, flip, dve_step = core.nc, core.PS, core.norm, core.flip, core.dve_step
    SETS, HEADS, DH = 4, 16, D // 16
    QB = SETS * C
    UNITS = NT * SETS
    w = core.arena(4)
    wq, wk, wv, wo = w.take(C, SETS * D), w.take(C, D), w.take(C, D), w.take(SETS * C, D)
    causal, head_of = w.take(S), w.take(8)
    scale = DH ** -0.5
    with ExitStack() as es:
        sb = lambda n, shape: core.sb("l1a_" + n, shape, es)
        two = lambda n, shape: [sb(f"{n}{i}", shape) for i in range(2)]
        sem = lambda n: core.sem("l1a_" + n)
        QT, KT = sb("QT", [P, QB, NT * P]), sb("KT", [P, C, NT * P])
        V = sb("V", [P, NT, HEADS // 2, 2, 2, DH])
        spread = two("spread", [P, C, TB, 8, S])
        scores, probsT = two("scores", [P, HEADS, S]), two("probsT", [P, HEADS, SETS, S])
        probs = [sb(f"probs{i}", [P, HEADS, S]) for i in range(3)]
        top, total = two("top", [P, HEADS]), two("total", [P, HEADS])
        rowsT = sb("rowsT", [P, C, SETS, TB, S])
        rows_done, zeros_set, qk_done, v_done = sem("rows_done"), sem("zeros_set"), sem("qk_done"), sem("v_done")
        qk_act, qk_dve, v_copied = sem("qk_act"), sem("qk_dve"), sem("v_copied")
        spread_done, scores_done, scores_read, shifted = sem("spread_done"), sem("scores_done"), sem("scores_read"), sem("shifted")
        exps_done, total_done, probs_done, probsT_done = sem("exps_done"), sem("total_done"), sem("probs_done"), sem("probsT_done")
        out_done, rowsT_act, rowsT_dve, proj_done, added = (sem(n) for n in ("out_done", "rowsT_act", "rowsT_dve", "proj_done", "added"))
        block = es.enter_context(nc.Block())

        @block.sync
        def _(sp):
            load_next(sp)

        @block.gpsimd
        def _(pool):
            nc.gpsimd.memset(V[:], 0.0).then_inc(zeros_set, 1)
            pool.wait_ge(core.weights_in[4], 16)
            pool.wait_ge(qk_act, C)
            pool.wait_ge(qk_dve, C)

            def spread_keys(t):
                if t >= 2:
                    pool.wait_ge(scores_done, SETS * (t - 1))
                for c in range(C):
                    done = nc.gpsimd.tensor_tensor(spread[t % 2][:, c], bcast(KT[:, c, t * P:(t + 1) * P].rearrange("p (b k) -> p b k", k=S), 2, 8),
                                                   bcast(bcast(head_of, 1, TB), 3, S), ALU.mult)
                done.then_inc(spread_done, 1)

            spread_keys(0)
            spread_keys(1)
            for n in range(UNITS):
                pool.wait_ge(total_done, n + 1)
                p = probs[n % 3][:]
                nc.gpsimd.tensor_tensor(p, p, bcast(total[n % 2][:], 2, S), ALU.mult).then_inc(probs_done, 1)
                if n % SETS == SETS - 1 and n // SETS + 2 < NT:
                    spread_keys(n // SETS + 2)

        @block.tensor
        def _(pe):
            pe.wait_ge(core.consts_in, 16)
            pe.wait_ge(core.weights_in[4], 16)
            flip.tensor(pe, core.H, rows_done, 0)
            flip.ready(pe, "pe")
            for n in range(C + QB):
                weight, at = (wk, n * P) if n < C else (wq, (n - C) * P)
                for half in range(2):
                    if n >= 2:
                        pe.wait_ge((qk_act, qk_dve)[half], n - 1)
                    for c in range(C):
                        done = nc.tensor.matmul(PS[:, 4 + 2 * (n % 2) + half, :], weight[:, c, at:at + P],
                                                core.HT[:, c, half * 512:(half + 1) * 512], start=(c == 0), stop=(c == 1))
                    done.then_inc(qk_done, 1)
            for t in range(NT):
                for c in range(C):
                    done = nc.tensor.matmul(PS[:, t // 2, (t % 2) * D:(t % 2 + 1) * D], core.HT[:, c, t * P:(t + 1) * P], wv[:, c, :],
                                            start=(c == 0), stop=(c == 1))
                if t % 2:
                    done.then_inc(v_done, 1)
            pe.wait_ge(v_copied, NT // 2)
            pe.wait_ge(qk_act, C + QB)
            pe.wait_ge(qk_dve, C + QB)

            def project(u):
                pe.wait_ge(rowsT_act, u + 1)
                pe.wait_ge(rowsT_dve, u + 1)
                if u:
                    pe.wait_ge(added, u)
                for m in range(SETS * C):
                    done = nc.tensor.matmul(PS[:, 2, 0:D], rowsT[:, m % C, m // C].rearrange("p b q -> p (b q)"), wo[:, m, :],
                                            start=(m == 0), stop=(m == SETS * C - 1))
                done.then_inc(proj_done, 1)

            for n in range(UNITS + SETS + 1):
                t, g = n // SETS, n % SETS
                if n < UNITS:
                    if g == 0:
                        pe.wait_ge(spread_done, t + 1)
                    if n >= 2:
                        pe.wait_ge(scores_read, n - 1)
                    for c in range(C):
                        for b in range(TB):
                            done = nc.tensor.matmul(PS[b * S:(b + 1) * S, n % 2, c * 256:(c + 1) * 256],
                                                    QT[:, C * g + c, t * P + b * S:t * P + (b + 1) * S],
                                                    spread[t % 2][:, c, b].rearrange("p h k -> p (h k)"), start=True, stop=True)
                    done.then_inc(scores_done, 1)
                if t >= 1 and g == 2:
                    u = t - 1
                    pe.wait_ge(probsT_done, SETS * t)
                    if u:
                        pe.wait_ge(rowsT_act, u)
                        pe.wait_ge(rowsT_dve, u)
                    for c in range(C):
                        for block_at in range(4):
                            for side in range(2):
                                h = 8 * c + 2 * block_at + side
                                for b in range(TB):
                                    r = slice(b * S, (b + 1) * S)
                                    done = nc.tensor.matmul(PS[block_at * 32:(block_at + 1) * 32, 4 + b, c * P:(c + 1) * P],
                                                            V[r, u, h // 2, side].rearrange("p two d -> p (two d)"),
                                                            probsT[u % 2][r, h].rearrange("p g q -> p (g q)"),
                                                            start=(side == 0), stop=(side == 1))
                    done.then_inc(out_done, 1)
                if t >= 2 and g == 0:
                    project(t - 2)

        @block.scalar
        def _(act):
            act.wait_ge(core.eps_set, 1)
            norm.scalar(act, core.eps5)
            flip.scalar(act, core.HT)
            for n in range(C + QB):
                act.wait_ge(qk_done, 2 * n + 1)
                dst = KT[:, n, :] if n < C else QT[:, n - C, :]
                nc.scalar.copy(dst[:, 0:512], PS[:, 4 + 2 * (n % 2), :]).then_inc(qk_act, 1)
            for n in range(UNITS + SETS):
                t, g = n // SETS, n % SETS
                if n < UNITS:
                    act.wait_ge(shifted, n + 1)
                    if n >= 3:
                        act.wait_ge(probsT_done, n - 2)
                    nc.scalar.activation(probs[n % 3][:], scores[n % 2][:], ACT.Exp, scale=scale).then_inc(exps_done, 1)
                if t >= 1 and g == 3:
                    act.wait_ge(out_done, t)
                    if t >= 2:
                        act.wait_ge(proj_done, t - 1)
                    nc.scalar.copy(rowsT[:, :, :, 0:2, :].rearrange("p c g b q -> p b (c g) q"),
                                   PS[:, 4:6, 0:C * P].rearrange("p b (e q) -> p b e q", q=S)).then_inc(rowsT_act, 1)

        @block.vector
        def _(dve):
            dve.wait_ge(core.x_in, 16)
            norm.vector(dve, core.X, core.H, rows_done)
            flip.vector(dve, core.HT)
            for n in range(C + QB):
                dve.wait_ge(qk_done, 2 * n + 2)
                dst = KT[:, n, :] if n < C else QT[:, n - C, :]
                nc.vector.tensor_copy(dst[:, 512:1024], PS[:, 5 + 2 * (n % 2), :]).then_inc(qk_dve, 1)
            dve.wait_ge(zeros_set, 1)
            for j in range(NT // 2):
                dve.wait_ge(v_done, j + 1)
                out = PS[:, j, :].rearrange("p (t h two d) -> p t h two d", t=2, two=2, d=DH)
                for side in range(2):
                    done = nc.vector.tensor_copy(V[:, 2 * j:2 * j + 2, :, side, side, :], out[:, :, :, side, :])
                done.then_inc(v_copied, 1)

            def add(u):
                dve.wait_ge(proj_done, u + 1)
                x = core.X[:, u, :]
                nc.vector.tensor_tensor(x, PS[:, 2, 0:D], x, ALU.add).then_inc(added, 1)

            for n in range(UNITS + SETS + 2):
                t, g = n // SETS, n % SETS
                if n < UNITS:
                    i = n % 2
                    s = scores[i][:]
                    dve.wait_ge(scores_done, n + 1)
                    if n >= 2:
                        dve.wait_ge(exps_done, n - 1)
                    nc.vector.tensor_tensor(s, PS[:, i, :].rearrange("p (h k) -> p h k", k=S), bcast(causal, 1, HEADS), ALU.add).then_inc(scores_read, 1)
                    dve.wait_ge(scores_read, n + 1)
                    dve_step(dve, nc.vector.reduce_max(top[i][:], s, AX.X))
                    nc.vector.tensor_tensor(s, s, bcast(top[i][:], 2, S), ALU.subtract).then_inc(shifted, 1)
                if 1 <= n <= UNITS:
                    m = n - 1
                    dve.wait_ge(exps_done, m + 1)
                    if m >= 2:
                        dve.wait_ge(probs_done, m - 1)
                    dve_step(dve, nc.vector.reduce_sum(total[m % 2][:], probs[m % 3][:], AX.X))
                    nc.vector.reciprocal(total[m % 2][:], total[m % 2][:]).then_inc(total_done, 1)
                if 2 <= n <= UNITS + 1:
                    m = n - 2
                    dve.wait_ge(probs_done, m + 1)
                    if m >= 2 * SETS:
                        dve.wait_ge(out_done, m // SETS - 1)
                    nc.vector.transpose(probsT[m // SETS % 2][:, :, m % SETS, :], probs[m % 3][:]).then_inc(probsT_done, 1)
                if 1 <= t <= NT and g == 3:
                    dve.wait_ge(out_done, t)
                    if t >= 2:
                        dve.wait_ge(proj_done, t - 1)
                    nc.vector.tensor_copy(rowsT[:, :, :, 2:4, :].rearrange("p c g b q -> p b (c g) q"),
                                          PS[:, 6:8, 0:C * P].rearrange("p b (e q) -> p b e q", q=S)).then_inc(rowsT_dve, 1)
                if t >= 2 and g == 1:
                    add(t - 2)


def l1_feed_forward(core, load_next):
    nc, PS, norm, flip, dve_step = core.nc, core.PS, core.norm, core.flip, core.dve_step
    E = EXPERTS[5][0] - 1
    w = core.arena(5)
    wg, bg, b2, number = w.take(C, E), w.take(E), w.take(D), w.take(E)
    with ExitStack() as es:
        ex = Experts(core, es, "l1f", 5, "swiglu", *EXPERTS[5])
        bias = OutputBias(core, es, "l1f", E + 1)
        sb = lambda n, shape: core.sb("l1f_" + n, shape, es)
        scores, biased, gate = sb("scores", [P, NT, E]), sb("biased", [P, NT, E]), sb("gate", [P, NT, E + 1])
        first, second = sb("first", [P, NT, E]), sb("second", [P, NT, E])
        best, place, total = sb("best", [P, NT]), sb("place", [P, NT]), sb("total", [P, NT])
        rows_done, routed = core.sem("l1f_rows_done"), core.sem("l1f_routed")
        shifted, exps_done, weighed = core.sem("l1f_shifted"), core.sem("l1f_exps_done"), core.sem("l1f_weighed")
        block = es.enter_context(nc.Block())

        @block.sync
        def _(sp):
            load_next(sp)
            ex.load(sp)

        @block.tensor
        def _(pe):
            pe.wait_ge(core.consts_in, 16)
            pe.wait_ge(core.weights_in[5], 16)
            flip.tensor(pe, core.H, rows_done, 0)
            flip.ready(pe, "pe")
            router_tensor(core, pe, core.HT, wg, routed)
            bias.tensor(pe, gate, weighed, b2)
            ex.tensor(pe, core.HT)

        @block.scalar
        def _(act):
            act.wait_ge(core.eps_set, 1)
            norm.scalar(act, core.eps5)
            flip.scalar(act, core.HT)
            act.wait_ge(shifted, 1)
            nc.scalar.activation(scores[:], scores[:], ACT.Exp).then_inc(exps_done, 1)
            ex.scalar(act)

        @block.vector
        def _(dve):
            nc.vector.memset(gate[:], 1.0)
            dve.wait_ge(core.x_in, 16)
            norm.vector(dve, core.X, core.H, rows_done)
            flip.vector(dve, core.HT)
            dve.wait_ge(core.weights_in[5], 16)
            dve.wait_ge(routed, 1)
            logits = PS[:, 4, 0:NT * E].rearrange("p (t e) -> p t e", e=E)
            dve_step(dve, nc.vector.reduce_max(best[:], logits, AX.X))
            nc.vector.tensor_tensor(scores[:], logits, bcast(best[:], 2, E), ALU.subtract).then_inc(shifted, 1)
            dve.wait_ge(exps_done, 1)
            dve_step(dve, nc.vector.reduce_sum(total[:], scores[:], AX.X))
            dve_step(dve, nc.vector.reciprocal(total[:], total[:]))
            dve_step(dve, nc.vector.tensor_tensor(scores[:], scores[:], bcast(total[:], 2, E), ALU.mult))
            dve_step(dve, nc.vector.tensor_tensor(biased[:], scores[:], bcast(bg, 1, NT), ALU.add))
            first_best(core, dve, biased, number, best, place, first)
            dve_step(dve, nc.vector.scalar_tensor_tensor(biased[:], first[:], NEG, biased[:], ALU.mult, ALU.add))
            first_best(core, dve, biased, number, best, place, second)
            dve_step(dve, nc.vector.tensor_tensor(first[:], first[:], second[:], ALU.add))
            nc.vector.tensor_tensor(gate[:, :, 0:E], first[:], scores[:], ALU.mult).then_inc(weighed, 1)
            dve.wait_ge(weighed, 1)
            bias.vector(dve)
            ex.vector(dve, core.X, gate)


def l2_cross(core, load_next):
    nc, PS, norm, flip, dve_step = core.nc, core.PS, core.norm, core.flip, core.dve_step
    w = core.arena(6)
    wq, wk, wv, wo = w.take(C, D), w.take(C, D), w.take(C, D), w.take(C, D)
    bq, bk, bv, bo = w.take(C), w.take(C), w.take(D), w.take(D)
    head_of = w.take(8)
    own = w.take(4)
    last_tokens = w.take(C, B)
    scale = 16.0 ** -0.5
    U = 4
    with ExitStack() as es:
        sb = lambda n, shape: core.sb("l2x_" + n, shape, es)
        two = lambda n, shape: [sb(f"{n}{i}", shape) for i in range(2)]
        sem = lambda n: core.sem("l2x_" + n)
        QT, AT = sb("QT", [P, C, NT * P]), sb("AT", [P, C, NT * P])
        ctxT, spread, kT = two("ctxT", [P, C, CTX]), two("spread", [P, C, 8, S]), two("kT", [P, C, CTX])
        V, V_last = two("V", [P, 2, D]), two("V_last", [P, U, 64])
        last_rows, V_last_all = sb("last_rows", [B, D]), sb("V_last_all", [U, B, U, 64])
        probs, probsT, probsT_last = two("probs", [P, U, CTX]), two("probsT", [P, 2, U * P]), two("probsT_last", [P, P])
        top, total, own_out = two("top", [P, U]), two("total", [P, U]), sb("own_out", [P, C, 4, S])
        rows_done, q_done, q_copied = sem("rows_done"), sem("q_done"), sem("q_copied")
        ctx_in = [sem("ctx_in0"), sem("ctx_in1")]
        spread_done, k_done, v_done, k_copied, v_copied = (sem(n) for n in ("spread_done", "k_done", "v_done", "k_copied", "v_copied"))
        sim_done, top_done, exps_done, probs_done = sem("sim_done"), sem("top_done"), sem("exps_done"), sem("probs_done")
        last_v_done, last_rows_done, last_placed, V_last_done = sem("last_v_done"), sem("last_rows_done"), sem("last_placed"), sem("V_last_done")
        zeros_set, last_stored = sem("zeros_set"), sem("last_stored")
        last_v_dram = nc.dram_tensor("l2x_last_v_dram", (B, D), F32).ap()
        pt_done, pt_copied_act, pt_copied_dve = sem("pt_done"), sem("pt_copied_act"), sem("pt_copied_dve")
        pv_done, own_done, at_done, out_done = (sem(n) for n in ("pv_done", "own_done", "at_done", "out_done"))
        block = es.enter_context(nc.Block())

        @block.sync
        def _(sp):
            for j in range(2):
                sp.dma_start(ctxT[j][:], core.dram["ctxT"][j]).then_inc(ctx_in[j], 16)
            load_next(sp)
            sp.wait_ge(last_rows_done, 1)
            sp.dma_start(last_v_dram, last_rows[:]).then_inc(last_stored, 16)
            sp.wait_ge(last_stored, 16)
            sp.wait_ge(zeros_set, 5)
            for u in range(U):
                sp.dma_start(V_last_all[u:u + 1, :, u, :], last_v_dram[:, u * 64:(u + 1) * 64].unsqueeze(0)).then_inc(last_placed, 16)
            with sp.Fori(0, B // 2 - 1) as i:
                for j in range(2):
                    sp.wait_ge(k_done, 4 * i + (2 * j + 2))
                    sp.dma_start(ctxT[j][:], core.dram["ctxT"][2 * i + (j + 2)]).then_inc(ctx_in[j], 16)

        @block.gpsimd
        def _(pool):
            nc.gpsimd.memset(V_last_all[:], 0.0).then_inc(zeros_set, 1)
            for j in range(2):
                nc.gpsimd.memset(V_last[j][:], 0.0).then_inc(zeros_set, 1)
                nc.gpsimd.memset(probsT_last[j][:], 0.0).then_inc(zeros_set, 1)
            pool.wait_ge(zeros_set, 5)
            pool.wait_ge(core.weights_in[6], 16)
            pool.wait_ge(q_copied, 4)

            def prepare(b, j):
                at_least(pool, sim_done, 2 * b - 2)
                for c in range(C):
                    last = nc.gpsimd.tensor_tensor(spread[j][:, c], bcast(QT[:, c, bass.ds(b * S, S)], 1, 8), bcast(head_of, 2, S), ALU.mult)
                last.then_inc(spread_done, 1)
                at_least(pool, pv_done, b - 1)
                nc.gpsimd.tensor_copy(V_last[j][0:U].unsqueeze(1), V_last_all[:, bass.ds(b, 1), :, :]).then_inc(V_last_done, 1)

            pool.wait_ge(last_placed, 16 * U)
            prepare(0, 0)
            prepare(1, 1)
            with pool.Fori(0, B // 2 - 1) as i:
                for j in range(2):
                    prepare(2 * i + (j + 2), j)

        @block.tensor
        def _(pe):
            pe.wait_ge(core.consts_in, 16)
            pe.wait_ge(core.weights_in[6], 16)
            flip.tensor(pe, core.H, rows_done, 0)
            flip.ready(pe, "pe")
            for n in range(4):
                o, half = n // 2, n % 2
                for c in range(C):
                    last = nc.tensor.matmul(PS[:, n, :], wq[:, c, o * P:(o + 1) * P], core.HT[:, c, half * 512:(half + 1) * 512],
                                            start=(c == 0), stop=(c == 1))
                last.then_inc(q_done, 1)

            for c in range(C):
                last = nc.tensor.matmul(PS[0:B, 7, 0:D], last_tokens[:, c, :], wv[:, c, :], start=(c == 0), stop=(c == 1))
            last.then_inc(last_v_done, 1)

            def keys_values(b, j):
                pe.wait_ge(ctx_in[j], 8 * b + (16 - 8 * j))
                for half in range(2):
                    for c in range(C):
                        last = nc.tensor.matmul(PS[:, 5, half * D:(half + 1) * D], ctxT[j][:, c, half * P:(half + 1) * P], wv[:, c, :], start=(c == 0), stop=(c == 1))
                last.then_inc(v_done, 1)
                for o in range(C):
                    for c in range(C):
                        last = nc.tensor.matmul(PS[:, 4 + 2 * o, 0:CTX], wk[:, c, o * P:(o + 1) * P], ctxT[j][:, c, :], start=(c == 0), stop=(c == 1))
                    last.then_inc(k_done, 1)

            def sim(b, j):
                pe.wait_ge(spread_done, b + 1)
                for u in range(U):
                    c = u // 2
                    last = nc.tensor.matmul(PS[:, u, 0:CTX], spread[j][:, c, 4 * (u % 2):4 * (u % 2) + 4, :].rearrange("p h q -> p (h q)"),
                                            kT[j][:, c, :], start=True, stop=True)
                    if u % 2:
                        last.then_inc(sim_done, 1)

            def flip_probs(b, j):
                pe.wait_ge(probs_done, b + 1)
                for half in (1, 0):
                    if exists(b + 1):
                        pe.wait_ge((k_copied, v_copied)[half], b + 2)
                    for u in range(U):
                        nc.tensor.transpose(PS[:, 4 + half, u * P:(u + 1) * P], probs[j][:, u, half * P:(half + 1) * P], core.ident[:])
                nc.tensor.transpose(PS[0:U, 6, 3 * P:4 * P], probs[j][:, :, 2 * P], core.ident[:]).then_inc(pt_done, 1)

            def weigh(b, j):
                pe.wait_ge(pt_copied_act, b + 1)
                pe.wait_ge(pt_copied_dve, b + 1)
                pe.wait_ge(V_last_done, b + 1)
                pe.wait_ge(own_done, b + 1)
                for c in range(C):
                    for par in range(2):
                        u = 2 * c + par
                        out = PS[64 * par:64 * (par + 1), 7, c * P:(c + 1) * P]
                        for half in range(2):
                            nc.tensor.matmul(out, V[j][:, half, u * 64:(u + 1) * 64], probsT[j][:, half, u * P:(u + 1) * P], start=(half == 0), stop=False)
                        last = nc.tensor.matmul(out, V_last[j][:, u, :], probsT_last[j][:], start=False, stop=True)
                last.then_inc(pv_done, 1)

            def first():
                pe.wait_ge(q_copied, 4)
                for b in range(2):
                    if b:
                        pe.wait_ge(v_copied, b)
                        pe.wait_ge(k_copied, b)
                    keys_values(b, b)
                pe.wait_ge(k_copied, 1)
                sim(0, 0)

            def turn(b, j):
                flip_probs(b, j)
                sim(b + 1, 1 - j)
                weigh(b, j)
                if exists(b + 2):
                    keys_values(b + 2, j)

            def last(b, j):
                flip_probs(b, j)
                weigh(b, j)

            over_batches(pe, first, turn, last)
            pe.wait_ge(at_done, B)
            for t in range(NT):
                for c in range(C):
                    done = nc.tensor.matmul(PS[:, 4 + t // 2, (t % 2) * D:(t % 2 + 1) * D], AT[:, c, t * P:(t + 1) * P],
                                            wo[:, c, :], start=(c == 0), stop=(c == 1))
                if t % 2:
                    done.then_inc(out_done, 1)

        @block.scalar
        def _(act):
            act.wait_ge(core.eps_set, 1)
            norm.scalar(act, core.eps5)
            flip.scalar(act, core.HT)
            act.wait_ge(core.weights_in[6], 16)
            for n in range(4):
                o, half = n // 2, n % 2
                act.wait_ge(q_done, n + 1)
                nc.scalar.activation(QT[:, o, half * 512:(half + 1) * 512], PS[:, n, :], ACT.Identity, bias=bq[:, o:o + 1]).then_inc(q_copied, 1)

            def copy_keys(b, j):
                for o in range(C):
                    act.wait_ge(k_done, 2 * b + (o + 1))
                    done = nc.scalar.activation(kT[j][:, o, :], PS[:, 4 + 2 * o, 0:CTX], ACT.Identity, bias=bk[:, o:o + 1])
                done.then_inc(k_copied, 1)

            def exps(b, j):
                for u in range(U):
                    if u % 2 == 0:
                        act.wait_ge(top_done, 2 * b + (u // 2 + 1))
                    done = nc.scalar.activation(probs[j][:, u, :], PS[:, u, 0:CTX], ACT.Exp, bias=top[j][:, u:u + 1], scale=scale,
                                                accum_out=total[j][:, u:u + 1])
                    if u % 2:
                        done.then_inc(exps_done, 1)

            def copy_probs(b, j):
                act.wait_ge(pt_done, b + 1)
                nc.scalar.copy(probsT[j][:, 0, :], PS[:, 4, :]).then_inc(pt_copied_act, 1)

            def first():
                copy_keys(0, 0)
                copy_keys(1, 1)
                exps(0, 0)

            def turn(b, j):
                copy_probs(b, j)
                exps(b + 1, 1 - j)
                if exists(b + 2):
                    copy_keys(b + 2, j)

            over_batches(act, first, turn, copy_probs)

        @block.vector
        def _(dve):
            dve.wait_ge(core.x_in, 16)
            norm.vector(dve, core.X, core.H, rows_done)
            flip.vector(dve, core.HT)
            dve.wait_ge(core.weights_in[6], 16)

            dve.wait_ge(zeros_set, 5)
            dve.wait_ge(last_v_done, 1)
            nc.vector.tensor_tensor(last_rows[:], PS[0:B, 7, 0:D], bv[0:B, :], ALU.add).then_inc(last_rows_done, 1)
            dve.sem_inc(own_done, 1)

            def copy_values(b, j):
                dve.wait_ge(v_done, b + 1)
                at_least(dve, pv_done, b - 1)
                nc.vector.tensor_tensor(V[j][:], PS[:, 5, :].rearrange("p (k d) -> p k d", k=2), bcast(bv, 1, 2), ALU.add).then_inc(v_copied, 1)

            def tops(b, j):
                for n in range(2):
                    dve.wait_ge(sim_done, 2 * b + (n + 1))
                    t = top[j][:, 2 * n:2 * n + 2]
                    dve_step(dve, nc.vector.reduce_max(t, PS[:, 2 * n:2 * n + 2, 0:CTX], AX.X))
                    nc.vector.tensor_scalar(t, t, -scale, None, ALU.mult).then_inc(top_done, 1)

            def weights(b, j):
                for n in range(2):
                    dve.wait_ge(exps_done, 2 * b + (n + 1))
                    t = total[j][:, 2 * n:2 * n + 2]
                    dve_step(dve, nc.vector.reciprocal(t, t))
                    for u in range(2 * n, 2 * n + 2):
                        done = nc.vector.tensor_scalar(probs[j][:, u, :], probs[j][:, u, :], total[j][:, u:u + 1], None, ALU.mult)
                done.then_inc(probs_done, 1)

            def copy_probs(b, j):
                dve.wait_ge(pt_done, b + 1)
                nc.vector.tensor_copy(probsT[j][:, 1, :], PS[:, 5, :])
                nc.vector.tensor_copy(probsT_last[j][0:U], PS[0:U, 6, 3 * P:4 * P]).then_inc(pt_copied_dve, 1)

            def keep_own(b, j):
                dve.wait_ge(pv_done, b + 1)
                nc.vector.tensor_tensor(own_out[:], PS[:, 7, 0:C * P].rearrange("p (c h q) -> p c h q", c=C, q=S),
                                        bcast(bcast(own, 1, C), 3, S), ALU.mult).then_inc(own_done, 1)
                dve.wait_ge(own_done, b + 2)
                nc.vector.reduce_sum(AT[:, :, bass.ds(b * S, S)], own_out[:].rearrange("p c h q -> p c q h"), AX.X).then_inc(at_done, 1)
                dve.wait_ge(at_done, b + 1)

            def first():
                copy_values(0, 0)
                copy_values(1, 1)
                tops(0, 0)
                weights(0, 0)

            def turn(b, j):
                copy_probs(b, j)
                tops(b + 1, 1 - j)
                keep_own(b, j)
                weights(b + 1, 1 - j)
                if exists(b + 2):
                    copy_values(b + 2, j)

            def last(b, j):
                copy_probs(b, j)
                keep_own(b, j)

            over_batches(dve, first, turn, last, lambda i: dve_step.enter(i, 8), dve_step.leave)
            for n in range(NT // 2):
                x = core.X[:, 2 * n:2 * n + 2, :]
                dve_step(dve, nc.vector.tensor_tensor(x, x, bcast(bo, 1, 2), ALU.add))
                dve.wait_ge(out_done, n + 1)
                nc.vector.tensor_tensor(x, PS[:, 4 + n, :].rearrange("p (t d) -> p t d", t=2), x, ALU.add)


def l2_self(core, load_next):
    nc, norm, flip, dve_step = core.nc, core.norm, core.flip, core.dve_step
    w = core.arena(7)
    wqk, wv, wo = w.take(C, 2 * D), w.take(C, D), w.take(C, D)
    cos, sin, causal, head_of = w.take(8), w.take(8), w.take(S), w.take(8)
    cap = 50.0
    with ExitStack() as es:
        at = SelfAttention(core, es, "l2a", "capped", cap)
        at.tanh_scale = 16.0 ** -0.5 / cap
        t1, t2 = (core.sb(f"l2a_t{i}", [P, NT, 16, 8], es) for i in range(2))
        squares = core.sb("l2a_squares", [P, NT, 16, 16], es)
        size = [core.sb(f"l2a_size{i}", [P, NT, 16], es) for i in range(2)]
        rows_done = core.sem("l2a_rows_done")
        summed, rooted = core.sem("l2a_summed"), core.sem("l2a_rooted")
        block = es.enter_context(nc.Block())

        @block.sync
        def _(sp):
            load_next(sp)

        @block.tensor
        def _(pe):
            pe.wait_ge(core.consts_in, 16)
            pe.wait_ge(core.weights_in[7], 16)
            flip.tensor(pe, core.H, rows_done, 0)
            flip.ready(pe, "pe")
            at.project(pe, core.HT, core.HT, wqk, wv)
            at.flip_tensor(pe)
            flip.ready(pe, "pe")
            at.attend_tensor(pe)
            at.output_tensor(pe, wo)

        @block.gpsimd
        def _(pool):
            pool.wait_ge(core.weights_in[7], 16)
            flip.uses["pool"] = flip.uses["pe"] - 1
            flip.ready(pool, "pool")
            at.spread_keys(pool, head_of)

        @block.scalar
        def _(act):
            act.wait_ge(core.eps_set, 1)
            norm.scalar(act, core.eps5)
            flip.scalar(act, core.HT)
            at.copy_qk(act)
            for n in range(2):
                act.wait_ge(summed, n + 1)
                nc.scalar.activation(size[n][:], size[n][:], ACT.Sqrt, bias=core.eps5, scale=1.0 / 16).then_inc(rooted, 1)
            flip.scalar(act, at.QT)
            flip.scalar(act, at.KT)
            at.attend_scalar(act)
            flip.scalar(act, core.HT)

        @block.vector
        def _(dve):
            dve.wait_ge(core.x_in, 16)
            norm.vector(dve, core.X, core.H, rows_done)
            flip.vector(dve, core.HT)
            at.copy_v(dve)
            dve.wait_ge(core.weights_in[7], 16)
            dve.wait_ge(at.qk_copied, NT)
            for n, rows in enumerate((at.Q, at.K)):
                heads = rows[:].rearrange("p t (h d) -> p t h d", h=16)
                dve_step(dve, nc.vector.tensor_tensor(squares[:], heads, heads, ALU.mult))
                nc.vector.reduce_sum(size[n][:], squares[:], AX.X).then_inc(summed, 1)
                dve.wait_ge(summed, n + 1)
            for n, (rows, done) in enumerate(((at.Q, at.q_rows), (at.K, at.k_rows))):
                dve.wait_ge(rooted, n + 1)
                heads = rows[:].rearrange("p t (h d) -> p t h d", h=16)
                dve_step(dve, nc.vector.reciprocal(size[n][:], size[n][:]))
                dve_step(dve, nc.vector.tensor_tensor(heads, heads, bcast(size[n][:], 3, 16), ALU.mult))
                rotate(core, dve, heads[:, :, :, 0:8], heads[:, :, :, 8:16], t1[:], t2[:], cos, sin, done)
            flip.vector(dve, at.QT)
            flip.vector(dve, at.KT)
            at.attend_vector(dve, causal)
            flip.vector(dve, core.HT)
            at.output_vector(dve)


def l2_feed_forward(core, load_next):
    nc, PS, norm, flip, dve_step = core.nc, core.PS, core.norm, core.flip, core.dve_step
    E = 8
    w = core.arena(8)
    experts, wg, number = w.take(C, E * D), w.take(C, E), w.take(E)
    with ExitStack() as es:
        sb = lambda n, shape: core.sb("l2f_" + n, shape, es)
        scores, gate = sb("scores", [P, NT, E]), sb("gate", [P, NT, E])
        best, place = sb("best", [P, NT]), sb("place", [P, NT])
        rows_done, routed = core.sem("l2f_rows_done"), core.sem("l2f_routed")
        expert_done, summed = core.sem("l2f_expert_done"), core.sem("l2f_summed")
        block = es.enter_context(nc.Block())

        @block.sync
        def _(sp):
            load_next(sp)

        @block.tensor
        def _(pe):
            pe.wait_ge(core.consts_in, 16)
            pe.wait_ge(core.weights_in[8], 16)
            flip.tensor(pe, core.H, rows_done, 0)
            flip.ready(pe, "pe")
            router_tensor(core, pe, core.HT, wg, routed)
            with pe.Fori(0, E // 2) as i:
                for t in range(NT):
                    pe.wait_ge(summed, i * NT + (t + 1))
                    for c in range(C):
                        last = nc.tensor.matmul(PS[:, t % 4, :], core.HT[:, c, t * P:(t + 1) * P],
                                                experts[:, c, bass.ds(i * (2 * D), 2 * D)], start=(c == 0), stop=(c == 1))
                    last.then_inc(expert_done, 1)

        @block.scalar
        def _(act):
            act.wait_ge(core.eps_set, 1)
            norm.scalar(act, core.eps5)
            flip.scalar(act, core.HT)

        @block.vector
        def _(dve):
            dve.sem_inc(summed, 4)
            dve.wait_ge(core.x_in, 16)
            norm.vector(dve, core.X, core.H, rows_done)
            flip.vector(dve, core.HT)
            dve.wait_ge(rows_done, NT)
            nc.vector.tensor_tensor(core.X[:], core.X[:], core.H[:], ALU.add)
            dve.wait_ge(core.weights_in[8], 16)
            dve.wait_ge(routed, 1)
            dve_step(dve, nc.vector.tensor_copy(scores[:], PS[:, 4, 0:NT * E].rearrange("p (t e) -> p t e", e=E)))
            first_best(core, dve, scores, number, best, place, gate)
            with dve.Fori(0, E // 2) as i:
                dve_step.enter(i, 2)
                for half in range(2):
                    for t in range(4 * half, 4 * half + 4):
                        dve.wait_ge(expert_done, i * NT + (t + 1))
                        bank = PS[:, t % 4, :].rearrange("p (e d) -> p e d", e=2)
                        step = nc.vector.scalar_tensor_tensor(core.X[:, t, :], bank[:, 0, :], gate[:, t, bass.ds(2 * i, 1)], core.X[:, t, :], ALU.mult, ALU.add)
                    dve_step(dve, step)
                    for t in range(4 * half, 4 * half + 4):
                        bank = PS[:, t % 4, :].rearrange("p (e d) -> p e d", e=2)
                        nc.vector.scalar_tensor_tensor(core.X[:, t, :], bank[:, 1, :], gate[:, t, bass.ds(2 * i + 1, 1)], core.X[:, t, :],
                                                       ALU.mult, ALU.add).then_inc(summed, 1)
                dve.wait_ge(summed, i * NT + (NT + 4))
                dve_step.leave(E // 2)


def l3_cross(core, load_next):
    nc, PS, norm, flip, cn = core.nc, core.PS, core.norm, core.flip, core.ctx_norm
    dve_step, pool_step = core.dve_step, core.pool_step
    HEADS, DH = 8, 64
    M = HEADS // 2
    KEYS, REST = CTX + S, CTX + S - 2 * P
    w = core.arena(9)
    wq, wkT, wv, wout = w.take(C, M * P), w.take(M, D), w.take(C, M * P), w.take(M, D)
    gm, bm, gl, bl = w.take(C), w.take(C), w.take(C), w.take(C)
    gm_row, bm_row, gl_row, bl_row = w.take(D), w.take(D), w.take(D), w.take(D)
    scale = DH ** 0.5
    with ExitStack() as es:
        sb = lambda n, shape: core.sb("l3x_" + n, shape, es)
        two = lambda n, shape: [sb(f"{n}{i}", shape) for i in range(2)]
        sem = lambda n: core.sem("l3x_" + n)
        QT = OT = sb("QT", [P, M, NT * P])
        QW = sb("QW", [P, C, HEADS, NT * P])
        last_cols, last_rows = sb("last_cols", [P, C, B]), sb("last_rows", [B, D])
        ctx, hat, tokens = two("ctx", [P, 2, D]), two("hat", [P, 2, D]), two("tokens", [P, 2, D])
        keysT, queries = two("keysT", [P, C, KEYS]), two("queries", [P, C, HEADS * S])
        probs, probsT = two("probs", [P, 2, KEYS]), two("probsT", [P, 2, HEADS * S])
        rest, probsT_rest = ([core.H[0:REST, k + j, :] for j in range(2)] for k in (0, 2))
        top, total = two("top", [P, 2]), two("total", [P, 2])
        latents_dram = nc.dram_tensor("latents_dram", (B * S, D), F32).ap()
        last_dram = nc.dram_tensor("last_dram", (B, D), F32).ap()
        if not cn.computed:
            cn.allocate(es, "l3x")
        rows_done, normed_done, affine_done, stored = sem("rows_done"), sem("normed_done"), sem("affine_done"), sem("stored")
        q_done, q_copied, qw_done, qw_act, qw_dve = sem("q_done"), sem("q_copied"), sem("qw_done"), sem("qw_act"), sem("qw_dve")
        rest_in = [sem("rest_in0"), sem("rest_in1")]
        last_done, hat_done, ctx_flipped, ctxT_copied = sem("last_done"), sem("hat_done"), sem("ctx_flipped"), sem("ctxT_copied")
        prep_done, tokens_done, sim_done, top_done = sem("prep_done"), sem("tokens_done"), sem("sim_done"), sem("top_done")
        exps_done, probs_done, pt_done, pt_act, pt_dve = (sem(n) for n in ("exps_done", "probs_done", "pt_done", "pt_act", "pt_dve"))
        pv_done, px_copied, out_done, out_act, out_dve, proj_done = (sem(n) for n in ("pv_done", "px_copied", "out_done", "out_act", "out_dve", "proj_done"))
        tile = lambda b: core.dram["ctx"][b, 0:2 * P, :].rearrange("(h p) d -> p h d", p=P)
        before = 16 * (cn.loads + (0 if cn.computed else B // 2))
        block = es.enter_context(nc.Block())

        @block.sync
        def _(sp):
            if cn.computed:
                for j in range(2):
                    sp.dma_start(ctx[j][:], tile(j)).then_inc(cn.slot_in[j], 16)
            else:
                cn.load(sp, ctx)
            load_next(sp)
            sp.wait_ge(last_done, 2)
            sp.dma_start(last_dram, last_rows[:]).then_inc(stored, 16)
            sp.wait_ge(affine_done, 1)
            for f in range(TB):
                sp.dma_start(latents_dram.rearrange("(t f q) d -> f q t d", f=TB, q=S)[f],
                             core.H[f * S:(f + 1) * S, :, :]).then_inc(stored, 16)
            sp.wait_ge(stored, 16 * (TB + 1))

            def load_rest(b, j):
                sp.dma_start(rest[j][0:S, :], latents_dram[bass.ds(b * S, S), :]).then_inc(rest_in[j], 16)
                sp.dma_start(rest[j][S:REST, :], last_dram[bass.ds(b, 1), :]).then_inc(rest_in[j], 16)

            def load_context(b, j):
                sp.wait_ge(hat_done, b - 1)
                sp.dma_start(ctx[j][:], tile(b)).then_inc(cn.slot_in[j], 16)

            def turn(b, j):
                if exists(b + 1):
                    load_context(b + 1, 1 - j)
                sp.wait_ge(pv_done, b - 1)
                load_rest(b, j)

            load_rest(0, 0)
            load_rest(1, 1)
            load_context(2, 0)
            with sp.Fori(0, B // 2 - 2) as i:
                turn(2 * i + 2, 0)
                turn(2 * i + 3, 1)
            turn(B - 2, 0)
            turn(B - 1, 1)

        @block.gpsimd
        def _(pool):
            pool.wait_ge(core.weights_in[9], 16)
            pool.wait_ge(last_done, 2)
            pool.wait_ge(qw_act, HEADS * C)
            pool.wait_ge(qw_dve, HEADS * C)

            def prepare(b, j):
                at_least(pool, sim_done, b - 1)
                nc.gpsimd.tensor_copy(queries[j][:].rearrange("p c (h q) -> p c h q", q=S), QW[:, :, :, bass.ds(b * S, S)])
                nc.gpsimd.tensor_copy(keysT[j][:, :, 2 * P:2 * P + S], core.HT[:, :, bass.ds(b * S, S)])
                nc.gpsimd.tensor_copy(keysT[j][:, :, KEYS - 1:KEYS], last_cols[:, :, bass.ds(b, 1)]).then_inc(prep_done, 1)

            def scale_tokens(b, j):
                pool.wait_ge(hat_done, b + 1)
                at_least(pool, pv_done, b - 1)
                pool_step(pool, nc.gpsimd.tensor_tensor(tokens[j][:], hat[j][:], bcast(gm_row, 1, 2), ALU.mult))
                nc.gpsimd.tensor_tensor(tokens[j][:], tokens[j][:], bcast(bm_row, 1, 2), ALU.add).then_inc(tokens_done, 1)
                pool.wait_ge(tokens_done, b + 1)

            def first():
                prepare(0, 0)
                scale_tokens(0, 0)
                prepare(1, 1)
                scale_tokens(1, 1)

            def turn(b, j):
                if exists(b + 2):
                    prepare(b + 2, j)
                    scale_tokens(b + 2, j)

            over_batches(pool, first, turn, lambda b, j: None, lambda i: pool_step.enter(i, 2), pool_step.leave)

        @block.tensor
        def _(pe):
            pe.wait_ge(core.consts_in, 16)
            pe.wait_ge(core.weights_in[9], 16)
            flip.tensor(pe, core.H, normed_done, 0)
            flip.ready(pe, "pe")
            for n in range(2 * M):
                m, half = n // 2, n % 2
                if n >= 4:
                    pe.wait_ge(q_copied, n - 3)
                for c in range(C):
                    done = nc.tensor.matmul(PS[:, 4 + n % 4, :], wq[:, c, m * P:(m + 1) * P], core.HT[:, c, half * 512:(half + 1) * 512],
                                            start=(c == 0), stop=(c == 1))
                done.then_inc(q_done, 1)
            pe.wait_ge(q_copied, 2 * M)
            for n in range(M * C * 2):
                m, c, half = n // (2 * C), n // 2 % C, n % 2
                if n >= 2:
                    pe.wait_ge(qw_act, n - 1)
                    pe.wait_ge(qw_dve, n - 1)
                for par in range(2):
                    rows = slice(DH * par, DH * (par + 1))
                    nc.tensor.matmul(PS[:, 4 + 2 * (n % 2) + par, :], wkT[rows, m, c * P:(c + 1) * P], QT[rows, m, half * 512:(half + 1) * 512],
                                     start=True, stop=True).then_inc(qw_done, 1)
            if not cn.computed:
                pe.wait_ge(qw_dve, HEADS * C)
                cn.tensor(pe)

            def flip_context(b, j):
                pe.wait_ge(hat_done, b + 1)
                at_least(pe, ctxT_copied, b)
                for c in range(C):
                    for half in range(2):
                        done = nc.tensor.transpose(PS[:, 6, (2 * c + half) * P:(2 * c + half + 1) * P], hat[j][:, half, c * P:(c + 1) * P], core.ident[:])
                done.then_inc(ctx_flipped, 1)

            def sim(b, j):
                pe.wait_ge(ctxT_copied, b + 1)
                pe.wait_ge(prep_done, b + 1)
                for u in range(2):
                    for c in range(C):
                        done = nc.tensor.matmul(PS[:, 2 * j + u, 0:KEYS], queries[j][:, c, u * P:(u + 1) * P], keysT[j][:, c, :],
                                                start=(c == 0), stop=(c == 1))
                done.then_inc(sim_done, 1)

            def flip_probs(b, j):
                pe.wait_ge(probs_done, b + 1)
                for u in range(2):
                    for half in range(2):
                        nc.tensor.transpose(PS[:, 4, half * 2 * P + u * P:half * 2 * P + (u + 1) * P], probs[j][:, u, half * P:(half + 1) * P], core.ident[:])
                    done = nc.tensor.transpose(PS[0:REST, 5, u * P:(u + 1) * P], probs[j][:, u, 2 * P:KEYS], core.ident[:])
                done.then_inc(pt_done, 1)

            def weigh(b, j):
                pe.wait_ge(pt_act, b + 1)
                pe.wait_ge(pt_dve, b + 1)
                pe.wait_ge(tokens_done, b + 1)
                pe.wait_ge(rest_in[j], 16 * b + (32 - 16 * j))
                pe.wait_ge(px_copied, b + 1)
                for c in range(C):
                    out = PS[:, 7, c * 2 * P:(c + 1) * 2 * P]
                    for half in range(2):
                        nc.tensor.matmul(out, tokens[j][:, half, c * P:(c + 1) * P], probsT[j][:, half, :], start=(half == 0), stop=False)
                    done = nc.tensor.matmul(out, rest[j][:, c * P:(c + 1) * P], probsT_rest[j], start=False, stop=True)
                done.then_inc(pv_done, 1)

            def first():
                pe.wait_ge(qw_act, HEADS * C)
                pe.wait_ge(qw_dve, HEADS * C)
                flip_context(0, 0)
                flip_context(1, 1)
                sim(0, 0)

            def turn(b, j):
                flip_probs(b, j)
                sim(b + 1, 1 - j)
                weigh(b, j)
                if exists(b + 2):
                    flip_context(b + 2, j)

            def last(b, j):
                flip_probs(b, j)
                weigh(b, j)

            over_batches(pe, first, turn, last)
            pe.wait_ge(px_copied, B + 1)
            for n in range(2 * M):
                m, half = n // 2, n % 2
                if n >= 2:
                    pe.wait_ge((out_act, out_dve)[n % 2], n // 2)
                for par in range(2):
                    for c in range(C):
                        at = (2 * m + par) * DH
                        done = nc.tensor.matmul(PS[DH * par:DH * (par + 1), n % 2, :], wv[:, c, at:at + DH], QW[:, c, 2 * m + par, half * 512:(half + 1) * 512],
                                                start=(c == 0), stop=(c == 1))
                done.then_inc(out_done, 1)
            pe.wait_ge(out_act, M)
            pe.wait_ge(out_dve, M)
            for t in range(NT):
                for m in range(M):
                    done = nc.tensor.matmul(PS[:, 4 + t // 2, (t % 2) * D:(t % 2 + 1) * D], OT[:, m, t * P:(t + 1) * P], wout[:, m, :],
                                            start=(m == 0), stop=(m == M - 1))
                if t % 2:
                    done.then_inc(proj_done, 1)

        @block.scalar
        def _(act):
            act.wait_ge(core.eps_set, 1)
            act.wait_ge(core.weights_in[9], 16)
            norm.scalar(act, core.eps5)
            norm.scalar(act, core.eps5)
            if not cn.computed:
                cn.scalar(act)
            flip.scalar(act, core.HT, gl, bl)
            for n in range(2 * M):
                act.wait_ge(q_done, n + 1)
                nc.scalar.copy(QT[:, n // 2, (n % 2) * 512:(n % 2 + 1) * 512], PS[:, 4 + n % 4, :]).then_inc(q_copied, 1)
            for n in range(M * C * 2):
                m, c, half = n // (2 * C), n // 2 % C, n % 2
                act.wait_ge(qw_done, 2 * n + 1)
                nc.scalar.copy(QW[:, c, 2 * m, half * 512:(half + 1) * 512], PS[:, 4 + 2 * (n % 2), :]).then_inc(qw_act, 1)
            act.wait_ge(last_done, 2)

            def normalise(b, j):
                act.wait_ge(cn.slot_in[j], 8 * b + (before + 16 - 8 * j))
                at_least(act, ctx_flipped, b - 1)
                at_least(act, tokens_done, b - 1)
                for h in range(2):
                    done = nc.scalar.activation(hat[j][:, h, :], ctx[j][:, h, :], ACT.Identity, bias=cn.shift[:, b, h:h + 1], scale=cn.rstd[:, b, h:h + 1])
                done.then_inc(hat_done, 1)

            def copy_context(b, j):
                act.wait_ge(ctx_flipped, b + 1)
                at_least(act, sim_done, b - 1)
                for c in range(C):
                    done = nc.scalar.activation(keysT[j][:, c, 0:2 * P], PS[:, 6, c * 2 * P:(c + 1) * 2 * P], ACT.Identity,
                                                bias=bm[:, c:c + 1], scale=gm[:, c:c + 1])
                done.then_inc(ctxT_copied, 1)

            def exps(b, j):
                act.wait_ge(top_done, b + 1)
                for u in range(2):
                    done = nc.scalar.activation(probs[j][:, u, :], PS[:, 2 * j + u, 0:KEYS], ACT.Exp, bias=top[j][:, u:u + 1], scale=scale,
                                                accum_out=total[j][:, u:u + 1])
                done.then_inc(exps_done, 1)

            def copy_probs(b, j):
                act.wait_ge(pt_done, b + 1)
                nc.scalar.copy(probsT[j][:].rearrange("p h e -> p (h e)"), PS[:, 4, :]).then_inc(pt_act, 1)

            def first():
                normalise(0, 0)
                normalise(1, 1)
                copy_context(0, 0)
                copy_context(1, 1)
                normalise(2, 0)
                exps(0, 0)

            def turn(b, j):
                copy_probs(b, j)
                exps(b + 1, 1 - j)
                if exists(b + 3):
                    normalise(b + 3, 1 - j)
                if exists(b + 2):
                    copy_context(b + 2, j)

            over_batches(act, first, turn, copy_probs)
            for n in range(0, 2 * M, 2):
                act.wait_ge(out_done, n + 1)
                nc.scalar.copy(OT[:, n // 2, 0:512], PS[:, 0, :]).then_inc(out_act, 1)

        @block.vector
        def _(dve):
            dve.wait_ge(core.x_in, 16)
            norm.vector(dve, core.X, core.H, rows_done)
            dve.wait_ge(rows_done, NT)
            norm.vector(dve, core.H, core.H, normed_done)
            dve.wait_ge(core.weights_in[9], 16)
            if not cn.computed:
                cn.vector_stats(dve, ctx)
            flip.vector(dve, core.HT, gl, bl)
            flip.ready(dve, "dve")
            dve.wait_ge(normed_done, NT)
            dve_step(dve, nc.vector.tensor_tensor(core.H[:], core.H[:], bcast(gl_row, 1, NT), ALU.mult))
            nc.vector.tensor_tensor(core.H[:], core.H[:], bcast(bl_row, 1, NT), ALU.add).then_inc(affine_done, 1)
            for n in range(M * C * 2):
                m, c, half = n // (2 * C), n // 2 % C, n % 2
                dve.wait_ge(qw_done, 2 * n + 2)
                nc.vector.tensor_copy(QW[:, c, 2 * m + 1, half * 512:(half + 1) * 512], PS[:, 5 + 2 * (n % 2), :]).then_inc(qw_dve, 1)
            if not cn.computed:
                cn.vector_finish(dve)
            for c in range(C):
                nc.vector.tensor_scalar(last_cols[:, c, :], cn.lastT[:, c, :], gm[:, c:c + 1], bm[:, c:c + 1], ALU.mult, ALU.add)
            nc.vector.tensor_tensor(last_rows[:], cn.last[:], gm_row[0:B, :], ALU.mult).then_inc(last_done, 1)
            dve.wait_ge(last_done, 1)
            nc.vector.tensor_tensor(last_rows[:], last_rows[:], bm_row[0:B, :], ALU.add).then_inc(last_done, 1)
            dve.wait_ge(stored, 16 * (TB + 1))
            dve.sem_inc(px_copied, 1)

            def tops(b, j):
                dve.wait_ge(sim_done, b + 1)
                dve_step(dve, nc.vector.reduce_max(top[j][:], PS[:, 2 * j:2 * j + 2, 0:KEYS], AX.X))
                nc.vector.tensor_scalar(top[j][:], top[j][:], -scale, None, ALU.mult).then_inc(top_done, 1)

            def weights(b, j):
                dve.wait_ge(exps_done, b + 1)
                dve_step(dve, nc.vector.reciprocal(total[j][:], total[j][:]))
                for u in range(2):
                    done = nc.vector.tensor_scalar(probs[j][:, u, :], probs[j][:, u, :], total[j][:, u:u + 1], None, ALU.mult)
                done.then_inc(probs_done, 1)

            def copy_rest(b, j):
                dve.wait_ge(pt_done, b + 1)
                nc.vector.tensor_copy(probsT_rest[j], PS[0:REST, 5, 0:HEADS * S]).then_inc(pt_dve, 1)

            def copy_px(b, j):
                dve.wait_ge(pv_done, b + 1)
                nc.vector.tensor_copy(QW[:, :, :, bass.ds(b * S, S)], PS[:, 7, :].rearrange("p (c h q) -> p c h q", c=C, q=S)).then_inc(px_copied, 1)

            def first():
                tops(0, 0)
                weights(0, 0)

            def turn(b, j):
                copy_rest(b, j)
                tops(b + 1, 1 - j)
                weights(b + 1, 1 - j)
                copy_px(b, j)

            def last(b, j):
                copy_rest(b, j)
                copy_px(b, j)

            over_batches(dve, first, turn, last, lambda i: dve_step.enter(i, 4), dve_step.leave)
            for n in range(1, 2 * M, 2):
                dve.wait_ge(out_done, n + 1)
                nc.vector.tensor_copy(OT[:, n // 2, 512:1024], PS[:, 1, :]).then_inc(out_dve, 1)
            for n in range(NT // 2):
                dve.wait_ge(proj_done, n + 1)
                x = core.X[:, 2 * n:2 * n + 2, :]
                nc.vector.tensor_tensor(x, PS[:, 4 + n, :].rearrange("p (t d) -> p t d", t=2), x, ALU.add)

        cn.loads, cn.computed = cn.loads + B // 2 * (1 if cn.computed else 2), True


def l3_self(core, load_next):
    nc, norm, flip, dve_step = core.nc, core.norm, core.flip, core.dve_step
    w = core.arena(10)
    wqk, wv, wo = w.take(C, 2 * D), w.take(C, D), w.take(C, D)
    gate = [w.take(16), w.take(16)]
    bo, ln_w, ln_b, head_of = w.take(D), w.take(C), w.take(C), w.take(8)
    sharp, threshold = 15.0, 0.29514
    with ExitStack() as es:
        at = SelfAttention(core, es, "l3a", "resonance", sharp)
        shift = core.sb("l3a_shift", [P, 1], es)
        at.resonance_bias = shift[:]
        products = core.sb("l3a_products", [P, NT, 16, 16], es)
        size = [core.sb(f"l3a_size{i}", [P, NT, 16], es) for i in range(2)]
        k_gate = core.sb("l3a_k_gate", [P, NT, 16], es)
        rows_done, normed_done = core.sem("l3a_rows_done"), core.sem("l3a_normed_done")
        summed, rooted, shift_set = core.sem("l3a_summed"), core.sem("l3a_rooted"), core.sem("l3a_shift_set")
        gated = core.sem("l3a_gated")
        block = es.enter_context(nc.Block())

        @block.sync
        def _(sp):
            load_next(sp)

        @block.tensor
        def _(pe):
            pe.wait_ge(core.consts_in, 16)
            pe.wait_ge(core.weights_in[10], 16)
            flip.tensor(pe, core.H, rows_done, 0)
            flip.tensor(pe, at.Q, normed_done, 0)
            flip.ready(pe, "pe")
            at.project(pe, at.QT, core.HT, wqk, wv)
            at.flip_tensor(pe)
            flip.ready(pe, "pe")
            pe.wait_ge(gated, 1)
            at.attend_tensor(pe)
            at.output_tensor(pe, wo)

        @block.gpsimd
        def _(pool):
            pool.wait_ge(core.weights_in[10], 16)
            flip.uses["pool"] = flip.uses["pe"] - 1
            flip.ready(pool, "pool")
            at.spread_keys(pool, head_of)

        @block.scalar
        def _(act):
            act.wait_ge(core.eps_set, 1)
            norm.scalar(act, core.eps5)
            flip.scalar(act, core.HT)
            norm.scalar(act, core.eps5)
            act.wait_ge(core.weights_in[10], 16)
            flip.scalar(act, at.QT, ln_w, ln_b)
            at.copy_qk(act)
            for n in range(2):
                act.wait_ge(summed, n + 1)
                nc.scalar.activation(size[n][:], size[n][:], ACT.Sqrt).then_inc(rooted, 1)
            flip.scalar(act, at.QT)
            flip.scalar(act, at.KT)
            act.wait_ge(shift_set, 1)
            at.attend_scalar(act)
            flip.scalar(act, core.HT)

        @block.vector
        def _(dve):
            nc.vector.memset(shift[:], -sharp * threshold).then_inc(shift_set, 1)
            dve.wait_ge(core.x_in, 16)
            norm.vector(dve, core.X, core.H, rows_done)
            flip.vector(dve, core.HT)
            norm.vector(dve, core.H, at.Q, normed_done)
            dve.wait_ge(core.weights_in[10], 16)
            flip.vector(dve, at.QT, ln_w, ln_b)
            at.copy_v(dve)
            dve.wait_ge(at.qk_copied, NT)
            for n, rows in enumerate((at.Q, at.K)):
                heads = rows[:].rearrange("p t (h d) -> p t h d", h=16)
                dve_step(dve, nc.vector.tensor_tensor(products[:], heads, heads, ALU.mult))
                nc.vector.reduce_sum(size[n][:], products[:], AX.X).then_inc(summed, 1)
                dve.wait_ge(summed, n + 1)
            for n, (rows, done, g) in enumerate(((at.Q, at.q_rows, at.factor), (at.K, at.k_rows, k_gate))):
                dve.wait_ge(rooted, n + 1)
                heads = rows[:].rearrange("p t (h d) -> p t h d", h=16)
                dve_step(dve, nc.vector.tensor_scalar(size[n][:], size[n][:], 1e-12, None, ALU.max))
                dve_step(dve, nc.vector.reciprocal(size[n][:], size[n][:]))
                nc.vector.tensor_tensor(heads, heads, bcast(size[n][:], 3, 16), ALU.mult).then_inc(done, NT)
                dve.wait_ge(done, NT)
                dve_step(dve, nc.vector.tensor_tensor(products[:], heads, bcast(bcast(gate[n], 1, NT), 2, 16), ALU.mult))
                dve_step(dve, nc.vector.reduce_sum(g[:], products[:], AX.X))
            values = at.V[:].rearrange("p t (h d) -> p t h d", h=16)
            nc.vector.tensor_tensor(values, values, bcast(k_gate[:], 3, 16), ALU.mult).then_inc(gated, 1)
            flip.vector(dve, at.QT)
            flip.vector(dve, at.KT)
            at.attend_vector(dve, None)
            flip.vector(dve, core.HT)
            at.output_vector(dve, bo)


def l3_feed_forward(core, load_next):
    nc, PS, norm, flip, dve_step = core.nc, core.PS, core.norm, core.flip, core.dve_step
    E = EXPERTS[11][0]
    w = core.arena(11)
    wg, bg, b2, number = w.take(C, E), w.take(E), w.take(D), w.take(E)
    with ExitStack() as es:
        ex = Experts(core, es, "l3f", 11, "gelu", *EXPERTS[11])
        bias = OutputBias(core, es, "l3f", E)
        sb = lambda n, shape: core.sb("l3f_" + n, shape, es)
        logits, gate, second = sb("logits", [P, NT, E]), sb("gate", [P, NT, E]), sb("second", [P, NT, E])
        best, next_best, place, odds = sb("best", [P, NT]), sb("next_best", [P, NT]), sb("place", [P, NT]), sb("odds", [P, NT])
        rows_done, routed = core.sem("l3f_rows_done"), core.sem("l3f_routed")
        gap_done, odds_done, weighed = core.sem("l3f_gap_done"), core.sem("l3f_odds_done"), core.sem("l3f_weighed")
        block = es.enter_context(nc.Block())

        @block.sync
        def _(sp):
            load_next(sp)
            ex.load(sp)

        @block.tensor
        def _(pe):
            pe.wait_ge(core.consts_in, 16)
            pe.wait_ge(core.weights_in[11], 16)
            flip.tensor(pe, core.H, rows_done, 0)
            flip.ready(pe, "pe")
            router_tensor(core, pe, core.HT, wg, routed)
            bias.tensor(pe, gate, weighed, b2)
            ex.tensor(pe, core.HT)

        @block.scalar
        def _(act):
            act.wait_ge(core.eps_set, 1)
            norm.scalar(act, core.eps5)
            flip.scalar(act, core.HT)
            act.wait_ge(gap_done, 1)
            nc.scalar.activation(odds[:], odds[:], ACT.Exp).then_inc(odds_done, 1)
            ex.scalar(act)

        @block.vector
        def _(dve):
            dve.wait_ge(core.x_in, 16)
            norm.vector(dve, core.X, core.H, rows_done)
            flip.vector(dve, core.HT)
            dve.wait_ge(core.weights_in[11], 16)
            dve.wait_ge(routed, 1)
            dve_step(dve, nc.vector.tensor_tensor(logits[:], PS[:, 4, 0:NT * E].rearrange("p (t e) -> p t e", e=E), bcast(bg, 1, NT), ALU.add))
            first_best(core, dve, logits, number, best, place, gate)
            dve_step(dve, nc.vector.scalar_tensor_tensor(logits[:], gate[:], NEG, logits[:], ALU.mult, ALU.add))
            first_best(core, dve, logits, number, next_best, place, second)
            nc.vector.tensor_tensor(odds[:], next_best[:], best[:], ALU.subtract).then_inc(gap_done, 1)
            dve.wait_ge(odds_done, 1)
            dve_step(dve, nc.vector.tensor_scalar(best[:], odds[:], 1.0, None, ALU.add))
            dve_step(dve, nc.vector.reciprocal(best[:], best[:]))
            dve_step(dve, nc.vector.tensor_tensor(odds[:], odds[:], best[:], ALU.mult))
            nc.vector.tensor_tensor(gate[:], gate[:], bcast(best[:], 2, E), ALU.mult)
            dve_step(dve, nc.vector.tensor_tensor(second[:], second[:], bcast(odds[:], 2, E), ALU.mult))
            nc.vector.tensor_tensor(gate[:], gate[:], second[:], ALU.add).then_inc(weighed, 1)
            dve.wait_ge(weighed, 1)
            bias.vector(dve)
            ex.vector(dve, core.X, gate)


SUBLAYERS = [l0_cross, l0_self, l0_feed_forward, l1_cross, l1_self, l1_feed_forward, l2_cross, l2_self, l2_feed_forward, l3_cross, l3_self, l3_feed_forward]


def begin(core, load_first):
    nc = core.nc
    with nc.Block(no_gpsimd_drain=True) as block:
        @block.sync
        def _(sp):
            sp.dma_start(core.X[:], core.dram["x"].rearrange("(t p) d -> p t d", p=P)).then_inc(core.x_in, 16)
            sp.dma_start(core.ident[:], core.dram["ident"]).then_inc(core.consts_in, 16)
            load_first(sp)

        @block.vector
        def _(dve):
            nc.vector.memset(core.eps[:, 0:1], 1e-5)
            nc.vector.memset(core.eps[:, 1:2], 1e-6).then_inc(core.eps_set, 1)


def finish(core):
    nc = core.nc
    stored = core.sem("stored")
    with nc.Block(no_gpsimd_drain=True) as block:
        @block.sync
        def _(sp):
            sp.dma_start(core.dram["out"].rearrange("(t p) d -> p t d", p=P), core.X[:]).then_inc(stored, 16)
            sp.wait_ge(stored, 16)


def program(nc, dram):
    with ExitStack() as es:
        core = Core(nc, es, dram)
        loads = [lambda sp, k=k: load_weights(core, sp, k) for k in LAYERS] + [lambda sp: None]
        begin(core, loads[0])
        for n, k in enumerate(LAYERS):
            SUBLAYERS[k](core, loads[n + 1])
            core.free_sems()
        finish(core)


def by_chunk(w):
    return w.reshape(-1, P, w.shape[1]).transpose(1, 0, 2).reshape(P, -1)


def to_all(v):
    return np.broadcast_to(np.asarray(v).reshape(1, -1), (P, np.asarray(v).size))


def column(v):
    return np.asarray(v).reshape(-1, P).T


def packed(parts):
    return np.ascontiguousarray(np.concatenate([np.asarray(p, np.float32) for p in parts], axis=1))


def constants():
    p = np.arange(P)
    angle = (np.arange(S, dtype=np.float32)[:, None] * (10000.0 ** (-2.0 * np.arange(8, dtype=np.float32) / 16)).astype(np.float32)).astype(np.float32)
    return {
        "cos": np.tile(np.cos(angle), (TB, 1)), "sin": np.tile(np.sin(angle), (TB, 1)),
        "causal": np.tile(np.where(np.tri(S, dtype=bool), 0.0, NEG), (TB, 1)),
        "ident": np.eye(P, dtype=np.float32),
        "head_of": (p[:, None] // 16 == np.arange(8)).astype(np.float32),
        "same_head": (p[:, None] // 16 == p // 16).astype(np.float32),
    }


def layout(a):
    k = constants()
    ctx = a["ctx_1024"]
    ctx_by_feature = ctx.transpose(0, 2, 1).reshape(B, C, P, CTX).transpose(0, 2, 1, 3)
    mask = a["mask_BxS2_ff1"]
    out = {"x": a["x"].reshape(B * S, D), "ident": k["ident"], "ctxT": ctx_by_feature}
    left_col = np.zeros((P, 1), np.float32)
    left_col[0:B, 0] = mask[:, CTX - 1]
    out["pack0"] = packed([
        by_chunk(a["L0_xattn_wq"]),
        by_chunk(np.concatenate([a["L0_xattn_wk"], a["L0_xattn_wv"]], axis=1)),
        by_chunk(a["L0_xattn_dense_w"]), to_all(a["L0_xattn_ln_gamma"]), to_all(a["L0_xattn_ln_beta"]),
        to_all(a["L0_xattn_dense_b"]), k["head_of"], k["same_head"],
        mask[:, 0:2 * P].reshape(B, 2, P).transpose(2, 0, 1).reshape(P, -1), left_col,
        ctx[:, CTX - 1, :].T.reshape(C, P, B).transpose(1, 0, 2).reshape(P, -1),
    ])
    first_of = lambda n: to_all(np.arange(n, dtype=np.float32) - n)
    rows = lambda m: np.concatenate([m, np.zeros((P - m.shape[0], m.shape[1]), np.float32)])
    out["pack1"] = packed([
        by_chunk(np.concatenate([a["L0_attn_W_Q"].T, a["L0_attn_W_K"].T], axis=1)),
        by_chunk(a["L0_attn_W_V"].T), by_chunk(a["L0_attn_W_O"].T),
        k["cos"], k["sin"], k["causal"], k["head_of"],
    ])
    out["pack2"] = packed([by_chunk(a["L0_ffn_centroids"].T), column(a["L0_ffn_scale"]), first_of(8)])
    out["experts2"] = np.stack([packed([by_chunk(u), by_chunk(d)]) for u, d in zip(a["L0_ffn_up_w"], a["L0_ffn_down_w"])])
    wkv = a["L1_xattn_Wkv"]
    out["ctx"] = ctx
    out["pack3"] = packed([
        by_chunk(a["L1_xattn_Wq"]), by_chunk(np.concatenate([wkv[:, 0:64], wkv[:, 0:64], wkv[:, 64:128]], axis=1)), by_chunk(a["L1_xattn_Wo"]),
        by_chunk(a["L1_xattn_Wff1"]), by_chunk(a["L1_xattn_Wff2"]), *(column(a[f"L1_xattn_{n}"]) for n in ("ln_g", "ln_b", "cln_g", "cln_b")),
        (np.arange(P)[:, None] // 64 == np.arange(2)[None]).astype(np.float32),
    ])
    w_attn = a["L1_attn_W_attn"].T
    out["pack4"] = packed([
        by_chunk(w_attn[:, 0:1024]), by_chunk(w_attn[:, 1024:1280]), by_chunk(w_attn[:, 1280:1536]), by_chunk(a["L1_attn_W_proj"].T),
        k["causal"], k["head_of"],
    ])
    split = lambda m: np.concatenate([m[..., 0::2], m[..., 1::2]], axis=-1)
    with_shared = lambda n: np.concatenate([a[f"L1_ffn_{n}"], a[f"L1_ffn_s{n}"][None]])
    out["pack5"] = packed([by_chunk(a["L1_ffn_gate_w"].T), to_all(a["L1_ffn_gate_b"]), rows(with_shared("b2")), first_of(8)])
    out["experts5"] = np.stack([
        packed([by_chunk(split(w1)), by_chunk(split(w3)), by_chunk(w2), column(split(b1)), column(split(b3))])
        for w1, w3, w2, b1, b3 in zip(*map(with_shared, ("w1", "w3", "w2", "b1", "b3")))])
    out["pack6"] = packed([
        *(by_chunk(a[f"L2_xattn_{n}"]) for n in ("Wq", "Wk", "Wv", "Wo")), column(a["L2_xattn_bq"]), column(a["L2_xattn_bk"]),
        to_all(a["L2_xattn_bv"]), to_all(a["L2_xattn_bo"]), k["head_of"],
        (np.arange(P)[:, None] % 64 // 16 == np.arange(4)[None]).astype(np.float32),
        ctx[:, CTX - 1, :].T.reshape(C, P, B).transpose(1, 0, 2).reshape(P, -1),
    ])
    four = lambda v: np.repeat(np.asarray(v).reshape(D, 4, 16), 4, axis=1).reshape(D, D)
    out["pack7"] = packed([
        by_chunk(np.concatenate([a["L2_attn_w_q"], four(a["L2_attn_w_k"])], axis=1)),
        by_chunk(four(a["L2_attn_w_v"])), by_chunk(a["L2_attn_w_o"]),
        k["cos"], k["sin"], k["causal"], k["head_of"],
    ])
    out["pack8"] = packed([by_chunk(a["L2_ffn_expert_w"].transpose(2, 0, 1).reshape(D, -1)), by_chunk(a["L2_ffn_gate_w"].T), first_of(8)])
    wk, wv = a["L3_xattn_Wkv"][:, 0:512], a["L3_xattn_Wkv"][:, 512:1024]
    affine = [a[f"L3_xattn_{n}"] for n in ("gm", "bm", "gl", "bl")]
    out["pack9"] = packed([
        by_chunk(a["L3_xattn_Wq"]), by_chunk(wk.T), by_chunk(wv), by_chunk(a["L3_xattn_Wout"]),
        *(column(v) for v in affine), *(to_all(v) for v in affine),
    ])
    out["pack10"] = packed([
        by_chunk(np.concatenate([a["L3_attn_Wq"], a["L3_attn_Wk"]], axis=1)),
        by_chunk(a["L3_attn_Wv"]), by_chunk(a["L3_attn_Wo"]), to_all(a["L3_attn_gq"]), to_all(a["L3_attn_gk"]),
        to_all(a["L3_attn_bo"]), column(a["L3_attn_ln_w"]), column(a["L3_attn_ln_b"]), k["head_of"],
    ])
    out["pack11"] = packed([by_chunk(a["L3_ffn_Wg"]), to_all(a["L3_ffn_bg"]), rows(a["L3_ffn_b2"]), first_of(6)])
    out["experts11"] = np.stack([packed([by_chunk(u), by_chunk(d), column(b)]) for u, d, b in zip(a["L3_ffn_W1"], a["L3_ffn_W2"], a["L3_ffn_b1"])])
    return {n: np.ascontiguousarray(v) for n, v in out.items()}


def kernel(**inputs):
    import concourse.bacc as bacc
    from concourse.bass_utils import run_bass_kernel_spmd

    arrays = layout({n: np.asarray(v) for n, v in inputs.items()})
    nc = bacc.Bacc("TRN2", target_bir_lowering=False, num_devices=1)
    dram = {n: nc.dram_tensor(f"in_{n}_dram", v.shape, F32, kind="ExternalInput").ap() for n, v in arrays.items()}
    dram["out"] = nc.dram_tensor("out_0_dram", (B * S, D), F32, kind="ExternalOutput").ap()
    program(nc, dram)
    got = run_bass_kernel_spmd(nc, [{f"in_{n}_dram": v for n, v in arrays.items()}], core_ids=[0])
    return got.results[0]["out_0_dram"].reshape(B, S, D)
```

```python
from contextlib import ExitStack

import concourse.bass as bass
import numpy as np
from concourse import mybir

F32 = mybir.dt.float32
ALU = mybir.AluOpType
ACT = mybir.ActivationFunctionType
AX = mybir.AxisListType

P = 128
B, S, D = 32, 32, 256
CTX = 257
NT = B * S // P
C = D // P
TB = P // S
NEG = -1e30
LAYERS = list(range(12))
EXPERTS = {2: (8, 3072), 5: (9, 5136), 11: (6, 2052)}
SHARED = 5


class Core:

    def __init__(self, nc, es, dram):
        self.nc, self.es, self.dram = nc, es, dram
        self.sems = []
        self.X = self.sb("X", [P, NT, D])
        self.H = self.sb("H", [P, NT, D])
        self.HT = self.sb("HT", [P, C, NT * P])
        self.weights = [self.sb("weights0", [P, 6400]), self.sb("weights1", [P, 10880])]
        self.consts = self.sb("consts", [P, 2 * P + NT * NT + 25])
        self.ident, self.lower = self.consts[:, 0:P], self.consts[:, P:2 * P]
        self.before = self.consts[:, 2 * P:2 * P + NT * NT].rearrange("p (a b) -> p a b", b=NT)
        self.numbers = self.consts[:, 2 * P + NT * NT:2 * P + NT * NT + 24]
        self.partition = self.consts[:, 2 * P + NT * NT + 24:2 * P + NT * NT + 25]
        self.eps = self.sb("eps", [P, 2])
        self.dve_step = Steps(self, "dve_step")
        self.act_step = Steps(self, "act_step")
        self.pool_step = Steps(self, "pool_step")
        self.stats = self.sb("stats", [P, NT, 6])
        self.moments = self.sb("moments", [P, NT, 2])
        self.std = self.sb("std", [P, NT])
        self.rstd = self.sb("rstd", [P, NT])
        self.warm = self.sb("warm", [P, 1])
        self.PS = es.enter_context(nc.psum_tensor("PS", [P, 8, 512], F32))
        self.consts_in = self.sem("consts_in")
        self.eps_set = self.sem("eps_set")
        self.weights_in = [self.sem(f"weights_in{i}") for i in range(12)]
        self.eps5, self.eps6 = self.eps[:, 0:1], self.eps[:, 1:2]
        self.x_in = self.sem("x_in")
        self.shared_in = self.sem("shared_in")
        self.norm = Norm(self)
        self.flip = Flip(self)
        self.ctx_norm = ContextNorm(self)
        self.sems = []

    def sb(self, name, shape, es=None):
        return (es or self.es).enter_context(self.nc.sbuf_tensor(name, shape, F32))

    def sem(self, name):
        self.sems.append(self.nc.alloc_semaphore(name=name))
        return self.sems[-1]

    def free_sems(self):
        self.nc.clear_and_free_semaphores(self.sems)
        self.sems = []
        self.nc.all_engine_barrier()

    def arena(self, layer):
        return Arena(self, layer)


class Arena:

    def __init__(self, core, layer):
        self.mem, self.at = core.weights[layer % 2], 2 * EXPERTS[layer][1] if layer in EXPERTS else 0

    def take(self, *shape):
        n = 1
        for s in shape:
            n *= s
        out = self.mem[:, self.at:self.at + n]
        self.at += n
        assert self.at <= self.mem.shape[1], self.at
        if len(shape) == 2:
            out = out.rearrange("p (a b) -> p a b", b=shape[1])
        elif len(shape) == 3:
            out = out.rearrange("p (a b c) -> p a b c", b=shape[1], c=shape[2])
        return out


def load_weights(core, sp, layer):
    w, mem = core.dram[f"pack{layer}"], core.weights[layer % 2]
    at = 0
    if layer in EXPERTS:
        n, width = EXPERTS[layer]
        at = 2 * width
    sp.dma_start(mem[:, at:at + w.shape[1]], w).then_inc(core.weights_in[layer], 16)
    if layer == SHARED:
        for part, columns in (("up", slice(0, width - 4 * D)), ("down", slice(width - 4 * D, width))):
            sp.dma_start(mem[:, columns], core.dram[f"experts{layer}_{part}"][n - 1]).then_inc(core.shared_in, 16)


class Steps:

    def __init__(self, core, name):
        self.sem, self.n, self.i = core.sem(name), 0, None

    def enter(self, i, per):
        self.i, self.per, self.k = i, per, 0

    def leave(self, trips):
        assert self.k == self.per, (self.k, self.per)
        self.n, self.i = self.n + trips * self.per, None

    def __call__(self, eng, instruction):
        instruction.then_inc(self.sem, 1)
        if self.i is None:
            self.n += 1
            eng.wait_ge(self.sem, self.n)
        else:
            self.k += 1
            eng.wait_ge(self.sem, self.i * self.per + (self.n + self.k))


class Norm:

    def __init__(self, core):
        self.core = core
        self.moments_done = core.sem("norm_moments_done")
        self.std_done = core.sem("norm_std_done")
        self.uses_dve = self.uses_act = 0

    def vector(self, dve, src, dst, rows_done):
        c, nc = self.core, self.core.nc
        for t in range(NT):
            done = nc.vector.bn_stats(c.stats[:, t, :], src[:, t, :])
        c.dve_step(dve, done)
        self.statistics(dve)
        for t in range(NT):
            nc.vector.tensor_scalar(dst[:, t, :], src[:, t, :], c.moments[:, t, 0:1], c.rstd[:, t:t + 1],
                                    ALU.subtract, ALU.mult).then_inc(rows_done, 1)

    def statistics(self, dve):
        c, nc = self.core, self.core.nc
        self.uses_dve += 1
        for t in range(NT):
            done = nc.vector.bn_aggr(c.moments[:, t, :], c.stats[:, t, :])
        done.then_inc(self.moments_done, 1)
        dve.wait_ge(self.std_done, self.uses_dve)
        c.dve_step(dve, nc.vector.reciprocal(c.rstd[:], c.std[:]))

    def begin(self, act):
        act.wait_ge(self.core.eps_set, 1)
        self.core.nc.scalar.activation(self.core.warm[:], self.core.eps5, ACT.Sqrt)

    def scalar(self, act, eps):
        c, nc = self.core, self.core.nc
        self.uses_act += 1
        act.wait_ge(self.moments_done, self.uses_act)
        nc.scalar.activation(c.std[:], c.moments[:, :, 1], ACT.Sqrt, bias=eps).then_inc(self.std_done, 1)


class Flip:

    def __init__(self, core):
        self.core = core
        self.flipped = core.sem("flipped")
        self.copied_act = core.sem("flip_copied_act")
        self.copied_dve = core.sem("flip_copied_dve")
        self.uses = {"pe": 0, "act": 0, "dve": 0}

    def tensor(self, pe, src, rows_done, before, order=None):
        c, nc = self.core, self.core.nc
        if self.uses["pe"]:
            self.ready(pe, "pe")
        self.uses["pe"] += 1
        for half in range(2):
            for ch in range(C):
                for t in range(4 * half, 4 * half + 4):
                    pe.wait_ge(rows_done, before + t + 1)
                    to, rows = c.PS[:, 2 * half + ch, (t % 4) * P:(t % 4 + 1) * P], src[:, t, ch * P:(ch + 1) * P]
                    if order is None:
                        last = nc.tensor.transpose(to, rows, c.ident[:])
                    else:
                        last = nc.tensor.matmul(to, rows, order, start=True, stop=True)
                last.then_inc(self.flipped, 1)

    def scalar(self, act, dst, scale=None, bias=None):
        c, nc, n = self.core, self.core.nc, self.uses["act"]
        self.uses["act"] += 1
        for half in range(2):
            act.wait_ge(self.flipped, 4 * n + 2 * half + 1)
            bank, to = c.PS[:, 2 * half, :], dst[:, 0, half * 512:(half + 1) * 512]
            if scale is None:
                last = nc.scalar.copy(to, bank)
            elif bias is None:
                last = nc.scalar.activation(to, bank, ACT.Copy, scale=scale[:, 0:1])
            else:
                last = nc.scalar.activation(to, bank, ACT.Identity, bias=bias[:, 0:1], scale=scale[:, 0:1])
            last.then_inc(self.copied_act, 1)

    def vector(self, dve, dst, scale=None, bias=None):
        c, nc, n = self.core, self.core.nc, self.uses["dve"]
        self.uses["dve"] += 1
        for half in range(2):
            dve.wait_ge(self.flipped, 4 * n + 2 * half + 2)
            bank, to = c.PS[:, 2 * half + 1, :], dst[:, 1, half * 512:(half + 1) * 512]
            if scale is None:
                last = nc.vector.tensor_copy(to, bank)
            elif bias is None:
                last = nc.vector.tensor_scalar(to, bank, scale[:, 1:2], None, ALU.mult)
            else:
                last = nc.vector.tensor_scalar(to, bank, scale[:, 1:2], bias[:, 1:2], ALU.mult, ALU.add)
            last.then_inc(self.copied_dve, 1)

    def ready(self, eng, key):
        eng.wait_ge(self.copied_act, 2 * self.uses[key])
        eng.wait_ge(self.copied_dve, 2 * self.uses[key])


def bcast(ap, axis, n):
    shape = list(ap.shape)
    shape.insert(axis, n)
    return ap.unsqueeze(axis).to_broadcast(shape)


class SelfAttention:

    def __init__(self, core, es, name, kind, scale):
        self.core, self.name, self.kind, self.scale = core, name, kind, scale
        sb = lambda n, shape: core.sb(f"{name}_{n}", shape, es)
        sem = lambda n: core.sem(f"{name}_{n}")
        self.Q, self.K, self.V = (sb(n, [P, NT, D]) for n in "QKV")
        self.QT, self.KT = (sb(n, [P, C, NT * P]) for n in ("QT", "KT"))
        self.spread = [sb(f"spread{i}", [P, C, TB, 8, S]) for i in range(2)]
        self.scores = [sb(f"scores{i}", [P, 16, S]) for i in range(2)]
        self.probs = [sb(f"probs{i}", [P, 16, S]) for i in range(2)]
        self.probsT = [sb(f"probsT{i}", [P, 16, S]) for i in range(2)]
        self.top = [sb(f"top{i}", [P, 16]) for i in range(2)]
        self.factor = sb("factor", [P, NT, 16])
        self.qk_done, self.v_done = sem("qk_done"), sem("v_done")
        self.qk_copied, self.v_copied = sem("qk_copied"), sem("v_copied")
        self.q_rows, self.k_rows = sem("q_rows"), sem("k_rows")
        self.spread_done, self.scores_done = sem("spread_done"), sem("scores_done")
        self.scores_read = sem("scores_read")
        self.shifted, self.probs_done = sem("shifted"), sem("probs_done")
        self.probsT_done, self.out_done, self.out_rows = sem("probsT_done"), sem("out_done"), sem("out_rows")
        self.proj_done = sem("proj_done")


    def project(self, pe, xT, xT_v, wqk, wv):
        nc, PS = self.core.nc, self.core.PS
        for t in range(NT):
            if t >= 2:
                pe.wait_ge(self.qk_copied, t - 1)
            for c in range(C):
                last = nc.tensor.matmul(PS[:, 4 + t % 2, :], xT[:, c, t * P:(t + 1) * P], wqk[:, c, :], start=(c == 0), stop=(c == 1))
            last.then_inc(self.qk_done, 1)
            if t >= 2:
                pe.wait_ge(self.v_copied, t - 1)
            for c in range(C):
                last = nc.tensor.matmul(PS[:, 6 + t % 2, 0:D], xT_v[:, c, t * P:(t + 1) * P], wv[:, c, :], start=(c == 0), stop=(c == 1))
            last.then_inc(self.v_done, 1)

    def copy_qk(self, act):
        nc, PS = self.core.nc, self.core.PS
        for t in range(NT):
            act.wait_ge(self.qk_done, t + 1)
            nc.scalar.copy(self.Q[:, t, :], PS[:, 4 + t % 2, 0:D])
            nc.scalar.copy(self.K[:, t, :], PS[:, 4 + t % 2, D:2 * D]).then_inc(self.qk_copied, 1)

    def copy_v(self, dve):
        nc, PS = self.core.nc, self.core.PS
        for t in range(NT):
            dve.wait_ge(self.v_done, t + 1)
            nc.vector.tensor_copy(self.V[:, t, :], PS[:, 6 + t % 2, 0:D]).then_inc(self.v_copied, 1)

    def flip_tensor(self, pe):
        self.core.flip.tensor(pe, self.Q, self.q_rows, 0)
        self.core.flip.tensor(pe, self.K, self.k_rows, 0)


    def spread_keys(self, pool, head_of):
        nc, flip = self.core.nc, self.core.flip
        for t in range(NT):
            if t >= 2:
                pool.wait_ge(self.scores_done, t - 1)
            for c in range(C):
                last = nc.gpsimd.tensor_tensor(self.spread[t % 2][:, c],
                                               bcast(self.KT[:, c, t * P:(t + 1) * P].rearrange("p (b k) -> p b k", k=S), 2, 8),
                                               bcast(bcast(head_of, 1, TB), 3, S), ALU.mult)
            last.then_inc(self.spread_done, 1)

    def attend_tensor(self, pe):
        nc, PS = self.core.nc, self.core.PS
        for t in range(NT + 2):
            if t < NT:
                pe.wait_ge(self.spread_done, t + 1)
                if t >= 2:
                    pe.wait_ge(self.scores_read, t - 1)
                for c in range(C):
                    for b in range(TB):
                        last = nc.tensor.matmul(PS[b * S:(b + 1) * S, 4 + t % 2, c * 256:(c + 1) * 256],
                                                self.QT[:, c, t * P + b * S:t * P + (b + 1) * S],
                                                self.spread[t % 2][:, c, b].rearrange("p h k -> p (h k)"), start=True, stop=True)
                last.then_inc(self.scores_done, 1)
            if t >= 2:
                u = t - 2
                pe.wait_ge(self.probsT_done, u + 1)
                if u >= 2:
                    pe.wait_ge(self.out_rows, u - 1)
                for h in range(16):
                    for b in range(TB):
                        rows = slice(b * S, (b + 1) * S)
                        last = nc.tensor.matmul(PS[rows, 6 + u % 2, h * 16:(h + 1) * 16], self.probsT[u % 2][rows, h, :],
                                                self.V[rows, u, h * 16:(h + 1) * 16], start=True, stop=True)
                last.then_inc(self.out_done, 1)

    def attend_scalar(self, act):
        nc, PS = self.core.nc, self.core.PS
        for t in range(NT):
            i = t % 2
            bank = PS[:, 4 + i, :].rearrange("p (h k) -> p h k", k=S)
            if self.kind == "resonance":
                act.wait_ge(self.scores_done, t + 1)
                if t >= 2:
                    act.wait_ge(self.probsT_done, t - 1)
                nc.scalar.activation(self.probs[i][:], bank, ACT.Sigmoid, scale=self.scale,
                                     bias=self.resonance_bias).then_inc(self.scores_read, 1)
                continue
            if self.kind == "capped":
                act.wait_ge(self.scores_done, t + 1)
                if t >= 2:
                    act.wait_ge(self.probs_done, t - 1)
                nc.scalar.activation(self.scores[i][:], bank, ACT.Tanh, scale=self.tanh_scale).then_inc(self.scores_read, 1)
            act.wait_ge(self.shifted, t + 1)
            if t >= 2:
                act.wait_ge(self.probsT_done, t - 1)
            nc.scalar.activation(self.probs[i][:], self.scores[i][:], ACT.Exp, scale=self.scale).then_inc(self.probs_done, 1)

    def attend_vector(self, dve, causal):
        nc, PS, step = self.core.nc, self.core.PS, self.core.dve_step
        for t in range(NT + 3):
            if t < NT and self.kind != "resonance":
                s = self.scores[t % 2]
                if self.kind == "capped":
                    dve.wait_ge(self.scores_read, t + 1)
                    step(dve, nc.vector.tensor_tensor(s[:], s[:], bcast(causal, 1, 16), ALU.add))
                else:
                    dve.wait_ge(self.scores_done, t + 1)
                    if t >= 2:
                        dve.wait_ge(self.probs_done, t - 1)
                    last = nc.vector.tensor_tensor(s[:], PS[:, 4 + t % 2, :].rearrange("p (h k) -> p h k", k=S),
                                                   bcast(causal, 1, 16), ALU.add)
                    last.then_inc(self.scores_read, 1)
                    dve.wait_ge(self.scores_read, t + 1)
                step(dve, nc.vector.reduce_max(self.top[t % 2][:], s[:], AX.X))
                nc.vector.tensor_tensor(s[:], s[:], bcast(self.top[t % 2][:], 2, S), ALU.subtract).then_inc(self.shifted, 1)
            if 1 <= t <= NT:
                u = t - 1
                p = self.probs[u % 2]
                if u >= 2:
                    dve.wait_ge(self.out_done, u - 1)
                if self.kind == "resonance":
                    dve.wait_ge(self.scores_read, u + 1)
                else:
                    dve.wait_ge(self.probs_done, u + 1)
                    step(dve, nc.vector.reduce_sum(self.factor[:, u, :], p[:], AX.X))
                    step(dve, nc.vector.reciprocal(self.factor[:, u, :], self.factor[:, u, :]))
                nc.vector.transpose(self.probsT[u % 2][:].rearrange("p h k -> p (h k)"),
                                    p[:].rearrange("p h k -> p (h k)")).then_inc(self.probsT_done, 1)
            if t >= 3:
                u = t - 3
                dve.wait_ge(self.out_done, u + 1)
                nc.vector.tensor_tensor(self.core.H[:, u, :].rearrange("p (h d) -> p h d", d=16),
                                        PS[:, 6 + u % 2, 0:D].rearrange("p (h d) -> p h d", d=16),
                                        bcast(self.factor[:, u, :], 2, 16), ALU.mult).then_inc(self.out_rows, 1)


    def output_tensor(self, pe, wo):
        nc, PS = self.core.nc, self.core.PS
        self.core.flip.tensor(pe, self.core.H, self.out_rows, 0)
        self.core.flip.ready(pe, "pe")
        for t in range(NT):
            for c in range(C):
                last = nc.tensor.matmul(PS[:, 4 + t // 2, (t % 2) * D:(t % 2 + 1) * D], self.core.HT[:, c, t * P:(t + 1) * P],
                                        wo[:, c, :], start=(c == 0), stop=(c == 1))
            if t % 2:
                last.then_inc(self.proj_done, 1)

    def output_vector(self, dve, bias=None):
        nc, PS, X = self.core.nc, self.core.PS, self.core.X
        for j in range(NT // 2):
            x = X[:, 2 * j:2 * j + 2, :]
            if bias is not None:
                self.core.dve_step(dve, nc.vector.tensor_tensor(x, x, bcast(bias, 1, 2), ALU.add))
            dve.wait_ge(self.proj_done, j + 1)
            nc.vector.tensor_tensor(x, PS[:, 4 + j, :].rearrange("p (t d) -> p t d", t=2), x, ALU.add)


def rotate(core, dve, first, second, t1, t2, cos, sin, done):
    nc, step = core.nc, core.dve_step
    cos, sin = (bcast(bcast(x, 1, NT), 2, 16) for x in (cos, sin))
    nc.vector.tensor_tensor(t1, first, sin, ALU.mult)
    nc.vector.tensor_tensor(t2, second, sin, ALU.mult)
    nc.vector.tensor_tensor(first, first, cos, ALU.mult)
    step(dve, nc.vector.tensor_tensor(second, second, cos, ALU.mult))
    nc.vector.tensor_tensor(first, first, t2, ALU.subtract)
    last = nc.vector.tensor_tensor(second, second, t1, ALU.add)
    last.then_inc(done, NT)
    dve.wait_ge(done, NT)


def at_least(eng, sem, value):
    if not isinstance(value, int) or value > 0:
        eng.wait_ge(sem, value)


class Places:

    def __init__(self, core, es, name, experts, choices):
        self.core, self.E, self.K, self.T = core, experts, choices, choices * NT + experts - 1
        E, T = self.E, self.T
        sb = lambda x, shape, dt=F32: es.enter_context(core.nc.sbuf_tensor(f"{name}_{x}", shape, dt))
        self.ones = sb("ones", [P, P])
        self.tile_counts, self.before = sb("tile_counts", [P, NT, E]), sb("before", [P, NT, E])
        self.pairs = sb("pairs", [P, NT, E, NT])
        self.count, self.tiles, self.start = sb("count", [P, E]), sb("tiles", [P, E]), sb("start", [P, E])
        self.places = sb("places", [P, NT, E])
        self.place, self.place_row = sb("place", [P, choices, NT]), sb("place_row", [P, choices, NT], mybir.dt.uint32)
        self.ended, self.expert = sb("ended", [P, T, E]), sb("expert", [P, T])
        self.weight_row = sb("weight_row", [P, T], mybir.dt.uint32)
        self.counted, self.done = core.sem(f"{name}_counted"), core.sem(f"{name}_placed")

    def tensor(self, pe, chosen, chosen_done):
        nc, PS, n = self.core.nc, self.core.PS, NT * self.E
        pe.wait_ge(chosen_done, 1)
        rows = chosen[:].rearrange("p t e -> p (t e)")
        nc.tensor.matmul(PS[:, 4, 0:n], self.core.lower, rows, start=True, stop=True)
        nc.tensor.matmul(PS[:, 4, n:2 * n], self.ones[:], rows, start=True, stop=True).then_inc(self.counted, 1)
        pe.wait_ge(self.done, 1)

    def vector(self, dve, choices):
        nc, PS, E, T = self.core.nc, self.core.PS, self.E, self.T
        step = lambda instruction: self.core.dve_step(dve, instruction)
        before_tile, before_expert = self.core.before[:, 0:NT, 0:NT], self.core.before[:, 0:E, 0:E]
        n = NT * E
        by_tile = lambda bank: bank.rearrange("p (t e) -> p t e", e=E)
        dve.wait_ge(self.counted, 1)
        step(nc.vector.tensor_copy(self.tile_counts[:], by_tile(PS[:, 4, n:2 * n])))
        counts = self.tile_counts[:].rearrange("p t e -> p e t")
        step(nc.vector.tensor_tensor(self.pairs[:], bcast(counts, 1, NT), bcast(before_tile, 2, E), ALU.mult))
        nc.vector.reduce_sum(self.before[:], self.pairs[:], AX.X)
        step(nc.vector.reduce_sum(self.count[:], counts, AX.X))
        over = self.pairs[:, 0, :, :]
        step(nc.vector.tensor_tensor(over, bcast(self.count[:], 2, NT), bcast(self.core.numbers[:, 0:NT], 1, E), ALU.is_gt))
        step(nc.vector.reduce_sum(self.tiles[:], over, AX.X))
        earlier = self.pairs[:, 1, :, 0:E]
        step(nc.vector.tensor_tensor(earlier, bcast(self.tiles[:], 1, E), before_expert, ALU.mult))
        step(nc.vector.reduce_sum(self.start[:], earlier, AX.X))
        nc.vector.tensor_tensor(self.places[:], self.before[:], by_tile(PS[:, 4, 0:n]), ALU.add)
        step(nc.vector.tensor_scalar(self.count[:], self.start[:], float(P), None, ALU.mult))
        step(nc.vector.tensor_tensor(self.places[:], self.places[:], bcast(self.count[:], 1, NT), ALU.add))
        for k in range(self.K):
            step(nc.vector.tensor_tensor(self.before[:], self.places[:], choices[k][:], ALU.mult))
            step(nc.vector.reduce_sum(self.place[:, k, :], self.before[:], AX.X))
        nc.vector.tensor_copy(self.place_row[:], self.place[:])
        step(nc.vector.tensor_tensor(self.tiles[:], self.tiles[:], self.start[:], ALU.add))
        step(nc.vector.tensor_scalar(self.tiles[:], self.tiles[:], float(P), None, ALU.mult))
        step(nc.vector.tensor_tensor(self.ended[:], bcast(self.tiles[:], 1, T), bcast(self.core.numbers[:, 0:T], 2, E), ALU.is_le))
        step(nc.vector.reduce_sum(self.expert[:], self.ended[:], AX.X))
        step(nc.vector.tensor_scalar(self.expert[:], self.expert[:], float(E - 1), float(P), ALU.min, ALU.mult))
        step(nc.vector.tensor_scalar(self.expert[:], self.expert[:], self.core.partition, None, ALU.add))
        nc.vector.tensor_copy(self.weight_row[:], self.expert[:]).then_inc(self.done, 1)
        dve.wait_ge(self.done, 1)


RING = 3


def before(q, j):
    return (q, j - 1) if j else (q - 1, RING - 1)


def after(q, j):
    return (q, j + 1) if j < RING - 1 else (q + 1, 0)


class SortedExperts:

    def __init__(self, core, es, name, layer, kind, choices, shared=False):
        self.core, self.name, self.kind, self.layer = core, name, kind, layer
        self.E, self.K, self.S = EXPERTS[layer][0] - shared, choices, NT * shared
        self.places = Places(core, es, name + "_sort", self.E, choices)
        self.T = self.places.T
        self.N = self.S + self.T
        self.begin = self.S + 1 if shared else RING
        self.trips = (self.N - RING - self.begin) // RING
        nc, T = core.nc, self.T
        sb = lambda x, shape: core.sb(f"{name}_{x}", shape, es)
        ring = lambda x, shape: [sb(f"{x}{i}", shape) for i in range(RING)]
        two = lambda x, shape: [sb(f"{x}{i}", shape) for i in range(2)]
        sem = lambda x: core.sem(f"{name}_{x}")
        self.units = 2 if kind == "swiglu" else 1
        self.hidden, self.side = ring("hidden", [P, 4, P]), ring("side", [P, 4, P])
        if kind == "swiglu":
            self.product, self.sigmoid = two("product", [P, 4, P]), sb("sigmoid", [P, 4, P])
            self.gated = sb("gated", [P, 4, P])
            self.gate_done, self.sigmoid_done = sem("gate_done"), sem("sigmoid_done")
        self.zeros, self.rows_in, self.xT, self.out = sb("zeros", [P, D]), ring("rows_in", [P, D]), ring("xT", [P, C, P]), ring("out", [P, D])
        self.gathered = sb("gathered", [P, NT, choices, D])
        self.sorted_dram = nc.dram_tensor(f"{name}_sorted_dram", (T * P, D), F32).ap()
        self.out_dram = nc.dram_tensor(f"{name}_out_dram", (T * P, D), F32).ap()
        self.zeros_set, self.zeroed, self.scattered = sem("zeros_set"), sem("zeroed"), sem("scattered")
        self.rows_loaded, self.stored, self.up_in, self.down_in = ([sem(f"{x}{j}") for j in range(RING)] for x in ("rows_loaded", "stored", "up_in", "down_in"))
        self.flipped, self.copied, self.up_done, self.side_done = sem("flipped"), sem("copied"), sem("up_done"), sem("side_done")
        self.hidden_done, self.down_done, self.out_copied = sem("hidden_done"), sem("down_done"), sem("out_copied")
        self.gather_done = [sem(f"gather_done{g}") for g in range(4)]
        width = EXPERTS[layer][1]
        slot = lambda i: core.weights[layer % 2][:, i * width:(i + 1) * width]
        self.slots = [sb("slot0", [P, width])[:], slot(1), sb("slot2", [P, width])[:] if shared else slot(0)]
        self.shared = self.views(slot(0)) if shared else None
        self.weights = [self.views(s) for s in self.slots]
        self.up_width = width - 4 * D

    def views(self, mem):
        out, at = {}, 0
        for key, shape in {"glu": [("up", (C, 1024))],
                           "swiglu": [("up1", (C, 1024)), ("up3", (C, 1024)), ("b1", (8,)), ("b3", (8,))],
                           "gelu": [("up", (C, 512)), ("b1", (4,))]}[self.kind] + [("down", (4, D))]:
            m = int(np.prod(shape))
            out[key] = mem[:, at:at + m]
            if len(shape) == 2:
                out[key] = out[key].rearrange("p (c n) -> p c n", c=shape[0])
            at += m
        assert at == mem.shape[1], (at, mem.shape)
        return out

    def over(self, eng, first, turn, last, steps=0):
        count = steps and eng is self.core.nc.vector

        def three(begin, trips, shared):
            with eng.Fori(0, trips) as i:
                if count:
                    self.core.dve_step.enter(i, RING * steps)
                for n in range(begin, begin + RING):
                    turn(i + n // RING, n % RING, shared)
                if count:
                    self.core.dve_step.leave(trips)

        first()
        if self.S:
            turn(0, 0, True)
            three(1, (self.S - 2) // RING, True)
            turn(*divmod(self.S - 1, RING), True)
        for n in range(self.S, self.begin):
            turn(*divmod(n, RING), False)
        three(self.begin, self.trips, False)
        for n in range(self.begin + RING * self.trips, self.N):
            turn(*divmod(n, RING), False)
        last()

    def nth(self, q, j):
        return q + (1 - (self.S - j + RING - 1) // RING)

    def sorted_next(self, n, shared):
        return (not isinstance(n, int) or n + 1 < self.N) and (not shared or (isinstance(n, int) and n == self.S - 1))


    def load(self, sp):
        S, of = self.S, lambda t: t.rearrange("(i p) d -> p i d", p=P)
        sp.wait_ge(self.zeros_set, 1)
        sp.dma_start(of(self.sorted_dram), bcast(self.zeros[:], 1, self.T)).then_inc(self.zeroed, 16)

        def load_rows(q, j):
            n = RING * q + j
            at_least(sp, self.flipped, n - (S + RING - 1))
            sp.dma_start(self.rows_in[j][:], self.sorted_dram[bass.ds((n - S) * P, P), :]).then_inc(self.rows_loaded[j], 16)

        def store(q, j):
            n = RING * q + j
            sp.wait_ge(self.out_copied, n + 1)
            sp.dma_start(self.out_dram[bass.ds((n - S) * P, P), :], self.out[j][:]).then_inc(self.stored[j], 16)

        def turn(q, j):
            if not isinstance(q, int) or RING * (q + 1) + j < self.N:
                load_rows(q + 1, j)
            if not isinstance(q, int) or RING * q + j > S:
                store(*before(q, j))

        sp.wait_ge(self.scattered, 16 * NT * self.K)
        for n in range(S, S + RING):
            load_rows(*divmod(n, RING))
        for n in range(S, self.begin):
            turn(*divmod(n, RING))
        with sp.Fori(0, self.trips) as i:
            for n in range(self.begin, self.begin + RING):
                turn(i + n // RING, n % RING)
        for n in range(self.begin + RING * self.trips, self.N):
            turn(*divmod(n, RING))
        store(*divmod(self.N - 1, RING))


    def scatter(self, pool, rows, rows_done, rows_before):
        nc, S, T, K, dram = self.core.nc, self.S, self.T, self.K, self.core.dram
        at = bass.IndirectOffsetOnAxis
        up_dram, down_dram = (dram[f"experts{self.layer}_{x}"].rearrange("e p n -> (e p) n") for x in ("up", "down"))
        nc.gpsimd.memset(self.zeros[:], 0.0).then_inc(self.zeros_set, 1)
        pool.wait_ge(self.places.done, 1)

        def load(i):
            j, row = (S + i) % RING, at(ap=self.places.weight_row[:, i:i + 1], axis=0)
            for part, loaded, read, columns in ((up_dram, self.up_in, self.hidden_done, slice(0, self.up_width)),
                                                (down_dram, self.down_in, self.down_done, slice(self.up_width, None))):
                if i >= RING:
                    pool.wait_ge(read, S + i - RING + 1)
                nc.gpsimd.indirect_dma_start(self.slots[j][:, columns], None, part, row).then_inc(loaded[j], 16)

        load(0)
        pool.wait_ge(rows_done, rows_before + NT)
        pool.wait_ge(self.zeroed, 16)
        for t in range(NT):
            for k in range(K):
                nc.gpsimd.indirect_dma_start(self.sorted_dram, at(ap=self.places.place_row[:, k, t:t + 1], axis=0), rows[:, t, :], None).then_inc(self.scattered, 16)
        for i in range(1, T):
            load(i)
        for n in range(self.N - RING, self.N):
            pool.wait_ge(self.stored[n % RING], 16 * self.nth(*divmod(n, RING)))
        for t in range(NT):
            for k in range(K):
                nc.gpsimd.indirect_dma_start(self.gathered[:, t, k, :], None, self.out_dram, at(ap=self.places.place_row[:, k, t:t + 1], axis=0)).then_inc(self.gather_done[t // 2], 16)


    def tensor(self, pe, xT):
        nc, PS, S, U = self.core.nc, self.core.PS, self.S, self.units

        def flip_rows(q, j):
            n = RING * q + j
            at_least(pe, self.copied, n - S)
            pe.wait_ge(self.rows_loaded[j], 16 * self.nth(q, j))
            for c in range(C):
                done = nc.tensor.transpose(PS[:, 6, c * P:(c + 1) * P], self.rows_in[j][:, c * P:(c + 1) * P], self.core.ident[:])
            done.then_inc(self.flipped, 1)

        def up(q, j, shared):
            n = RING * q + j
            w = self.shared if shared else self.weights[j]
            if not shared:
                pe.wait_ge(self.up_in[j], 16 * self.nth(q, j))
                pe.wait_ge(self.copied, n + (1 - S))
            for u in range(U):
                if U == 2:
                    at_least(pe, (self.gate_done, self.hidden_done)[u], n)
                    bank, mats = 2 * u, [w[key][:, :, 512 * u:512 * (u + 1)] for key in ("up1", "up3")]
                else:
                    at_least(pe, self.hidden_done, n - (RING - 1))
                    bank, mats = 2 * j, [w["up"][:, :, a:a + 512] for a in range(0, w["up"].shape[2], 512)]
                for a, mat in enumerate(mats):
                    for m in range(4):
                        for c in range(C):
                            x = xT[:, c, bass.ds(n * P, P)] if shared else self.xT[j][:, c, :]
                            done = nc.tensor.matmul(PS[:, bank + a, m * P:(m + 1) * P], mat[:, c, m * P:(m + 1) * P], x, start=(c == 0), stop=(c == 1))
                done.then_inc(self.up_done, 1)

        def down(q, j, shared):
            n = RING * q + j
            w = self.shared if shared else self.weights[j]
            pe.wait_ge(self.hidden_done, n + 1)
            at_least(pe, self.out_copied, n)
            if not shared:
                pe.wait_ge(self.down_in[j], 16 * self.nth(q, j))
            for m in range(4):
                done = nc.tensor.matmul(PS[:, 7, 0:D], self.hidden[j][:, m, :], w["down"][:, m, :], start=(m == 0), stop=(m == 3))
            done.then_inc(self.down_done, 1)

        def turn(q, j, shared):
            n = RING * q + j
            if self.sorted_next(n, shared):
                flip_rows(*after(q, j))
            up(q, j, shared)
            if not isinstance(n, int) or n:
                down(*before(q, j), shared or (isinstance(n, int) and n == S))

        self.over(pe, lambda: S or flip_rows(0, 0), turn, lambda: down(*divmod(self.N - 1, RING), False))


    def scalar(self, act, scale=None):
        nc, PS, S = self.core.nc, self.core.PS, self.S

        def copy_rows(q, j):
            n = RING * q + j
            act.wait_ge(self.flipped, n + (1 - S))
            at_least(act, self.up_done, self.units * (n - (RING - 1)))
            if scale is None:
                done = nc.scalar.copy(self.xT[j][:].rearrange("p c n -> p (c n)"), PS[:, 6, 0:C * P])
            else:
                for c in range(C):
                    done = nc.scalar.activation(self.xT[j][:, c, :], PS[:, 6, c * P:(c + 1) * P], ACT.Copy, scale=scale[:, c:c + 1])
            done.then_inc(self.copied, 1)

        def turn(q, j, shared):
            n = RING * q + j
            w = self.shared if shared else self.weights[j]
            if self.sorted_next(n, shared):
                copy_rows(*after(q, j))
            if self.kind == "glu":
                act.wait_ge(self.up_done, n + 1)
                at_least(act, self.hidden_done, n - (RING - 1))
                nc.scalar.activation(self.side[j][:].rearrange("p m n -> p (m n)"), PS[:, 2 * j + 1, :], ACT.Silu).then_inc(self.side_done, 1)
            elif self.kind == "gelu":
                act.wait_ge(self.up_done, n + 1)
                at_least(act, self.down_done, n - (RING - 1))
                for m in range(4):
                    done = nc.scalar.activation(self.hidden[j][:, m, :], PS[:, 2 * j, m * P:(m + 1) * P], ACT.Gelu, bias=w["b1"][:, m:m + 1])
                done.then_inc(self.hidden_done, 1)
            else:
                for u in range(2):
                    act.wait_ge(self.up_done, 2 * n + (u + 1))
                    at_least(act, (self.gate_done, self.hidden_done)[u], n)
                    for m in range(4):
                        done = nc.scalar.activation(self.side[u][:, m, :], PS[:, 2 * u, m * P:(m + 1) * P], ACT.Identity, bias=w["b1"][:, 4 * u + m:4 * u + m + 1])
                    done.then_inc(self.side_done, 1)
                    if u == 0:
                        act.wait_ge(self.gate_done, n + 1)
                        at_least(act, self.hidden_done, n)
                        nc.scalar.activation(self.sigmoid[:], self.gated[:], ACT.Sigmoid, scale=1.702).then_inc(self.sigmoid_done, 1)

        self.over(act, lambda: S or copy_rows(0, 0), turn, lambda: None)


    def vector(self, dve, weights):
        nc, PS, X, S, step = self.core.nc, self.core.PS, self.core.X, self.S, self.core.dve_step

        def copy_out(q, j, shared):
            n = RING * q + j
            dve.wait_ge(self.down_done, n + 1)
            if shared:
                x = X[:, bass.ds(n, 1), :].rearrange("p t d -> p (t d)")
                nc.vector.tensor_tensor(x, PS[:, 7, 0:D], x, ALU.add).then_inc(self.out_copied, 1)
                return
            if not isinstance(n, int) or n >= S + RING:
                dve.wait_ge(self.stored[j], 16 * (self.nth(q, j) - 1))
            nc.vector.tensor_copy(self.out[j][:], PS[:, 7, 0:D]).then_inc(self.out_copied, 1)

        def hidden_units(q, j, shared):
            n = RING * q + j
            w = self.shared if shared else self.weights[j]
            if self.kind == "glu":
                dve.wait_ge(self.side_done, n + 1)
                at_least(dve, self.down_done, n - (RING - 1))
                nc.vector.tensor_tensor(self.hidden[j][:].rearrange("p m n -> p (m n)"), PS[:, 2 * j, :],
                                        self.side[j][:].rearrange("p m n -> p (m n)"), ALU.mult).then_inc(self.hidden_done, 1)
            elif self.kind == "swiglu":
                for u in range(2):
                    p = self.product[u]
                    dve.wait_ge(self.side_done, 2 * n + (u + 1))
                    for m in range(4):
                        done = nc.vector.scalar_tensor_tensor(p[:, m, :], PS[:, 2 * u + 1, m * P:(m + 1) * P], w["b3"][:, 4 * u + m:4 * u + m + 1],
                                                              self.side[u][:, m, :], ALU.add, ALU.mult)
                    step(dve, done)
                    if u == 0:
                        at_least(dve, self.sigmoid_done, n)
                        nc.vector.tensor_scalar(self.gated[:], p[:], 7.0, None, ALU.min).then_inc(self.gate_done, 1)
                        dve.wait_ge(self.gate_done, n + 1)
                step(dve, nc.vector.tensor_scalar(p[:], p[:], -7.0, 7.0, ALU.max, ALU.min))
                step(dve, nc.vector.scalar_tensor_tensor(p[:], p[:], 1.0, self.gated[:], ALU.add, ALU.mult))
                dve.wait_ge(self.sigmoid_done, n + 1)
                at_least(dve, self.down_done, n)
                nc.vector.tensor_tensor(self.hidden[j][:], p[:], self.sigmoid[:], ALU.mult).then_inc(self.hidden_done, 1)

        def turn(q, j, shared):
            n = RING * q + j
            hidden_units(q, j, shared)
            if not isinstance(n, int) or n:
                copy_out(*before(q, j), shared or (isinstance(n, int) and n == S))

        self.over(dve, lambda: None, turn, lambda: copy_out(*divmod(self.N - 1, RING), False), steps=4 if self.kind == "swiglu" else 0)
        for t in range(NT):
            if t % 2 == 0:
                dve.wait_ge(self.gather_done[t // 2], 32 * self.K)
            for k in range(self.K):
                x, y = X[:, t, :], self.gathered[:, t, k, :]
                if weights[k] is None:
                    nc.vector.tensor_tensor(x, y, x, ALU.add)
                else:
                    done = nc.vector.scalar_tensor_tensor(x, y, weights[k][:, t:t + 1], x, ALU.mult, ALU.add)
                    if k < self.K - 1:
                        step(dve, done)


def first_best(core, dve, values, number, best, place, chosen):
    nc, step = core.nc, core.dve_step
    n = values.shape[2]
    step(dve, nc.vector.reduce_max(best[:], values[:], AX.X))
    step(dve, nc.vector.tensor_tensor(chosen[:], values[:], bcast(best[:], 2, n), ALU.is_equal))
    step(dve, nc.vector.tensor_tensor(chosen[:], chosen[:], bcast(number, 1, NT), ALU.mult))
    step(dve, nc.vector.tensor_reduce(place[:], chosen[:], AX.X, ALU.min))
    step(dve, nc.vector.tensor_tensor(chosen[:], bcast(number, 1, NT), bcast(place[:], 2, n), ALU.is_equal))


def router_tensor(core, pe, xT, wg, done):
    nc, PS, n = core.nc, core.PS, wg.shape[2]
    for t in range(NT):
        for c in range(C):
            last = nc.tensor.matmul(PS[:, 4, t * n:(t + 1) * n], xT[:, c, t * P:(t + 1) * P], wg[:, c, :], start=(c == 0), stop=(c == 1))
    last.then_inc(done, 1)


class OutputBias:

    def __init__(self, core, es, name, n):
        self.core, self.n = core, n
        self.gateT = core.sb(f"{name}_gateT", [n, NT * P], es)
        self.flipped, self.copied, self.done, self.added = (core.sem(f"{name}_bias_{x}") for x in ("flipped", "copied", "done", "added"))

    def tensor(self, pe, gate, gate_done, b2):
        nc, PS = self.core.nc, self.core.PS
        pe.wait_ge(gate_done, 1)
        for t in range(NT):
            last = nc.tensor.transpose(PS[0:self.n, 4 + t // 4, (t % 4) * P:(t % 4 + 1) * P], gate[:, t, :], self.core.ident[:])
        last.then_inc(self.flipped, 1)
        pe.wait_ge(self.copied, 1)
        for t in range(NT):
            last = nc.tensor.matmul(PS[:, 4 + t // 2, (t % 2) * D:(t % 2 + 1) * D], self.gateT[:, t * P:(t + 1) * P], b2[0:self.n, :],
                                    start=True, stop=True)
        last.then_inc(self.done, 1)
        pe.wait_ge(self.added, 1)

    def vector(self, dve):
        nc, PS, X = self.core.nc, self.core.PS, self.core.X
        dve.wait_ge(self.flipped, 1)
        nc.vector.tensor_copy(self.gateT[:], PS[0:self.n, 4:6, :].rearrange("e a n -> e (a n)")).then_inc(self.copied, 1)
        dve.wait_ge(self.done, 1)
        nc.vector.tensor_tensor(X[:], PS[:, 4:8, :].rearrange("p a (t d) -> p (a t) d", d=D), X[:], ALU.add).then_inc(self.added, 1)
        dve.wait_ge(self.added, 1)


def exists(b):
    return not isinstance(b, int) or b < B


def over_batches(eng, first, turn, last, enter=None, leave=None):
    first()
    trips = (B - 4) // 2
    with eng.Fori(0, trips) as i:
        if enter:
            enter(i)
        turn(2 * i, 0)
        turn(2 * i + 1, 1)
        if leave:
            leave(trips)
    for b in range(2 * trips, B - 1):
        turn(b, b % 2)
    last(B - 1, 1)


class ContextNorm:

    def __init__(self, core):
        self.core = core
        self.mean, self.rstd = core.sb("ctx_mean", [P, B, 2]), core.sb("ctx_rstd", [P, B, 2])
        self.shift = core.sb("ctx_shift", [P, B, 2])
        self.last, self.lastT = core.sb("ctx_last", [B, D]), core.sb("ctx_lastT", [P, C, B])
        self.slot_in = [core.sem("ctx_slot_in0"), core.sem("ctx_slot_in1")]
        self.last_in, self.stats_done = core.sem("ctx_last_in"), core.sem("ctx_stats_done")
        self.spread_done, self.std_done = core.sem("ctx_spread_done"), core.sem("ctx_std_done")
        self.ready, self.flipped, self.lastT_done = core.sem("ctx_ready"), core.sem("ctx_flipped"), core.sem("ctx_lastT_done")
        self.computed, self.loads = False, 0

    def allocate(self, es, name):
        self.stats = self.core.sb(name + "_ctx_stats", [P, B, 2, 6], es)
        self.stats_last, self.moments_last = self.core.sb(name + "_ctx_stats_last", [B, 6], es), self.core.sb(name + "_ctx_moments_last", [B, 2], es)
        self.std, self.std_last = self.core.sb(name + "_ctx_std", [P, B, 2], es), self.core.sb(name + "_ctx_std_last", [B, 1], es)
        self.gap = self.core.sb(name + "_ctx_gap", [P, B, 2], es)

    def load(self, sp, slots):
        ctx = self.core.dram["ctx"]
        tile = lambda b: ctx[b, 0:2 * P, :].rearrange("(h p) d -> p h d", p=P)
        sp.dma_start(self.last[:], ctx[:, CTX - 1, :]).then_inc(self.last_in, 16)
        for j in range(2):
            sp.dma_start(slots[j][:], tile(j)).then_inc(self.slot_in[j], 16)
        with sp.Fori(0, B // 2 - 1) as i:
            for j in range(2):
                sp.wait_ge(self.stats_done, 2 * i + (j + 1))
                sp.dma_start(slots[j][:], tile(2 * i + (j + 2))).then_inc(self.slot_in[j], 16)
        for j in range(2):
            sp.wait_ge(self.stats_done, B - 1 + j)
            sp.dma_start(slots[j][:], tile(j)).then_inc(self.slot_in[j], 16)

    def vector_stats(self, dve, slots):
        nc, step = self.core.nc, self.core.dve_step
        with dve.Fori(0, B // 2) as i:
            for j in range(2):
                dve.wait_ge(self.slot_in[j], 16 * i + 16)
                for h in range(2):
                    done = nc.vector.bn_stats(self.stats[:, 2 * i + j, h, :], slots[j][:, h, :])
                done.then_inc(self.stats_done, 1)
        dve.wait_ge(self.stats_done, B)
        dve.wait_ge(self.last_in, 16)
        step(dve, nc.vector.bn_stats(self.stats_last[:], self.last[:]))
        m0, s0, m1, s1 = (self.stats[:, :, :, n] for n in (1, 2, 4, 5))
        nc.vector.bn_aggr(self.moments_last[:], self.stats_last[:])
        nc.vector.tensor_tensor(self.gap[:], m0, m1, ALU.subtract)
        step(dve, nc.vector.tensor_tensor(self.mean[:], m0, m1, ALU.add))
        nc.vector.tensor_scalar(self.mean[:], self.mean[:], 0.5, None, ALU.mult)
        step(dve, nc.vector.tensor_tensor(self.std[:], s0, s1, ALU.add))
        step(dve, nc.vector.tensor_tensor(self.gap[:], self.gap[:], self.gap[:], ALU.mult))
        step(dve, nc.vector.tensor_scalar(self.gap[:], self.gap[:], 0.25, None, ALU.mult))
        nc.vector.scalar_tensor_tensor(self.std[:], self.std[:], 1.0 / D, self.gap[:], ALU.mult, ALU.add).then_inc(self.spread_done, 1)

    def vector_finish(self, dve):
        nc, step = self.core.nc, self.core.dve_step
        dve.wait_ge(self.std_done, 1)
        nc.vector.reciprocal(self.rstd[:], self.std[:])
        step(dve, nc.vector.reciprocal(self.std_last[:], self.std_last[:]))
        nc.vector.scalar_tensor_tensor(self.shift[:], self.mean[:], -1.0, self.rstd[:], ALU.mult, ALU.mult)
        nc.vector.tensor_scalar(self.last[:], self.last[:], self.moments_last[:, 0:1], self.std_last[:], ALU.subtract, ALU.mult).then_inc(self.ready, 1)
        dve.wait_ge(self.flipped, 1)
        nc.vector.tensor_copy(self.lastT[:], self.core.PS[:, 7, 0:C * B].rearrange("p (c b) -> p c b", c=C)).then_inc(self.lastT_done, 1)
        dve.wait_ge(self.lastT_done, 1)

    def scalar(self, act):
        nc = self.core.nc
        act.wait_ge(self.spread_done, 1)
        nc.scalar.activation(self.std_last[:], self.moments_last[:, 1:2], ACT.Sqrt, bias=self.core.eps5[0:B, :])
        nc.scalar.activation(self.std[:], self.std[:], ACT.Sqrt, bias=self.core.eps5).then_inc(self.std_done, 1)

    def tensor(self, pe):
        nc = self.core.nc
        pe.wait_ge(self.ready, 1)
        for c in range(C):
            done = nc.tensor.transpose(self.core.PS[:, 7, c * B:(c + 1) * B], self.last[:, c * P:(c + 1) * P], self.core.ident[0:B, 0:B])
        done.then_inc(self.flipped, 1)
        pe.wait_ge(self.lastT_done, 1)


def l0_cross(core, load_next):
    nc, PS, norm, flip, dve_step, pool_step = core.nc, core.PS, core.norm, core.flip, core.dve_step, core.pool_step
    KVW = P + 8
    RW = P + 2
    w = core.arena(0)
    wqkv = w.take(6, D)
    dense = w.take(C, D)
    gamma, beta, dense_b = w.take(D), w.take(D), w.take(D)
    head_of = w.take(8)
    same_head = w.take(P)
    em_in = w.take(B, 2)
    em_left_in = w.take(1)
    cleft = w.take(C, B)
    order = w.take(P)
    with ExitStack() as es:
        sb = lambda name, shape: core.sb("l0x_" + name, shape, es)
        ctxT = [sb(f"ctxT{i}", [P, C, CTX]) for i in range(2)]
        wsum, sq = sb("wsum", [P, 6]), sb("sq", [P, NT, D])
        em = sb("em", [P, B, 2, 2])
        eml = sb("eml", [B, 2])
        ss = [sb(f"ss{i}", [P, 4]) for i in range(2)]
        std = [sb(f"std{i}", [P, 4]) for i in range(2)]
        rstd = [sb(f"rstd{i}", [P, 4]) for i in range(2)]
        kp = [sb(f"kp{i}", [P, 2, D]) for i in range(2)]
        vr = [sb(f"vr{i}", [P, 2, C, RW]) for i in range(2)]
        kp_left, vr_left = sb("kp_left", [B, D]), sb("vr_left", [B, C, RW])
        vr_one = [sb(f"vr_one{i}", [B, C, RW]) for i in range(2)]
        kv_tmp = [sb(f"kv_tmp{i}", [P, C, P]) for i in range(2)]
        scale_v, shift_v = sb("scale_v", [P, C, P]), sb("shift_v", [P, C, P])
        KV = sb("KV", [P, B, C, KVW])
        qss, qstd, qrstd = sb("qss", [P, NT]), sb("qstd", [P, NT]), sb("qrstd", [P, NT])
        z = [sb(f"z{i}", [P, C, 8]) for i in range(2)]

        ctx_in = [core.sem(f"l0x_ctx_in{i}") for i in range(2)]
        rows_done = core.sem("l0x_rows_done")
        centered = core.sem("l0x_centered")
        q_done = core.sem("l0x_q_done")
        q_squared = core.sem("l0x_q_squared")
        q_std = core.sem("l0x_q_std")
        proj_done = core.sem("l0x_proj_done")
        std_done = core.sem("l0x_std_done")
        scale_ready = core.sem("l0x_scale_ready")
        v_ready = core.sem("l0x_v_ready")
        kv_ready = core.sem("l0x_kv_ready")
        kv_done = core.sem("l0x_kv_done")
        kv_kept = core.sem("l0x_kv_kept")
        att_done = core.sem("l0x_att_done")
        att_rows = core.sem("l0x_att_rows")
        dense_done = core.sem("l0x_dense_done")

        att_stored = [core.sem(f"l0x_att_stored{i}") for i in range(2)]
        att_in = core.sem("l0x_att_in")
        q_scaled, x_shifted = core.sem("l0x_q_scaled"), core.sem("l0x_x_shifted")
        att_dram = nc.dram_tensor("att_dram", (NT, 16, P, 16), F32).ap()
        AR = sb("AR", [P, NT, D])

        block = es.enter_context(nc.Block())

        def load_attention(eng, half):
            eng.wait_ge(att_stored[half], 4 * 16)
            eng.dma_start(AR[:, 4 * half:4 * half + 4, :],
                          att_dram[4 * half:4 * half + 4].rearrange("t h p e -> (h p e) t")
                          .rearrange("(p d) t -> p t d", d=D)).then_inc(att_in, 16)

        @block.sync
        def _(sp):
            for j in range(2):
                sp.dma_start(ctxT[j][:], core.dram["ctxT"][j]).then_inc(ctx_in[j], 16)
            load_next(sp)
            with sp.Fori(0, B // 2 - 1) as i:
                for j in range(2):
                    sp.wait_ge(proj_done, 2 * i + (j + 2))
                    sp.dma_start(ctxT[j][:], core.dram["ctxT"][2 * i + (j + 2)]).then_inc(ctx_in[j], 16)
            for t in range(NT):
                sp.wait_ge(att_rows, t + 1)
                sp.dma_start(att_dram[t].rearrange("h p e -> p h e"),
                             core.H[:, t, :].rearrange("p (h e) -> p h e", e=16)).then_inc(att_stored[t // 4], 16)
            load_attention(sp, 1)

        @block.gpsimd
        def _(pool):
            pool.wait_ge(q_scaled, 1)
            pool_step(pool, nc.gpsimd.tensor_tensor(core.H[:], core.H[:], bcast(beta, 1, NT), ALU.add))
            for t in range(NT):
                nc.gpsimd.tensor_scalar(core.H[:, t, :], core.H[:, t, :], 0.0, 1e-6, ALU.max, ALU.add).then_inc(rows_done, 1)
            nc.gpsimd.tensor_tensor(core.X[:], core.X[:], bcast(beta, 1, NT), ALU.add).then_inc(x_shifted, 1)

        @block.tensor
        def _(pe):
            pe.wait_ge(core.consts_in, 16)
            flip.tensor(pe, core.H, rows_done, 0)
            flip.ready(pe, "pe")
            pe.wait_ge(centered, 1)
            for t in range(NT):
                for c in range(C):
                    last = nc.tensor.matmul(PS[:, 4 + t // 2, (t % 2) * D:(t % 2 + 1) * D],
                                            core.HT[:, c, t * P:(t + 1) * P], wqkv[:, c, :], start=(c == 0), stop=(c == 1))
                last.then_inc(q_done, 1)
            kw = wqkv[:, 2:6, :].rearrange("p (c k) d -> p c (k d)", c=C)

            for c in range(C):
                last = nc.tensor.matmul(PS[0:B, 2, :], cleft[:, c, :], kw[:, c, :], start=(c == 0), stop=(c == 1))
            last.then_inc(proj_done, 1)

            def proj_batch(b, j):
                pe.wait_ge(ctx_in[j], 8 * b + (16 - 8 * j))
                for k in range(2):
                    for half in range(2):
                        for c in range(C):
                            last = nc.tensor.matmul(PS[:, 2 * j + k, half * D:(half + 1) * D], ctxT[j][:, c, half * P:(half + 1) * P],
                                                    kw[:, c, k * D:(k + 1) * D], start=(c == 0), stop=(c == 1))
                last.then_inc(proj_done, 1)

            def kv_batch(b, j):
                pe.wait_ge(v_ready, b + 1)
                pe.wait_ge(kv_ready, b + 3)
                for c in range(C):
                    acc = PS[:, 4 + j, c * RW:(c + 1) * RW]
                    for half in range(2):
                        nc.tensor.matmul(acc, kp[j][:, half, c * P:(c + 1) * P], vr[j][:, half, c, :],
                                         start=(half == 0), stop=False)
                    last = nc.tensor.matmul(acc, kp_left[:, c * P:(c + 1) * P], vr_one[j][:, c, :], start=False, stop=True)
                last.then_inc(kv_done, 1)

            proj_batch(0, 0)
            with pe.Fori(0, B // 2 - 1) as i:
                pe.wait_ge(kv_ready, 2 * i + 2)
                proj_batch(2 * i + 1, 1)
                pe.wait_ge(kv_kept, 2 * i + 1)
                kv_batch(2 * i, 0)
                proj_batch(2 * i + 2, 0)
                pe.wait_ge(kv_kept, 2 * i + 2)
                kv_batch(2 * i + 1, 1)
            pe.wait_ge(kv_ready, B)
            proj_batch(B - 1, 1)
            pe.wait_ge(kv_kept, B - 1)
            kv_batch(B - 2, 0)
            pe.wait_ge(kv_kept, B)
            kv_batch(B - 1, 1)
            flip.tensor(pe, core.H, rows_done, NT)
            flip.ready(pe, "pe")
            pe.wait_ge(kv_kept, B + 2)
            for t in range(NT):
                if t >= 2:
                    pe.wait_ge(att_rows, t - 1)
                for b in range(TB * t, TB * t + TB):
                    r = S * (b % TB)
                    for c in range(C):
                        last = nc.tensor.matmul(PS[r:r + S, 6 + t % 2, c * KVW:(c + 1) * KVW],
                                                core.HT[:, c, b * S:(b + 1) * S], KV[:, b, c, :], start=True, stop=True)
                last.then_inc(att_done, 1)
            pe.wait_ge(att_in, 32)
            flip.tensor(pe, AR, att_rows, 0, order)
            flip.ready(pe, "pe")
            for t in range(NT):
                for c in range(C):
                    last = nc.tensor.matmul(PS[:, 4 + t // 2, (t % 2) * D:(t % 2 + 1) * D],
                                            core.HT[:, c, t * P:(t + 1) * P], dense[:, c, :], start=(c == 0), stop=(c == 1))
                last.then_inc(dense_done, 1)

        @block.scalar
        def _(act):
            norm.begin(act)
            norm.scalar(act, core.eps5)
            flip.scalar(act, core.HT)
            for t in range(NT):
                act.wait_ge(q_done, (t | 1) + 1)
                last = nc.scalar.activation(sq[:, t, :], PS[:, 4 + t // 2, (t % 2) * D:(t % 2 + 1) * D], ACT.Square,
                                            accum_out=qss[:, t:t + 1])
            core.act_step(act, last)
            nc.scalar.activation(qstd[:], qss[:], ACT.Sqrt, bias=core.eps6, scale=1.0 / D).then_inc(q_std, 1)
            act.wait_ge(proj_done, 1)
            for h in range(2):
                last = nc.scalar.activation(sq[0:B, h, :], PS[0:B, 2, h * D:(h + 1) * D], ACT.Square,
                                            accum_out=ss[1][0:B, h:h + 1])
            core.act_step(act, last)
            nc.scalar.activation(std[1][0:B, 0:2], ss[1][0:B, 0:2], ACT.Sqrt, bias=core.eps6[0:B, :], scale=1.0 / D).then_inc(std_done, 1)
            with act.Fori(0, B // 2) as i:
                core.act_step.enter(i, 2)
                for j in range(2):
                    act.wait_ge(proj_done, 2 * i + (j + 2))
                    for half in range(2):
                        for h in range(2):
                            last = nc.scalar.activation(sq[:, 4 * j + 2 * half + h, :], PS[:, 2 * j + h, half * D:(half + 1) * D], ACT.Square,
                                                        accum_out=ss[j][:, 2 * half + h:2 * half + h + 1])
                    core.act_step(act, last)
                    act.wait_ge(kv_ready, 2 * i + (j + 1))
                    nc.scalar.activation(std[j][:], ss[j][:], ACT.Sqrt, bias=core.eps6, scale=1.0 / D).then_inc(std_done, 1)
                    act.wait_ge(scale_ready, 2 * i + (j + 1))
                    for half in range(2):
                        last = nc.scalar.activation(vr[j][:, half, :, 0:P], PS[:, 2 * j + 1, half * D:(half + 1) * D].rearrange("p (c d) -> p c d", c=C),
                                                    ACT.Copy, scale=rstd[j][:, 2 * half + 1:2 * half + 2])
                    last.then_inc(v_ready, 1)
                core.act_step.leave(B // 2)
            flip.scalar(act, core.HT)
            load_attention(act, 0)
            flip.scalar(act, core.HT)
            norm.scalar(act, core.eps6)

        @block.vector
        def _(dve):
            dve.wait_ge(core.x_in, 16)
            norm.vector(dve, core.X, core.H, rows_done)
            flip.vector(dve, core.HT)
            dve.wait_ge(core.weights_in[0], 16)
            dve_step(dve, nc.vector.reduce_sum(wsum[:], wqkv, AX.X))
            dve_step(dve, nc.vector.tensor_scalar(wsum[:], wsum[:], 1.0 / D, None, ALU.mult))
            nc.vector.tensor_tensor(wqkv, wqkv, bcast(wsum[:], 2, D), ALU.subtract).then_inc(centered, 1)
            nc.vector.tensor_copy(em[:, :, :, 0], em_in)
            nc.vector.tensor_tensor(em[:, :, :, 1], em_in, em_in, ALU.mult)
            nc.vector.tensor_copy(eml[:, 0:1], em_left_in[0:B])
            dve_step(dve, nc.vector.tensor_tensor(eml[:, 1:2], em_left_in[0:B], em_left_in[0:B], ALU.mult))
            nc.vector.tensor_tensor(scale_v[:], bcast(same_head, 1, C), gamma.rearrange("p (c d) -> p c d", c=C), ALU.mult)
            nc.vector.tensor_tensor(shift_v[:], bcast(same_head, 1, C), beta.rearrange("p (c d) -> p c d", c=C), ALU.mult)
            dve.wait_ge(q_std, 1)
            dve.wait_ge(rows_done, NT)
            flip.ready(dve, "dve")
            dve_step(dve, nc.vector.reciprocal(qrstd[:], qstd[:]))
            for t in range(NT):
                last = nc.vector.scalar_tensor_tensor(core.H[:, t, :], PS[:, 4 + t // 2, (t % 2) * D:(t % 2 + 1) * D],
                                                      qrstd[:, t:t + 1], gamma, ALU.mult, ALU.mult)
            last.then_inc(q_scaled, 1)

            def keys(k_rows, psum, scale):
                m, n = psum.shape[0], psum.shape[1]
                for h in range(n):
                    last = nc.vector.scalar_tensor_tensor(k_rows[:, h, :], psum[:, h, :], scale[:, 2 * h:2 * h + 1],
                                                          gamma[0:m, :], ALU.mult, ALU.mult)
                dve_step(dve, last)
                dve_step(dve, nc.vector.tensor_tensor(k_rows, k_rows, bcast(beta[0:m, :], 1, n), ALU.add))
                return nc.vector.tensor_scalar(k_rows, k_rows, 0.0, 1e-6, ALU.max, ALU.add)

            def keep(b, j):
                dve.wait_ge(kv_done, b + 1)
                A = PS[:, 4 + j, 0:C * RW].rearrange("p (c r) -> p c r", c=C)
                first = nc.vector.tensor_tensor(kv_tmp[j][:], A[:, :, 0:P], scale_v[:], ALU.mult)
                nc.vector.tensor_tensor(KV[:, b, :, P:KVW], bcast(head_of, 1, C), bcast(A[:, :, P], 2, 8), ALU.mult)
                dve_step(dve, first)
                for c in range(C):
                    last = nc.vector.scalar_tensor_tensor(KV[:, b, c, 0:P], shift_v[:, c, :], A[:, c, P + 1:P + 2],
                                                          kv_tmp[j][:, c, :], ALU.mult, ALU.add)
                last.then_inc(kv_kept, 1)

            def prepare(b, j):
                dve.wait_ge(std_done, b + 2)
                dve_step(dve, nc.vector.reciprocal(rstd[j][:], std[j][:]))
                scale = rstd[j][:].rearrange("p (h k) -> p h k", k=2)[:, :, 1]
                nc.vector.tensor_tensor(scale, scale, em[:, b, :, 1], ALU.mult).then_inc(scale_ready, 1)
                nc.vector.tensor_scalar(vr_one[j][:], vr_left[:], core.ident[0:B, bass.ds(b, 1)], None, ALU.mult)
                nc.vector.tensor_copy(vr[j][:, :, :, P:RW], bcast(em[:, b, :, :], 2, C))
                keys(kp[j][:], PS[:, 2 * j, :].rearrange("p (t d) -> p t d", d=D), rstd[j][:]).then_inc(kv_ready, 1)

            dve.wait_ge(std_done, 1)
            left_scale = rstd[1][0:B, 0:2]
            dve_step(dve, nc.vector.reciprocal(left_scale, std[1][0:B, 0:2]))
            dve_step(dve, nc.vector.tensor_tensor(left_scale[:, 1:2], left_scale[:, 1:2], eml[:, 1:2], ALU.mult))
            nc.vector.tensor_scalar(vr_left[:, :, 0:P], PS[0:B, 2, D:2 * D].rearrange("p (c d) -> p c d", c=C), left_scale[:, 1:2], None, ALU.mult)
            nc.vector.tensor_copy(vr_left[:, :, P:RW], bcast(eml[:], 1, C))
            keys(kp_left[:].unsqueeze(1), PS[0:B, 2:3, 0:D], left_scale).then_inc(kv_ready, 2)
            dve.wait_ge(kv_ready, 2)
            dve.sem_inc(kv_kept, 2)
            prepare(0, 0)
            with dve.Fori(0, B // 2 - 1) as i:
                dve_step.enter(i, 8)
                prepare(2 * i + 1, 1)
                keep(2 * i, 0)
                prepare(2 * i + 2, 0)
                keep(2 * i + 1, 1)
                dve_step.leave(B // 2 - 1)
            prepare(B - 1, 1)
            keep(B - 2, 0)
            keep(B - 1, 1)
            flip.vector(dve, core.HT)
            flip.ready(dve, "dve")
            for t in range(NT):
                dve.wait_ge(att_done, t + 1)
                acc = PS[:, 6 + t % 2, 0:C * KVW].rearrange("p (c r) -> p c r", c=C)
                dve_step(dve, nc.vector.tensor_scalar(z[t % 2][:], acc[:, :, P:KVW], 1e-6, None, ALU.add))
                dve_step(dve, nc.vector.reciprocal(z[t % 2][:], z[t % 2][:]))
                nc.vector.tensor_tensor(core.H[:, t, :].rearrange("p (c h d) -> p c h d", c=C, h=8),
                                        acc[:, :, 0:P].rearrange("p c (h d) -> p c h d", h=8),
                                        bcast(z[t % 2][:], 3, 16), ALU.mult).then_inc(att_rows, 1)
            flip.vector(dve, core.HT)
            flip.ready(dve, "dve")
            for t in range(0, NT, 2):
                dve.wait_ge(dense_done, t + 2)
                dve_step(dve, nc.vector.tensor_tensor(core.H[:, t:t + 2, :], PS[:, 4 + t // 2, :].rearrange("p (t d) -> p t d", d=D),
                                                      bcast(dense_b, 1, 2), ALU.add))
                for u in (t, t + 1):
                    done = nc.vector.bn_stats(core.stats[:, u, :], core.H[:, u, :])
            dve_step(dve, done)
            norm.statistics(dve)
            for t in range(NT):
                last = nc.vector.scalar_tensor_tensor(core.H[:, t, :], core.H[:, t, :], core.moments[:, t, 0:1], gamma, ALU.subtract, ALU.mult)
            dve_step(dve, last)
            dve.wait_ge(x_shifted, 1)
            for t in range(NT):
                nc.vector.scalar_tensor_tensor(core.X[:, t, :], core.H[:, t, :], core.rstd[:, t:t + 1], core.X[:, t, :], ALU.mult, ALU.add)


def l0_self(core, load_next):
    nc, norm, flip, dve_step = core.nc, core.norm, core.flip, core.dve_step
    w = core.arena(1)
    wqk, wv, wo = w.take(C, 2 * D), w.take(C, D), w.take(C, D)
    cos, sin, causal, head_of = w.take(8), w.take(8), w.take(S), w.take(8)
    with ExitStack() as es:
        at = SelfAttention(core, es, "l0a", "softmax", 16.0 ** -0.5)
        t1, t2 = (core.sb(f"l0a_t{i}", [P, NT, 16, 8], es) for i in range(2))
        rows_done = core.sem("l0a_rows_done")
        block = es.enter_context(nc.Block())

        @block.sync
        def _(sp):
            load_next(sp)

        @block.tensor
        def _(pe):
            pe.wait_ge(core.consts_in, 16)
            pe.wait_ge(core.weights_in[1], 16)
            flip.tensor(pe, core.H, rows_done, 0)
            flip.ready(pe, "pe")
            at.project(pe, core.HT, core.HT, wqk, wv)
            at.flip_tensor(pe)
            flip.ready(pe, "pe")
            at.attend_tensor(pe)
            at.output_tensor(pe, wo)

        @block.gpsimd
        def _(pool):
            pool.wait_ge(core.weights_in[1], 16)
            flip.uses["pool"] = flip.uses["pe"] - 1
            flip.ready(pool, "pool")
            at.spread_keys(pool, head_of)

        @block.scalar
        def _(act):
            norm.begin(act)
            norm.scalar(act, core.eps5)
            flip.scalar(act, core.HT)
            at.copy_qk(act)
            flip.scalar(act, at.QT)
            flip.scalar(act, at.KT)
            at.attend_scalar(act)
            flip.scalar(act, core.HT)

        @block.vector
        def _(dve):
            dve.wait_ge(core.x_in, 16)
            norm.vector(dve, core.X, core.H, rows_done)
            flip.vector(dve, core.HT)
            at.copy_v(dve)
            dve.wait_ge(core.weights_in[1], 16)
            dve.wait_ge(at.qk_copied, NT)
            for rows, done in ((at.Q, at.q_rows), (at.K, at.k_rows)):
                pairs = rows[:].rearrange("p t (h d two) -> p t h d two", h=16, two=2)
                rotate(core, dve, pairs[:, :, :, :, 0], pairs[:, :, :, :, 1], t1[:], t2[:], cos, sin, done)
            flip.vector(dve, at.QT)
            flip.vector(dve, at.KT)
            at.attend_vector(dve, causal)
            flip.vector(dve, core.HT)
            at.output_vector(dve)


def l0_feed_forward(core, load_next):
    nc, PS, norm, flip, dve_step = core.nc, core.PS, core.norm, core.flip, core.dve_step
    E = EXPERTS[2][0]
    w = core.arena(2)
    cent, scale, number = w.take(C, E), w.take(C), w.take(E)
    with ExitStack() as es:
        ex = SortedExperts(core, es, "l0f", 2, "glu", 1)
        sb = lambda n, shape: core.sb("l0f_" + n, shape, es)
        R, squares = sb("R", [P, NT, D]), sb("squares", [P, NT, D])
        XT, XT2 = sb("XT", [P, C, NT * P]), sb("XT2", [P, C, NT * P])
        size, least = sb("size", [P, NT]), sb("least", [P, NT])
        cent2, centm2, ones = sb("cent2", [P, C, E]), sb("centm2", [P, C, E]), ex.places.ones
        dist, gate = sb("dist", [P, NT, E]), sb("gate", [P, NT, E])
        rows_done, rms_rows = core.sem("l0f_rows_done"), core.sem("l0f_rms_rows")
        summed, rooted = core.sem("l0f_ms_summed"), core.sem("l0f_ms_rooted")
        dist_ready, dist_done = core.sem("l0f_dist_ready"), core.sem("l0f_dist_done")
        gate_done = core.sem("l0f_gate_done")
        block = es.enter_context(nc.Block())

        @block.sync
        def _(sp):
            load_next(sp)
            ex.load(sp)

        @block.gpsimd
        def _(pool):
            ex.scatter(pool, R, rms_rows, 0)

        @block.tensor
        def _(pe):
            pe.wait_ge(core.consts_in, 16)
            flip.tensor(pe, R, rms_rows, 0)
            pe.wait_ge(dist_ready, 1)
            flip.ready(pe, "pe")
            for t in range(NT):
                for c in range(C):
                    tok = slice(t * P, (t + 1) * P)
                    nc.tensor.matmul(PS[:, 4, t * E:(t + 1) * E], XT2[:, c, tok], ones[:, 0:E], start=(c == 0), stop=False)
                    nc.tensor.matmul(PS[:, 4, t * E:(t + 1) * E], ones[:], cent2[:, c, :], start=False, stop=False)
                    last = nc.tensor.matmul(PS[:, 4, t * E:(t + 1) * E], XT[:, c, tok], centm2[:, c, :], start=False, stop=(c == 1))
            last.then_inc(dist_done, 1)
            ex.places.tensor(pe, gate, gate_done)
            ex.tensor(pe, XT)

        @block.scalar
        def _(act):
            norm.begin(act)
            norm.scalar(act, core.eps5)
            for t in range(NT):
                act.wait_ge(rows_done, t + 1)
                last = nc.scalar.activation(squares[:, t, :], core.H[:, t, :], ACT.Square, accum_out=size[:, t:t + 1])
            core.act_step(act, last)
            nc.scalar.activation(size[:], size[:], ACT.Sqrt, bias=core.eps6, scale=1.0 / D).then_inc(rooted, 1)
            act.wait_ge(core.weights_in[2], 16)
            flip.scalar(act, XT, scale)
            ex.scalar(act, scale)

        @block.vector
        def _(dve):
            nc.vector.memset(ones[:], 1.0)
            dve.wait_ge(core.x_in, 16)
            norm.vector(dve, core.X, core.H, rows_done)
            dve.wait_ge(core.weights_in[2], 16)
            nc.vector.tensor_scalar(centm2[:], cent, -2.0, None, ALU.mult)
            nc.vector.tensor_tensor(cent2[:], cent, cent, ALU.mult)
            dve.wait_ge(rooted, 1)
            dve_step(dve, nc.vector.reciprocal(size[:], size[:]))
            for t in range(NT):
                nc.vector.tensor_scalar(R[:, t, :], core.H[:, t, :], size[:, t:t + 1], None, ALU.mult).then_inc(rms_rows, 1)
            dve_step(dve, nc.vector.tensor_tensor(core.X[:], core.X[:], core.H[:], ALU.add))
            flip.vector(dve, XT, scale)
            flip.ready(dve, "dve")
            nc.vector.tensor_tensor(XT2[:], XT[:], XT[:], ALU.mult).then_inc(dist_ready, 1)
            dve.wait_ge(dist_done, 1)
            dve_step(dve, nc.vector.tensor_copy(dist[:], PS[:, 4, 0:NT * E].rearrange("p (t e) -> p t e", e=E)))
            dve_step(dve, nc.vector.tensor_reduce(least[:], dist[:], AX.X, ALU.min))
            dve_step(dve, nc.vector.tensor_tensor(dist[:], dist[:], bcast(least[:], 2, E), ALU.is_equal))
            dve_step(dve, nc.vector.tensor_tensor(dist[:], dist[:], bcast(number, 1, NT), ALU.mult))
            dve_step(dve, nc.vector.tensor_reduce(least[:], dist[:], AX.X, ALU.min))
            nc.vector.tensor_tensor(gate[:], bcast(number, 1, NT), bcast(least[:], 2, E), ALU.is_equal).then_inc(gate_done, 1)
            dve.wait_ge(gate_done, 1)
            ex.places.vector(dve, (gate,))
            ex.vector(dve, (None,))


def l1_cross(core, load_next):
    nc, PS, norm, flip, dve_step, cn = core.nc, core.PS, core.norm, core.flip, core.dve_step, core.ctx_norm
    HB = 8
    DH = 64
    w = core.arena(3)
    wq, wkv, wo = w.take(C, HB * P), w.take(C, 3 * DH), w.take(HB, D)
    ff1, ff2 = w.take(C, 2 * HB * P), w.take(HB, D)
    ln_g, ln_b, cln_g, cln_b = w.take(C), w.take(C), w.take(C), w.take(C)
    half_of = w.take(2)
    scale = DH ** -0.5
    U = 4
    with ExitStack() as es:
        sb = lambda n, shape: core.sb("l1x_" + n, shape, es)
        two = lambda n, shape: [sb(f"{n}{i}", shape) for i in range(2)]
        sem = lambda n: core.sem("l1x_" + n)
        QT = sb("QT", [P, HB, NT * P])
        hidden = AT = sb("AT", [P, HB, NT * P])
        side = [core.H[:, 2 * i:2 * i + 2, :].rearrange("p t d -> p (t d)") for i in range(2)]
        last_cols = sb("last_cols", [P, C, B])
        ctx, ctx_n, ctxT = two("ctx", [P, 2, D]), two("ctx_n", [P, 2, D]), two("ctxT", [P, C, CTX])
        queries, kT, V, V_last = two("queries", [P, 2, HB, S]), two("kT", [P, CTX]), two("V", [P, 2, DH]), two("V_last", [P, U, DH])
        last_rows = sb("last_rows", [B, DH])
        V_last_all = core.HT[0:U, :, :].rearrange("p c n -> p (c n)").rearrange("p (b d) -> p b d", d=DH)
        probs, probsT, probsT_last = two("probs", [P, U, CTX]), two("probsT", [P, 2, U * P]), two("probsT_last", [P, P])
        top, total = two("top", [P, U]), two("total", [P, U])
        cn.allocate(es, "l1x")
        rows_done, normed_done, q_done, q_copied = sem("rows_done"), sem("normed_done"), sem("q_done"), sem("q_copied")
        up_done, side_done, hidden_done, ff_done, ff_added = (sem(n) for n in ("up_done", "side_done", "hidden_done", "ff_done", "ff_added"))
        last_cols_done, ctx_normed, ctx_flipped, ctxT_copied = (sem(n) for n in ("last_cols_done", "ctx_normed", "ctx_flipped", "ctxT_copied"))
        last_v_done, last_rows_done, last_stored = sem("last_v_done"), sem("last_rows_done"), sem("last_stored")
        zeros_set, last_placed, V_last_done = sem("zeros_set"), sem("last_placed"), sem("V_last_done")
        last_v_dram = nc.dram_tensor("l1x_last_v_dram", (B, DH), F32).ap()
        queries_done, k_done, v_done, k_copied, v_copied = (sem(n) for n in ("queries_done", "k_done", "v_done", "k_copied", "v_copied"))
        sim_done, top_done, exps_done, probs_done = (sem(n) for n in ("sim_done", "top_done", "exps_done", "probs_done"))
        pt_done, pt_copied_act, pt_copied_dve = sem("pt_done"), sem("pt_copied_act"), sem("pt_copied_dve")
        pv_done, out_copied, out_done = sem("pv_done"), sem("out_copied"), sem("out_done")
        block = es.enter_context(nc.Block())

        @block.sync
        def _(sp):
            cn.load(sp, ctx)
            load_next(sp)
            sp.wait_ge(last_rows_done, 1)
            sp.dma_start(last_v_dram, last_rows[:]).then_inc(last_stored, 16)
            sp.wait_ge(last_stored, 16)
            for u in range(U):
                sp.dma_start(V_last_all[u:u + 1, :, :], last_v_dram.unsqueeze(0)).then_inc(last_placed, 16)
            with sp.Fori(0, B // 2 - 1) as i:
                for j in range(2):
                    sp.wait_ge(ctx_normed, 2 * i + (j + 1))
                    sp.dma_start(ctx[j][:], core.dram["ctx"][2 * i + (j + 2), 0:2 * P, :].rearrange("(h p) d -> p h d", p=P)).then_inc(cn.slot_in[j], 16)

        @block.gpsimd
        def _(pool):
            for j in range(2):
                nc.gpsimd.memset(V_last[j][:], 0.0).then_inc(zeros_set, 1)
                nc.gpsimd.memset(probsT_last[j][:], 0.0).then_inc(zeros_set, 1)
            pool.wait_ge(zeros_set, 4)
            pool.wait_ge(q_copied, 2 * HB)
            pool.wait_ge(last_cols_done, 1)
            pool.wait_ge(last_placed, 16 * U)
            pool.wait_ge(core.consts_in, 16)

            def prepare(b, j):
                at_least(pool, sim_done, 2 * b - 2)
                nc.gpsimd.tensor_copy(ctxT[j][:, :, 2 * P:CTX], last_cols[:, :, bass.ds(b, 1)])
                nc.gpsimd.tensor_tensor(queries[j][:], bcast(QT[:, :, bass.ds(b * S, S)], 1, 2), bcast(bcast(half_of, 2, HB), 3, S), ALU.mult).then_inc(queries_done, 1)
                at_least(pool, pv_done, b - 1)
                nc.gpsimd.tensor_tensor(V_last[j][0:U], V_last_all[:, bass.ds(b, 1), :].to_broadcast([U, U, DH]), bcast(core.ident[0:U, 0:U], 2, DH), ALU.mult).then_inc(V_last_done, 1)

            prepare(0, 0)
            prepare(1, 1)
            with pool.Fori(0, B // 2 - 1) as i:
                for j in range(2):
                    prepare(2 * i + (j + 2), j)

        @block.tensor
        def _(pe):
            pe.wait_ge(core.consts_in, 16)
            pe.wait_ge(core.weights_in[3], 16)
            flip.tensor(pe, core.H, normed_done, 0)
            flip.ready(pe, "pe")
            for n in range(2 * HB):
                o, half = n // 2, n % 2
                if n >= 4:
                    pe.wait_ge(q_copied, n - 3)
                for c in range(C):
                    done = nc.tensor.matmul(PS[:, 4 + n % 4, :], wq[:, c, o * P:(o + 1) * P], core.HT[:, c, half * 512:(half + 1) * 512],
                                            start=(c == 0), stop=(c == 1))
                done.then_inc(q_done, 1)
            for n in range(2 * HB):
                m, half = n // 2, n % 2
                if n >= 2:
                    pe.wait_ge(hidden_done, n - 1)
                for g in range(2):
                    for c in range(C):
                        done = nc.tensor.matmul(PS[:, 2 * (n % 2) + g, :], ff1[:, c, (g * HB + m) * P:(g * HB + m + 1) * P],
                                                core.HT[:, c, half * 512:(half + 1) * 512], start=(c == 0), stop=(c == 1))
                done.then_inc(up_done, 1)
            pe.wait_ge(hidden_done, 2 * HB)
            pe.wait_ge(q_copied, 2 * HB)
            for t in range(NT):
                if t >= 3:
                    pe.wait_ge(ff_added, t - 2)
                for m in range(HB):
                    done = nc.tensor.matmul(PS[:, 4 + t % 3, 0:D], hidden[:, m, t * P:(t + 1) * P], ff2[:, m, :], start=(m == 0), stop=(m == HB - 1))
                done.then_inc(ff_done, 1)
            if not cn.computed:
                cn.tensor(pe)

            pe.wait_ge(ff_added, NT)
            pe.wait_ge(last_cols_done, 1)
            for c in range(C):
                done = nc.tensor.matmul(PS[0:B, 6, 0:DH], last_cols[:, c, :], wkv[:, c, P:P + DH], start=(c == 0), stop=(c == 1))
            done.then_inc(last_v_done, 1)

            def flip_context(b, j):
                pe.wait_ge(ctx_normed, b + 1)
                for c in range(C):
                    for half in range(2):
                        done = nc.tensor.transpose(PS[:, 5, (2 * c + half) * P:(2 * c + half + 1) * P], ctx_n[j][:, half, c * P:(c + 1) * P], core.ident[:])
                done.then_inc(ctx_flipped, 1)

            def keys_values(b, j):
                pe.wait_ge(ctxT_copied, b + 1)
                pe.wait_ge(queries_done, b + 1)
                for half in range(2):
                    for c in range(C):
                        done = nc.tensor.matmul(PS[:, 6, half * DH:(half + 1) * DH], ctxT[j][:, c, half * P:(half + 1) * P], wkv[:, c, P:P + DH], start=(c == 0), stop=(c == 1))
                done.then_inc(v_done, 1)
                for c in range(C):
                    done = nc.tensor.matmul(PS[:, 4, 0:CTX], wkv[:, c, 0:P], ctxT[j][:, c, :], start=(c == 0), stop=(c == 1))
                done.then_inc(k_done, 1)

            def sim(b, j):
                pe.wait_ge(queries_done, b + 1)
                for u in range(U):
                    done = nc.tensor.matmul(PS[:, u, 0:CTX], queries[j][:, u // 2, 4 * (u % 2):4 * (u % 2) + 4, :].rearrange("p h q -> p (h q)"),
                                            kT[j][:], start=True, stop=True)
                    if u % 2:
                        done.then_inc(sim_done, 1)

            def flip_probs(b, j):
                pe.wait_ge(probs_done, b + 1)
                for half in (1, 0):
                    if not half and exists(b + 1):
                        pe.wait_ge(k_copied, b + 2)
                        pe.wait_ge(v_copied, b + 2)
                    elif half and exists(b + 2):
                        pe.wait_ge(ctxT_copied, b + 3)
                    for u in range(U):
                        nc.tensor.transpose(PS[:, 4 + half, u * P:(u + 1) * P], probs[j][:, u, half * P:(half + 1) * P], core.ident[:])
                nc.tensor.transpose(PS[0:U, 6, 3 * P:4 * P], probs[j][:, :, 2 * P], core.ident[:]).then_inc(pt_done, 1)

            def weigh(b, j):
                pe.wait_ge(pt_copied_act, b + 1)
                pe.wait_ge(pt_copied_dve, b + 1)
                pe.wait_ge(V_last_done, b + 1)
                pe.wait_ge(out_copied, b + 1)
                for n in range(2):
                    for key in range(3):
                        for par in range(2):
                            u = 2 * par + n
                            value, weight = ((V[j][:, key, :], probsT[j][:, key, u * P:(u + 1) * P]) if key < 2 else
                                             (V_last[j][:, u, :], probsT_last[j][:]))
                            done = nc.tensor.matmul(PS[DH * par:DH * (par + 1), 7, n * P:(n + 1) * P], value, weight, start=(key == 0), stop=(key == 2))
                done.then_inc(pv_done, 1)

            def first():
                flip_context(0, 0)
                pe.wait_ge(ctxT_copied, 1)
                flip_context(1, 1)
                pe.wait_ge(last_rows_done, 1)
                keys_values(0, 0)
                pe.wait_ge(ctxT_copied, 2)
                flip_context(2, 0)
                pe.wait_ge(v_copied, 1)
                pe.wait_ge(k_copied, 1)
                keys_values(1, 1)
                sim(0, 0)

            def turn(b, j):
                flip_probs(b, j)
                sim(b + 1, 1 - j)
                weigh(b, j)
                if exists(b + 3):
                    flip_context(b + 3, 1 - j)
                if exists(b + 2):
                    keys_values(b + 2, j)

            def last(b, j):
                flip_probs(b, j)
                weigh(b, j)

            over_batches(pe, first, turn, last)
            pe.wait_ge(out_copied, B + 1)
            for t in range(NT):
                for m in range(HB):
                    done = nc.tensor.matmul(PS[:, 4 + t // 2, (t % 2) * D:(t % 2 + 1) * D], AT[:, m, t * P:(t + 1) * P],
                                            wo[:, m, :], start=(m == 0), stop=(m == HB - 1))
                if t % 2:
                    done.then_inc(out_done, 1)

        @block.scalar
        def _(act):
            norm.begin(act)
            act.wait_ge(core.weights_in[3], 16)
            norm.scalar(act, core.eps5)
            norm.scalar(act, core.eps5)
            flip.scalar(act, core.HT, ln_g, ln_b)
            for n in range(2 * HB):
                o, half = n // 2, n % 2
                act.wait_ge(q_done, n + 1)
                nc.scalar.copy(QT[:, o, half * 512:(half + 1) * 512], PS[:, 4 + n % 4, :]).then_inc(q_copied, 1)
            for n in range(2 * HB):
                act.wait_ge(up_done, n + 1)
                if n >= 2:
                    act.wait_ge(hidden_done, n - 1)
                nc.scalar.activation(side[n % 2], PS[:, 2 * (n % 2) + 1, :], ACT.Silu).then_inc(side_done, 1)
            if not cn.computed:
                cn.scalar(act)

            def copy_context(b, j):
                act.wait_ge(ctx_flipped, b + 1)
                at_least(act, k_done, b - 1)
                for c in range(C):
                    done = nc.scalar.activation(ctxT[j][:, c, 0:2 * P], PS[:, 5, c * 2 * P:(c + 1) * 2 * P], ACT.Identity, bias=cln_b[:, c:c + 1], scale=cln_g[:, c:c + 1])
                done.then_inc(ctxT_copied, 1)

            def copy_keys(b, j):
                act.wait_ge(k_done, b + 1)
                nc.scalar.copy(kT[j][:], PS[:, 4, 0:CTX]).then_inc(k_copied, 1)

            def exps(b, j):
                for u in range(U):
                    if u % 2 == 0:
                        act.wait_ge(top_done, 2 * b + (u // 2 + 1))
                    done = nc.scalar.activation(probs[j][:, u, :], PS[:, u, 0:CTX], ACT.Exp, bias=top[j][:, u:u + 1], scale=scale,
                                                accum_out=total[j][:, u:u + 1])
                    if u % 2:
                        done.then_inc(exps_done, 1)

            def copy_probs(b, j):
                act.wait_ge(pt_done, b + 1)
                nc.scalar.copy(probsT[j][:, 0, :], PS[:, 4, :]).then_inc(pt_copied_act, 1)

            def copy_out(b, j):
                act.wait_ge(pv_done, b + 1)
                nc.scalar.copy(AT[:, :, bass.ds(b * S, S)], PS[:, 7, 0:2 * P].rearrange("p (m q) -> p m q", m=HB)).then_inc(out_copied, 1)

            def first():
                act.wait_ge(ff_done, NT)
                act.sem_inc(out_copied, 1)
                copy_context(0, 0)
                copy_context(1, 1)
                copy_keys(0, 0)
                copy_context(2, 0)
                copy_keys(1, 1)
                exps(0, 0)

            def turn(b, j):
                copy_probs(b, j)
                exps(b + 1, 1 - j)
                copy_out(b, j)
                if exists(b + 3):
                    copy_context(b + 3, 1 - j)
                if exists(b + 2):
                    copy_keys(b + 2, j)

            def last(b, j):
                copy_probs(b, j)
                copy_out(b, j)

            over_batches(act, first, turn, last)

        @block.vector
        def _(dve):
            dve.wait_ge(core.x_in, 16)
            norm.vector(dve, core.X, core.H, rows_done)
            dve.wait_ge(rows_done, NT)
            norm.vector(dve, core.H, core.H, normed_done)
            dve.wait_ge(core.weights_in[3], 16)
            flip.vector(dve, core.HT, ln_g, ln_b)
            if not cn.computed:
                cn.vector_stats(dve, ctx)
            for n in range(2 * HB):
                m, half = n // 2, n % 2
                dve.wait_ge(side_done, n + 1)
                nc.vector.tensor_tensor(hidden[:, m, half * 512:(half + 1) * 512], PS[:, 2 * (n % 2), :], side[n % 2], ALU.mult).then_inc(hidden_done, 1)
            for t in range(NT):
                dve.wait_ge(ff_done, t + 1)
                nc.vector.tensor_tensor(core.X[:, t, :], PS[:, 4 + t % 3, 0:D], core.X[:, t, :], ALU.add).then_inc(ff_added, 1)
            if not cn.computed:
                cn.vector_finish(dve)
            for c in range(C):
                done = nc.vector.tensor_scalar(last_cols[:, c, :], cn.lastT[:, c, :], cln_g[:, c:c + 1], cln_b[:, c:c + 1], ALU.mult, ALU.add)
            done.then_inc(last_cols_done, 1)
            dve.wait_ge(last_cols_done, 1)
            before = 16 * (cn.loads + (0 if cn.computed else B // 2))

            dve.wait_ge(zeros_set, 4)
            dve.wait_ge(last_v_done, 1)
            nc.vector.tensor_copy(last_rows[:], PS[0:B, 6, 0:DH]).then_inc(last_rows_done, 1)

            def norm_context(b, j):
                at_least(dve, ctx_flipped, b - 1)
                dve.wait_ge(cn.slot_in[j], 8 * b + (before + 16 - 8 * j))
                for h in range(2):
                    done = nc.vector.tensor_scalar(ctx_n[j][:, h, :], ctx[j][:, h, :], cn.rstd[:, b, h:h + 1], cn.shift[:, b, h:h + 1], ALU.mult, ALU.add)
                done.then_inc(ctx_normed, 1)

            def copy_values(b, j):
                dve.wait_ge(v_done, b + 1)
                at_least(dve, pv_done, b - 1)
                nc.vector.tensor_copy(V[j][:].rearrange("p h d -> p (h d)"), PS[:, 6, 0:2 * DH]).then_inc(v_copied, 1)

            def tops(b, j):
                for n in range(2):
                    dve.wait_ge(sim_done, 2 * b + (n + 1))
                    t = top[j][:, 2 * n:2 * n + 2]
                    dve_step(dve, nc.vector.reduce_max(t, PS[:, 2 * n:2 * n + 2, 0:CTX], AX.X))
                    nc.vector.tensor_scalar(t, t, -scale, None, ALU.mult).then_inc(top_done, 1)

            def weights(b, j):
                for n in range(2):
                    dve.wait_ge(exps_done, 2 * b + (n + 1))
                    t = total[j][:, 2 * n:2 * n + 2]
                    dve_step(dve, nc.vector.reciprocal(t, t))
                    for u in range(2 * n, 2 * n + 2):
                        done = nc.vector.tensor_scalar(probs[j][:, u, :], probs[j][:, u, :], total[j][:, u:u + 1], None, ALU.mult)
                done.then_inc(probs_done, 1)

            def copy_probs(b, j):
                dve.wait_ge(pt_done, b + 1)
                nc.vector.tensor_copy(probsT[j][:, 1, :], PS[:, 5, :])
                nc.vector.tensor_copy(probsT_last[j][0:U], PS[0:U, 6, 3 * P:4 * P]).then_inc(pt_copied_dve, 1)

            def first():
                norm_context(0, 0)
                norm_context(1, 1)
                norm_context(2, 0)
                copy_values(0, 0)
                copy_values(1, 1)
                tops(0, 0)
                weights(0, 0)

            def turn(b, j):
                copy_probs(b, j)
                if exists(b + 3):
                    norm_context(b + 3, 1 - j)
                tops(b + 1, 1 - j)
                weights(b + 1, 1 - j)
                if exists(b + 2):
                    copy_values(b + 2, j)

            def last(b, j):
                copy_probs(b, j)

            over_batches(dve, first, turn, last, lambda i: dve_step.enter(i, 8), dve_step.leave)
            for n in range(NT // 2):
                dve.wait_ge(out_done, n + 1)
                x = core.X[:, 2 * n:2 * n + 2, :]
                nc.vector.tensor_tensor(x, PS[:, 4 + n, :].rearrange("p (t d) -> p t d", t=2), x, ALU.add)

        cn.loads, cn.computed = cn.loads + B // 2 * (1 if cn.computed else 2), True


def l1_self(core, load_next):
    nc, PS, norm, flip, dve_step = core.nc, core.PS, core.norm, core.flip, core.dve_step
    SETS, HEADS, DH = 4, 16, D // 16
    QB = SETS * C
    UNITS = NT * SETS
    w = core.arena(4)
    wq, wk, wv, wo = w.take(C, SETS * D), w.take(C, D), w.take(C, D), w.take(SETS * C, D)
    causal, head_of = w.take(S), w.take(8)
    scale = DH ** -0.5
    with ExitStack() as es:
        sb = lambda n, shape: core.sb("l1a_" + n, shape, es)
        two = lambda n, shape: [sb(f"{n}{i}", shape) for i in range(2)]
        sem = lambda n: core.sem("l1a_" + n)
        QT, KT = sb("QT", [P, QB, NT * P]), sb("KT", [P, C, NT * P])
        V = sb("V", [P, NT, HEADS // 2, 2, 2, DH])
        spread = two("spread", [P, C, TB, 8, S])
        scores, probsT = two("scores", [P, HEADS, S]), two("probsT", [P, HEADS, SETS, S])
        probs = [sb(f"probs{i}", [P, HEADS, S]) for i in range(3)]
        top, total = two("top", [P, HEADS]), two("total", [P, HEADS])
        rowsT = sb("rowsT", [P, C, SETS, TB, S])
        rows_done, zeros_set, qk_done, v_done = sem("rows_done"), sem("zeros_set"), sem("qk_done"), sem("v_done")
        qk_act, qk_dve, v_copied = sem("qk_act"), sem("qk_dve"), sem("v_copied")
        spread_done, scores_done, scores_read, shifted = sem("spread_done"), sem("scores_done"), sem("scores_read"), sem("shifted")
        exps_done, total_done, probs_done, probsT_done = sem("exps_done"), sem("total_done"), sem("probs_done"), sem("probsT_done")
        out_done, rowsT_act, rowsT_dve, proj_done, added = (sem(n) for n in ("out_done", "rowsT_act", "rowsT_dve", "proj_done", "added"))
        block = es.enter_context(nc.Block())

        @block.sync
        def _(sp):
            load_next(sp)

        @block.gpsimd
        def _(pool):
            nc.gpsimd.memset(V[:], 0.0).then_inc(zeros_set, 1)
            pool.wait_ge(core.weights_in[4], 16)
            pool.wait_ge(qk_act, C)
            pool.wait_ge(qk_dve, C)

            def spread_keys(t):
                if t >= 2:
                    pool.wait_ge(scores_done, SETS * (t - 1))
                for c in range(C):
                    done = nc.gpsimd.tensor_tensor(spread[t % 2][:, c], bcast(KT[:, c, t * P:(t + 1) * P].rearrange("p (b k) -> p b k", k=S), 2, 8),
                                                   bcast(bcast(head_of, 1, TB), 3, S), ALU.mult)
                done.then_inc(spread_done, 1)

            spread_keys(0)
            spread_keys(1)
            for n in range(UNITS):
                pool.wait_ge(total_done, n + 1)
                p = probs[n % 3][:]
                nc.gpsimd.tensor_tensor(p, p, bcast(total[n % 2][:], 2, S), ALU.mult).then_inc(probs_done, 1)
                if n % SETS == SETS - 1 and n // SETS + 2 < NT:
                    spread_keys(n // SETS + 2)

        @block.tensor
        def _(pe):
            pe.wait_ge(core.consts_in, 16)
            pe.wait_ge(core.weights_in[4], 16)
            flip.tensor(pe, core.H, rows_done, 0)
            flip.ready(pe, "pe")
            for n in range(C + QB):
                weight, at = (wk, n * P) if n < C else (wq, (n - C) * P)
                for half in range(2):
                    if n >= 2:
                        pe.wait_ge((qk_act, qk_dve)[half], n - 1)
                    for c in range(C):
                        done = nc.tensor.matmul(PS[:, 4 + 2 * (n % 2) + half, :], weight[:, c, at:at + P],
                                                core.HT[:, c, half * 512:(half + 1) * 512], start=(c == 0), stop=(c == 1))
                    done.then_inc(qk_done, 1)
            for t in range(NT):
                for c in range(C):
                    done = nc.tensor.matmul(PS[:, t // 2, (t % 2) * D:(t % 2 + 1) * D], core.HT[:, c, t * P:(t + 1) * P], wv[:, c, :],
                                            start=(c == 0), stop=(c == 1))
                if t % 2:
                    done.then_inc(v_done, 1)
            pe.wait_ge(v_copied, NT // 2)
            pe.wait_ge(qk_act, C + QB)
            pe.wait_ge(qk_dve, C + QB)

            def project(u):
                pe.wait_ge(rowsT_act, u + 1)
                pe.wait_ge(rowsT_dve, u + 1)
                if u:
                    pe.wait_ge(added, u)
                for m in range(SETS * C):
                    done = nc.tensor.matmul(PS[:, 2, 0:D], rowsT[:, m % C, m // C].rearrange("p b q -> p (b q)"), wo[:, m, :],
                                            start=(m == 0), stop=(m == SETS * C - 1))
                done.then_inc(proj_done, 1)

            for n in range(UNITS + SETS + 1):
                t, g = n // SETS, n % SETS
                if n < UNITS:
                    if g == 0:
                        pe.wait_ge(spread_done, t + 1)
                    if n >= 2:
                        pe.wait_ge(scores_read, n - 1)
                    for c in range(C):
                        for b in range(TB):
                            done = nc.tensor.matmul(PS[b * S:(b + 1) * S, n % 2, c * 256:(c + 1) * 256],
                                                    QT[:, C * g + c, t * P + b * S:t * P + (b + 1) * S],
                                                    spread[t % 2][:, c, b].rearrange("p h k -> p (h k)"), start=True, stop=True)
                    done.then_inc(scores_done, 1)
                if t >= 1 and g == 2:
                    u = t - 1
                    pe.wait_ge(probsT_done, SETS * t)
                    if u:
                        pe.wait_ge(rowsT_act, u)
                        pe.wait_ge(rowsT_dve, u)
                    for c in range(C):
                        for block_at in range(4):
                            for side in range(2):
                                h = 8 * c + 2 * block_at + side
                                for b in range(TB):
                                    r = slice(b * S, (b + 1) * S)
                                    done = nc.tensor.matmul(PS[block_at * 32:(block_at + 1) * 32, 4 + b, c * P:(c + 1) * P],
                                                            V[r, u, h // 2, side].rearrange("p two d -> p (two d)"),
                                                            probsT[u % 2][r, h].rearrange("p g q -> p (g q)"),
                                                            start=(side == 0), stop=(side == 1))
                    done.then_inc(out_done, 1)
                if t >= 2 and g == 0:
                    project(t - 2)

        @block.scalar
        def _(act):
            norm.begin(act)
            norm.scalar(act, core.eps5)
            flip.scalar(act, core.HT)
            for n in range(C + QB):
                act.wait_ge(qk_done, 2 * n + 1)
                dst = KT[:, n, :] if n < C else QT[:, n - C, :]
                nc.scalar.copy(dst[:, 0:512], PS[:, 4 + 2 * (n % 2), :]).then_inc(qk_act, 1)
            for n in range(UNITS + SETS):
                t, g = n // SETS, n % SETS
                if n < UNITS:
                    act.wait_ge(shifted, n + 1)
                    if n >= 3:
                        act.wait_ge(probsT_done, n - 2)
                    nc.scalar.activation(probs[n % 3][:], scores[n % 2][:], ACT.Exp, scale=scale).then_inc(exps_done, 1)
                if t >= 1 and g == 3:
                    act.wait_ge(out_done, t)
                    if t >= 2:
                        act.wait_ge(proj_done, t - 1)
                    nc.scalar.copy(rowsT[:, :, :, 0:2, :].rearrange("p c g b q -> p b (c g) q"),
                                   PS[:, 4:6, 0:C * P].rearrange("p b (e q) -> p b e q", q=S)).then_inc(rowsT_act, 1)

        @block.vector
        def _(dve):
            dve.wait_ge(core.x_in, 16)
            norm.vector(dve, core.X, core.H, rows_done)
            flip.vector(dve, core.HT)
            for n in range(C + QB):
                dve.wait_ge(qk_done, 2 * n + 2)
                dst = KT[:, n, :] if n < C else QT[:, n - C, :]
                nc.vector.tensor_copy(dst[:, 512:1024], PS[:, 5 + 2 * (n % 2), :]).then_inc(qk_dve, 1)
            dve.wait_ge(zeros_set, 1)
            for j in range(NT // 2):
                dve.wait_ge(v_done, j + 1)
                out = PS[:, j, :].rearrange("p (t h two d) -> p t h two d", t=2, two=2, d=DH)
                for side in range(2):
                    done = nc.vector.tensor_copy(V[:, 2 * j:2 * j + 2, :, side, side, :], out[:, :, :, side, :])
                done.then_inc(v_copied, 1)

            def add(u):
                dve.wait_ge(proj_done, u + 1)
                x = core.X[:, u, :]
                nc.vector.tensor_tensor(x, PS[:, 2, 0:D], x, ALU.add).then_inc(added, 1)

            for n in range(UNITS + SETS + 2):
                t, g = n // SETS, n % SETS
                if n < UNITS:
                    i = n % 2
                    s = scores[i][:]
                    dve.wait_ge(scores_done, n + 1)
                    if n >= 2:
                        dve.wait_ge(exps_done, n - 1)
                    nc.vector.tensor_tensor(s, PS[:, i, :].rearrange("p (h k) -> p h k", k=S), bcast(causal, 1, HEADS), ALU.add).then_inc(scores_read, 1)
                    dve.wait_ge(scores_read, n + 1)
                    dve_step(dve, nc.vector.reduce_max(top[i][:], s, AX.X))
                    nc.vector.tensor_tensor(s, s, bcast(top[i][:], 2, S), ALU.subtract).then_inc(shifted, 1)
                if 1 <= n <= UNITS:
                    m = n - 1
                    dve.wait_ge(exps_done, m + 1)
                    if m >= 2:
                        dve.wait_ge(probs_done, m - 1)
                    dve_step(dve, nc.vector.reduce_sum(total[m % 2][:], probs[m % 3][:], AX.X))
                    nc.vector.reciprocal(total[m % 2][:], total[m % 2][:]).then_inc(total_done, 1)
                if 2 <= n <= UNITS + 1:
                    m = n - 2
                    dve.wait_ge(probs_done, m + 1)
                    if m >= 2 * SETS:
                        dve.wait_ge(out_done, m // SETS - 1)
                    nc.vector.transpose(probsT[m // SETS % 2][:, :, m % SETS, :], probs[m % 3][:]).then_inc(probsT_done, 1)
                if 1 <= t <= NT and g == 3:
                    dve.wait_ge(out_done, t)
                    if t >= 2:
                        dve.wait_ge(proj_done, t - 1)
                    nc.vector.tensor_copy(rowsT[:, :, :, 2:4, :].rearrange("p c g b q -> p b (c g) q"),
                                          PS[:, 6:8, 0:C * P].rearrange("p b (e q) -> p b e q", q=S)).then_inc(rowsT_dve, 1)
                if t >= 2 and g == 1:
                    add(t - 2)


def l1_feed_forward(core, load_next):
    nc, PS, norm, flip, dve_step = core.nc, core.PS, core.norm, core.flip, core.dve_step
    E = EXPERTS[5][0] - 1
    w = core.arena(5)
    wg, bg, b2, number = w.take(C, E), w.take(E), w.take(D), w.take(E)
    with ExitStack() as es:
        ex = SortedExperts(core, es, "l1f", 5, "swiglu", 2, shared=True)
        bias = OutputBias(core, es, "l1f", E + 1)
        sb = lambda n, shape: core.sb("l1f_" + n, shape, es)
        scores, biased, gate = sb("scores", [P, NT, E]), sb("biased", [P, NT, E]), sb("gate", [P, NT, E + 1])
        first, second, chosen = sb("first", [P, NT, E]), sb("second", [P, NT, E]), sb("chosen", [P, NT, E])
        share = [sb(f"share{k}", [P, NT]) for k in range(2)]
        best, place, total = sb("best", [P, NT]), sb("place", [P, NT]), sb("total", [P, NT])
        rows_done, routed, chosen_done = core.sem("l1f_rows_done"), core.sem("l1f_routed"), core.sem("l1f_chosen_done")
        shifted, exps_done, weighed = core.sem("l1f_shifted"), core.sem("l1f_exps_done"), core.sem("l1f_weighed")
        block = es.enter_context(nc.Block())

        @block.sync
        def _(sp):
            load_next(sp)
            ex.load(sp)

        @block.gpsimd
        def _(pool):
            ex.scatter(pool, core.H, rows_done, 0)

        @block.tensor
        def _(pe):
            pe.wait_ge(core.consts_in, 16)
            pe.wait_ge(core.weights_in[5], 16)
            flip.tensor(pe, core.H, rows_done, 0)
            flip.ready(pe, "pe")
            router_tensor(core, pe, core.HT, wg, routed)
            ex.places.tensor(pe, chosen, chosen_done)
            bias.tensor(pe, gate, weighed, b2)
            pe.wait_ge(core.shared_in, 32)
            ex.tensor(pe, core.HT)

        @block.scalar
        def _(act):
            norm.begin(act)
            norm.scalar(act, core.eps5)
            flip.scalar(act, core.HT)
            act.wait_ge(shifted, 1)
            nc.scalar.activation(scores[:], scores[:], ACT.Exp).then_inc(exps_done, 1)
            act.wait_ge(core.shared_in, 32)
            ex.scalar(act)

        @block.vector
        def _(dve):
            nc.vector.memset(ex.places.ones[:], 1.0)
            nc.vector.memset(gate[:], 1.0)
            dve.wait_ge(core.x_in, 16)
            norm.vector(dve, core.X, core.H, rows_done)
            flip.vector(dve, core.HT)
            dve.wait_ge(core.weights_in[5], 16)
            dve.wait_ge(routed, 1)
            logits = PS[:, 4, 0:NT * E].rearrange("p (t e) -> p t e", e=E)
            dve_step(dve, nc.vector.reduce_max(best[:], logits, AX.X))
            nc.vector.tensor_tensor(scores[:], logits, bcast(best[:], 2, E), ALU.subtract).then_inc(shifted, 1)
            dve.wait_ge(exps_done, 1)
            dve_step(dve, nc.vector.reduce_sum(total[:], scores[:], AX.X))
            dve_step(dve, nc.vector.reciprocal(total[:], total[:]))
            dve_step(dve, nc.vector.tensor_tensor(scores[:], scores[:], bcast(total[:], 2, E), ALU.mult))
            dve_step(dve, nc.vector.tensor_tensor(biased[:], scores[:], bcast(bg, 1, NT), ALU.add))
            first_best(core, dve, biased, number, best, place, first)
            dve_step(dve, nc.vector.scalar_tensor_tensor(biased[:], first[:], NEG, biased[:], ALU.mult, ALU.add))
            first_best(core, dve, biased, number, best, place, second)
            nc.vector.tensor_tensor(chosen[:], first[:], second[:], ALU.add).then_inc(chosen_done, 1)
            dve.wait_ge(chosen_done, 1)
            ex.places.vector(dve, (first, second))
            for k, choice in enumerate((first, second)):
                dve_step(dve, nc.vector.tensor_tensor(choice[:], choice[:], scores[:], ALU.mult))
                dve_step(dve, nc.vector.reduce_sum(share[k][:], choice[:], AX.X))
            nc.vector.tensor_tensor(gate[:, :, 0:E], first[:], second[:], ALU.add).then_inc(weighed, 1)
            dve.wait_ge(weighed, 1)
            bias.vector(dve)
            ex.vector(dve, share)


def l2_cross(core, load_next):
    nc, PS, norm, flip, dve_step = core.nc, core.PS, core.norm, core.flip, core.dve_step
    w = core.arena(6)
    wq, wk, wv, wo = w.take(C, D), w.take(C, D), w.take(C, D), w.take(C, D)
    bq, bk, bv, bo = w.take(C), w.take(C), w.take(D), w.take(D)
    head_of = w.take(8)
    own = w.take(4)
    last_tokens = w.take(C, B)
    scale = 16.0 ** -0.5
    U = 4
    with ExitStack() as es:
        sb = lambda n, shape: core.sb("l2x_" + n, shape, es)
        two = lambda n, shape: [sb(f"{n}{i}", shape) for i in range(2)]
        sem = lambda n: core.sem("l2x_" + n)
        QT, AT = sb("QT", [P, C, NT * P]), sb("AT", [P, C, NT * P])
        ctxT, spread, kT = two("ctxT", [P, C, CTX]), two("spread", [P, C, 8, S]), two("kT", [P, C, CTX])
        V, V_last = two("V", [P, 2, D]), two("V_last", [P, U, 64])
        last_rows, V_last_all = sb("last_rows", [B, D]), sb("V_last_all", [U, B, U, 64])
        probs, probsT, probsT_last = two("probs", [P, U, CTX]), two("probsT", [P, 2, U * P]), two("probsT_last", [P, P])
        top, total, own_out = two("top", [P, U]), two("total", [P, U]), sb("own_out", [P, C, 4, S])
        rows_done, q_done, q_copied = sem("rows_done"), sem("q_done"), sem("q_copied")
        ctx_in = [sem("ctx_in0"), sem("ctx_in1")]
        spread_done, k_done, v_done, k_copied, v_copied = (sem(n) for n in ("spread_done", "k_done", "v_done", "k_copied", "v_copied"))
        sim_done, top_done, exps_done, probs_done = sem("sim_done"), sem("top_done"), sem("exps_done"), sem("probs_done")
        last_v_done, last_rows_done, last_placed, V_last_done = sem("last_v_done"), sem("last_rows_done"), sem("last_placed"), sem("V_last_done")
        zeros_set, last_stored = sem("zeros_set"), sem("last_stored")
        last_v_dram = nc.dram_tensor("l2x_last_v_dram", (B, D), F32).ap()
        pt_done, pt_copied_act, pt_copied_dve = sem("pt_done"), sem("pt_copied_act"), sem("pt_copied_dve")
        pv_done, own_done, at_done, out_done = (sem(n) for n in ("pv_done", "own_done", "at_done", "out_done"))
        block = es.enter_context(nc.Block())

        @block.sync
        def _(sp):
            for j in range(2):
                sp.dma_start(ctxT[j][:], core.dram["ctxT"][j]).then_inc(ctx_in[j], 16)
            load_next(sp)
            sp.wait_ge(last_rows_done, 1)
            sp.dma_start(last_v_dram, last_rows[:]).then_inc(last_stored, 16)
            sp.wait_ge(last_stored, 16)
            sp.wait_ge(zeros_set, 5)
            for u in range(U):
                sp.dma_start(V_last_all[u:u + 1, :, u, :], last_v_dram[:, u * 64:(u + 1) * 64].unsqueeze(0)).then_inc(last_placed, 16)
            with sp.Fori(0, B // 2 - 1) as i:
                for j in range(2):
                    sp.wait_ge(k_done, 4 * i + (2 * j + 2))
                    sp.dma_start(ctxT[j][:], core.dram["ctxT"][2 * i + (j + 2)]).then_inc(ctx_in[j], 16)

        @block.gpsimd
        def _(pool):
            nc.gpsimd.memset(V_last_all[:], 0.0).then_inc(zeros_set, 1)
            for j in range(2):
                nc.gpsimd.memset(V_last[j][:], 0.0).then_inc(zeros_set, 1)
                nc.gpsimd.memset(probsT_last[j][:], 0.0).then_inc(zeros_set, 1)
            pool.wait_ge(zeros_set, 5)
            pool.wait_ge(core.weights_in[6], 16)
            pool.wait_ge(q_copied, 4)

            def prepare(b, j):
                at_least(pool, sim_done, 2 * b - 2)
                for c in range(C):
                    last = nc.gpsimd.tensor_tensor(spread[j][:, c], bcast(QT[:, c, bass.ds(b * S, S)], 1, 8), bcast(head_of, 2, S), ALU.mult)
                last.then_inc(spread_done, 1)
                at_least(pool, pv_done, b - 1)
                nc.gpsimd.tensor_copy(V_last[j][0:U].unsqueeze(1), V_last_all[:, bass.ds(b, 1), :, :]).then_inc(V_last_done, 1)

            pool.wait_ge(last_placed, 16 * U)
            prepare(0, 0)
            prepare(1, 1)
            with pool.Fori(0, B // 2 - 1) as i:
                for j in range(2):
                    prepare(2 * i + (j + 2), j)

        @block.tensor
        def _(pe):
            pe.wait_ge(core.consts_in, 16)
            pe.wait_ge(core.weights_in[6], 16)
            flip.tensor(pe, core.H, rows_done, 0)
            flip.ready(pe, "pe")
            for n in range(4):
                o, half = n // 2, n % 2
                for c in range(C):
                    last = nc.tensor.matmul(PS[:, n, :], wq[:, c, o * P:(o + 1) * P], core.HT[:, c, half * 512:(half + 1) * 512],
                                            start=(c == 0), stop=(c == 1))
                last.then_inc(q_done, 1)

            for c in range(C):
                last = nc.tensor.matmul(PS[0:B, 7, 0:D], last_tokens[:, c, :], wv[:, c, :], start=(c == 0), stop=(c == 1))
            last.then_inc(last_v_done, 1)

            def keys_values(b, j):
                pe.wait_ge(ctx_in[j], 8 * b + (16 - 8 * j))
                for half in range(2):
                    for c in range(C):
                        last = nc.tensor.matmul(PS[:, 5, half * D:(half + 1) * D], ctxT[j][:, c, half * P:(half + 1) * P], wv[:, c, :], start=(c == 0), stop=(c == 1))
                last.then_inc(v_done, 1)
                for o in range(C):
                    for c in range(C):
                        last = nc.tensor.matmul(PS[:, 4 + 2 * o, 0:CTX], wk[:, c, o * P:(o + 1) * P], ctxT[j][:, c, :], start=(c == 0), stop=(c == 1))
                    last.then_inc(k_done, 1)

            def sim(b, j):
                pe.wait_ge(spread_done, b + 1)
                for u in range(U):
                    c = u // 2
                    last = nc.tensor.matmul(PS[:, u, 0:CTX], spread[j][:, c, 4 * (u % 2):4 * (u % 2) + 4, :].rearrange("p h q -> p (h q)"),
                                            kT[j][:, c, :], start=True, stop=True)
                    if u % 2:
                        last.then_inc(sim_done, 1)

            def flip_probs(b, j):
                pe.wait_ge(probs_done, b + 1)
                for half in (1, 0):
                    if exists(b + 1):
                        pe.wait_ge((k_copied, v_copied)[half], b + 2)
                    for u in range(U):
                        nc.tensor.transpose(PS[:, 4 + half, u * P:(u + 1) * P], probs[j][:, u, half * P:(half + 1) * P], core.ident[:])
                nc.tensor.transpose(PS[0:U, 6, 3 * P:4 * P], probs[j][:, :, 2 * P], core.ident[:]).then_inc(pt_done, 1)

            def weigh(b, j):
                pe.wait_ge(pt_copied_act, b + 1)
                pe.wait_ge(pt_copied_dve, b + 1)
                pe.wait_ge(V_last_done, b + 1)
                pe.wait_ge(own_done, b + 1)
                for c in range(C):
                    for par in range(2):
                        u = 2 * c + par
                        out = PS[64 * par:64 * (par + 1), 7, c * P:(c + 1) * P]
                        for half in range(2):
                            nc.tensor.matmul(out, V[j][:, half, u * 64:(u + 1) * 64], probsT[j][:, half, u * P:(u + 1) * P], start=(half == 0), stop=False)
                        last = nc.tensor.matmul(out, V_last[j][:, u, :], probsT_last[j][:], start=False, stop=True)
                last.then_inc(pv_done, 1)

            def first():
                pe.wait_ge(q_copied, 4)
                for b in range(2):
                    if b:
                        pe.wait_ge(v_copied, b)
                        pe.wait_ge(k_copied, b)
                    keys_values(b, b)
                pe.wait_ge(k_copied, 1)
                sim(0, 0)

            def turn(b, j):
                flip_probs(b, j)
                sim(b + 1, 1 - j)
                weigh(b, j)
                if exists(b + 2):
                    keys_values(b + 2, j)

            def last(b, j):
                flip_probs(b, j)
                weigh(b, j)

            over_batches(pe, first, turn, last)
            pe.wait_ge(at_done, B)
            for t in range(NT):
                for c in range(C):
                    done = nc.tensor.matmul(PS[:, 4 + t // 2, (t % 2) * D:(t % 2 + 1) * D], AT[:, c, t * P:(t + 1) * P],
                                            wo[:, c, :], start=(c == 0), stop=(c == 1))
                if t % 2:
                    done.then_inc(out_done, 1)

        @block.scalar
        def _(act):
            norm.begin(act)
            norm.scalar(act, core.eps5)
            flip.scalar(act, core.HT)
            act.wait_ge(core.weights_in[6], 16)
            for n in range(4):
                o, half = n // 2, n % 2
                act.wait_ge(q_done, n + 1)
                nc.scalar.activation(QT[:, o, half * 512:(half + 1) * 512], PS[:, n, :], ACT.Identity, bias=bq[:, o:o + 1]).then_inc(q_copied, 1)

            def copy_keys(b, j):
                for o in range(C):
                    act.wait_ge(k_done, 2 * b + (o + 1))
                    done = nc.scalar.activation(kT[j][:, o, :], PS[:, 4 + 2 * o, 0:CTX], ACT.Identity, bias=bk[:, o:o + 1])
                done.then_inc(k_copied, 1)

            def exps(b, j):
                for u in range(U):
                    if u % 2 == 0:
                        act.wait_ge(top_done, 2 * b + (u // 2 + 1))
                    done = nc.scalar.activation(probs[j][:, u, :], PS[:, u, 0:CTX], ACT.Exp, bias=top[j][:, u:u + 1], scale=scale,
                                                accum_out=total[j][:, u:u + 1])
                    if u % 2:
                        done.then_inc(exps_done, 1)

            def copy_probs(b, j):
                act.wait_ge(pt_done, b + 1)
                nc.scalar.copy(probsT[j][:, 0, :], PS[:, 4, :]).then_inc(pt_copied_act, 1)

            def first():
                copy_keys(0, 0)
                copy_keys(1, 1)
                exps(0, 0)

            def turn(b, j):
                copy_probs(b, j)
                exps(b + 1, 1 - j)
                if exists(b + 2):
                    copy_keys(b + 2, j)

            over_batches(act, first, turn, copy_probs)

        @block.vector
        def _(dve):
            dve.wait_ge(core.x_in, 16)
            norm.vector(dve, core.X, core.H, rows_done)
            flip.vector(dve, core.HT)
            dve.wait_ge(core.weights_in[6], 16)

            dve.wait_ge(zeros_set, 5)
            dve.wait_ge(last_v_done, 1)
            nc.vector.tensor_tensor(last_rows[:], PS[0:B, 7, 0:D], bv[0:B, :], ALU.add).then_inc(last_rows_done, 1)
            dve.sem_inc(own_done, 1)

            def copy_values(b, j):
                dve.wait_ge(v_done, b + 1)
                at_least(dve, pv_done, b - 1)
                nc.vector.tensor_tensor(V[j][:], PS[:, 5, :].rearrange("p (k d) -> p k d", k=2), bcast(bv, 1, 2), ALU.add).then_inc(v_copied, 1)

            def tops(b, j):
                for n in range(2):
                    dve.wait_ge(sim_done, 2 * b + (n + 1))
                    t = top[j][:, 2 * n:2 * n + 2]
                    dve_step(dve, nc.vector.reduce_max(t, PS[:, 2 * n:2 * n + 2, 0:CTX], AX.X))
                    nc.vector.tensor_scalar(t, t, -scale, None, ALU.mult).then_inc(top_done, 1)

            def weights(b, j):
                for n in range(2):
                    dve.wait_ge(exps_done, 2 * b + (n + 1))
                    t = total[j][:, 2 * n:2 * n + 2]
                    dve_step(dve, nc.vector.reciprocal(t, t))
                    for u in range(2 * n, 2 * n + 2):
                        done = nc.vector.tensor_scalar(probs[j][:, u, :], probs[j][:, u, :], total[j][:, u:u + 1], None, ALU.mult)
                done.then_inc(probs_done, 1)

            def copy_probs(b, j):
                dve.wait_ge(pt_done, b + 1)
                nc.vector.tensor_copy(probsT[j][:, 1, :], PS[:, 5, :])
                nc.vector.tensor_copy(probsT_last[j][0:U], PS[0:U, 6, 3 * P:4 * P]).then_inc(pt_copied_dve, 1)

            def keep_own(b, j):
                dve.wait_ge(pv_done, b + 1)
                nc.vector.tensor_tensor(own_out[:], PS[:, 7, 0:C * P].rearrange("p (c h q) -> p c h q", c=C, q=S),
                                        bcast(bcast(own, 1, C), 3, S), ALU.mult).then_inc(own_done, 1)
                dve.wait_ge(own_done, b + 2)
                nc.vector.reduce_sum(AT[:, :, bass.ds(b * S, S)], own_out[:].rearrange("p c h q -> p c q h"), AX.X).then_inc(at_done, 1)
                dve.wait_ge(at_done, b + 1)

            def first():
                copy_values(0, 0)
                copy_values(1, 1)
                tops(0, 0)
                weights(0, 0)

            def turn(b, j):
                copy_probs(b, j)
                tops(b + 1, 1 - j)
                keep_own(b, j)
                weights(b + 1, 1 - j)
                if exists(b + 2):
                    copy_values(b + 2, j)

            def last(b, j):
                copy_probs(b, j)
                keep_own(b, j)

            over_batches(dve, first, turn, last, lambda i: dve_step.enter(i, 8), dve_step.leave)
            for n in range(NT // 2):
                x = core.X[:, 2 * n:2 * n + 2, :]
                dve_step(dve, nc.vector.tensor_tensor(x, x, bcast(bo, 1, 2), ALU.add))
                dve.wait_ge(out_done, n + 1)
                nc.vector.tensor_tensor(x, PS[:, 4 + n, :].rearrange("p (t d) -> p t d", t=2), x, ALU.add)


def l2_self(core, load_next):
    nc, norm, flip, dve_step = core.nc, core.norm, core.flip, core.dve_step
    w = core.arena(7)
    wqk, wv, wo = w.take(C, 2 * D), w.take(C, D), w.take(C, D)
    cos, sin, causal, head_of = w.take(8), w.take(8), w.take(S), w.take(8)
    cap = 50.0
    with ExitStack() as es:
        at = SelfAttention(core, es, "l2a", "capped", cap)
        at.tanh_scale = 16.0 ** -0.5 / cap
        t1, t2 = (core.sb(f"l2a_t{i}", [P, NT, 16, 8], es) for i in range(2))
        squares = core.sb("l2a_squares", [P, NT, 16, 16], es)
        size = [core.sb(f"l2a_size{i}", [P, NT, 16], es) for i in range(2)]
        rows_done = core.sem("l2a_rows_done")
        summed, rooted = core.sem("l2a_summed"), core.sem("l2a_rooted")
        block = es.enter_context(nc.Block())

        @block.sync
        def _(sp):
            load_next(sp)

        @block.tensor
        def _(pe):
            pe.wait_ge(core.consts_in, 16)
            pe.wait_ge(core.weights_in[7], 16)
            flip.tensor(pe, core.H, rows_done, 0)
            flip.ready(pe, "pe")
            at.project(pe, core.HT, core.HT, wqk, wv)
            at.flip_tensor(pe)
            flip.ready(pe, "pe")
            at.attend_tensor(pe)
            at.output_tensor(pe, wo)

        @block.gpsimd
        def _(pool):
            pool.wait_ge(core.weights_in[7], 16)
            flip.uses["pool"] = flip.uses["pe"] - 1
            flip.ready(pool, "pool")
            at.spread_keys(pool, head_of)

        @block.scalar
        def _(act):
            norm.begin(act)
            norm.scalar(act, core.eps5)
            flip.scalar(act, core.HT)
            at.copy_qk(act)
            for n in range(2):
                act.wait_ge(summed, n + 1)
                nc.scalar.activation(size[n][:], size[n][:], ACT.Sqrt, bias=core.eps5, scale=1.0 / 16).then_inc(rooted, 1)
            flip.scalar(act, at.QT)
            flip.scalar(act, at.KT)
            at.attend_scalar(act)
            flip.scalar(act, core.HT)

        @block.vector
        def _(dve):
            dve.wait_ge(core.x_in, 16)
            norm.vector(dve, core.X, core.H, rows_done)
            flip.vector(dve, core.HT)
            at.copy_v(dve)
            dve.wait_ge(core.weights_in[7], 16)
            dve.wait_ge(at.qk_copied, NT)
            for n, rows in enumerate((at.Q, at.K)):
                heads = rows[:].rearrange("p t (h d) -> p t h d", h=16)
                dve_step(dve, nc.vector.tensor_tensor(squares[:], heads, heads, ALU.mult))
                nc.vector.reduce_sum(size[n][:], squares[:], AX.X).then_inc(summed, 1)
                dve.wait_ge(summed, n + 1)
            for n, (rows, done) in enumerate(((at.Q, at.q_rows), (at.K, at.k_rows))):
                dve.wait_ge(rooted, n + 1)
                heads = rows[:].rearrange("p t (h d) -> p t h d", h=16)
                dve_step(dve, nc.vector.reciprocal(size[n][:], size[n][:]))
                dve_step(dve, nc.vector.tensor_tensor(heads, heads, bcast(size[n][:], 3, 16), ALU.mult))
                rotate(core, dve, heads[:, :, :, 0:8], heads[:, :, :, 8:16], t1[:], t2[:], cos, sin, done)
            flip.vector(dve, at.QT)
            flip.vector(dve, at.KT)
            at.attend_vector(dve, causal)
            flip.vector(dve, core.HT)
            at.output_vector(dve)


def l2_feed_forward(core, load_next):
    nc, PS, norm, flip, dve_step = core.nc, core.PS, core.norm, core.flip, core.dve_step
    E = 8
    w = core.arena(8)
    experts, wg, number = w.take(C, E * D), w.take(C, E), w.take(E)
    with ExitStack() as es:
        sb = lambda n, shape: core.sb("l2f_" + n, shape, es)
        scores, gate = sb("scores", [P, NT, E]), sb("gate", [P, NT, E])
        best, place = sb("best", [P, NT]), sb("place", [P, NT])
        rows_done, routed = core.sem("l2f_rows_done"), core.sem("l2f_routed")
        expert_done, summed = core.sem("l2f_expert_done"), core.sem("l2f_summed")
        block = es.enter_context(nc.Block())

        @block.sync
        def _(sp):
            load_next(sp)

        @block.tensor
        def _(pe):
            pe.wait_ge(core.consts_in, 16)
            pe.wait_ge(core.weights_in[8], 16)
            flip.tensor(pe, core.H, rows_done, 0)
            flip.ready(pe, "pe")
            router_tensor(core, pe, core.HT, wg, routed)
            with pe.Fori(0, E // 2) as i:
                for t in range(NT):
                    pe.wait_ge(summed, i * NT + (t + 1))
                    for c in range(C):
                        last = nc.tensor.matmul(PS[:, t % 4, :], core.HT[:, c, t * P:(t + 1) * P],
                                                experts[:, c, bass.ds(i * (2 * D), 2 * D)], start=(c == 0), stop=(c == 1))
                    last.then_inc(expert_done, 1)

        @block.scalar
        def _(act):
            norm.begin(act)
            norm.scalar(act, core.eps5)
            flip.scalar(act, core.HT)

        @block.vector
        def _(dve):
            dve.sem_inc(summed, 4)
            dve.wait_ge(core.x_in, 16)
            norm.vector(dve, core.X, core.H, rows_done)
            flip.vector(dve, core.HT)
            dve.wait_ge(rows_done, NT)
            nc.vector.tensor_tensor(core.X[:], core.X[:], core.H[:], ALU.add)
            dve.wait_ge(core.weights_in[8], 16)
            dve.wait_ge(routed, 1)
            dve_step(dve, nc.vector.tensor_copy(scores[:], PS[:, 4, 0:NT * E].rearrange("p (t e) -> p t e", e=E)))
            first_best(core, dve, scores, number, best, place, gate)
            with dve.Fori(0, E // 2) as i:
                dve_step.enter(i, 2)
                for half in range(2):
                    for t in range(4 * half, 4 * half + 4):
                        dve.wait_ge(expert_done, i * NT + (t + 1))
                        bank = PS[:, t % 4, :].rearrange("p (e d) -> p e d", e=2)
                        step = nc.vector.scalar_tensor_tensor(core.X[:, t, :], bank[:, 0, :], gate[:, t, bass.ds(2 * i, 1)], core.X[:, t, :], ALU.mult, ALU.add)
                    dve_step(dve, step)
                    for t in range(4 * half, 4 * half + 4):
                        bank = PS[:, t % 4, :].rearrange("p (e d) -> p e d", e=2)
                        nc.vector.scalar_tensor_tensor(core.X[:, t, :], bank[:, 1, :], gate[:, t, bass.ds(2 * i + 1, 1)], core.X[:, t, :],
                                                       ALU.mult, ALU.add).then_inc(summed, 1)
                dve.wait_ge(summed, i * NT + (NT + 4))
                dve_step.leave(E // 2)


def l3_cross(core, load_next):
    nc, PS, norm, flip, cn = core.nc, core.PS, core.norm, core.flip, core.ctx_norm
    dve_step, pool_step = core.dve_step, core.pool_step
    HEADS, DH = 8, 64
    M = HEADS // 2
    KEYS, REST = CTX + S, CTX + S - 2 * P
    w = core.arena(9)
    wq, wkT, wv, wout = w.take(C, M * P), w.take(M, D), w.take(C, M * P), w.take(M, D)
    gm, bm, gl, bl = w.take(C), w.take(C), w.take(C), w.take(C)
    gm_row, bm_row, gl_row, bl_row = w.take(D), w.take(D), w.take(D), w.take(D)
    scale = DH ** 0.5
    with ExitStack() as es:
        sb = lambda n, shape: core.sb("l3x_" + n, shape, es)
        two = lambda n, shape: [sb(f"{n}{i}", shape) for i in range(2)]
        sem = lambda n: core.sem("l3x_" + n)
        QT = OT = sb("QT", [P, M, NT * P])
        QW = sb("QW", [P, C, HEADS, NT * P])
        last_cols, last_rows = sb("last_cols", [P, C, B]), sb("last_rows", [B, D])
        ctx, hat, tokens = two("ctx", [P, 2, D]), two("hat", [P, 2, D]), two("tokens", [P, 2, D])
        keysT, queries = two("keysT", [P, C, KEYS]), two("queries", [P, C, HEADS * S])
        probs, probsT = two("probs", [P, 2, KEYS]), two("probsT", [P, 2, HEADS * S])
        rest, probsT_rest = ([core.H[0:REST, k + j, :] for j in range(2)] for k in (0, 2))
        top, total = two("top", [P, 2]), two("total", [P, 2])
        latents_dram = nc.dram_tensor("latents_dram", (B * S, D), F32).ap()
        last_dram = nc.dram_tensor("last_dram", (B, D), F32).ap()
        if not cn.computed:
            cn.allocate(es, "l3x")
        rows_done, normed_done, affine_done, stored = sem("rows_done"), sem("normed_done"), sem("affine_done"), sem("stored")
        q_done, q_copied, qw_done, qw_act, qw_dve = sem("q_done"), sem("q_copied"), sem("qw_done"), sem("qw_act"), sem("qw_dve")
        rest_in = [sem("rest_in0"), sem("rest_in1")]
        last_done, hat_done, ctx_flipped, ctxT_copied = sem("last_done"), sem("hat_done"), sem("ctx_flipped"), sem("ctxT_copied")
        prep_done, tokens_done, sim_done, top_done = sem("prep_done"), sem("tokens_done"), sem("sim_done"), sem("top_done")
        exps_done, probs_done, pt_done, pt_act, pt_dve = (sem(n) for n in ("exps_done", "probs_done", "pt_done", "pt_act", "pt_dve"))
        pv_done, px_copied, out_done, out_act, out_dve, proj_done = (sem(n) for n in ("pv_done", "px_copied", "out_done", "out_act", "out_dve", "proj_done"))
        tile = lambda b: core.dram["ctx"][b, 0:2 * P, :].rearrange("(h p) d -> p h d", p=P)
        before = 16 * (cn.loads + (0 if cn.computed else B // 2))
        block = es.enter_context(nc.Block())

        @block.sync
        def _(sp):
            if cn.computed:
                for j in range(2):
                    sp.dma_start(ctx[j][:], tile(j)).then_inc(cn.slot_in[j], 16)
            else:
                cn.load(sp, ctx)
            load_next(sp)
            sp.wait_ge(last_done, 2)
            sp.dma_start(last_dram, last_rows[:]).then_inc(stored, 16)
            sp.wait_ge(affine_done, 1)
            for f in range(TB):
                sp.dma_start(latents_dram.rearrange("(t f q) d -> f q t d", f=TB, q=S)[f],
                             core.H[f * S:(f + 1) * S, :, :]).then_inc(stored, 16)
            sp.wait_ge(stored, 16 * (TB + 1))

            def load_rest(b, j):
                sp.dma_start(rest[j][0:S, :], latents_dram[bass.ds(b * S, S), :]).then_inc(rest_in[j], 16)
                sp.dma_start(rest[j][S:REST, :], last_dram[bass.ds(b, 1), :]).then_inc(rest_in[j], 16)

            def load_context(b, j):
                sp.wait_ge(hat_done, b - 1)
                sp.dma_start(ctx[j][:], tile(b)).then_inc(cn.slot_in[j], 16)

            def turn(b, j):
                if exists(b + 1):
                    load_context(b + 1, 1 - j)
                sp.wait_ge(pv_done, b - 1)
                load_rest(b, j)

            load_rest(0, 0)
            load_rest(1, 1)
            load_context(2, 0)
            with sp.Fori(0, B // 2 - 2) as i:
                turn(2 * i + 2, 0)
                turn(2 * i + 3, 1)
            turn(B - 2, 0)
            turn(B - 1, 1)

        @block.gpsimd
        def _(pool):
            pool.wait_ge(core.weights_in[9], 16)
            pool.wait_ge(last_done, 2)
            pool.wait_ge(qw_act, HEADS * C)
            pool.wait_ge(qw_dve, HEADS * C)

            def prepare(b, j):
                at_least(pool, sim_done, b - 1)
                nc.gpsimd.tensor_copy(queries[j][:].rearrange("p c (h q) -> p c h q", q=S), QW[:, :, :, bass.ds(b * S, S)])
                nc.gpsimd.tensor_copy(keysT[j][:, :, 2 * P:2 * P + S], core.HT[:, :, bass.ds(b * S, S)])
                nc.gpsimd.tensor_copy(keysT[j][:, :, KEYS - 1:KEYS], last_cols[:, :, bass.ds(b, 1)]).then_inc(prep_done, 1)

            def scale_tokens(b, j):
                pool.wait_ge(hat_done, b + 1)
                at_least(pool, pv_done, b - 1)
                pool_step(pool, nc.gpsimd.tensor_tensor(tokens[j][:], hat[j][:], bcast(gm_row, 1, 2), ALU.mult))
                nc.gpsimd.tensor_tensor(tokens[j][:], tokens[j][:], bcast(bm_row, 1, 2), ALU.add).then_inc(tokens_done, 1)
                pool.wait_ge(tokens_done, b + 1)

            def first():
                prepare(0, 0)
                scale_tokens(0, 0)
                prepare(1, 1)
                scale_tokens(1, 1)

            def turn(b, j):
                if exists(b + 2):
                    prepare(b + 2, j)
                    scale_tokens(b + 2, j)

            over_batches(pool, first, turn, lambda b, j: None, lambda i: pool_step.enter(i, 2), pool_step.leave)

        @block.tensor
        def _(pe):
            pe.wait_ge(core.consts_in, 16)
            pe.wait_ge(core.weights_in[9], 16)
            flip.tensor(pe, core.H, normed_done, 0)
            flip.ready(pe, "pe")
            for n in range(2 * M):
                m, half = n // 2, n % 2
                if n >= 4:
                    pe.wait_ge(q_copied, n - 3)
                for c in range(C):
                    done = nc.tensor.matmul(PS[:, 4 + n % 4, :], wq[:, c, m * P:(m + 1) * P], core.HT[:, c, half * 512:(half + 1) * 512],
                                            start=(c == 0), stop=(c == 1))
                done.then_inc(q_done, 1)
            pe.wait_ge(q_copied, 2 * M)
            for n in range(M * C * 2):
                m, c, half = n // (2 * C), n // 2 % C, n % 2
                if n >= 2:
                    pe.wait_ge(qw_act, n - 1)
                    pe.wait_ge(qw_dve, n - 1)
                for par in range(2):
                    rows = slice(DH * par, DH * (par + 1))
                    nc.tensor.matmul(PS[:, 4 + 2 * (n % 2) + par, :], wkT[rows, m, c * P:(c + 1) * P], QT[rows, m, half * 512:(half + 1) * 512],
                                     start=True, stop=True).then_inc(qw_done, 1)
            if not cn.computed:
                pe.wait_ge(qw_dve, HEADS * C)
                cn.tensor(pe)

            def flip_context(b, j):
                pe.wait_ge(hat_done, b + 1)
                at_least(pe, ctxT_copied, b)
                for c in range(C):
                    for half in range(2):
                        done = nc.tensor.transpose(PS[:, 6, (2 * c + half) * P:(2 * c + half + 1) * P], hat[j][:, half, c * P:(c + 1) * P], core.ident[:])
                done.then_inc(ctx_flipped, 1)

            def sim(b, j):
                pe.wait_ge(ctxT_copied, b + 1)
                pe.wait_ge(prep_done, b + 1)
                for u in range(2):
                    for c in range(C):
                        done = nc.tensor.matmul(PS[:, 2 * j + u, 0:KEYS], queries[j][:, c, u * P:(u + 1) * P], keysT[j][:, c, :],
                                                start=(c == 0), stop=(c == 1))
                done.then_inc(sim_done, 1)

            def flip_probs(b, j):
                pe.wait_ge(probs_done, b + 1)
                for u in range(2):
                    for half in range(2):
                        nc.tensor.transpose(PS[:, 4, half * 2 * P + u * P:half * 2 * P + (u + 1) * P], probs[j][:, u, half * P:(half + 1) * P], core.ident[:])
                    done = nc.tensor.transpose(PS[0:REST, 5, u * P:(u + 1) * P], probs[j][:, u, 2 * P:KEYS], core.ident[:])
                done.then_inc(pt_done, 1)

            def weigh(b, j):
                pe.wait_ge(pt_act, b + 1)
                pe.wait_ge(pt_dve, b + 1)
                pe.wait_ge(tokens_done, b + 1)
                pe.wait_ge(rest_in[j], 16 * b + (32 - 16 * j))
                pe.wait_ge(px_copied, b + 1)
                for c in range(C):
                    out = PS[:, 7, c * 2 * P:(c + 1) * 2 * P]
                    for half in range(2):
                        nc.tensor.matmul(out, tokens[j][:, half, c * P:(c + 1) * P], probsT[j][:, half, :], start=(half == 0), stop=False)
                    done = nc.tensor.matmul(out, rest[j][:, c * P:(c + 1) * P], probsT_rest[j], start=False, stop=True)
                done.then_inc(pv_done, 1)

            def first():
                pe.wait_ge(qw_act, HEADS * C)
                pe.wait_ge(qw_dve, HEADS * C)
                flip_context(0, 0)
                flip_context(1, 1)
                sim(0, 0)

            def turn(b, j):
                flip_probs(b, j)
                sim(b + 1, 1 - j)
                weigh(b, j)
                if exists(b + 2):
                    flip_context(b + 2, j)

            def last(b, j):
                flip_probs(b, j)
                weigh(b, j)

            over_batches(pe, first, turn, last)
            pe.wait_ge(px_copied, B + 1)
            for n in range(2 * M):
                m, half = n // 2, n % 2
                if n >= 2:
                    pe.wait_ge((out_act, out_dve)[n % 2], n // 2)
                for par in range(2):
                    for c in range(C):
                        at = (2 * m + par) * DH
                        done = nc.tensor.matmul(PS[DH * par:DH * (par + 1), n % 2, :], wv[:, c, at:at + DH], QW[:, c, 2 * m + par, half * 512:(half + 1) * 512],
                                                start=(c == 0), stop=(c == 1))
                done.then_inc(out_done, 1)
            pe.wait_ge(out_act, M)
            pe.wait_ge(out_dve, M)
            for t in range(NT):
                for m in range(M):
                    done = nc.tensor.matmul(PS[:, 4 + t // 2, (t % 2) * D:(t % 2 + 1) * D], OT[:, m, t * P:(t + 1) * P], wout[:, m, :],
                                            start=(m == 0), stop=(m == M - 1))
                if t % 2:
                    done.then_inc(proj_done, 1)

        @block.scalar
        def _(act):
            norm.begin(act)
            act.wait_ge(core.weights_in[9], 16)
            norm.scalar(act, core.eps5)
            norm.scalar(act, core.eps5)
            if not cn.computed:
                cn.scalar(act)
            flip.scalar(act, core.HT, gl, bl)
            for n in range(2 * M):
                act.wait_ge(q_done, n + 1)
                nc.scalar.copy(QT[:, n // 2, (n % 2) * 512:(n % 2 + 1) * 512], PS[:, 4 + n % 4, :]).then_inc(q_copied, 1)
            for n in range(M * C * 2):
                m, c, half = n // (2 * C), n // 2 % C, n % 2
                act.wait_ge(qw_done, 2 * n + 1)
                nc.scalar.copy(QW[:, c, 2 * m, half * 512:(half + 1) * 512], PS[:, 4 + 2 * (n % 2), :]).then_inc(qw_act, 1)
            act.wait_ge(last_done, 2)

            def normalise(b, j):
                act.wait_ge(cn.slot_in[j], 8 * b + (before + 16 - 8 * j))
                at_least(act, ctx_flipped, b - 1)
                at_least(act, tokens_done, b - 1)
                for h in range(2):
                    done = nc.scalar.activation(hat[j][:, h, :], ctx[j][:, h, :], ACT.Identity, bias=cn.shift[:, b, h:h + 1], scale=cn.rstd[:, b, h:h + 1])
                done.then_inc(hat_done, 1)

            def copy_context(b, j):
                act.wait_ge(ctx_flipped, b + 1)
                at_least(act, sim_done, b - 1)
                for c in range(C):
                    done = nc.scalar.activation(keysT[j][:, c, 0:2 * P], PS[:, 6, c * 2 * P:(c + 1) * 2 * P], ACT.Identity,
                                                bias=bm[:, c:c + 1], scale=gm[:, c:c + 1])
                done.then_inc(ctxT_copied, 1)

            def exps(b, j):
                act.wait_ge(top_done, b + 1)
                for u in range(2):
                    done = nc.scalar.activation(probs[j][:, u, :], PS[:, 2 * j + u, 0:KEYS], ACT.Exp, bias=top[j][:, u:u + 1], scale=scale,
                                                accum_out=total[j][:, u:u + 1])
                done.then_inc(exps_done, 1)

            def copy_probs(b, j):
                act.wait_ge(pt_done, b + 1)
                nc.scalar.copy(probsT[j][:].rearrange("p h e -> p (h e)"), PS[:, 4, :]).then_inc(pt_act, 1)

            def first():
                normalise(0, 0)
                normalise(1, 1)
                copy_context(0, 0)
                copy_context(1, 1)
                normalise(2, 0)
                exps(0, 0)

            def turn(b, j):
                copy_probs(b, j)
                exps(b + 1, 1 - j)
                if exists(b + 3):
                    normalise(b + 3, 1 - j)
                if exists(b + 2):
                    copy_context(b + 2, j)

            over_batches(act, first, turn, copy_probs)
            for n in range(0, 2 * M, 2):
                act.wait_ge(out_done, n + 1)
                nc.scalar.copy(OT[:, n // 2, 0:512], PS[:, 0, :]).then_inc(out_act, 1)

        @block.vector
        def _(dve):
            dve.wait_ge(core.x_in, 16)
            norm.vector(dve, core.X, core.H, rows_done)
            dve.wait_ge(rows_done, NT)
            norm.vector(dve, core.H, core.H, normed_done)
            dve.wait_ge(core.weights_in[9], 16)
            if not cn.computed:
                cn.vector_stats(dve, ctx)
            flip.vector(dve, core.HT, gl, bl)
            flip.ready(dve, "dve")
            dve.wait_ge(normed_done, NT)
            dve_step(dve, nc.vector.tensor_tensor(core.H[:], core.H[:], bcast(gl_row, 1, NT), ALU.mult))
            nc.vector.tensor_tensor(core.H[:], core.H[:], bcast(bl_row, 1, NT), ALU.add).then_inc(affine_done, 1)
            for n in range(M * C * 2):
                m, c, half = n // (2 * C), n // 2 % C, n % 2
                dve.wait_ge(qw_done, 2 * n + 2)
                nc.vector.tensor_copy(QW[:, c, 2 * m + 1, half * 512:(half + 1) * 512], PS[:, 5 + 2 * (n % 2), :]).then_inc(qw_dve, 1)
            if not cn.computed:
                cn.vector_finish(dve)
            for c in range(C):
                nc.vector.tensor_scalar(last_cols[:, c, :], cn.lastT[:, c, :], gm[:, c:c + 1], bm[:, c:c + 1], ALU.mult, ALU.add)
            nc.vector.tensor_tensor(last_rows[:], cn.last[:], gm_row[0:B, :], ALU.mult).then_inc(last_done, 1)
            dve.wait_ge(last_done, 1)
            nc.vector.tensor_tensor(last_rows[:], last_rows[:], bm_row[0:B, :], ALU.add).then_inc(last_done, 1)
            dve.wait_ge(stored, 16 * (TB + 1))
            dve.sem_inc(px_copied, 1)

            def tops(b, j):
                dve.wait_ge(sim_done, b + 1)
                dve_step(dve, nc.vector.reduce_max(top[j][:], PS[:, 2 * j:2 * j + 2, 0:KEYS], AX.X))
                nc.vector.tensor_scalar(top[j][:], top[j][:], -scale, None, ALU.mult).then_inc(top_done, 1)

            def weights(b, j):
                dve.wait_ge(exps_done, b + 1)
                dve_step(dve, nc.vector.reciprocal(total[j][:], total[j][:]))
                for u in range(2):
                    done = nc.vector.tensor_scalar(probs[j][:, u, :], probs[j][:, u, :], total[j][:, u:u + 1], None, ALU.mult)
                done.then_inc(probs_done, 1)

            def copy_rest(b, j):
                dve.wait_ge(pt_done, b + 1)
                nc.vector.tensor_copy(probsT_rest[j], PS[0:REST, 5, 0:HEADS * S]).then_inc(pt_dve, 1)

            def copy_px(b, j):
                dve.wait_ge(pv_done, b + 1)
                nc.vector.tensor_copy(QW[:, :, :, bass.ds(b * S, S)], PS[:, 7, :].rearrange("p (c h q) -> p c h q", c=C, q=S)).then_inc(px_copied, 1)

            def first():
                tops(0, 0)
                weights(0, 0)

            def turn(b, j):
                copy_rest(b, j)
                tops(b + 1, 1 - j)
                weights(b + 1, 1 - j)
                copy_px(b, j)

            def last(b, j):
                copy_rest(b, j)
                copy_px(b, j)

            over_batches(dve, first, turn, last, lambda i: dve_step.enter(i, 4), dve_step.leave)
            for n in range(1, 2 * M, 2):
                dve.wait_ge(out_done, n + 1)
                nc.vector.tensor_copy(OT[:, n // 2, 512:1024], PS[:, 1, :]).then_inc(out_dve, 1)
            for n in range(NT // 2):
                dve.wait_ge(proj_done, n + 1)
                x = core.X[:, 2 * n:2 * n + 2, :]
                nc.vector.tensor_tensor(x, PS[:, 4 + n, :].rearrange("p (t d) -> p t d", t=2), x, ALU.add)

        cn.loads, cn.computed = cn.loads + B // 2 * (1 if cn.computed else 2), True


def l3_self(core, load_next):
    nc, norm, flip, dve_step = core.nc, core.norm, core.flip, core.dve_step
    w = core.arena(10)
    wqk, wv, wo = w.take(C, 2 * D), w.take(C, D), w.take(C, D)
    gate = [w.take(16), w.take(16)]
    bo, ln_w, ln_b, head_of = w.take(D), w.take(C), w.take(C), w.take(8)
    sharp, threshold = 15.0, 0.29514
    with ExitStack() as es:
        at = SelfAttention(core, es, "l3a", "resonance", sharp)
        shift = core.sb("l3a_shift", [P, 1], es)
        at.resonance_bias = shift[:]
        products = core.sb("l3a_products", [P, NT, 16, 16], es)
        size = [core.sb(f"l3a_size{i}", [P, NT, 16], es) for i in range(2)]
        k_gate = core.sb("l3a_k_gate", [P, NT, 16], es)
        rows_done, normed_done = core.sem("l3a_rows_done"), core.sem("l3a_normed_done")
        summed, rooted, shift_set = core.sem("l3a_summed"), core.sem("l3a_rooted"), core.sem("l3a_shift_set")
        gated = core.sem("l3a_gated")
        block = es.enter_context(nc.Block())

        @block.sync
        def _(sp):
            load_next(sp)

        @block.tensor
        def _(pe):
            pe.wait_ge(core.consts_in, 16)
            pe.wait_ge(core.weights_in[10], 16)
            flip.tensor(pe, core.H, rows_done, 0)
            flip.tensor(pe, at.Q, normed_done, 0)
            flip.ready(pe, "pe")
            at.project(pe, at.QT, core.HT, wqk, wv)
            at.flip_tensor(pe)
            flip.ready(pe, "pe")
            pe.wait_ge(gated, 1)
            at.attend_tensor(pe)
            at.output_tensor(pe, wo)

        @block.gpsimd
        def _(pool):
            pool.wait_ge(core.weights_in[10], 16)
            flip.uses["pool"] = flip.uses["pe"] - 1
            flip.ready(pool, "pool")
            at.spread_keys(pool, head_of)

        @block.scalar
        def _(act):
            norm.begin(act)
            norm.scalar(act, core.eps5)
            flip.scalar(act, core.HT)
            norm.scalar(act, core.eps5)
            act.wait_ge(core.weights_in[10], 16)
            flip.scalar(act, at.QT, ln_w, ln_b)
            at.copy_qk(act)
            for n in range(2):
                act.wait_ge(summed, n + 1)
                nc.scalar.activation(size[n][:], size[n][:], ACT.Sqrt).then_inc(rooted, 1)
            flip.scalar(act, at.QT)
            flip.scalar(act, at.KT)
            act.wait_ge(shift_set, 1)
            at.attend_scalar(act)
            flip.scalar(act, core.HT)

        @block.vector
        def _(dve):
            nc.vector.memset(shift[:], -sharp * threshold).then_inc(shift_set, 1)
            dve.wait_ge(core.x_in, 16)
            norm.vector(dve, core.X, core.H, rows_done)
            flip.vector(dve, core.HT)
            norm.vector(dve, core.H, at.Q, normed_done)
            dve.wait_ge(core.weights_in[10], 16)
            flip.vector(dve, at.QT, ln_w, ln_b)
            at.copy_v(dve)
            dve.wait_ge(at.qk_copied, NT)
            for n, rows in enumerate((at.Q, at.K)):
                heads = rows[:].rearrange("p t (h d) -> p t h d", h=16)
                dve_step(dve, nc.vector.tensor_tensor(products[:], heads, heads, ALU.mult))
                nc.vector.reduce_sum(size[n][:], products[:], AX.X).then_inc(summed, 1)
                dve.wait_ge(summed, n + 1)
            for n, (rows, done, g) in enumerate(((at.Q, at.q_rows, at.factor), (at.K, at.k_rows, k_gate))):
                dve.wait_ge(rooted, n + 1)
                heads = rows[:].rearrange("p t (h d) -> p t h d", h=16)
                dve_step(dve, nc.vector.tensor_scalar(size[n][:], size[n][:], 1e-12, None, ALU.max))
                dve_step(dve, nc.vector.reciprocal(size[n][:], size[n][:]))
                nc.vector.tensor_tensor(heads, heads, bcast(size[n][:], 3, 16), ALU.mult).then_inc(done, NT)
                dve.wait_ge(done, NT)
                dve_step(dve, nc.vector.tensor_tensor(products[:], heads, bcast(bcast(gate[n], 1, NT), 2, 16), ALU.mult))
                dve_step(dve, nc.vector.reduce_sum(g[:], products[:], AX.X))
            values = at.V[:].rearrange("p t (h d) -> p t h d", h=16)
            nc.vector.tensor_tensor(values, values, bcast(k_gate[:], 3, 16), ALU.mult).then_inc(gated, 1)
            flip.vector(dve, at.QT)
            flip.vector(dve, at.KT)
            at.attend_vector(dve, None)
            flip.vector(dve, core.HT)
            at.output_vector(dve, bo)


def l3_feed_forward(core, load_next):
    nc, PS, norm, flip, dve_step = core.nc, core.PS, core.norm, core.flip, core.dve_step
    E = EXPERTS[11][0]
    w = core.arena(11)
    wg, bg, b2, number = w.take(C, E), w.take(E), w.take(D), w.take(E)
    with ExitStack() as es:
        ex = SortedExperts(core, es, "l3f", 11, "gelu", 2)
        bias = OutputBias(core, es, "l3f", E)
        sb = lambda n, shape: core.sb("l3f_" + n, shape, es)
        logits, gate = sb("logits", [P, NT, E]), sb("gate", [P, NT, E])
        first, second, chosen = sb("first", [P, NT, E]), sb("second", [P, NT, E]), sb("chosen", [P, NT, E])
        best, next_best, place, odds = sb("best", [P, NT]), sb("next_best", [P, NT]), sb("place", [P, NT]), sb("odds", [P, NT])
        rows_done, routed, chosen_done = core.sem("l3f_rows_done"), core.sem("l3f_routed"), core.sem("l3f_chosen_done")
        gap_done, odds_done, weighed = core.sem("l3f_gap_done"), core.sem("l3f_odds_done"), core.sem("l3f_weighed")
        block = es.enter_context(nc.Block())

        @block.sync
        def _(sp):
            load_next(sp)
            ex.load(sp)

        @block.gpsimd
        def _(pool):
            ex.scatter(pool, core.H, rows_done, 0)

        @block.tensor
        def _(pe):
            pe.wait_ge(core.consts_in, 16)
            pe.wait_ge(core.weights_in[11], 16)
            flip.tensor(pe, core.H, rows_done, 0)
            flip.ready(pe, "pe")
            router_tensor(core, pe, core.HT, wg, routed)
            ex.places.tensor(pe, chosen, chosen_done)
            bias.tensor(pe, gate, weighed, b2)
            ex.tensor(pe, core.HT)

        @block.scalar
        def _(act):
            norm.begin(act)
            norm.scalar(act, core.eps5)
            flip.scalar(act, core.HT)
            act.wait_ge(gap_done, 1)
            nc.scalar.activation(odds[:], odds[:], ACT.Exp).then_inc(odds_done, 1)
            ex.scalar(act)

        @block.vector
        def _(dve):
            nc.vector.memset(ex.places.ones[:], 1.0)
            dve.wait_ge(core.x_in, 16)
            norm.vector(dve, core.X, core.H, rows_done)
            flip.vector(dve, core.HT)
            dve.wait_ge(core.weights_in[11], 16)
            dve.wait_ge(routed, 1)
            dve_step(dve, nc.vector.tensor_tensor(logits[:], PS[:, 4, 0:NT * E].rearrange("p (t e) -> p t e", e=E), bcast(bg, 1, NT), ALU.add))
            first_best(core, dve, logits, number, best, place, first)
            dve_step(dve, nc.vector.scalar_tensor_tensor(logits[:], first[:], NEG, logits[:], ALU.mult, ALU.add))
            first_best(core, dve, logits, number, next_best, place, second)
            nc.vector.tensor_tensor(odds[:], next_best[:], best[:], ALU.subtract).then_inc(gap_done, 1)
            nc.vector.tensor_tensor(chosen[:], first[:], second[:], ALU.add).then_inc(chosen_done, 1)
            ex.places.vector(dve, (first, second))
            dve.wait_ge(odds_done, 1)
            dve_step(dve, nc.vector.tensor_scalar(best[:], odds[:], 1.0, None, ALU.add))
            dve_step(dve, nc.vector.reciprocal(best[:], best[:]))
            dve_step(dve, nc.vector.tensor_tensor(odds[:], odds[:], best[:], ALU.mult))
            nc.vector.tensor_tensor(gate[:], first[:], bcast(best[:], 2, E), ALU.mult)
            dve_step(dve, nc.vector.tensor_tensor(second[:], second[:], bcast(odds[:], 2, E), ALU.mult))
            nc.vector.tensor_tensor(gate[:], gate[:], second[:], ALU.add).then_inc(weighed, 1)
            dve.wait_ge(weighed, 1)
            bias.vector(dve)
            ex.vector(dve, (best, odds))


SUBLAYERS = [l0_cross, l0_self, l0_feed_forward, l1_cross, l1_self, l1_feed_forward, l2_cross, l2_self, l2_feed_forward, l3_cross, l3_self, l3_feed_forward]


def begin(core, load_first):
    nc = core.nc
    with nc.Block(no_gpsimd_drain=True) as block:
        @block.sync
        def _(sp):
            sp.dma_start(core.X[:], core.dram["x"].rearrange("(t p) d -> p t d", p=P)).then_inc(core.x_in, 16)
            sp.dma_start(core.consts[:], core.dram["consts"]).then_inc(core.consts_in, 16)
            load_first(sp)

        @block.vector
        def _(dve):
            nc.vector.memset(core.eps[:, 0:1], 1e-5)
            nc.vector.memset(core.eps[:, 1:2], 1e-6).then_inc(core.eps_set, 1)


def finish(core):
    nc = core.nc
    stored = core.sem("stored")
    with nc.Block(no_gpsimd_drain=True) as block:
        @block.sync
        def _(sp):
            sp.dma_start(core.dram["out"].rearrange("(t p) d -> p t d", p=P), core.X[:]).then_inc(stored, 16)
            sp.wait_ge(stored, 16)


def program(nc, dram):
    with ExitStack() as es:
        core = Core(nc, es, dram)
        loads = [lambda sp, k=k: load_weights(core, sp, k) for k in LAYERS] + [lambda sp: None]
        begin(core, loads[0])
        for n, k in enumerate(LAYERS):
            SUBLAYERS[k](core, loads[n + 1])
            core.free_sems()
        finish(core)


def by_chunk(w):
    return w.reshape(-1, P, w.shape[1]).transpose(1, 0, 2).reshape(P, -1)


def to_all(v):
    return np.broadcast_to(np.asarray(v).reshape(1, -1), (P, np.asarray(v).size))


def column(v):
    return np.asarray(v).reshape(-1, P).T


def packed(parts):
    return np.ascontiguousarray(np.concatenate([np.asarray(p, np.float32) for p in parts], axis=1))


def constants():
    p = np.arange(P)
    angle = (np.arange(S, dtype=np.float32)[:, None] * (10000.0 ** (-2.0 * np.arange(8, dtype=np.float32) / 16)).astype(np.float32)).astype(np.float32)
    return {
        "cos": np.tile(np.cos(angle), (TB, 1)), "sin": np.tile(np.sin(angle), (TB, 1)),
        "causal": np.tile(np.where(np.tri(S, dtype=bool), 0.0, NEG), (TB, 1)),
        "consts": packed([np.eye(P), p[:, None] < p[None], to_all(np.tri(NT, k=-1)), to_all(P * np.arange(24)), p[:, None]]),
        "head_of": (p[:, None] // 16 == np.arange(8)).astype(np.float32),
        "same_head": (p[:, None] // 16 == p // 16).astype(np.float32),
        "order": np.eye(P)[p // 2 % TB * S + p // (2 * TB) * 2 + p % 2],
    }


def layout(a):
    k = constants()
    ctx = a["ctx_1024"]
    ctx_by_feature = ctx.transpose(0, 2, 1).reshape(B, C, P, CTX).transpose(0, 2, 1, 3)
    mask = a["mask_BxS2_ff1"]
    out = {"x": a["x"].reshape(B * S, D), "consts": k["consts"], "ctxT": ctx_by_feature}
    left_col = np.zeros((P, 1), np.float32)
    left_col[0:B, 0] = mask[:, CTX - 1]
    out["pack0"] = packed([
        by_chunk(a["L0_xattn_wq"]),
        by_chunk(np.concatenate([a["L0_xattn_wk"], a["L0_xattn_wv"]], axis=1)),
        by_chunk(a["L0_xattn_dense_w"]), to_all(a["L0_xattn_ln_gamma"]), to_all(a["L0_xattn_ln_beta"]),
        to_all(a["L0_xattn_dense_b"]), k["head_of"], k["same_head"],
        mask[:, 0:2 * P].reshape(B, 2, P).transpose(2, 0, 1).reshape(P, -1), left_col,
        ctx[:, CTX - 1, :].T.reshape(C, P, B).transpose(1, 0, 2).reshape(P, -1), k["order"],
    ])
    first_of = lambda n: to_all(np.arange(n, dtype=np.float32) - n)
    rows = lambda m: np.concatenate([m, np.zeros((P - m.shape[0], m.shape[1]), np.float32)])
    out["pack1"] = packed([
        by_chunk(np.concatenate([a["L0_attn_W_Q"].T, a["L0_attn_W_K"].T], axis=1)),
        by_chunk(a["L0_attn_W_V"].T), by_chunk(a["L0_attn_W_O"].T),
        k["cos"], k["sin"], k["causal"], k["head_of"],
    ])
    out["pack2"] = packed([by_chunk(a["L0_ffn_centroids"].T), column(a["L0_ffn_scale"]), first_of(8)])
    out["experts2_up"], out["experts2_down"] = (np.stack([by_chunk(w) for w in a[f"L0_ffn_{n}_w"]]) for n in ("up", "down"))
    wkv = a["L1_xattn_Wkv"]
    out["ctx"] = ctx
    out["pack3"] = packed([
        by_chunk(a["L1_xattn_Wq"]), by_chunk(np.concatenate([wkv[:, 0:64], wkv[:, 0:64], wkv[:, 64:128]], axis=1)), by_chunk(a["L1_xattn_Wo"]),
        by_chunk(a["L1_xattn_Wff1"]), by_chunk(a["L1_xattn_Wff2"]), *(column(a[f"L1_xattn_{n}"]) for n in ("ln_g", "ln_b", "cln_g", "cln_b")),
        (np.arange(P)[:, None] // 64 == np.arange(2)[None]).astype(np.float32),
    ])
    w_attn = a["L1_attn_W_attn"].T
    out["pack4"] = packed([
        by_chunk(w_attn[:, 0:1024]), by_chunk(w_attn[:, 1024:1280]), by_chunk(w_attn[:, 1280:1536]), by_chunk(a["L1_attn_W_proj"].T),
        k["causal"], k["head_of"],
    ])
    split = lambda m: np.concatenate([m[..., 0::2], m[..., 1::2]], axis=-1)
    with_shared = lambda n: np.concatenate([a[f"L1_ffn_{n}"], a[f"L1_ffn_s{n}"][None]])
    out["pack5"] = packed([by_chunk(a["L1_ffn_gate_w"].T), to_all(a["L1_ffn_gate_b"]), rows(with_shared("b2")), first_of(8)])
    out["experts5_up"], out["experts5_down"] = (np.stack(part) for part in zip(*(
        (packed([by_chunk(split(w1)), by_chunk(split(w3)), column(split(b1)), column(split(b3))]), packed([by_chunk(w2)]))
        for w1, w3, w2, b1, b3 in zip(*map(with_shared, ("w1", "w3", "w2", "b1", "b3"))))))
    out["pack6"] = packed([
        *(by_chunk(a[f"L2_xattn_{n}"]) for n in ("Wq", "Wk", "Wv", "Wo")), column(a["L2_xattn_bq"]), column(a["L2_xattn_bk"]),
        to_all(a["L2_xattn_bv"]), to_all(a["L2_xattn_bo"]), k["head_of"],
        (np.arange(P)[:, None] % 64 // 16 == np.arange(4)[None]).astype(np.float32),
        ctx[:, CTX - 1, :].T.reshape(C, P, B).transpose(1, 0, 2).reshape(P, -1),
    ])
    four = lambda v: np.repeat(np.asarray(v).reshape(D, 4, 16), 4, axis=1).reshape(D, D)
    out["pack7"] = packed([
        by_chunk(np.concatenate([a["L2_attn_w_q"], four(a["L2_attn_w_k"])], axis=1)),
        by_chunk(four(a["L2_attn_w_v"])), by_chunk(a["L2_attn_w_o"]),
        k["cos"], k["sin"], k["causal"], k["head_of"],
    ])
    out["pack8"] = packed([by_chunk(a["L2_ffn_expert_w"].transpose(2, 0, 1).reshape(D, -1)), by_chunk(a["L2_ffn_gate_w"].T), first_of(8)])
    wk, wv = a["L3_xattn_Wkv"][:, 0:512], a["L3_xattn_Wkv"][:, 512:1024]
    affine = [a[f"L3_xattn_{n}"] for n in ("gm", "bm", "gl", "bl")]
    out["pack9"] = packed([
        by_chunk(a["L3_xattn_Wq"]), by_chunk(wk.T), by_chunk(wv), by_chunk(a["L3_xattn_Wout"]),
        *(column(v) for v in affine), *(to_all(v) for v in affine),
    ])
    out["pack10"] = packed([
        by_chunk(np.concatenate([a["L3_attn_Wq"], a["L3_attn_Wk"]], axis=1)),
        by_chunk(a["L3_attn_Wv"]), by_chunk(a["L3_attn_Wo"]), to_all(a["L3_attn_gq"]), to_all(a["L3_attn_gk"]),
        to_all(a["L3_attn_bo"]), column(a["L3_attn_ln_w"]), column(a["L3_attn_ln_b"]), k["head_of"],
    ])
    out["pack11"] = packed([by_chunk(a["L3_ffn_Wg"]), to_all(a["L3_ffn_bg"]), rows(a["L3_ffn_b2"]), first_of(6)])
    out["experts11_up"] = np.stack([packed([by_chunk(w), column(b)]) for w, b in zip(a["L3_ffn_W1"], a["L3_ffn_b1"])])
    out["experts11_down"] = np.stack([by_chunk(w) for w in a["L3_ffn_W2"]])
    return {n: np.ascontiguousarray(v) for n, v in out.items()}


def kernel(**inputs):
    import concourse.bacc as bacc
    from concourse.bass_utils import run_bass_kernel_spmd

    arrays = layout({n: np.asarray(v) for n, v in inputs.items()})
    nc = bacc.Bacc("TRN2", target_bir_lowering=False, num_devices=1)
    dram = {n: nc.dram_tensor(f"in_{n}_dram", v.shape, F32, kind="ExternalInput").ap() for n, v in arrays.items()}
    dram["out"] = nc.dram_tensor("out_0_dram", (B * S, D), F32, kind="ExternalOutput").ap()
    program(nc, dram)
    got = run_bass_kernel_spmd(nc, [{f"in_{n}_dram": v for n, v in arrays.items()}], core_ids=[0])
    return got.results[0]["out_0_dram"].reshape(B, S, D)
```

```python
from contextlib import ExitStack

import concourse.bass as bass
import numpy as np
from concourse import mybir

F32 = mybir.dt.float32
ALU = mybir.AluOpType
ACT = mybir.ActivationFunctionType
AX = mybir.AxisListType

P = 128
B, S, D = 32, 32, 256
CTX = 257
NT = B * S // P
C = D // P
TB = P // S
NEG = -1e30
LAYERS = range(12)
EXPERTS = {2: (8, 3072), 5: (9, 5136), 11: (6, 2052)}
SHARED = 5


class Core:

    def __init__(self, nc, es, dram):
        self.nc, self.es, self.dram = nc, es, dram
        self.sems = []
        self.X = self.sb("X", [P, NT, D])
        self.H = self.sb("H", [P, NT, D])
        self.HT = self.sb("HT", [P, C, NT * P])
        self.weights = [self.sb("weights0", [P, 6424]), self.sb("weights1", [P, 10640])]
        self.consts = self.sb("consts", [P, 2 * P + NT * NT + 25])
        self.ident, self.lower = self.consts[:, 0:P], self.consts[:, P:2 * P]
        self.before = self.consts[:, 2 * P:2 * P + NT * NT].rearrange("p (a b) -> p a b", b=NT)
        self.numbers = self.consts[:, 2 * P + NT * NT:2 * P + NT * NT + 24]
        self.partition = self.consts[:, 2 * P + NT * NT + 24:2 * P + NT * NT + 25]
        self.eps = self.sb("eps", [P, 3])
        self.dve_step = Steps(self, "dve_step")
        self.act_step = Steps(self, "act_step")
        self.pool_step = Steps(self, "pool_step")
        self.stats = self.sb("stats", [P, NT, 6])
        self.moments = self.sb("moments", [P, NT, 2])
        self.std = self.sb("std", [P, NT])
        self.rstd = self.sb("rstd", [P, NT])
        self.warm = self.sb("warm", [P, 1])
        self.PS = es.enter_context(nc.psum_tensor("PS", [P, 8, 512], F32))
        self.consts_in = self.sem("consts_in")
        self.eps_set = self.sem("eps_set")
        self.weights_in = [self.sem(f"weights_in{i}") for i in range(12)]
        self.eps5, self.eps10, self.eps6 = (self.eps[:, i:i + 1] for i in range(3))
        self.x_in = self.sem("x_in")
        self.shared_in = self.sem("shared_in")
        self.norm = Norm(self)
        self.flip = Flip(self)
        self.ctx_norm = ContextNorm(self)
        self.sems = []

    def sb(self, name, shape, es=None):
        return (es or self.es).enter_context(self.nc.sbuf_tensor(name, shape, F32))

    def sem(self, name):
        self.sems.append(self.nc.alloc_semaphore(name=name))
        return self.sems[-1]

    def free_sems(self):
        self.nc.clear_and_free_semaphores(self.sems)
        self.sems = []
        self.nc.all_engine_barrier()

    def arena(self, layer):
        return Arena(self, layer)


class Arena:

    def __init__(self, core, layer):
        self.mem, self.at = core.weights[layer % 2], 2 * EXPERTS[layer][1] if layer in EXPERTS else 0

    def take(self, *shape):
        n = 1
        for s in shape:
            n *= s
        out = self.mem[:, self.at:self.at + n]
        self.at += n
        assert self.at <= self.mem.shape[1], self.at
        if len(shape) == 2:
            out = out.rearrange("p (a b) -> p a b", b=shape[1])
        elif len(shape) == 3:
            out = out.rearrange("p (a b c) -> p a b c", b=shape[1], c=shape[2])
        return out


def load_weights(core, sp, layer):
    w, mem = core.dram[f"pack{layer}"], core.weights[layer % 2]
    at = 0
    if layer in EXPERTS:
        n, width = EXPERTS[layer]
        at = 2 * width
    sp.dma_start(mem[:, at:at + w.shape[1]], w).then_inc(core.weights_in[layer], 16)
    if layer == SHARED:
        for part, columns in (("up", slice(0, width - 4 * D)), ("down", slice(width - 4 * D, width))):
            sp.dma_start(mem[:, columns], core.dram[f"experts{layer}_{part}"][n - 1]).then_inc(core.shared_in, 16)


class Steps:

    def __init__(self, core, name):
        self.sem, self.n, self.i = core.sem(name), 0, None

    def enter(self, i, per):
        self.i, self.per, self.k = i, per, 0

    def leave(self, trips):
        assert self.k == self.per, (self.k, self.per)
        self.n, self.i = self.n + trips * self.per, None

    def __call__(self, eng, instruction):
        instruction.then_inc(self.sem, 1)
        if self.i is None:
            self.n += 1
            eng.wait_ge(self.sem, self.n)
        else:
            self.k += 1
            eng.wait_ge(self.sem, self.i * self.per + (self.n + self.k))


class Norm:

    def __init__(self, core):
        self.core = core
        self.moments_done = core.sem("norm_moments_done")
        self.std_done = core.sem("norm_std_done")
        self.uses_dve = self.uses_act = 0
        self.taken = False

    def vector(self, dve, src, dst, rows_done):
        c, nc = self.core, self.core.nc
        if src is c.X and self.taken:
            dve.sem_inc(self.moments_done, 1)
            self.deviations(dve)
            self.taken = False
        else:
            for t in range(NT):
                done = nc.vector.bn_stats(c.stats[:, t, :], src[:, t, :])
            c.dve_step(dve, done)
            self.statistics(dve)
        self.rows(dve, src, dst, rows_done)

    def rows(self, dve, src, dst, rows_done):
        c, nc = self.core, self.core.nc
        for t in range(NT):
            nc.vector.tensor_scalar(dst[:, t, :], src[:, t, :], c.moments[:, t, 0:1], c.rstd[:, t:t + 1],
                                    ALU.subtract, ALU.mult).then_inc(rows_done, 1)

    def statistics(self, dve):
        c, nc = self.core, self.core.nc
        for t in range(NT):
            done = nc.vector.bn_aggr(c.moments[:, t, :], c.stats[:, t, :])
        done.then_inc(self.moments_done, 1)
        self.deviations(dve)

    def take(self, dve, written, tiles):
        c, nc = self.core, self.core.nc
        if written is not None:
            c.dve_step(dve, written)
        for t in tiles:
            done = nc.vector.bn_stats(c.stats[:, t, :], c.X[:, t, :])
        c.dve_step(dve, done)
        for t in tiles:
            nc.vector.bn_aggr(c.moments[:, t, :], c.stats[:, t, :])
        self.taken = True

    def deviations(self, dve):
        c, nc = self.core, self.core.nc
        self.uses_dve += 1
        dve.wait_ge(self.std_done, self.uses_dve)
        c.dve_step(dve, nc.vector.reciprocal(c.rstd[:], c.std[:]))

    def load_table(self, act):
        act.wait_ge(self.core.eps_set, 1)
        self.core.nc.scalar.activation(self.core.warm[:], self.core.eps5, ACT.Sqrt)

    def scalar_twice(self, act):
        self.scalar(act, self.core.eps10, 1 + 1e-5)

    def vector_again(self, dve, src, dst, rows_done):
        dve.sem_inc(self.moments_done, 1)
        self.deviations(dve)
        self.rows(dve, src, dst, rows_done)

    def scalar(self, act, eps, scale=1.0):
        c, nc = self.core, self.core.nc
        self.uses_act += 1
        act.wait_ge(self.moments_done, self.uses_act)
        nc.scalar.activation(c.std[:], c.moments[:, :, 1], ACT.Sqrt, bias=eps, scale=scale).then_inc(self.std_done, 1)


class Flip:

    def __init__(self, core):
        self.core = core
        self.flipped = core.sem("flipped")
        self.copied_act = core.sem("flip_copied_act")
        self.copied_dve = core.sem("flip_copied_dve")
        self.uses = {"pe": 0, "act": 0, "dve": 0}

    def tensor(self, pe, src, rows_done, before, order=None):
        c, nc = self.core, self.core.nc
        if self.uses["pe"]:
            self.ready(pe, "pe")
        self.uses["pe"] += 1
        for half in range(2):
            for ch in range(C):
                for t in range(4 * half, 4 * half + 4):
                    pe.wait_ge(rows_done, before + t + 1)
                    to, rows = c.PS[:, 2 * half + ch, (t % 4) * P:(t % 4 + 1) * P], src[:, t, ch * P:(ch + 1) * P]
                    if order is None:
                        last = nc.tensor.transpose(to, rows, c.ident[:])
                    else:
                        last = nc.tensor.matmul(to, rows, order, start=True, stop=True)
                last.then_inc(self.flipped, 1)

    def scalar(self, act, dst, scale=None, bias=None):
        c, nc, n = self.core, self.core.nc, self.uses["act"]
        self.uses["act"] += 1
        for half in range(2):
            act.wait_ge(self.flipped, 4 * n + 2 * half + 1)
            bank, to = c.PS[:, 2 * half, :], dst[:, 0, half * 512:(half + 1) * 512]
            if scale is None:
                last = nc.scalar.copy(to, bank)
            elif bias is None:
                last = nc.scalar.activation(to, bank, ACT.Copy, scale=scale[:, 0:1])
            else:
                last = nc.scalar.activation(to, bank, ACT.Identity, bias=bias[:, 0:1], scale=scale[:, 0:1])
            last.then_inc(self.copied_act, 1)

    def vector(self, dve, dst, scale=None, bias=None):
        c, nc, n = self.core, self.core.nc, self.uses["dve"]
        self.uses["dve"] += 1
        for half in range(2):
            dve.wait_ge(self.flipped, 4 * n + 2 * half + 2)
            bank, to = c.PS[:, 2 * half + 1, :], dst[:, 1, half * 512:(half + 1) * 512]
            if scale is None:
                last = nc.vector.tensor_copy(to, bank)
            elif bias is None:
                last = nc.vector.tensor_scalar(to, bank, scale[:, 1:2], None, ALU.mult)
            else:
                last = nc.vector.tensor_scalar(to, bank, scale[:, 1:2], bias[:, 1:2], ALU.mult, ALU.add)
            last.then_inc(self.copied_dve, 1)

    def ready(self, eng, key):
        eng.wait_ge(self.copied_act, 2 * self.uses[key])
        eng.wait_ge(self.copied_dve, 2 * self.uses[key])


def bcast(ap, axis, n):
    shape = list(ap.shape)
    shape.insert(axis, n)
    return ap.unsqueeze(axis).to_broadcast(shape)


class SelfAttention:

    def __init__(self, core, es, name, kind, scale):
        self.core, self.name, self.kind, self.scale = core, name, kind, scale
        sb = lambda n, shape: core.sb(f"{name}_{n}", shape, es)
        sem = lambda n: core.sem(f"{name}_{n}")
        self.QK, self.V = sb("QK", [P, NT, 2 * D]), sb("V", [P, NT, 8, 2, 2, 16])
        self.Q, self.K = self.QK[:, :, 0:D], self.QK[:, :, D:2 * D]
        self.QT, self.KT = (sb(n, [P, C, NT * P]) for n in ("QT", "KT"))
        self.spread = [sb(f"spread{i}", [P, C, TB, 8, S]) for i in range(2)]
        self.scores = [sb(f"scores{i}", [P, 16, S]) for i in range(2)]
        self.probs = [sb(f"probs{i}", [P, 16, S]) for i in range(2)]
        self.probsT = [sb(f"probsT{i}", [P, 16, S]) for i in range(2)]
        self.blocks = [sb(f"blocks{i}", [P, 16, TB, S]) for i in range(2)]
        self.top = [sb(f"top{i}", [P, 16]) for i in range(2)]
        self.factor = sb("factor", [P, NT, 16])
        self.qk_done, self.v_done = sem("qk_done"), sem("v_done")
        self.qk_copied, self.v_copied = sem("qk_copied"), sem("v_copied")
        self.summed, self.rooted, self.qk_rows = sem("summed"), sem("rooted"), sem("qk_rows")
        self.spread_done, self.scores_done = sem("spread_done"), sem("scores_done")
        self.scores_read = sem("scores_read")
        self.shifted, self.probs_done = sem("shifted"), sem("probs_done")
        self.weighed, self.probsT_done, self.blocks_done = sem("weighed"), sem("probsT_done"), sem("blocks_done")
        self.out_done, self.out_copied, self.proj_done = sem("out_done"), sem("out_copied"), sem("proj_done")
        self.zeros_set = sem("zeros_set")


    def project(self, pe, xT, xT_v, wqk, wv):
        nc, PS = self.core.nc, self.core.PS
        for t in range(NT):
            if t >= 2:
                pe.wait_ge(self.qk_copied, t - 1)
            for c in range(C):
                last = nc.tensor.matmul(PS[:, 4 + t % 2, :], xT[:, c, t * P:(t + 1) * P], wqk[:, c, :], start=(c == 0), stop=(c == 1))
            last.then_inc(self.qk_done, 1)
            if t >= 2:
                pe.wait_ge(self.v_copied, t - 1)
            for c in range(C):
                last = nc.tensor.matmul(PS[:, 6 + t % 2, 0:D], xT_v[:, c, t * P:(t + 1) * P], wv[:, c, :], start=(c == 0), stop=(c == 1))
            last.then_inc(self.v_done, 1)

    def copy_projections(self, act, squares=None, size=None, **root):
        nc, PS = self.core.nc, self.core.PS

        def roots(t):
            act.wait_ge(self.summed, t + 1)
            nc.scalar.activation(size[:, t, :], size[:, t, :], ACT.Sqrt, **root).then_inc(self.rooted, 1)

        for t in range(NT):
            act.wait_ge(self.qk_done, t + 1)
            bank = PS[:, 4 + t % 2, :]
            done = nc.scalar.copy(self.QK[:, t, :], bank)
            if squares is not None:
                if t >= 2:
                    act.wait_ge(self.summed, t - 1)
                done = nc.scalar.activation(squares[t % 2][:], bank, ACT.Square)
            done.then_inc(self.qk_copied, 1)
            act.wait_ge(self.v_done, t + 1)
            if t == 0:
                act.wait_ge(self.zeros_set, 1)
            for side in range(2):
                done = nc.scalar.copy(self.values(t, side), PS[:, 6 + t % 2, 0:D].rearrange("p (h two d) -> p h two d", two=2, d=16)[:, :, side, :])
            done.then_inc(self.v_copied, 1)
            if squares is not None and t >= 1:
                roots(t - 1)
        if squares is not None:
            roots(NT - 1)

    def values(self, t, side):
        return self.V[:, t, :, side, side, :]

    def set_zeros(self, pool):
        self.core.nc.gpsimd.memset(self.V[:], 0.0).then_inc(self.zeros_set, 1)

    def sum_squares(self, dve, t, squares, size):
        dve.wait_ge(self.qk_copied, t + 1)
        self.core.nc.vector.reduce_sum(size[:, t, :], squares[t % 2][:].rearrange("p (h d) -> p h d", d=16), AX.X).then_inc(self.summed, 1)

    def flip_tensor(self, pe):
        self.core.flip.tensor(pe, self.Q, self.qk_rows, 0)
        self.core.flip.tensor(pe, self.K, self.qk_rows, 0)


    def spread_keys(self, pool, head_of):
        nc = self.core.nc
        for t in range(NT):
            if t >= 2:
                pool.wait_ge(self.scores_done, t - 1)
            for c in range(C):
                last = nc.gpsimd.tensor_tensor(self.spread[t % 2][:, c],
                                               bcast(self.KT[:, c, t * P:(t + 1) * P].rearrange("p (b k) -> p b k", k=S), 2, 8),
                                               bcast(bcast(head_of, 1, TB), 3, S), ALU.mult)
            last.then_inc(self.spread_done, 1)

    def attend_tensor(self, pe, wo):
        nc, PS, HT = self.core.nc, self.core.PS, self.core.HT
        for t in range(NT + 5):
            if t < NT:
                pe.wait_ge(self.spread_done, t + 1)
                if t >= 2:
                    pe.wait_ge(self.scores_read, t - 1)
                for c in range(C):
                    for b in range(TB):
                        last = nc.tensor.matmul(PS[b * S:(b + 1) * S, 4 + t % 2, c * 256:(c + 1) * 256],
                                                self.QT[:, c, t * P + b * S:t * P + (b + 1) * S],
                                                self.spread[t % 2][:, c, b].rearrange("p h k -> p (h k)"), start=True, stop=True)
                last.then_inc(self.scores_done, 1)
            if 0 <= t - 3 < NT:
                u = t - 3
                pe.wait_ge(self.blocks_done, u + 1)
                if u >= 2:
                    pe.wait_ge(self.out_copied, u - 1)
                for c in range(C):
                    for side in range(2):
                        for block_at in range(4):
                            h = 8 * c + 2 * block_at + side
                            last = nc.tensor.matmul(PS[block_at * 32:(block_at + 1) * 32, 6 + u % 2, c * P:(c + 1) * P],
                                                    self.V[:, u, h // 2, side].rearrange("p two d -> p (two d)"),
                                                    self.blocks[u % 2][:, h].rearrange("p b q -> p (b q)"),
                                                    start=(side == 0), stop=(side == 1))
                last.then_inc(self.out_done, 1)
            if t >= 5:
                u = t - 5
                pe.wait_ge(self.out_copied, u + 1)
                for c in range(C):
                    last = nc.tensor.matmul(PS[:, u // 2, (u % 2) * D:(u % 2 + 1) * D], HT[:, c, u * P:(u + 1) * P], wo[:, c, :],
                                            start=(c == 0), stop=(c == 1))
                last.then_inc(self.proj_done, 1)

    def attend_scalar(self, act, batch_of):
        nc, PS = self.core.nc, self.core.PS

        def spread_weights(u):
            act.wait_ge(self.probsT_done, u + 1)
            if u >= 2:
                act.wait_ge(self.out_done, u - 1)
            for b in range(TB):
                done = nc.scalar.activation(self.blocks[u % 2][:, :, b, :], self.probsT[u % 2][:], ACT.Copy, scale=batch_of[:, b:b + 1])
            done.then_inc(self.blocks_done, 1)

        def cap(t):
            act.wait_ge(self.scores_done, t + 1)
            if t >= 2:
                act.wait_ge(self.probs_done, t - 1)
            nc.scalar.activation(self.scores[t % 2][:], PS[:, 4 + t % 2, :].rearrange("p (h k) -> p h k", k=S), ACT.Tanh,
                                 scale=self.tanh_scale).then_inc(self.scores_read, 1)

        if self.kind == "capped":
            cap(0)
        for t in range(NT + 1):
            i = t % 2
            if t < NT:
                if self.kind == "resonance":
                    act.wait_ge(self.scores_done, t + 1)
                else:
                    act.wait_ge(self.shifted, t + 1)
                if t >= 2:
                    act.wait_ge(self.probsT_done, t - 1)
                if self.kind == "resonance":
                    nc.scalar.activation(self.probs[i][:], PS[:, 4 + i, :].rearrange("p (h k) -> p h k", k=S), ACT.Sigmoid,
                                         scale=self.scale, bias=self.resonance_bias).then_inc(self.scores_read, 1)
                else:
                    nc.scalar.activation(self.probs[i][:], self.scores[i][:], ACT.Exp, scale=self.scale).then_inc(self.probs_done, 1)
            if self.kind == "capped" and t + 1 < NT:
                cap(t + 1)
            if t >= 1:
                spread_weights(t - 1)

    def attend_vector(self, dve, causal):
        nc, PS, X, step = self.core.nc, self.core.PS, self.core.X, self.core.dve_step
        for t in range(NT + 6):
            if t < NT and self.kind != "resonance":
                s = self.scores[t % 2]
                if self.kind == "capped":
                    dve.wait_ge(self.scores_read, t + 1)
                    step(dve, nc.vector.tensor_tensor(s[:], s[:], bcast(causal, 1, 16), ALU.add))
                else:
                    dve.wait_ge(self.scores_done, t + 1)
                    if t >= 2:
                        dve.wait_ge(self.probs_done, t - 1)
                    last = nc.vector.tensor_tensor(s[:], PS[:, 4 + t % 2, :].rearrange("p (h k) -> p h k", k=S),
                                                   bcast(causal, 1, 16), ALU.add)
                    last.then_inc(self.scores_read, 1)
                    dve.wait_ge(self.scores_read, t + 1)
                step(dve, nc.vector.reduce_max(self.top[t % 2][:], s[:], AX.X))
                nc.vector.tensor_tensor(s[:], s[:], bcast(self.top[t % 2][:], 2, S), ALU.subtract).then_inc(self.shifted, 1)
            if 1 <= t <= NT:
                u = t - 1
                p = self.probs[u % 2]
                if self.kind == "resonance":
                    dve.wait_ge(self.scores_read, u + 1)
                else:
                    dve.wait_ge(self.probs_done, u + 1)
                    step(dve, nc.vector.reduce_sum(self.factor[:, u, :], p[:], AX.X))
                    step(dve, nc.vector.reciprocal(self.factor[:, u, :], self.factor[:, u, :]))
                nc.vector.tensor_tensor(p[:], p[:], bcast(self.factor[:, u, :], 2, S), ALU.mult).then_inc(self.weighed, 1)
                dve.wait_ge(self.weighed, u + 1)
                if u >= 2:
                    dve.wait_ge(self.blocks_done, u - 1)
                nc.vector.transpose(self.probsT[u % 2][:].rearrange("p h k -> p (h k)"),
                                    p[:].rearrange("p h k -> p (h k)")).then_inc(self.probsT_done, 1)
            if 0 <= t - 4 < NT:
                u = t - 4
                dve.wait_ge(self.out_done, u + 1)
                nc.vector.tensor_copy(self.core.HT[:, :, u * P:(u + 1) * P], PS[:, 6 + u % 2, 0:D].rearrange("p (c n) -> p c n", c=C)).then_inc(self.out_copied, 1)
            if t >= 7 and t % 2 == 1:
                j = (t - 7) // 2
                x = X[:, 2 * j:2 * j + 2, :]
                dve.wait_ge(self.proj_done, 2 * j + 2)
                written = nc.vector.tensor_tensor(x, PS[:, j, :].rearrange("p (t d) -> p t d", t=2), x, ALU.add)
                self.core.norm.take(dve, written, (2 * j, 2 * j + 1))


class Rotation:

    def __init__(self, core, es, at, pairs, cos, sin, rows_ready):
        self.core, self.at, self.pairs, self.rows_ready = core, at, pairs, rows_ready
        self.cos, self.sin = bcast(cos, 1, 32), bcast(sin, 1, 32)
        self.cosines, self.sines = ([core.sb(f"{at.name}_{n}{i}", [P, 2, 32, 8], es) for i in range(2)] for n in ("cosines", "sines"))
        self.cosines_done, self.sines_done = core.sem(f"{at.name}_cosines_done"), core.sem(f"{at.name}_sines_done")

    def products(self, engine, t, buffers, by):
        for k, half in enumerate(self.pairs(self.at.QK[:, t, :])):
            done = engine.tensor_tensor(buffers[t % 2][:, k], half, by, ALU.mult)
        return done

    def gpsimd(self, pool):
        for t in range(NT):
            pool.wait_ge(self.rows_ready, t + 1)
            if t >= 2:
                pool.wait_ge(self.at.qk_rows, t - 1)
            self.products(self.core.nc.gpsimd, t, self.sines, self.sin).then_inc(self.sines_done, 1)

    def cosine_products(self, dve, t):
        dve.wait_ge(self.rows_ready, t + 1)
        if t >= 2:
            dve.wait_ge(self.at.qk_rows, t - 1)
        self.products(self.core.nc.vector, t, self.cosines, self.cos).then_inc(self.cosines_done, 1)

    def combine(self, dve, t):
        nc, (first, second) = self.core.nc, self.pairs(self.at.QK[:, t, :])
        cosines, sines = self.cosines[t % 2], self.sines[t % 2]
        dve.wait_ge(self.cosines_done, t + 1)
        dve.wait_ge(self.sines_done, t + 1)
        nc.vector.tensor_tensor(first, cosines[:, 0], sines[:, 1], ALU.subtract)
        nc.vector.tensor_tensor(second, cosines[:, 1], sines[:, 0], ALU.add).then_inc(self.at.qk_rows, 1)


def at_least(eng, sem, value):
    if not isinstance(value, int) or value > 0:
        eng.wait_ge(sem, value)


class Places:

    def __init__(self, core, es, name, experts, choices):
        self.core, self.E, self.K, self.T = core, experts, choices, choices * NT + experts - 1
        E, T = self.E, self.T
        sb = lambda x, shape, dt=F32: es.enter_context(core.nc.sbuf_tensor(f"{name}_{x}", shape, dt))
        self.ones = sb("ones", [P, P])
        self.tile_counts, self.before = sb("tile_counts", [P, NT, E]), sb("before", [P, NT, E])
        self.pairs = sb("pairs", [P, NT, E, NT])
        self.count, self.tiles, self.start = sb("count", [P, E]), sb("tiles", [P, E]), sb("start", [P, E])
        self.places = sb("places", [P, NT, E])
        self.place, self.place_row = sb("place", [P, choices, NT]), sb("place_row", [P, choices, NT], mybir.dt.uint32)
        self.ended, self.expert = sb("ended", [P, T, E]), sb("expert", [P, T])
        self.weight_row = sb("weight_row", [P, T], mybir.dt.uint32)
        self.counted, self.done = core.sem(f"{name}_counted"), core.sem(f"{name}_placed")

    def tensor(self, pe, chosen, chosen_done):
        nc, PS, n = self.core.nc, self.core.PS, NT * self.E
        pe.wait_ge(chosen_done, 1)
        rows = chosen[:].rearrange("p t e -> p (t e)")
        nc.tensor.matmul(PS[:, 4, 0:n], self.core.lower, rows, start=True, stop=True)
        nc.tensor.matmul(PS[:, 4, n:2 * n], self.ones[:], rows, start=True, stop=True).then_inc(self.counted, 1)
        pe.wait_ge(self.done, 1)

    def vector(self, dve, choices):
        nc, PS, E, T = self.core.nc, self.core.PS, self.E, self.T
        step = lambda instruction: self.core.dve_step(dve, instruction)
        before_tile, before_expert = self.core.before[:, 0:NT, 0:NT], self.core.before[:, 0:E, 0:E]
        n = NT * E
        by_tile = lambda bank: bank.rearrange("p (t e) -> p t e", e=E)
        dve.wait_ge(self.counted, 1)
        step(nc.vector.tensor_copy(self.tile_counts[:], by_tile(PS[:, 4, n:2 * n])))
        counts = self.tile_counts[:].rearrange("p t e -> p e t")
        step(nc.vector.tensor_tensor(self.pairs[:], bcast(counts, 1, NT), bcast(before_tile, 2, E), ALU.mult))
        nc.vector.reduce_sum(self.before[:], self.pairs[:], AX.X)
        step(nc.vector.reduce_sum(self.count[:], counts, AX.X))
        over = self.pairs[:, 0, :, :]
        step(nc.vector.tensor_tensor(over, bcast(self.count[:], 2, NT), bcast(self.core.numbers[:, 0:NT], 1, E), ALU.is_gt))
        step(nc.vector.reduce_sum(self.tiles[:], over, AX.X))
        earlier = self.pairs[:, 1, :, 0:E]
        step(nc.vector.tensor_tensor(earlier, bcast(self.tiles[:], 1, E), before_expert, ALU.mult))
        step(nc.vector.reduce_sum(self.start[:], earlier, AX.X))
        nc.vector.tensor_tensor(self.places[:], self.before[:], by_tile(PS[:, 4, 0:n]), ALU.add)
        step(nc.vector.tensor_scalar(self.count[:], self.start[:], float(P), None, ALU.mult))
        step(nc.vector.tensor_tensor(self.places[:], self.places[:], bcast(self.count[:], 1, NT), ALU.add))
        for k in range(self.K):
            step(nc.vector.tensor_tensor(self.before[:], self.places[:], choices[k][:], ALU.mult))
            step(nc.vector.reduce_sum(self.place[:, k, :], self.before[:], AX.X))
        nc.vector.tensor_copy(self.place_row[:], self.place[:])
        step(nc.vector.tensor_tensor(self.tiles[:], self.tiles[:], self.start[:], ALU.add))
        step(nc.vector.tensor_scalar(self.tiles[:], self.tiles[:], float(P), None, ALU.mult))
        step(nc.vector.tensor_tensor(self.ended[:], bcast(self.tiles[:], 1, T), bcast(self.core.numbers[:, 0:T], 2, E), ALU.is_le))
        step(nc.vector.reduce_sum(self.expert[:], self.ended[:], AX.X))
        step(nc.vector.tensor_scalar(self.expert[:], self.expert[:], float(E - 1), float(P), ALU.min, ALU.mult))
        step(nc.vector.tensor_scalar(self.expert[:], self.expert[:], self.core.partition, None, ALU.add))
        nc.vector.tensor_copy(self.weight_row[:], self.expert[:]).then_inc(self.done, 1)
        dve.wait_ge(self.done, 1)


RING = 3


def before(q, j):
    return (q, j - 1) if j else (q - 1, RING - 1)


def after(q, j):
    return (q, j + 1) if j < RING - 1 else (q + 1, 0)


class SortedExperts:

    def __init__(self, core, es, name, layer, kind, choices, shared=False):
        self.core, self.name, self.kind, self.layer = core, name, kind, layer
        self.E, self.K, self.S = EXPERTS[layer][0] - shared, choices, NT * shared
        self.places = Places(core, es, name + "_sort", self.E, choices)
        self.T = self.places.T
        self.N = self.S + self.T
        self.begin = self.S + 1 if shared else RING
        self.trips = (self.N - RING - self.begin) // RING
        nc, T = core.nc, self.T
        sb = lambda x, shape: core.sb(f"{name}_{x}", shape, es)
        ring = lambda x, shape: [sb(f"{x}{i}", shape) for i in range(RING)]
        two = lambda x, shape: [sb(f"{x}{i}", shape) for i in range(2)]
        sem = lambda x: core.sem(f"{name}_{x}")
        self.units = 2 if kind == "swiglu" else 1
        self.hidden, self.side = ring("hidden", [P, 4, P]), ring("side", [P, 4, P])
        if kind == "swiglu":
            self.product, self.sigmoid = two("product", [P, 4, P]), sb("sigmoid", [P, 4, P])
            self.gated = sb("gated", [P, 4, P])
            self.gate_done, self.sigmoid_done = sem("gate_done"), sem("sigmoid_done")
        self.zeros, self.rows_in, self.xT, self.out = sb("zeros", [P, D]), ring("rows_in", [P, D]), ring("xT", [P, C, P]), ring("out", [P, D])
        self.gathered = sb("gathered", [P, NT, choices, D])
        self.sorted_dram = nc.dram_tensor(f"{name}_sorted_dram", (T * P, D), F32).ap()
        self.out_dram = nc.dram_tensor(f"{name}_out_dram", (T * P, D), F32).ap()
        self.zeros_set, self.zeroed, self.scattered = sem("zeros_set"), sem("zeroed"), sem("scattered")
        self.rows_loaded, self.stored, self.up_in, self.down_in = ([sem(f"{x}{j}") for j in range(RING)] for x in ("rows_loaded", "stored", "up_in", "down_in"))
        self.flipped, self.copied, self.up_done, self.side_done = sem("flipped"), sem("copied"), sem("up_done"), sem("side_done")
        self.hidden_done, self.down_done, self.out_copied = sem("hidden_done"), sem("down_done"), sem("out_copied")
        self.gather_done = [sem(f"gather_done{g}") for g in range(4)]
        width = EXPERTS[layer][1]
        slot = lambda i: core.weights[layer % 2][:, i * width:(i + 1) * width]
        self.slots = [sb("slot0", [P, width])[:], slot(1), sb("slot2", [P, width])[:] if shared else slot(0)]
        self.shared = self.views(slot(0)) if shared else None
        self.weights = [self.views(s) for s in self.slots]
        self.up_width = width - 4 * D

    def views(self, mem):
        out, at = {}, 0
        for key, shape in {"glu": [("up", (C, 1024))],
                           "swiglu": [("up1", (C, 1024)), ("up3", (C, 1024)), ("b1", (8,)), ("b3", (8,))],
                           "gelu": [("up", (C, 512)), ("b1", (4,))]}[self.kind] + [("down", (4, D))]:
            m = int(np.prod(shape))
            out[key] = mem[:, at:at + m]
            if len(shape) == 2:
                out[key] = out[key].rearrange("p (c n) -> p c n", c=shape[0])
            at += m
        assert at == mem.shape[1], (at, mem.shape)
        return out

    def over(self, eng, first, turn, last, steps=0):
        count = steps and eng is self.core.nc.vector

        def three(begin, trips, shared):
            with eng.Fori(0, trips) as i:
                if count:
                    self.core.dve_step.enter(i, RING * steps)
                for n in range(begin, begin + RING):
                    turn(i + n // RING, n % RING, shared)
                if count:
                    self.core.dve_step.leave(trips)

        first()
        if self.S:
            turn(0, 0, True)
            three(1, (self.S - 2) // RING, True)
            turn(*divmod(self.S - 1, RING), True)
        for n in range(self.S, self.begin):
            turn(*divmod(n, RING), False)
        three(self.begin, self.trips, False)
        for n in range(self.begin + RING * self.trips, self.N):
            turn(*divmod(n, RING), False)
        last()

    def nth(self, q, j):
        return q + (1 - (self.S - j + RING - 1) // RING)

    def sorted_next(self, n, shared):
        return (not isinstance(n, int) or n + 1 < self.N) and (not shared or (isinstance(n, int) and n == self.S - 1))


    def load(self, sp):
        S, of = self.S, lambda t: t.rearrange("(i p) d -> p i d", p=P)
        sp.wait_ge(self.zeros_set, 1)
        sp.dma_start(of(self.sorted_dram), bcast(self.zeros[:], 1, self.T)).then_inc(self.zeroed, 16)

        def load_rows(q, j):
            n = RING * q + j
            at_least(sp, self.flipped, n - (S + RING - 1))
            sp.dma_start(self.rows_in[j][:], self.sorted_dram[bass.ds((n - S) * P, P), :]).then_inc(self.rows_loaded[j], 16)

        def store(q, j):
            n = RING * q + j
            sp.wait_ge(self.out_copied, n + 1)
            sp.dma_start(self.out_dram[bass.ds((n - S) * P, P), :], self.out[j][:]).then_inc(self.stored[j], 16)

        def turn(q, j):
            if not isinstance(q, int) or RING * (q + 1) + j < self.N:
                load_rows(q + 1, j)
            if not isinstance(q, int) or RING * q + j > S:
                store(*before(q, j))

        sp.wait_ge(self.scattered, 16 * NT * self.K)
        for n in range(S, S + RING):
            load_rows(*divmod(n, RING))
        for n in range(S, self.begin):
            turn(*divmod(n, RING))
        with sp.Fori(0, self.trips) as i:
            for n in range(self.begin, self.begin + RING):
                turn(i + n // RING, n % RING)
        for n in range(self.begin + RING * self.trips, self.N):
            turn(*divmod(n, RING))
        store(*divmod(self.N - 1, RING))


    def scatter(self, pool, rows, rows_done, rows_before):
        nc, S, T, K, dram = self.core.nc, self.S, self.T, self.K, self.core.dram
        at = bass.IndirectOffsetOnAxis
        up_dram, down_dram = (dram[f"experts{self.layer}_{x}"].rearrange("e p n -> (e p) n") for x in ("up", "down"))
        nc.gpsimd.memset(self.zeros[:], 0.0).then_inc(self.zeros_set, 1)
        pool.wait_ge(self.places.done, 1)

        def load(i):
            j, row = (S + i) % RING, at(ap=self.places.weight_row[:, i:i + 1], axis=0)
            for part, loaded, read, columns in ((up_dram, self.up_in, self.hidden_done, slice(0, self.up_width)),
                                                (down_dram, self.down_in, self.down_done, slice(self.up_width, None))):
                if i >= RING:
                    pool.wait_ge(read, S + i - RING + 1)
                nc.gpsimd.indirect_dma_start(self.slots[j][:, columns], None, part, row).then_inc(loaded[j], 16)

        load(0)
        pool.wait_ge(rows_done, rows_before + NT)
        pool.wait_ge(self.zeroed, 16)
        for t in range(NT):
            for k in range(K):
                nc.gpsimd.indirect_dma_start(self.sorted_dram, at(ap=self.places.place_row[:, k, t:t + 1], axis=0), rows[:, t, :], None).then_inc(self.scattered, 16)
        for i in range(1, T):
            load(i)
        for n in range(self.N - RING, self.N):
            pool.wait_ge(self.stored[n % RING], 16 * self.nth(*divmod(n, RING)))
        for t in range(NT):
            for k in range(K):
                nc.gpsimd.indirect_dma_start(self.gathered[:, t, k, :], None, self.out_dram, at(ap=self.places.place_row[:, k, t:t + 1], axis=0)).then_inc(self.gather_done[t // 2], 16)


    def tensor(self, pe, xT, between=lambda: None):
        nc, PS, S, U = self.core.nc, self.core.PS, self.S, self.units

        def flip_rows(q, j):
            n = RING * q + j
            at_least(pe, self.copied, n - S)
            pe.wait_ge(self.rows_loaded[j], 16 * self.nth(q, j))
            for c in range(C):
                done = nc.tensor.transpose(PS[:, 6, c * P:(c + 1) * P], self.rows_in[j][:, c * P:(c + 1) * P], self.core.ident[:])
            done.then_inc(self.flipped, 1)

        def up(q, j, shared):
            n = RING * q + j
            w = self.shared if shared else self.weights[j]
            if not shared:
                pe.wait_ge(self.up_in[j], 16 * self.nth(q, j))
                pe.wait_ge(self.copied, n + (1 - S))
            for u in range(U):
                if U == 2:
                    at_least(pe, (self.gate_done, self.hidden_done)[u], n)
                    bank, mats = 2 * u, [w[key][:, :, 512 * u:512 * (u + 1)] for key in ("up1", "up3")]
                else:
                    at_least(pe, self.hidden_done, n - (RING - 1))
                    bank, mats = 2 * j, [w["up"][:, :, a:a + 512] for a in range(0, w["up"].shape[2], 512)]
                for a, mat in enumerate(mats):
                    for m in range(4):
                        for c in range(C):
                            x = xT[:, c, bass.ds(n * P, P)] if shared else self.xT[j][:, c, :]
                            done = nc.tensor.matmul(PS[:, bank + a, m * P:(m + 1) * P], mat[:, c, m * P:(m + 1) * P], x, start=(c == 0), stop=(c == 1))
                done.then_inc(self.up_done, 1)

        def down(q, j, shared):
            n = RING * q + j
            w = self.shared if shared else self.weights[j]
            pe.wait_ge(self.hidden_done, n + 1)
            at_least(pe, self.out_copied, n)
            if not shared:
                pe.wait_ge(self.down_in[j], 16 * self.nth(q, j))
            for m in range(4):
                done = nc.tensor.matmul(PS[:, 7, 0:D], self.hidden[j][:, m, :], w["down"][:, m, :], start=(m == 0), stop=(m == 3))
            done.then_inc(self.down_done, 1)

        def turn(q, j, shared):
            n = RING * q + j
            if self.sorted_next(n, shared):
                flip_rows(*after(q, j))
            up(q, j, shared)
            if isinstance(n, int) and n == 0:
                between()
            if not isinstance(n, int) or n:
                down(*before(q, j), shared or (isinstance(n, int) and n == S))

        self.over(pe, lambda: S or flip_rows(0, 0), turn, lambda: down(*divmod(self.N - 1, RING), False))


    def scalar(self, act):
        nc, PS, S = self.core.nc, self.core.PS, self.S

        def copy_rows(q, j):
            n = RING * q + j
            act.wait_ge(self.flipped, n + (1 - S))
            at_least(act, self.up_done, self.units * (n - (RING - 1)))
            done = nc.scalar.copy(self.xT[j][:].rearrange("p c n -> p (c n)"), PS[:, 6, 0:C * P])
            done.then_inc(self.copied, 1)

        def turn(q, j, shared):
            n = RING * q + j
            w = self.shared if shared else self.weights[j]
            if self.sorted_next(n, shared):
                copy_rows(*after(q, j))
            if self.kind == "glu":
                act.wait_ge(self.up_done, n + 1)
                at_least(act, self.hidden_done, n - (RING - 1))
                nc.scalar.activation(self.side[j][:].rearrange("p m n -> p (m n)"), PS[:, 2 * j + 1, :], ACT.Silu).then_inc(self.side_done, 1)
            elif self.kind == "gelu":
                act.wait_ge(self.up_done, n + 1)
                at_least(act, self.down_done, n - (RING - 1))
                for m in range(4):
                    done = nc.scalar.activation(self.hidden[j][:, m, :], PS[:, 2 * j, m * P:(m + 1) * P], ACT.Gelu, bias=w["b1"][:, m:m + 1])
                done.then_inc(self.hidden_done, 1)
            else:
                for u in range(2):
                    act.wait_ge(self.up_done, 2 * n + (u + 1))
                    at_least(act, (self.gate_done, self.hidden_done)[u], n)
                    for m in range(4):
                        done = nc.scalar.activation(self.side[u][:, m, :], PS[:, 2 * u, m * P:(m + 1) * P], ACT.Identity, bias=w["b1"][:, 4 * u + m:4 * u + m + 1])
                    done.then_inc(self.side_done, 1)
                    if u == 0:
                        act.wait_ge(self.gate_done, n + 1)
                        at_least(act, self.hidden_done, n)
                        nc.scalar.activation(self.sigmoid[:], self.gated[:], ACT.Sigmoid, scale=1.702).then_inc(self.sigmoid_done, 1)

        self.over(act, lambda: S or copy_rows(0, 0), turn, lambda: None)


    def vector(self, dve, weights, between=lambda: None, final=False):
        nc, PS, X, S, step = self.core.nc, self.core.PS, self.core.X, self.S, self.core.dve_step

        def copy_out(q, j, shared):
            n = RING * q + j
            dve.wait_ge(self.down_done, n + 1)
            if shared:
                x = X[:, bass.ds(n, 1), :].rearrange("p t d -> p (t d)")
                nc.vector.tensor_tensor(x, PS[:, 7, 0:D], x, ALU.add).then_inc(self.out_copied, 1)
                return
            if not isinstance(n, int) or n >= S + RING:
                dve.wait_ge(self.stored[j], 16 * (self.nth(q, j) - 1))
            nc.vector.tensor_copy(self.out[j][:], PS[:, 7, 0:D]).then_inc(self.out_copied, 1)

        def hidden_units(q, j, shared):
            n = RING * q + j
            w = self.shared if shared else self.weights[j]
            if self.kind == "glu":
                dve.wait_ge(self.side_done, n + 1)
                at_least(dve, self.down_done, n - (RING - 1))
                nc.vector.tensor_tensor(self.hidden[j][:].rearrange("p m n -> p (m n)"), PS[:, 2 * j, :],
                                        self.side[j][:].rearrange("p m n -> p (m n)"), ALU.mult).then_inc(self.hidden_done, 1)
            elif self.kind == "swiglu":
                for u in range(2):
                    p = self.product[u]
                    dve.wait_ge(self.side_done, 2 * n + (u + 1))
                    for m in range(4):
                        done = nc.vector.scalar_tensor_tensor(p[:, m, :], PS[:, 2 * u + 1, m * P:(m + 1) * P], w["b3"][:, 4 * u + m:4 * u + m + 1],
                                                              self.side[u][:, m, :], ALU.add, ALU.mult)
                    step(dve, done)
                    if u == 0:
                        at_least(dve, self.sigmoid_done, n)
                        nc.vector.tensor_scalar(self.gated[:], p[:], 7.0, None, ALU.min).then_inc(self.gate_done, 1)
                        dve.wait_ge(self.gate_done, n + 1)
                step(dve, nc.vector.tensor_scalar(p[:], p[:], -7.0, 7.0, ALU.max, ALU.min))
                step(dve, nc.vector.scalar_tensor_tensor(p[:], p[:], 1.0, self.gated[:], ALU.add, ALU.mult))
                dve.wait_ge(self.sigmoid_done, n + 1)
                at_least(dve, self.down_done, n)
                nc.vector.tensor_tensor(self.hidden[j][:], p[:], self.sigmoid[:], ALU.mult).then_inc(self.hidden_done, 1)

        def turn(q, j, shared):
            n = RING * q + j
            hidden_units(q, j, shared)
            if not isinstance(n, int) or n:
                copy_out(*before(q, j), shared or (isinstance(n, int) and n == S))

        self.over(dve, lambda: None, turn, lambda: copy_out(*divmod(self.N - 1, RING), False), steps=4 if self.kind == "swiglu" else 0)
        between()
        for t in range(NT):
            if t % 2 == 0:
                dve.wait_ge(self.gather_done[t // 2], 32 * self.K)
            for k in range(self.K):
                x, y = X[:, t, :], self.gathered[:, t, k, :]
                if weights[k] is None:
                    done = nc.vector.tensor_tensor(x, y, x, ALU.add)
                else:
                    done = nc.vector.scalar_tensor_tensor(x, y, weights[k][:, t:t + 1], x, ALU.mult, ALU.add)
                if k < self.K - 1:
                    step(dve, done)
            if t % 2 and not final:
                self.core.norm.take(dve, done, (t - 1, t))


def first_best(core, dve, values, number, best, place, chosen):
    nc, step = core.nc, core.dve_step
    n = values.shape[2]
    step(dve, nc.vector.reduce_max(best[:], values[:], AX.X))
    step(dve, nc.vector.tensor_tensor(chosen[:], values[:], bcast(best[:], 2, n), ALU.is_equal))
    step(dve, nc.vector.tensor_tensor(chosen[:], chosen[:], bcast(number, 1, NT), ALU.mult))
    step(dve, nc.vector.tensor_reduce(place[:], chosen[:], AX.X, ALU.min))
    step(dve, nc.vector.tensor_tensor(chosen[:], bcast(number, 1, NT), bcast(place[:], 2, n), ALU.is_equal))


def router_tensor(core, pe, xT, wg, done):
    nc, PS, n = core.nc, core.PS, wg.shape[2]
    for t in range(NT):
        for c in range(C):
            last = nc.tensor.matmul(PS[:, 4, t * n:(t + 1) * n], xT[:, c, t * P:(t + 1) * P], wg[:, c, :], start=(c == 0), stop=(c == 1))
    last.then_inc(done, 1)


class OutputBias:

    def __init__(self, core, es, name, n):
        self.core, self.n = core, n
        self.gateT = core.sb(f"{name}_gateT", [n, NT * P], es)
        self.flipped, self.copied, self.done, self.added = (core.sem(f"{name}_bias_{x}") for x in ("flipped", "copied", "done", "added"))

    def tensor(self, pe, gate, gate_done, b2):
        nc, PS = self.core.nc, self.core.PS
        pe.wait_ge(gate_done, 1)
        for t in range(NT):
            last = nc.tensor.transpose(PS[0:self.n, 4 + t // 4, (t % 4) * P:(t % 4 + 1) * P], gate[:, t, :], self.core.ident[:])
        last.then_inc(self.flipped, 1)
        pe.wait_ge(self.copied, 1)
        for t in range(NT):
            last = nc.tensor.matmul(PS[:, 4 + t // 2, (t % 2) * D:(t % 2 + 1) * D], self.gateT[:, t * P:(t + 1) * P], b2[0:self.n, :],
                                    start=True, stop=True)
        last.then_inc(self.done, 1)
        pe.wait_ge(self.added, 1)

    def vector(self, dve):
        nc, PS, X = self.core.nc, self.core.PS, self.core.X
        dve.wait_ge(self.flipped, 1)
        nc.vector.tensor_copy(self.gateT[:], PS[0:self.n, 4:6, :].rearrange("e a n -> e (a n)")).then_inc(self.copied, 1)
        dve.wait_ge(self.done, 1)
        nc.vector.tensor_tensor(X[:], PS[:, 4:8, :].rearrange("p a (t d) -> p (a t) d", d=D), X[:], ALU.add).then_inc(self.added, 1)
        dve.wait_ge(self.added, 1)


def exists(b):
    return not isinstance(b, int) or b < B


def over_batches(eng, first, turn, last, enter=None, leave=None):
    first()
    trips = (B - 4) // 2
    with eng.Fori(0, trips) as i:
        if enter:
            enter(i)
        turn(2 * i, 0)
        turn(2 * i + 1, 1)
        if leave:
            leave(trips)
    for b in range(2 * trips, B - 1):
        turn(b, b % 2)
    last(B - 1, 1)


class ContextNorm:

    SLOTS = 4

    def __init__(self, core):
        self.core = core
        self.mean, self.rstd = core.sb("ctx_mean", [P, B, 2]), core.sb("ctx_rstd", [P, B, 2])
        self.shift = core.sb("ctx_shift", [P, B, 2])
        self.last, self.lastT = core.sb("ctx_last", [B, D]), core.sb("ctx_lastT", [P, C, B])
        self.slot_in = [core.sem(f"ctx_slot_in{j}") for j in range(self.SLOTS)]
        self.last_in, self.stats_done = core.sem("ctx_last_in"), core.sem("ctx_stats_done")
        self.spread_done, self.std_done = core.sem("ctx_spread_done"), core.sem("ctx_std_done")
        self.ready, self.flipped, self.lastT_done = core.sem("ctx_ready"), core.sem("ctx_flipped"), core.sem("ctx_lastT_done")
        self.loads = 0

    def allocate(self, es, name):
        self.stats = self.core.sb(name + "_ctx_stats", [P, B, 2, 6], es)
        self.stats_last, self.moments_last = self.core.sb(name + "_ctx_stats_last", [B, 6], es), self.core.sb(name + "_ctx_moments_last", [B, 2], es)
        self.std, self.std_last = self.core.sb(name + "_ctx_std", [P, B, 2], es), self.core.sb(name + "_ctx_std_last", [B, 1], es)
        self.gap = self.core.sb(name + "_ctx_gap", [P, B, 2], es)

    def load(self, sp, slots):
        ctx = self.core.dram["ctx"]
        tile = lambda b: ctx[b, 0:2 * P, :].rearrange("(h p) d -> p h d", p=P)
        sp.dma_start(self.last[:], ctx[:, CTX - 1, :]).then_inc(self.last_in, 16)
        n = self.SLOTS
        for j in range(n):
            sp.dma_start(slots[j][:], tile(j)).then_inc(self.slot_in[j], 16)
        with sp.Fori(0, B // n - 1) as i:
            for j in range(n):
                sp.wait_ge(self.stats_done, n * i + (j + 1))
                sp.dma_start(slots[j][:], tile(n * i + (j + n))).then_inc(self.slot_in[j], 16)
        for j in range(2):
            sp.wait_ge(self.stats_done, B - n + j + 1)
            sp.dma_start(slots[j][:], tile(j)).then_inc(self.slot_in[j], 16)

    def vector_stats(self, dve, slots):
        nc, step = self.core.nc, self.core.dve_step
        n = self.SLOTS
        with dve.Fori(0, B // n) as i:
            for j in range(n):
                dve.wait_ge(self.slot_in[j], 16 * i + 16)
                for h in range(2):
                    done = nc.vector.bn_stats(self.stats[:, n * i + j, h, :], slots[j][:, h, :])
                done.then_inc(self.stats_done, 1)
        dve.wait_ge(self.stats_done, B)
        dve.wait_ge(self.last_in, 16)
        step(dve, nc.vector.bn_stats(self.stats_last[:], self.last[:]))
        m0, s0, m1, s1 = (self.stats[:, :, :, n] for n in (1, 2, 4, 5))
        nc.vector.bn_aggr(self.moments_last[:], self.stats_last[:])
        nc.vector.tensor_tensor(self.gap[:], m0, m1, ALU.subtract)
        step(dve, nc.vector.tensor_tensor(self.mean[:], m0, m1, ALU.add))
        nc.vector.tensor_scalar(self.mean[:], self.mean[:], 0.5, None, ALU.mult)
        step(dve, nc.vector.tensor_tensor(self.std[:], s0, s1, ALU.add))
        step(dve, nc.vector.tensor_tensor(self.gap[:], self.gap[:], self.gap[:], ALU.mult))
        step(dve, nc.vector.tensor_scalar(self.gap[:], self.gap[:], 0.25, None, ALU.mult))
        nc.vector.scalar_tensor_tensor(self.std[:], self.std[:], 1.0 / D, self.gap[:], ALU.mult, ALU.add).then_inc(self.spread_done, 1)

    def vector_finish(self, dve):
        nc, step = self.core.nc, self.core.dve_step
        dve.wait_ge(self.std_done, 1)
        nc.vector.reciprocal(self.rstd[:], self.std[:])
        step(dve, nc.vector.reciprocal(self.std_last[:], self.std_last[:]))
        nc.vector.scalar_tensor_tensor(self.shift[:], self.mean[:], -1.0, self.rstd[:], ALU.mult, ALU.mult)
        nc.vector.tensor_scalar(self.last[:], self.last[:], self.moments_last[:, 0:1], self.std_last[:], ALU.subtract, ALU.mult).then_inc(self.ready, 1)
        dve.wait_ge(self.flipped, 1)
        nc.vector.tensor_copy(self.lastT[:], self.core.PS[:, 7, 0:C * B].rearrange("p (c b) -> p c b", c=C)).then_inc(self.lastT_done, 1)
        dve.wait_ge(self.lastT_done, 1)

    def scalar(self, act):
        nc = self.core.nc
        act.wait_ge(self.spread_done, 1)
        nc.scalar.activation(self.std_last[:], self.moments_last[:, 1:2], ACT.Sqrt, bias=self.core.eps5[0:B, :])
        nc.scalar.activation(self.std[:], self.std[:], ACT.Sqrt, bias=self.core.eps5).then_inc(self.std_done, 1)

    def tensor(self, pe):
        nc = self.core.nc
        pe.wait_ge(self.ready, 1)
        for c in range(C):
            done = nc.tensor.transpose(self.core.PS[:, 7, c * B:(c + 1) * B], self.last[:, c * P:(c + 1) * P], self.core.ident[0:B, 0:B])
        done.then_inc(self.flipped, 1)
        pe.wait_ge(self.lastT_done, 1)


def l0_cross(core, load_next):
    nc, PS, norm, flip, dve_step, pool_step = core.nc, core.PS, core.norm, core.flip, core.dve_step, core.pool_step
    KVW = P + 8
    RW = P + 2
    w = core.arena(0)
    wqkv = w.take(6, D)
    dense = w.take(C, D)
    gamma, beta, dense_b = w.take(D), w.take(D), w.take(D)
    head_of = w.take(8)
    same_head = w.take(P)
    em_in = w.take(B, 2)
    em_left_in = w.take(1)
    cleft = w.take(C, B)
    order = w.take(P)
    with ExitStack() as es:
        sb = lambda name, shape: core.sb("l0x_" + name, shape, es)
        ctxT = [sb(f"ctxT{i}", [P, C, CTX]) for i in range(2)]
        wsum, sq = sb("wsum", [P, 6]), sb("sq", [P, NT, D])
        em = sb("em", [P, B, 2, 2])
        eml = sb("eml", [B, 2])
        ss = [sb(f"ss{i}", [P, 4]) for i in range(2)]
        std = [sb(f"std{i}", [P, 4]) for i in range(2)]
        rstd = [sb(f"rstd{i}", [P, 4]) for i in range(2)]
        kp = [sb(f"kp{i}", [P, 2, D]) for i in range(2)]
        vr = [sb(f"vr{i}", [P, 2, C, RW]) for i in range(2)]
        kp_left, vr_left = sb("kp_left", [B, D]), sb("vr_left", [B, C, RW])
        vr_one = [sb(f"vr_one{i}", [B, C, RW]) for i in range(2)]
        kv_tmp = [sb(f"kv_tmp{i}", [P, C, P]) for i in range(2)]
        scale_v, shift_v = sb("scale_v", [P, C, P]), sb("shift_v", [P, C, P])
        KV = sb("KV", [P, B, C, KVW])
        qss, qstd, qrstd = sb("qss", [P, NT]), sb("qstd", [P, NT]), sb("qrstd", [P, NT])
        z = [sb(f"z{i}", [P, C, 8]) for i in range(2)]

        ctx_in = [core.sem(f"l0x_ctx_in{i}") for i in range(2)]
        rows_done = core.sem("l0x_rows_done")
        centered = core.sem("l0x_centered")
        q_done = core.sem("l0x_q_done")
        q_std = core.sem("l0x_q_std")
        proj_done = core.sem("l0x_proj_done")
        std_done = core.sem("l0x_std_done")
        scale_ready = core.sem("l0x_scale_ready")
        v_ready = core.sem("l0x_v_ready")
        kv_ready = core.sem("l0x_kv_ready")
        kv_done = core.sem("l0x_kv_done")
        kv_kept = core.sem("l0x_kv_kept")
        att_done = core.sem("l0x_att_done")
        att_rows = core.sem("l0x_att_rows")
        dense_done = core.sem("l0x_dense_done")

        att_stored = [core.sem(f"l0x_att_stored{i}") for i in range(2)]
        att_in = core.sem("l0x_att_in")
        q_scaled, x_shifted = core.sem("l0x_q_scaled"), core.sem("l0x_x_shifted")
        att_dram = nc.dram_tensor("att_dram", (NT, 16, P, 16), F32).ap()
        AR = sb("AR", [P, NT, D])

        block = es.enter_context(nc.Block())

        def load_attention(eng, half):
            eng.wait_ge(att_stored[half], 4 * 16)
            eng.dma_start(AR[:, 4 * half:4 * half + 4, :],
                          att_dram[4 * half:4 * half + 4].rearrange("t h p e -> (h p e) t")
                          .rearrange("(p d) t -> p t d", d=D)).then_inc(att_in, 16)

        @block.sync
        def _(sp):
            for j in range(2):
                sp.dma_start(ctxT[j][:], core.dram["ctxT"][j]).then_inc(ctx_in[j], 16)
            load_next(sp)
            with sp.Fori(0, B // 2 - 1) as i:
                for j in range(2):
                    sp.wait_ge(proj_done, 2 * i + (j + 2))
                    sp.dma_start(ctxT[j][:], core.dram["ctxT"][2 * i + (j + 2)]).then_inc(ctx_in[j], 16)
            for t in range(NT):
                sp.wait_ge(att_rows, t + 1)
                sp.dma_start(att_dram[t].rearrange("h p e -> p h e"),
                             core.H[:, t, :].rearrange("p (h e) -> p h e", e=16)).then_inc(att_stored[t // 4], 16)
            load_attention(sp, 1)

        @block.gpsimd
        def _(pool):
            pool.wait_ge(q_scaled, 1)
            pool_step(pool, nc.gpsimd.tensor_tensor(core.H[:], core.H[:], bcast(beta, 1, NT), ALU.add))
            for t in range(NT):
                nc.gpsimd.tensor_scalar(core.H[:, t, :], core.H[:, t, :], 0.0, 1e-6, ALU.max, ALU.add).then_inc(rows_done, 1)
            nc.gpsimd.tensor_tensor(core.X[:], core.X[:], bcast(beta, 1, NT), ALU.add).then_inc(x_shifted, 1)

        @block.tensor
        def _(pe):
            pe.wait_ge(core.consts_in, 16)
            flip.tensor(pe, core.H, rows_done, 0)
            flip.ready(pe, "pe")
            pe.wait_ge(centered, 1)
            for t in range(NT):
                for c in range(C):
                    last = nc.tensor.matmul(PS[:, 4 + t // 2, (t % 2) * D:(t % 2 + 1) * D],
                                            core.HT[:, c, t * P:(t + 1) * P], wqkv[:, c, :], start=(c == 0), stop=(c == 1))
                last.then_inc(q_done, 1)
            kw = wqkv[:, 2:6, :].rearrange("p (c k) d -> p c (k d)", c=C)

            for c in range(C):
                last = nc.tensor.matmul(PS[0:B, 2, :], cleft[:, c, :], kw[:, c, :], start=(c == 0), stop=(c == 1))
            last.then_inc(proj_done, 1)

            def proj_batch(b, j):
                pe.wait_ge(ctx_in[j], 8 * b + (16 - 8 * j))
                for k in range(2):
                    for half in range(2):
                        for c in range(C):
                            last = nc.tensor.matmul(PS[:, 2 * j + k, half * D:(half + 1) * D], ctxT[j][:, c, half * P:(half + 1) * P],
                                                    kw[:, c, k * D:(k + 1) * D], start=(c == 0), stop=(c == 1))
                last.then_inc(proj_done, 1)

            def kv_batch(b, j):
                pe.wait_ge(v_ready, b + 1)
                pe.wait_ge(kv_ready, b + 3)
                for c in range(C):
                    acc = PS[:, 4 + j, c * RW:(c + 1) * RW]
                    for half in range(2):
                        nc.tensor.matmul(acc, kp[j][:, half, c * P:(c + 1) * P], vr[j][:, half, c, :],
                                         start=(half == 0), stop=False)
                    last = nc.tensor.matmul(acc, kp_left[:, c * P:(c + 1) * P], vr_one[j][:, c, :], start=False, stop=True)
                last.then_inc(kv_done, 1)

            proj_batch(0, 0)
            with pe.Fori(0, B // 2 - 1) as i:
                pe.wait_ge(kv_ready, 2 * i + 2)
                proj_batch(2 * i + 1, 1)
                pe.wait_ge(kv_kept, 2 * i + 1)
                kv_batch(2 * i, 0)
                proj_batch(2 * i + 2, 0)
                pe.wait_ge(kv_kept, 2 * i + 2)
                kv_batch(2 * i + 1, 1)
            pe.wait_ge(kv_ready, B)
            proj_batch(B - 1, 1)
            pe.wait_ge(kv_kept, B - 1)
            kv_batch(B - 2, 0)
            pe.wait_ge(kv_kept, B)
            kv_batch(B - 1, 1)
            flip.tensor(pe, core.H, rows_done, NT)
            flip.ready(pe, "pe")
            pe.wait_ge(kv_kept, B + 2)
            for t in range(NT):
                if t >= 2:
                    pe.wait_ge(att_rows, t - 1)
                for b in range(TB * t, TB * t + TB):
                    r = S * (b % TB)
                    for c in range(C):
                        last = nc.tensor.matmul(PS[r:r + S, 6 + t % 2, c * KVW:(c + 1) * KVW],
                                                core.HT[:, c, b * S:(b + 1) * S], KV[:, b, c, :], start=True, stop=True)
                last.then_inc(att_done, 1)
            pe.wait_ge(att_in, 32)
            flip.tensor(pe, AR, att_rows, 0, order)
            flip.ready(pe, "pe")
            for t in range(NT):
                for c in range(C):
                    last = nc.tensor.matmul(PS[:, 4 + t // 2, (t % 2) * D:(t % 2 + 1) * D],
                                            core.HT[:, c, t * P:(t + 1) * P], dense[:, c, :], start=(c == 0), stop=(c == 1))
                last.then_inc(dense_done, 1)

        @block.scalar
        def _(act):
            norm.load_table(act)
            norm.scalar(act, core.eps5)
            flip.scalar(act, core.HT)
            for t in range(NT):
                act.wait_ge(q_done, (t | 1) + 1)
                last = nc.scalar.activation(sq[:, t, :], PS[:, 4 + t // 2, (t % 2) * D:(t % 2 + 1) * D], ACT.Square,
                                            accum_out=qss[:, t:t + 1])
            core.act_step(act, last)
            nc.scalar.activation(qstd[:], qss[:], ACT.Sqrt, bias=core.eps6, scale=1.0 / D).then_inc(q_std, 1)
            act.wait_ge(proj_done, 1)
            for h in range(2):
                last = nc.scalar.activation(sq[0:B, h, :], PS[0:B, 2, h * D:(h + 1) * D], ACT.Square,
                                            accum_out=ss[1][0:B, h:h + 1])
            core.act_step(act, last)
            nc.scalar.activation(std[1][0:B, 0:2], ss[1][0:B, 0:2], ACT.Sqrt, bias=core.eps6[0:B, :], scale=1.0 / D).then_inc(std_done, 1)
            with act.Fori(0, B // 2) as i:
                core.act_step.enter(i, 2)
                for j in range(2):
                    act.wait_ge(proj_done, 2 * i + (j + 2))
                    for half in range(2):
                        for h in range(2):
                            last = nc.scalar.activation(sq[:, 4 * j + 2 * half + h, :], PS[:, 2 * j + h, half * D:(half + 1) * D], ACT.Square,
                                                        accum_out=ss[j][:, 2 * half + h:2 * half + h + 1])
                    core.act_step(act, last)
                    act.wait_ge(kv_ready, 2 * i + (j + 1))
                    nc.scalar.activation(std[j][:], ss[j][:], ACT.Sqrt, bias=core.eps6, scale=1.0 / D).then_inc(std_done, 1)
                    act.wait_ge(scale_ready, 2 * i + (j + 1))
                    for half in range(2):
                        last = nc.scalar.activation(vr[j][:, half, :, 0:P], PS[:, 2 * j + 1, half * D:(half + 1) * D].rearrange("p (c d) -> p c d", c=C),
                                                    ACT.Copy, scale=rstd[j][:, 2 * half + 1:2 * half + 2])
                    last.then_inc(v_ready, 1)
                core.act_step.leave(B // 2)
            flip.scalar(act, core.HT)
            load_attention(act, 0)
            flip.scalar(act, core.HT)
            norm.scalar(act, core.eps6)
            norm.load_table(act)

        @block.vector
        def _(dve):
            dve.wait_ge(core.x_in, 16)
            norm.vector(dve, core.X, core.H, rows_done)
            flip.vector(dve, core.HT)
            dve.wait_ge(core.weights_in[0], 16)
            dve_step(dve, nc.vector.reduce_sum(wsum[:], wqkv, AX.X))
            dve_step(dve, nc.vector.tensor_scalar(wsum[:], wsum[:], 1.0 / D, None, ALU.mult))
            nc.vector.tensor_tensor(wqkv, wqkv, bcast(wsum[:], 2, D), ALU.subtract).then_inc(centered, 1)
            nc.vector.tensor_copy(em[:, :, :, 0], em_in)
            nc.vector.tensor_tensor(em[:, :, :, 1], em_in, em_in, ALU.mult)
            nc.vector.tensor_copy(eml[:, 0:1], em_left_in[0:B])
            dve_step(dve, nc.vector.tensor_tensor(eml[:, 1:2], em_left_in[0:B], em_left_in[0:B], ALU.mult))
            nc.vector.tensor_tensor(scale_v[:], bcast(same_head, 1, C), gamma.rearrange("p (c d) -> p c d", c=C), ALU.mult)
            nc.vector.tensor_tensor(shift_v[:], bcast(same_head, 1, C), beta.rearrange("p (c d) -> p c d", c=C), ALU.mult)
            dve.wait_ge(q_std, 1)
            dve.wait_ge(rows_done, NT)
            flip.ready(dve, "dve")
            dve_step(dve, nc.vector.reciprocal(qrstd[:], qstd[:]))
            for t in range(NT):
                last = nc.vector.scalar_tensor_tensor(core.H[:, t, :], PS[:, 4 + t // 2, (t % 2) * D:(t % 2 + 1) * D],
                                                      qrstd[:, t:t + 1], gamma, ALU.mult, ALU.mult)
            last.then_inc(q_scaled, 1)

            def keys(k_rows, psum, scale):
                m, n = psum.shape[0], psum.shape[1]
                for h in range(n):
                    last = nc.vector.scalar_tensor_tensor(k_rows[:, h, :], psum[:, h, :], scale[:, 2 * h:2 * h + 1],
                                                          gamma[0:m, :], ALU.mult, ALU.mult)
                dve_step(dve, last)
                dve_step(dve, nc.vector.tensor_tensor(k_rows, k_rows, bcast(beta[0:m, :], 1, n), ALU.add))
                return nc.vector.tensor_scalar(k_rows, k_rows, 0.0, 1e-6, ALU.max, ALU.add)

            def keep(b, j):
                dve.wait_ge(kv_done, b + 1)
                A = PS[:, 4 + j, 0:C * RW].rearrange("p (c r) -> p c r", c=C)
                first = nc.vector.tensor_tensor(kv_tmp[j][:], A[:, :, 0:P], scale_v[:], ALU.mult)
                nc.vector.tensor_tensor(KV[:, b, :, P:KVW], bcast(head_of, 1, C), bcast(A[:, :, P], 2, 8), ALU.mult)
                dve_step(dve, first)
                for c in range(C):
                    last = nc.vector.scalar_tensor_tensor(KV[:, b, c, 0:P], shift_v[:, c, :], A[:, c, P + 1:P + 2],
                                                          kv_tmp[j][:, c, :], ALU.mult, ALU.add)
                last.then_inc(kv_kept, 1)

            def prepare(b, j):
                dve.wait_ge(std_done, b + 2)
                dve_step(dve, nc.vector.reciprocal(rstd[j][:], std[j][:]))
                scale = rstd[j][:].rearrange("p (h k) -> p h k", k=2)[:, :, 1]
                nc.vector.tensor_tensor(scale, scale, em[:, b, :, 1], ALU.mult).then_inc(scale_ready, 1)
                nc.vector.tensor_scalar(vr_one[j][:], vr_left[:], core.ident[0:B, bass.ds(b, 1)], None, ALU.mult)
                nc.vector.tensor_copy(vr[j][:, :, :, P:RW], bcast(em[:, b, :, :], 2, C))
                keys(kp[j][:], PS[:, 2 * j, :].rearrange("p (t d) -> p t d", d=D), rstd[j][:]).then_inc(kv_ready, 1)

            dve.wait_ge(std_done, 1)
            left_scale = rstd[1][0:B, 0:2]
            dve_step(dve, nc.vector.reciprocal(left_scale, std[1][0:B, 0:2]))
            dve_step(dve, nc.vector.tensor_tensor(left_scale[:, 1:2], left_scale[:, 1:2], eml[:, 1:2], ALU.mult))
            nc.vector.tensor_scalar(vr_left[:, :, 0:P], PS[0:B, 2, D:2 * D].rearrange("p (c d) -> p c d", c=C), left_scale[:, 1:2], None, ALU.mult)
            nc.vector.tensor_copy(vr_left[:, :, P:RW], bcast(eml[:], 1, C))
            keys(kp_left[:].unsqueeze(1), PS[0:B, 2:3, 0:D], left_scale).then_inc(kv_ready, 2)
            dve.wait_ge(kv_ready, 2)
            dve.sem_inc(kv_kept, 2)
            prepare(0, 0)
            with dve.Fori(0, B // 2 - 1) as i:
                dve_step.enter(i, 8)
                prepare(2 * i + 1, 1)
                keep(2 * i, 0)
                prepare(2 * i + 2, 0)
                keep(2 * i + 1, 1)
                dve_step.leave(B // 2 - 1)
            prepare(B - 1, 1)
            keep(B - 2, 0)
            keep(B - 1, 1)
            flip.vector(dve, core.HT)
            flip.ready(dve, "dve")
            for t in range(NT):
                dve.wait_ge(att_done, t + 1)
                acc = PS[:, 6 + t % 2, 0:C * KVW].rearrange("p (c r) -> p c r", c=C)
                dve_step(dve, nc.vector.tensor_scalar(z[t % 2][:], acc[:, :, P:KVW], 1e-6, None, ALU.add))
                dve_step(dve, nc.vector.reciprocal(z[t % 2][:], z[t % 2][:]))
                nc.vector.tensor_tensor(core.H[:, t, :].rearrange("p (c h d) -> p c h d", c=C, h=8),
                                        acc[:, :, 0:P].rearrange("p c (h d) -> p c h d", h=8),
                                        bcast(z[t % 2][:], 3, 16), ALU.mult).then_inc(att_rows, 1)
            flip.vector(dve, core.HT)
            flip.ready(dve, "dve")
            for t in range(0, NT, 2):
                dve.wait_ge(dense_done, t + 2)
                dve_step(dve, nc.vector.tensor_tensor(core.H[:, t:t + 2, :], PS[:, 4 + t // 2, :].rearrange("p (t d) -> p t d", d=D),
                                                      bcast(dense_b, 1, 2), ALU.add))
                for u in (t, t + 1):
                    done = nc.vector.bn_stats(core.stats[:, u, :], core.H[:, u, :])
            dve_step(dve, done)
            norm.statistics(dve)
            for t in range(NT):
                last = nc.vector.scalar_tensor_tensor(core.H[:, t, :], core.H[:, t, :], core.moments[:, t, 0:1], gamma, ALU.subtract, ALU.mult)
            dve_step(dve, last)
            dve.wait_ge(x_shifted, 1)
            for t in range(NT):
                nc.vector.scalar_tensor_tensor(core.X[:, t, :], core.H[:, t, :], core.rstd[:, t:t + 1], core.X[:, t, :], ALU.mult, ALU.add)


def l0_self(core, load_next):
    nc, norm, flip = core.nc, core.norm, core.flip
    w = core.arena(1)
    wqk, wv, wo = w.take(C, 2 * D), w.take(C, D), w.take(C, D)
    cos, sin, causal, head_of, batch_of = w.take(8), w.take(8), w.take(S), w.take(8), w.take(TB)
    with ExitStack() as es:
        at = SelfAttention(core, es, "l0a", "softmax", 16.0 ** -0.5)

        def pairs(rows):
            two = rows.rearrange("p (h d two) -> p h d two", h=32, two=2)
            return two[:, :, :, 0], two[:, :, :, 1]

        rotation = Rotation(core, es, at, pairs, cos, sin, at.qk_copied)
        rows_done = core.sem("l0a_rows_done")
        block = es.enter_context(nc.Block())

        @block.sync
        def _(sp):
            load_next(sp)

        @block.tensor
        def _(pe):
            pe.wait_ge(core.consts_in, 16)
            pe.wait_ge(core.weights_in[1], 16)
            flip.tensor(pe, core.H, rows_done, 0)
            flip.ready(pe, "pe")
            at.project(pe, core.HT, core.HT, wqk, wv)
            at.flip_tensor(pe)
            flip.ready(pe, "pe")
            at.attend_tensor(pe, wo)

        @block.gpsimd
        def _(pool):
            at.set_zeros(pool)
            pool.wait_ge(core.weights_in[1], 16)
            rotation.gpsimd(pool)
            flip.uses["pool"] = flip.uses["pe"]
            flip.ready(pool, "pool")
            at.spread_keys(pool, head_of)

        @block.scalar
        def _(act):
            norm.scalar(act, core.eps5)
            flip.scalar(act, core.HT)
            at.copy_projections(act)
            flip.scalar(act, at.QT)
            flip.scalar(act, at.KT)
            at.attend_scalar(act, batch_of)
            norm.load_table(act)

        @block.vector
        def _(dve):
            dve.wait_ge(core.x_in, 16)
            norm.vector(dve, core.X, core.H, rows_done)
            flip.vector(dve, core.HT)
            dve.wait_ge(core.weights_in[1], 16)
            for t in range(NT + 1):
                if t < NT:
                    rotation.cosine_products(dve, t)
                if t >= 1:
                    rotation.combine(dve, t - 1)
            flip.vector(dve, at.QT)
            flip.vector(dve, at.KT)
            at.attend_vector(dve, causal)


def l0_feed_forward(core, load_next):
    nc, PS, norm, flip, dve_step = core.nc, core.PS, core.norm, core.flip, core.dve_step
    E = EXPERTS[2][0]
    w = core.arena(2)
    cent, scale, number = w.take(C, E), w.take(D), w.take(E)
    with ExitStack() as es:
        ex = SortedExperts(core, es, "l0f", 2, "glu", 1)
        sb = lambda n, shape: core.sb("l0f_" + n, shape, es)
        R, squares = sb("R", [P, NT, D]), sb("squares", [P, NT, D])
        XT, size, lengths, least = sb("XT", [P, C, NT * P]), sb("size", [P, NT]), sb("lengths", [P, NT]), sb("least", [P, NT])
        cent2, centm2, ones = sb("cent2", [P, C, E]), sb("centm2", [P, C, E]), ex.places.ones
        dist, gate = sb("dist", [P, NT, E]), sb("gate", [P, NT, E])
        rows_done, rms_rows = core.sem("l0f_rows_done"), core.sem("l0f_rms_rows")
        rooted, lengths_done = core.sem("l0f_ms_rooted"), core.sem("l0f_lengths_done")
        dist_ready, dist_done = core.sem("l0f_dist_ready"), core.sem("l0f_dist_done")
        gate_done = core.sem("l0f_gate_done")
        block = es.enter_context(nc.Block())

        @block.sync
        def _(sp):
            load_next(sp)
            ex.load(sp)

        @block.gpsimd
        def _(pool):
            ex.scatter(pool, R, rms_rows, 0)

        @block.tensor
        def _(pe):
            pe.wait_ge(core.consts_in, 16)
            flip.tensor(pe, R, rms_rows, 0)
            pe.wait_ge(dist_ready, 1)
            for c in range(C):
                nc.tensor.matmul(PS[:, 4, NT * E:NT * E + E], ones[:], cent2[:, c, :], start=(c == 0), stop=(c == 1))
            flip.ready(pe, "pe")
            for t in range(NT):
                for c in range(C):
                    last = nc.tensor.matmul(PS[:, 4, t * E:(t + 1) * E], XT[:, c, t * P:(t + 1) * P], centm2[:, c, :], start=(c == 0), stop=(c == 1))
            last.then_inc(dist_done, 1)
            ex.places.tensor(pe, gate, gate_done)
            ex.tensor(pe, XT)

        @block.scalar
        def _(act):
            norm.scalar(act, core.eps5)
            for t in range(NT):
                act.wait_ge(rows_done, t + 1)
                last = nc.scalar.activation(squares[:, t, :], core.H[:, t, :], ACT.Square, accum_out=size[:, t:t + 1])
            core.act_step(act, last)
            nc.scalar.activation(size[:], size[:], ACT.Sqrt, bias=core.eps6, scale=1.0 / D).then_inc(rooted, 1)
            flip.scalar(act, XT)
            for t in range(NT):
                act.wait_ge(rms_rows, t + 1)
                last = nc.scalar.activation(squares[:, t, :], R[:, t, :], ACT.Square, accum_out=lengths[:, t:t + 1])
            last.then_inc(lengths_done, 1)
            ex.scalar(act)
            norm.load_table(act)

        @block.vector
        def _(dve):
            nc.vector.memset(ones[:], 1.0)
            dve.wait_ge(core.x_in, 16)
            norm.vector(dve, core.X, core.H, rows_done)
            dve.wait_ge(core.weights_in[2], 16)
            nc.vector.tensor_scalar(centm2[:], cent, -2.0, None, ALU.mult)
            nc.vector.tensor_tensor(cent2[:], cent, cent, ALU.mult).then_inc(dist_ready, 1)
            dve.wait_ge(rooted, 1)
            dve_step(dve, nc.vector.reciprocal(size[:], size[:]))
            for t in range(NT):
                nc.vector.scalar_tensor_tensor(R[:, t, :], core.H[:, t, :], size[:, t:t + 1], scale, ALU.mult, ALU.mult).then_inc(rms_rows, 1)
            dve_step(dve, nc.vector.tensor_tensor(core.X[:], core.X[:], core.H[:], ALU.add))
            flip.vector(dve, XT)
            dve.wait_ge(lengths_done, 1)
            dve.wait_ge(dist_done, 1)
            dve_step(dve, nc.vector.tensor_tensor(dist[:], PS[:, 4, 0:NT * E].rearrange("p (t e) -> p t e", e=E),
                                                  bcast(lengths[:], 2, E), ALU.add))
            dve_step(dve, nc.vector.tensor_tensor(dist[:], dist[:], bcast(PS[:, 4, NT * E:NT * E + E], 1, NT), ALU.add))
            dve_step(dve, nc.vector.tensor_reduce(least[:], dist[:], AX.X, ALU.min))
            dve_step(dve, nc.vector.tensor_tensor(dist[:], dist[:], bcast(least[:], 2, E), ALU.is_equal))
            dve_step(dve, nc.vector.tensor_tensor(dist[:], dist[:], bcast(number, 1, NT), ALU.mult))
            dve_step(dve, nc.vector.tensor_reduce(least[:], dist[:], AX.X, ALU.min))
            nc.vector.tensor_tensor(gate[:], bcast(number, 1, NT), bcast(least[:], 2, E), ALU.is_equal).then_inc(gate_done, 1)
            dve.wait_ge(gate_done, 1)
            ex.places.vector(dve, (gate,))
            ex.vector(dve, (None,))


def l1_cross(core, load_next):
    nc, PS, norm, flip, dve_step, cn = core.nc, core.PS, core.norm, core.flip, core.dve_step, core.ctx_norm
    HB = 8
    DH = 64
    w = core.arena(3)
    wq, wkv, wo = w.take(C, HB * P), w.take(C, 3 * DH), w.take(HB, D)
    ff1, ff2 = w.take(C, 2 * HB * P), w.take(HB, D)
    ln_g, ln_b, cln_g, cln_b = w.take(C), w.take(C), w.take(C), w.take(C)
    half_of = w.take(2)
    scale = DH ** -0.5
    U = 4
    with ExitStack() as es:
        sb = lambda n, shape: core.sb("l1x_" + n, shape, es)
        two = lambda n, shape: [sb(f"{n}{i}", shape) for i in range(2)]
        sem = lambda n: core.sem("l1x_" + n)
        QT = sb("QT", [P, HB, NT * P])
        hidden = AT = sb("AT", [P, HB, NT * P])
        side = [core.H[:, 2 * i:2 * i + 2, :].rearrange("p t d -> p (t d)") for i in range(2)]
        last_cols = sb("last_cols", [P, C, B])
        ctx, ctx_n, ctxT = two("ctx", [P, 2, D]), two("ctx_n", [P, 2, D]), two("ctxT", [P, C, CTX])
        queries, kT, V, V_last = two("queries", [P, 2, HB, S]), two("kT", [P, CTX]), two("V", [P, 2, DH]), two("V_last", [P, U, DH])
        last_rows = sb("last_rows", [B, DH])
        V_last_all = core.HT[0:U, :, :].rearrange("p c n -> p (c n)").rearrange("p (b d) -> p b d", d=DH)
        probs, probsT, probsT_last = two("probs", [P, U, CTX]), two("probsT", [P, 2, U * P]), two("probsT_last", [P, P])
        top, total = two("top", [P, U]), two("total", [P, U])
        cn.allocate(es, "l1x")
        normed_done, q_done, q_copied = sem("normed_done"), sem("q_done"), sem("q_copied")
        up_done, side_done, hidden_done, ff_done, ff_added = (sem(n) for n in ("up_done", "side_done", "hidden_done", "ff_done", "ff_added"))
        last_cols_done, ctx_normed, ctx_flipped, ctxT_copied = (sem(n) for n in ("last_cols_done", "ctx_normed", "ctx_flipped", "ctxT_copied"))
        last_v_done, last_rows_done, last_stored = sem("last_v_done"), sem("last_rows_done"), sem("last_stored")
        zeros_set, last_placed, V_last_done = sem("zeros_set"), sem("last_placed"), sem("V_last_done")
        last_v_dram = nc.dram_tensor("l1x_last_v_dram", (B, DH), F32).ap()
        queries_done, k_done, v_done, k_copied, v_copied = (sem(n) for n in ("queries_done", "k_done", "v_done", "k_copied", "v_copied"))
        sim_done, top_done, exps_done, probs_done = (sem(n) for n in ("sim_done", "top_done", "exps_done", "probs_done"))
        pt_done, pt_copied_act, pt_copied_dve = sem("pt_done"), sem("pt_copied_act"), sem("pt_copied_dve")
        pv_done, out_copied, out_done = sem("pv_done"), sem("out_copied"), sem("out_done")
        block = es.enter_context(nc.Block())

        @block.sync
        def _(sp):
            cn.load(sp, ctx + ctx_n)
            load_next(sp)
            sp.wait_ge(last_rows_done, 1)
            sp.dma_start(last_v_dram, last_rows[:]).then_inc(last_stored, 16)
            sp.wait_ge(last_stored, 16)
            sp.wait_ge(up_done, 2 * HB)
            for u in range(U):
                sp.dma_start(V_last_all[u:u + 1, :, :], last_v_dram.unsqueeze(0)).then_inc(last_placed, 16)
            with sp.Fori(0, B // 2 - 1) as i:
                for j in range(2):
                    sp.wait_ge(ctx_normed, 2 * i + (j + 1))
                    sp.dma_start(ctx[j][:], core.dram["ctx"][2 * i + (j + 2), 0:2 * P, :].rearrange("(h p) d -> p h d", p=P)).then_inc(cn.slot_in[j], 16)

        @block.gpsimd
        def _(pool):
            for j in range(2):
                nc.gpsimd.memset(V_last[j][:], 0.0).then_inc(zeros_set, 1)
                nc.gpsimd.memset(probsT_last[j][:], 0.0).then_inc(zeros_set, 1)
            pool.wait_ge(zeros_set, 4)
            pool.wait_ge(q_copied, 2 * HB)
            pool.wait_ge(last_cols_done, 1)
            pool.wait_ge(last_placed, 16 * U)
            pool.wait_ge(core.consts_in, 16)

            def prepare(b, j):
                at_least(pool, sim_done, 2 * b - 2)
                nc.gpsimd.tensor_copy(ctxT[j][:, :, 2 * P:CTX], last_cols[:, :, bass.ds(b, 1)])
                nc.gpsimd.tensor_tensor(queries[j][:], bcast(QT[:, :, bass.ds(b * S, S)], 1, 2), bcast(bcast(half_of, 2, HB), 3, S), ALU.mult).then_inc(queries_done, 1)
                at_least(pool, pv_done, b - 1)
                nc.gpsimd.tensor_tensor(V_last[j][0:U], V_last_all[:, bass.ds(b, 1), :].to_broadcast([U, U, DH]), bcast(core.ident[0:U, 0:U], 2, DH), ALU.mult).then_inc(V_last_done, 1)

            prepare(0, 0)
            prepare(1, 1)
            with pool.Fori(0, B // 2 - 1) as i:
                for j in range(2):
                    prepare(2 * i + (j + 2), j)

        @block.tensor
        def _(pe):
            pe.wait_ge(core.consts_in, 16)
            pe.wait_ge(core.weights_in[3], 16)
            flip.tensor(pe, core.H, normed_done, 0)
            flip.ready(pe, "pe")
            for n in range(2 * HB):
                o, half = n // 2, n % 2
                if n >= 4:
                    pe.wait_ge(q_copied, n - 3)
                for c in range(C):
                    done = nc.tensor.matmul(PS[:, 4 + n % 4, :], wq[:, c, o * P:(o + 1) * P], core.HT[:, c, half * 512:(half + 1) * 512],
                                            start=(c == 0), stop=(c == 1))
                done.then_inc(q_done, 1)
            for n in range(2 * HB):
                m, half = n // 2, n % 2
                if n == 2:
                    pe.wait_ge(q_copied, 2 * HB)
                    cn.tensor(pe)
                if n == 4:
                    pe.wait_ge(q_copied, 2 * HB)
                    pe.wait_ge(last_cols_done, 1)
                    for c in range(C):
                        done = nc.tensor.matmul(PS[0:B, 6, 0:DH], last_cols[:, c, :], wkv[:, c, P:P + DH], start=(c == 0), stop=(c == 1))
                    done.then_inc(last_v_done, 1)
                if n >= 2:
                    pe.wait_ge(hidden_done, n - 1)
                for g in range(2):
                    for c in range(C):
                        done = nc.tensor.matmul(PS[:, 2 * (n % 2) + g, :], ff1[:, c, (g * HB + m) * P:(g * HB + m + 1) * P],
                                                core.HT[:, c, half * 512:(half + 1) * 512], start=(c == 0), stop=(c == 1))
                done.then_inc(up_done, 1)
            def flip_context(b, j):
                pe.wait_ge(ctx_normed, b + 1)
                for c in range(C):
                    for half in range(2):
                        done = nc.tensor.transpose(PS[:, 5, (2 * c + half) * P:(2 * c + half + 1) * P], ctx_n[j][:, half, c * P:(c + 1) * P], core.ident[:])
                done.then_inc(ctx_flipped, 1)

            def keys_values(b, j):
                pe.wait_ge(ctxT_copied, b + 1)
                pe.wait_ge(queries_done, b + 1)
                for half in range(2):
                    for c in range(C):
                        done = nc.tensor.matmul(PS[:, 6, half * DH:(half + 1) * DH], ctxT[j][:, c, half * P:(half + 1) * P], wkv[:, c, P:P + DH], start=(c == 0), stop=(c == 1))
                done.then_inc(v_done, 1)
                for c in range(C):
                    done = nc.tensor.matmul(PS[:, 4, 0:CTX], wkv[:, c, 0:P], ctxT[j][:, c, :], start=(c == 0), stop=(c == 1))
                done.then_inc(k_done, 1)

            def sim(b, j):
                pe.wait_ge(queries_done, b + 1)
                for u in range(U):
                    done = nc.tensor.matmul(PS[:, u, 0:CTX], queries[j][:, u // 2, 4 * (u % 2):4 * (u % 2) + 4, :].rearrange("p h q -> p (h q)"),
                                            kT[j][:], start=True, stop=True)
                    if u % 2:
                        done.then_inc(sim_done, 1)

            def flip_probs(b, j):
                pe.wait_ge(probs_done, b + 1)
                for half in (1, 0):
                    if not half and exists(b + 1):
                        pe.wait_ge(k_copied, b + 2)
                        pe.wait_ge(v_copied, b + 2)
                    elif half and exists(b + 2):
                        pe.wait_ge(ctxT_copied, b + 3)
                    for u in range(U):
                        nc.tensor.transpose(PS[:, 4 + half, u * P:(u + 1) * P], probs[j][:, u, half * P:(half + 1) * P], core.ident[:])
                nc.tensor.transpose(PS[0:U, 6, 3 * P:4 * P], probs[j][:, :, 2 * P], core.ident[:]).then_inc(pt_done, 1)

            def weigh(b, j):
                pe.wait_ge(pt_copied_act, b + 1)
                pe.wait_ge(pt_copied_dve, b + 1)
                pe.wait_ge(V_last_done, b + 1)
                pe.wait_ge(out_copied, b + 1)
                for n in range(2):
                    for key in range(3):
                        for par in range(2):
                            u = 2 * par + n
                            value, weight = ((V[j][:, key, :], probsT[j][:, key, u * P:(u + 1) * P]) if key < 2 else
                                             (V_last[j][:, u, :], probsT_last[j][:]))
                            done = nc.tensor.matmul(PS[DH * par:DH * (par + 1), 7, n * P:(n + 1) * P], value, weight, start=(key == 0), stop=(key == 2))
                done.then_inc(pv_done, 1)

            def first():
                pe.wait_ge(hidden_done, 2 * HB)
                flip_context(0, 0)
                for t in range(NT):
                    if t >= 3:
                        pe.wait_ge(ff_added, t - 2)
                    for m in range(HB):
                        done = nc.tensor.matmul(PS[:, t % 3, 0:D], hidden[:, m, t * P:(t + 1) * P], ff2[:, m, :], start=(m == 0), stop=(m == HB - 1))
                    done.then_inc(ff_done, 1)
                    if t == 0:
                        pe.wait_ge(ctxT_copied, 1)
                        flip_context(1, 1)
                    elif t == 2:
                        pe.wait_ge(last_rows_done, 1)
                        keys_values(0, 0)
                    elif t == 3:
                        pe.wait_ge(ctxT_copied, 2)
                        flip_context(2, 0)
                    elif t == 5:
                        pe.wait_ge(v_copied, 1)
                        pe.wait_ge(k_copied, 1)
                        keys_values(1, 1)
                pe.wait_ge(ff_added, NT)
                sim(0, 0)

            def turn(b, j):
                flip_probs(b, j)
                sim(b + 1, 1 - j)
                weigh(b, j)
                if exists(b + 3):
                    flip_context(b + 3, 1 - j)
                if exists(b + 2):
                    keys_values(b + 2, j)

            def last(b, j):
                flip_probs(b, j)
                weigh(b, j)

            over_batches(pe, first, turn, last)
            pe.wait_ge(out_copied, B + 1)
            for t in range(NT):
                for m in range(HB):
                    done = nc.tensor.matmul(PS[:, 4 + t // 2, (t % 2) * D:(t % 2 + 1) * D], AT[:, m, t * P:(t + 1) * P],
                                            wo[:, m, :], start=(m == 0), stop=(m == HB - 1))
                if t % 2:
                    done.then_inc(out_done, 1)

        @block.scalar
        def _(act):
            act.wait_ge(core.weights_in[3], 16)
            norm.scalar_twice(act)
            flip.scalar(act, core.HT, ln_g, ln_b)
            for n in range(2 * HB):
                o, half = n // 2, n % 2
                act.wait_ge(q_done, n + 1)
                nc.scalar.copy(QT[:, o, half * 512:(half + 1) * 512], PS[:, 4 + n % 4, :]).then_inc(q_copied, 1)
            cn.scalar(act)
            for n in range(2 * HB):
                act.wait_ge(up_done, n + 1)
                if n >= 2:
                    act.wait_ge(hidden_done, n - 1)
                nc.scalar.activation(side[n % 2], PS[:, 2 * (n % 2) + 1, :], ACT.Silu).then_inc(side_done, 1)

            def copy_context(b, j):
                act.wait_ge(ctx_flipped, b + 1)
                at_least(act, k_done, b - 1)
                for c in range(C):
                    done = nc.scalar.activation(ctxT[j][:, c, 0:2 * P], PS[:, 5, c * 2 * P:(c + 1) * 2 * P], ACT.Identity, bias=cln_b[:, c:c + 1], scale=cln_g[:, c:c + 1])
                done.then_inc(ctxT_copied, 1)

            def copy_keys(b, j):
                act.wait_ge(k_done, b + 1)
                nc.scalar.copy(kT[j][:], PS[:, 4, 0:CTX]).then_inc(k_copied, 1)

            def exps(b, j):
                for u in range(U):
                    if u % 2 == 0:
                        act.wait_ge(top_done, 2 * b + (u // 2 + 1))
                    done = nc.scalar.activation(probs[j][:, u, :], PS[:, u, 0:CTX], ACT.Exp, bias=top[j][:, u:u + 1], scale=scale,
                                                accum_out=total[j][:, u:u + 1])
                    if u % 2:
                        done.then_inc(exps_done, 1)

            def copy_probs(b, j):
                act.wait_ge(pt_done, b + 1)
                nc.scalar.copy(probsT[j][:, 0, :], PS[:, 4, :]).then_inc(pt_copied_act, 1)

            def copy_out(b, j):
                act.wait_ge(pv_done, b + 1)
                nc.scalar.copy(AT[:, :, bass.ds(b * S, S)], PS[:, 7, 0:2 * P].rearrange("p (m q) -> p m q", m=HB)).then_inc(out_copied, 1)

            def first():
                copy_context(0, 0)
                copy_context(1, 1)
                copy_keys(0, 0)
                copy_context(2, 0)
                copy_keys(1, 1)
                act.wait_ge(ff_done, NT)
                act.sem_inc(out_copied, 1)
                exps(0, 0)

            def turn(b, j):
                copy_probs(b, j)
                exps(b + 1, 1 - j)
                copy_out(b, j)
                if exists(b + 3):
                    copy_context(b + 3, 1 - j)
                if exists(b + 2):
                    copy_keys(b + 2, j)

            def last(b, j):
                copy_probs(b, j)
                copy_out(b, j)

            over_batches(act, first, turn, last)
            norm.load_table(act)

        @block.vector
        def _(dve):
            dve.wait_ge(core.x_in, 16)
            norm.vector(dve, core.X, core.H, normed_done)
            dve.wait_ge(core.weights_in[3], 16)
            flip.vector(dve, core.HT, ln_g, ln_b)
            cn.vector_stats(dve, ctx + ctx_n)
            cn.vector_finish(dve)
            for c in range(C):
                done = nc.vector.tensor_scalar(last_cols[:, c, :], cn.lastT[:, c, :], cln_g[:, c:c + 1], cln_b[:, c:c + 1], ALU.mult, ALU.add)
            done.then_inc(last_cols_done, 1)
            dve.wait_ge(last_cols_done, 1)
            before = 16 * (B // cn.SLOTS)

            dve.wait_ge(zeros_set, 4)

            def norm_context(b, j):
                at_least(dve, ctx_flipped, b - 1)
                dve.wait_ge(cn.slot_in[j], 8 * b + (before + 16 - 8 * j))
                for h in range(2):
                    done = nc.vector.tensor_scalar(ctx_n[j][:, h, :], ctx[j][:, h, :], cn.rstd[:, b, h:h + 1], cn.shift[:, b, h:h + 1], ALU.mult, ALU.add)
                done.then_inc(ctx_normed, 1)

            def copy_values(b, j):
                dve.wait_ge(v_done, b + 1)
                at_least(dve, pv_done, b - 1)
                nc.vector.tensor_copy(V[j][:].rearrange("p h d -> p (h d)"), PS[:, 6, 0:2 * DH]).then_inc(v_copied, 1)

            def tops(b, j):
                for n in range(2):
                    dve.wait_ge(sim_done, 2 * b + (n + 1))
                    t = top[j][:, 2 * n:2 * n + 2]
                    dve_step(dve, nc.vector.reduce_max(t, PS[:, 2 * n:2 * n + 2, 0:CTX], AX.X))
                    nc.vector.tensor_scalar(t, t, -scale, None, ALU.mult).then_inc(top_done, 1)

            def weights(b, j):
                for n in range(2):
                    dve.wait_ge(exps_done, 2 * b + (n + 1))
                    t = total[j][:, 2 * n:2 * n + 2]
                    dve_step(dve, nc.vector.reciprocal(t, t))
                    for u in range(2 * n, 2 * n + 2):
                        done = nc.vector.tensor_scalar(probs[j][:, u, :], probs[j][:, u, :], total[j][:, u:u + 1], None, ALU.mult)
                done.then_inc(probs_done, 1)

            def copy_probs(b, j):
                dve.wait_ge(pt_done, b + 1)
                nc.vector.tensor_copy(probsT[j][:, 1, :], PS[:, 5, :])
                nc.vector.tensor_copy(probsT_last[j][0:U], PS[0:U, 6, 3 * P:4 * P]).then_inc(pt_copied_dve, 1)

            def first():
                for n in range(2 * HB):
                    m, half = n // 2, n % 2
                    dve.wait_ge(side_done, n + 1)
                    nc.vector.tensor_tensor(hidden[:, m, half * 512:(half + 1) * 512], PS[:, 2 * (n % 2), :], side[n % 2], ALU.mult).then_inc(hidden_done, 1)
                    if n == 2:
                        dve.wait_ge(last_v_done, 1)
                        nc.vector.tensor_copy(last_rows[:], PS[0:B, 6, 0:DH]).then_inc(last_rows_done, 1)
                    elif 4 <= n < 6:
                        norm_context(n - 4, n - 4)
                for t in range(NT):
                    dve.wait_ge(ff_done, t + 1)
                    nc.vector.tensor_tensor(core.X[:, t, :], PS[:, t % 3, 0:D], core.X[:, t, :], ALU.add).then_inc(ff_added, 1)
                    if t == 0:
                        norm_context(2, 0)
                    elif t == 3:
                        copy_values(0, 0)
                    elif t == 6:
                        copy_values(1, 1)
                tops(0, 0)
                weights(0, 0)

            def turn(b, j):
                copy_probs(b, j)
                if exists(b + 3):
                    norm_context(b + 3, 1 - j)
                tops(b + 1, 1 - j)
                weights(b + 1, 1 - j)
                if exists(b + 2):
                    copy_values(b + 2, j)

            def last(b, j):
                copy_probs(b, j)

            over_batches(dve, first, turn, last, lambda i: dve_step.enter(i, 8), dve_step.leave)
            for n in range(NT // 2):
                dve.wait_ge(out_done, n + 1)
                x = core.X[:, 2 * n:2 * n + 2, :]
                written = nc.vector.tensor_tensor(x, PS[:, 4 + n, :].rearrange("p (t d) -> p t d", t=2), x, ALU.add)
                norm.take(dve, written, (2 * n, 2 * n + 1))

        cn.loads = B // cn.SLOTS + B // 2


def l1_self(core, load_next):
    nc, PS, norm, flip, dve_step, pool_step = core.nc, core.PS, core.norm, core.flip, core.dve_step, core.pool_step
    SETS, HEADS, DH = 4, 16, D // 16
    QB = SETS * C
    UNITS = NT * SETS
    LAG = SETS + 3
    PROJECT = LAG + SETS + 1
    assert SETS == TB
    w = core.arena(4)
    wq, wk, wv, wo = w.take(C, SETS * D), w.take(C, D), w.take(C, D), w.take(SETS * C, D)
    causal, head_of, batch_of = w.take(S), w.take(8), w.take(TB)
    scale = DH ** -0.5
    with ExitStack() as es:
        sb = lambda n, shape: core.sb("l1a_" + n, shape, es)
        two = lambda n, shape: [sb(f"{n}{i}", shape) for i in range(2)]
        sem = lambda n: core.sem("l1a_" + n)
        QT, KT = sb("QT", [P, QB, NT * P]), sb("KT", [P, C, NT * P])
        V = core.H[:].rearrange("p t (h two d) -> p t h two d", two=2, d=DH)
        padded = two("padded", [P, TB, HEADS // 2, 2, 2, DH])
        spread = two("spread", [P, C, TB, 8, S])
        scores, probsT = two("scores", [P, HEADS, S]), two("probsT", [P, HEADS, SETS, S])
        probs = [sb(f"probs{i}", [P, HEADS, S]) for i in range(3)]
        top, total = two("top", [P, HEADS]), two("total", [P, HEADS])
        rowsT = two("rowsT", [P, C, SETS, TB, S])
        rows_done, padded_done, qk_done, v_done = sem("rows_done"), sem("padded_done"), sem("qk_done"), sem("v_done")
        qk_act, qk_dve, v_copied = sem("qk_act"), sem("qk_dve"), sem("v_copied")
        spread_done, scores_done, scores_read, shifted = sem("spread_done"), sem("scores_done"), sem("scores_read"), sem("shifted")
        exps_done, total_done, probs_done, probsT_done = sem("exps_done"), sem("total_done"), sem("probs_done"), sem("probsT_done")
        out_done, rowsT_done, proj_done, added = (sem(n) for n in ("out_done", "rowsT_done", "proj_done", "added"))
        block = es.enter_context(nc.Block())

        @block.sync
        def _(sp):
            load_next(sp)

        @block.gpsimd
        def _(pool):
            for i in range(2):
                zeroed = nc.gpsimd.memset(padded[i][:], 0.0)
            pool_step(pool, zeroed)
            pool.wait_ge(core.weights_in[4], 16)
            pool.wait_ge(qk_act, C)
            pool.wait_ge(qk_dve, C)

            def spread_keys(t):
                if t >= 2:
                    pool.wait_ge(scores_done, SETS * (t - 1))
                for c in range(C):
                    done = nc.gpsimd.tensor_tensor(spread[t % 2][:, c], bcast(KT[:, c, t * P:(t + 1) * P].rearrange("p (b k) -> p b k", k=S), 2, 8),
                                                   bcast(bcast(head_of, 1, TB), 3, S), ALU.mult)
                done.then_inc(spread_done, 1)

            def pad_values(u):
                if u == 0:
                    pool.wait_ge(v_copied, NT // 2)
                if u >= 2:
                    pool.wait_ge(out_done, TB * (u - 1))
                for side in range(2):
                    done = nc.gpsimd.tensor_tensor(padded[u % 2][:, :, :, side, side, :], bcast(V[:, u, :, side, :], 1, TB),
                                                   bcast(bcast(batch_of, 2, HEADS // 2), 3, DH), ALU.mult)
                done.then_inc(padded_done, 1)

            spread_keys(0)
            spread_keys(1)
            for n in range(UNITS):
                if n % SETS == 0 and n:
                    pad_values(n // SETS - 1)
                pool.wait_ge(total_done, n + 1)
                p = probs[n % 3][:]
                nc.gpsimd.tensor_tensor(p, p, bcast(total[n % 2][:], 2, S), ALU.mult).then_inc(probs_done, 1)
                if n % SETS == SETS - 1 and n // SETS + 2 < NT:
                    spread_keys(n // SETS + 2)
            pad_values(NT - 1)

        @block.tensor
        def _(pe):
            pe.wait_ge(core.consts_in, 16)
            pe.wait_ge(core.weights_in[4], 16)
            flip.tensor(pe, core.H, rows_done, 0)
            flip.ready(pe, "pe")
            for t in range(NT):
                for c in range(C):
                    done = nc.tensor.matmul(PS[:, t // 2, (t % 2) * D:(t % 2 + 1) * D], core.HT[:, c, t * P:(t + 1) * P], wv[:, c, :],
                                            start=(c == 0), stop=(c == 1))
                if t % 2:
                    done.then_inc(v_done, 1)

            def by_feature(n):
                weight, at = (wk, n * P) if n < C else (wq, (n - C) * P)
                for half in range(2):
                    if n >= 2:
                        pe.wait_ge((qk_act, qk_dve)[half], n - 1)
                    for c in range(C):
                        done = nc.tensor.matmul(PS[:, 4 + 2 * (n % 2) + half, :], weight[:, c, at:at + P],
                                                core.HT[:, c, half * 512:(half + 1) * 512], start=(c == 0), stop=(c == 1))
                    done.then_inc(qk_done, 1)

            def values(u, b):
                if b == 0:
                    pe.wait_ge(probsT_done, SETS * (u + 1))
                    pe.wait_ge(padded_done, u + 1)
                if u:
                    pe.wait_ge(rowsT_done, TB * (u - 1) + b + 1)
                for c in range(C):
                    for side in range(2):
                        for block_at in range(4):
                            h = 8 * c + 2 * block_at + side
                            done = nc.tensor.matmul(PS[block_at * 32:(block_at + 1) * 32, 4 + b, c * P:(c + 1) * P],
                                                    padded[u % 2][:, b, h // 2, side].rearrange("p two d -> p (two d)"),
                                                    probsT[u % 2][:, h].rearrange("p g q -> p (g q)"),
                                                    start=(side == 0), stop=(side == 1))
                done.then_inc(out_done, 1)

            def project(u, part):
                if part == 0:
                    pe.wait_ge(rowsT_done, TB * (u + 1))
                    if u:
                        pe.wait_ge(added, u)
                for m in range(C * part, C * part + C):
                    done = nc.tensor.matmul(PS[:, 2, 0:D], rowsT[u % 2][:, m % C, m // C].rearrange("p b q -> p (b q)"), wo[:, m, :],
                                            start=(m == 0), stop=(m == SETS * C - 1))
                if part == SETS - 1:
                    done.then_inc(proj_done, 1)

            by_feature(0)
            by_feature(1)
            pe.wait_ge(v_copied, NT // 2)
            for n in range(UNITS + PROJECT):
                t, g = n // SETS, n % SETS
                if n < SETS:
                    for m in range(C):
                        by_feature(C * (n + 1) + m)
                    pe.wait_ge(qk_act, C * (n + 2))
                    pe.wait_ge(qk_dve, C * (n + 2))
                if n < UNITS:
                    if g == 0:
                        pe.wait_ge(spread_done, t + 1)
                    if n >= 2:
                        pe.wait_ge(scores_read, n - 1)
                    for c in range(C):
                        for b in range(TB):
                            done = nc.tensor.matmul(PS[b * S:(b + 1) * S, n % 2, c * 256:(c + 1) * 256],
                                                    QT[:, C * g + c, t * P + b * S:t * P + (b + 1) * S],
                                                    spread[t % 2][:, c, b].rearrange("p h k -> p (h k)"), start=True, stop=True)
                    done.then_inc(scores_done, 1)
                if 0 <= n - LAG < UNITS:
                    values((n - LAG) // TB, (n - LAG) % TB)
                if n >= PROJECT:
                    project((n - PROJECT) // SETS, (n - PROJECT) % SETS)

        @block.scalar
        def _(act):
            norm.scalar(act, core.eps5)
            flip.scalar(act, core.HT)

            def by_feature(n):
                act.wait_ge(qk_done, 2 * n + 1)
                dst = KT[:, n, :] if n < C else QT[:, n - C, :]
                nc.scalar.copy(dst[:, 0:512], PS[:, 4 + 2 * (n % 2), :]).then_inc(qk_act, 1)

            by_feature(0)
            by_feature(1)
            for n in range(UNITS + LAG):
                if n < SETS:
                    for m in range(C):
                        by_feature(C * (n + 1) + m)
                if n < UNITS:
                    act.wait_ge(shifted, n + 1)
                    if n >= 3:
                        act.wait_ge(probsT_done, n - 2)
                    nc.scalar.activation(probs[n % 3][:], scores[n % 2][:], ACT.Exp, scale=scale).then_inc(exps_done, 1)
                if n >= LAG:
                    u, b = (n - LAG) // TB, (n - LAG) % TB
                    act.wait_ge(out_done, n - LAG + 1)
                    if u >= 2 and b == 0:
                        act.wait_ge(proj_done, u - 1)
                    nc.scalar.copy(rowsT[u % 2][:, :, :, b, :], PS[:, 4 + b, 0:C * P].rearrange("p (c g q) -> p c g q", c=C, q=S)).then_inc(rowsT_done, 1)
            norm.load_table(act)

        @block.vector
        def _(dve):
            dve.wait_ge(core.x_in, 16)
            norm.vector(dve, core.X, core.H, rows_done)
            flip.vector(dve, core.HT)
            for j in range(NT // 2):
                dve.wait_ge(v_done, j + 1)
                done = nc.vector.tensor_copy(V[:, 2 * j:2 * j + 2].rearrange("p t h two d -> p (t h two d)"), PS[:, j, :])
                done.then_inc(v_copied, 1)

            def by_feature(n):
                dve.wait_ge(qk_done, 2 * n + 2)
                dst = KT[:, n, :] if n < C else QT[:, n - C, :]
                nc.vector.tensor_copy(dst[:, 512:1024], PS[:, 5 + 2 * (n % 2), :]).then_inc(qk_dve, 1)

            def add(u):
                dve.wait_ge(proj_done, u + 1)
                x = core.X[:, u, :]
                nc.vector.tensor_tensor(x, PS[:, 2, 0:D], x, ALU.add).then_inc(added, 1)
                if u % 2:
                    dve.wait_ge(added, u + 1)
                    norm.take(dve, None, (u - 1, u))

            by_feature(0)
            by_feature(1)
            for n in range(UNITS + PROJECT + 1):
                if n < SETS:
                    for m in range(C):
                        by_feature(C * (n + 1) + m)
                if n < UNITS:
                    i = n % 2
                    s = scores[i][:]
                    dve.wait_ge(scores_done, n + 1)
                    if n >= 2:
                        dve.wait_ge(exps_done, n - 1)
                    nc.vector.tensor_tensor(s, PS[:, i, :].rearrange("p (h k) -> p h k", k=S), bcast(causal, 1, HEADS), ALU.add).then_inc(scores_read, 1)
                    dve.wait_ge(scores_read, n + 1)
                    dve_step(dve, nc.vector.reduce_max(top[i][:], s, AX.X))
                    nc.vector.tensor_tensor(s, s, bcast(top[i][:], 2, S), ALU.subtract).then_inc(shifted, 1)
                if 1 <= n <= UNITS:
                    m = n - 1
                    dve.wait_ge(exps_done, m + 1)
                    if m >= 2:
                        dve.wait_ge(probs_done, m - 1)
                    dve_step(dve, nc.vector.reduce_sum(total[m % 2][:], probs[m % 3][:], AX.X))
                    nc.vector.reciprocal(total[m % 2][:], total[m % 2][:]).then_inc(total_done, 1)
                if 2 <= n <= UNITS + 1:
                    m = n - 2
                    dve.wait_ge(probs_done, m + 1)
                    if m >= 2 * SETS:
                        dve.wait_ge(out_done, TB * (m // SETS - 1))
                    nc.vector.transpose(probsT[m // SETS % 2][:, :, m % SETS, :], probs[m % 3][:]).then_inc(probsT_done, 1)
                if n >= PROJECT + SETS and (n - PROJECT) % SETS == 0:
                    add((n - PROJECT) // SETS - 1)


def l1_feed_forward(core, load_next):
    nc, PS, norm, flip, dve_step = core.nc, core.PS, core.norm, core.flip, core.dve_step
    E = EXPERTS[5][0] - 1
    w = core.arena(5)
    wg, bg, b2, number = w.take(C, E), w.take(E), w.take(D), w.take(E)
    with ExitStack() as es:
        ex = SortedExperts(core, es, "l1f", 5, "swiglu", 2, shared=True)
        bias = OutputBias(core, es, "l1f", E + 1)
        sb = lambda n, shape: core.sb("l1f_" + n, shape, es)
        scores, biased, gate = sb("scores", [P, NT, E]), sb("biased", [P, NT, E]), sb("gate", [P, NT, E + 1])
        first, second, chosen = sb("first", [P, NT, E]), sb("second", [P, NT, E]), sb("chosen", [P, NT, E])
        share = [sb(f"share{k}", [P, NT]) for k in range(2)]
        best, place, total = sb("best", [P, NT]), sb("place", [P, NT]), sb("total", [P, NT])
        rows_done, routed, chosen_done = core.sem("l1f_rows_done"), core.sem("l1f_routed"), core.sem("l1f_chosen_done")
        shifted, exps_done, weighed = core.sem("l1f_shifted"), core.sem("l1f_exps_done"), core.sem("l1f_weighed")
        block = es.enter_context(nc.Block())

        @block.sync
        def _(sp):
            load_next(sp)
            ex.load(sp)

        @block.gpsimd
        def _(pool):
            ex.scatter(pool, core.H, rows_done, 0)

        @block.tensor
        def _(pe):
            pe.wait_ge(core.consts_in, 16)
            pe.wait_ge(core.weights_in[5], 16)
            flip.tensor(pe, core.H, rows_done, 0)
            flip.ready(pe, "pe")
            router_tensor(core, pe, core.HT, wg, routed)
            pe.wait_ge(core.shared_in, 32)
            ex.tensor(pe, core.HT, lambda: ex.places.tensor(pe, chosen, chosen_done))
            pe.wait_ge(ex.out_copied, ex.N)
            bias.tensor(pe, gate, weighed, b2)

        @block.scalar
        def _(act):
            norm.scalar(act, core.eps5)
            flip.scalar(act, core.HT)
            act.wait_ge(shifted, 1)
            nc.scalar.activation(scores[:], scores[:], ACT.Exp).then_inc(exps_done, 1)
            act.wait_ge(core.shared_in, 32)
            ex.scalar(act)
            norm.load_table(act)

        @block.vector
        def _(dve):
            nc.vector.memset(ex.places.ones[:], 1.0)
            nc.vector.memset(gate[:], 1.0)
            dve.wait_ge(core.x_in, 16)
            norm.vector(dve, core.X, core.H, rows_done)
            flip.vector(dve, core.HT)
            dve.wait_ge(core.weights_in[5], 16)
            dve.wait_ge(routed, 1)
            logits = PS[:, 4, 0:NT * E].rearrange("p (t e) -> p t e", e=E)
            dve_step(dve, nc.vector.reduce_max(best[:], logits, AX.X))
            nc.vector.tensor_tensor(scores[:], logits, bcast(best[:], 2, E), ALU.subtract).then_inc(shifted, 1)
            dve.wait_ge(exps_done, 1)
            dve_step(dve, nc.vector.reduce_sum(total[:], scores[:], AX.X))
            dve_step(dve, nc.vector.reciprocal(total[:], total[:]))
            dve_step(dve, nc.vector.tensor_tensor(scores[:], scores[:], bcast(total[:], 2, E), ALU.mult))
            dve_step(dve, nc.vector.tensor_tensor(biased[:], scores[:], bcast(bg, 1, NT), ALU.add))
            first_best(core, dve, biased, number, best, place, first)
            dve_step(dve, nc.vector.scalar_tensor_tensor(biased[:], first[:], NEG, biased[:], ALU.mult, ALU.add))
            first_best(core, dve, biased, number, best, place, second)
            nc.vector.tensor_tensor(chosen[:], first[:], second[:], ALU.add).then_inc(chosen_done, 1)
            dve.wait_ge(chosen_done, 1)
            ex.places.vector(dve, (first, second))
            for k, choice in enumerate((first, second)):
                dve_step(dve, nc.vector.tensor_tensor(choice[:], choice[:], scores[:], ALU.mult))
                dve_step(dve, nc.vector.reduce_sum(share[k][:], choice[:], AX.X))
            nc.vector.tensor_tensor(gate[:, :, 0:E], first[:], second[:], ALU.add).then_inc(weighed, 1)
            ex.vector(dve, share, lambda: bias.vector(dve))


def l2_cross(core, load_next):
    nc, PS, norm, flip, dve_step = core.nc, core.PS, core.norm, core.flip, core.dve_step
    w = core.arena(6)
    wq, wk, wv, wo = w.take(C, D), w.take(C, D), w.take(C, D), w.take(C, D)
    bq, bk, bv, bo = w.take(C), w.take(C), w.take(D), w.take(D)
    head_of = w.take(8)
    own = w.take(4)
    last_tokens = w.take(C, B)
    scale = 16.0 ** -0.5
    U = 4
    with ExitStack() as es:
        sb = lambda n, shape: core.sb("l2x_" + n, shape, es)
        two = lambda n, shape: [sb(f"{n}{i}", shape) for i in range(2)]
        sem = lambda n: core.sem("l2x_" + n)
        QT, AT = sb("QT", [P, C, NT * P]), sb("AT", [P, C, NT * P])
        ctxT, spread, kT = two("ctxT", [P, C, CTX]), two("spread", [P, C, 8, S]), two("kT", [P, C, CTX])
        V, V_last = two("V", [P, 2, D]), two("V_last", [P, U, 64])
        last_rows, V_last_all = sb("last_rows", [B, D]), sb("V_last_all", [U, B, U, 64])
        probs, probsT, probsT_last = two("probs", [P, U, CTX]), two("probsT", [P, 2, U * P]), two("probsT_last", [P, P])
        top, total, own_out = two("top", [P, U]), two("total", [P, U]), sb("own_out", [P, C, 4, S])
        rows_done, q_done, q_copied = sem("rows_done"), sem("q_done"), sem("q_copied")
        ctx_in = [sem("ctx_in0"), sem("ctx_in1")]
        spread_done, k_done, v_done, k_copied, v_copied = (sem(n) for n in ("spread_done", "k_done", "v_done", "k_copied", "v_copied"))
        sim_done, top_done, exps_done, probs_done = sem("sim_done"), sem("top_done"), sem("exps_done"), sem("probs_done")
        last_v_done, last_rows_done, last_placed, V_last_done = sem("last_v_done"), sem("last_rows_done"), sem("last_placed"), sem("V_last_done")
        zeros_set, last_stored = sem("zeros_set"), sem("last_stored")
        last_v_dram = nc.dram_tensor("l2x_last_v_dram", (B, D), F32).ap()
        pt_done, pt_copied_act, pt_copied_dve = sem("pt_done"), sem("pt_copied_act"), sem("pt_copied_dve")
        pv_done, own_done, at_done, out_done = (sem(n) for n in ("pv_done", "own_done", "at_done", "out_done"))
        block = es.enter_context(nc.Block())

        @block.sync
        def _(sp):
            for j in range(2):
                sp.dma_start(ctxT[j][:], core.dram["ctxT"][j]).then_inc(ctx_in[j], 16)
            load_next(sp)
            sp.wait_ge(last_rows_done, 1)
            sp.dma_start(last_v_dram, last_rows[:]).then_inc(last_stored, 16)
            sp.wait_ge(last_stored, 16)
            sp.wait_ge(zeros_set, 5)
            for u in range(U):
                sp.dma_start(V_last_all[u:u + 1, :, u, :], last_v_dram[:, u * 64:(u + 1) * 64].unsqueeze(0)).then_inc(last_placed, 16)
            with sp.Fori(0, B // 2 - 1) as i:
                for j in range(2):
                    sp.wait_ge(k_done, 4 * i + (2 * j + 2))
                    sp.dma_start(ctxT[j][:], core.dram["ctxT"][2 * i + (j + 2)]).then_inc(ctx_in[j], 16)

        @block.gpsimd
        def _(pool):
            nc.gpsimd.memset(V_last_all[:], 0.0).then_inc(zeros_set, 1)
            for j in range(2):
                nc.gpsimd.memset(V_last[j][:], 0.0).then_inc(zeros_set, 1)
                nc.gpsimd.memset(probsT_last[j][:], 0.0).then_inc(zeros_set, 1)
            pool.wait_ge(zeros_set, 5)
            pool.wait_ge(core.weights_in[6], 16)
            pool.wait_ge(q_copied, 4)

            def prepare(b, j):
                at_least(pool, sim_done, 2 * b - 2)
                for c in range(C):
                    last = nc.gpsimd.tensor_tensor(spread[j][:, c], bcast(QT[:, c, bass.ds(b * S, S)], 1, 8), bcast(head_of, 2, S), ALU.mult)
                last.then_inc(spread_done, 1)
                at_least(pool, pv_done, b - 1)
                nc.gpsimd.tensor_copy(V_last[j][0:U].unsqueeze(1), V_last_all[:, bass.ds(b, 1), :, :]).then_inc(V_last_done, 1)

            pool.wait_ge(last_placed, 16 * U)
            prepare(0, 0)
            prepare(1, 1)
            with pool.Fori(0, B // 2 - 1) as i:
                for j in range(2):
                    prepare(2 * i + (j + 2), j)

        @block.tensor
        def _(pe):
            pe.wait_ge(core.consts_in, 16)
            pe.wait_ge(core.weights_in[6], 16)
            flip.tensor(pe, core.H, rows_done, 0)
            flip.ready(pe, "pe")
            for n in range(4):
                o, half = n // 2, n % 2
                for c in range(C):
                    last = nc.tensor.matmul(PS[:, n, :], wq[:, c, o * P:(o + 1) * P], core.HT[:, c, half * 512:(half + 1) * 512],
                                            start=(c == 0), stop=(c == 1))
                last.then_inc(q_done, 1)

            for c in range(C):
                last = nc.tensor.matmul(PS[0:B, 7, 0:D], last_tokens[:, c, :], wv[:, c, :], start=(c == 0), stop=(c == 1))
            last.then_inc(last_v_done, 1)

            def keys_values(b, j):
                pe.wait_ge(ctx_in[j], 8 * b + (16 - 8 * j))
                for half in range(2):
                    for c in range(C):
                        last = nc.tensor.matmul(PS[:, 5, half * D:(half + 1) * D], ctxT[j][:, c, half * P:(half + 1) * P], wv[:, c, :], start=(c == 0), stop=(c == 1))
                last.then_inc(v_done, 1)
                for o in range(C):
                    for c in range(C):
                        last = nc.tensor.matmul(PS[:, 4 + 2 * o, 0:CTX], wk[:, c, o * P:(o + 1) * P], ctxT[j][:, c, :], start=(c == 0), stop=(c == 1))
                    last.then_inc(k_done, 1)

            def sim(b, j):
                pe.wait_ge(spread_done, b + 1)
                for u in range(U):
                    c = u // 2
                    last = nc.tensor.matmul(PS[:, u, 0:CTX], spread[j][:, c, 4 * (u % 2):4 * (u % 2) + 4, :].rearrange("p h q -> p (h q)"),
                                            kT[j][:, c, :], start=True, stop=True)
                    if u % 2:
                        last.then_inc(sim_done, 1)

            def flip_probs(b, j):
                pe.wait_ge(probs_done, b + 1)
                for half in (1, 0):
                    if exists(b + 1):
                        pe.wait_ge((k_copied, v_copied)[half], b + 2)
                    for u in range(U):
                        nc.tensor.transpose(PS[:, 4 + half, u * P:(u + 1) * P], probs[j][:, u, half * P:(half + 1) * P], core.ident[:])
                nc.tensor.transpose(PS[0:U, 6, 3 * P:4 * P], probs[j][:, :, 2 * P], core.ident[:]).then_inc(pt_done, 1)

            def weigh(b, j):
                pe.wait_ge(pt_copied_act, b + 1)
                pe.wait_ge(pt_copied_dve, b + 1)
                pe.wait_ge(V_last_done, b + 1)
                pe.wait_ge(own_done, b + 1)
                for c in range(C):
                    for par in range(2):
                        u = 2 * c + par
                        out = PS[64 * par:64 * (par + 1), 7, c * P:(c + 1) * P]
                        for half in range(2):
                            nc.tensor.matmul(out, V[j][:, half, u * 64:(u + 1) * 64], probsT[j][:, half, u * P:(u + 1) * P], start=(half == 0), stop=False)
                        last = nc.tensor.matmul(out, V_last[j][:, u, :], probsT_last[j][:], start=False, stop=True)
                last.then_inc(pv_done, 1)

            def first():
                pe.wait_ge(q_copied, 4)
                for b in range(2):
                    if b:
                        pe.wait_ge(v_copied, b)
                        pe.wait_ge(k_copied, b)
                    keys_values(b, b)
                pe.wait_ge(k_copied, 1)
                sim(0, 0)

            def turn(b, j):
                flip_probs(b, j)
                sim(b + 1, 1 - j)
                weigh(b, j)
                if exists(b + 2):
                    keys_values(b + 2, j)

            def last(b, j):
                flip_probs(b, j)
                weigh(b, j)

            over_batches(pe, first, turn, last)
            pe.wait_ge(at_done, B)
            for t in range(NT):
                for c in range(C):
                    done = nc.tensor.matmul(PS[:, 4 + t // 2, (t % 2) * D:(t % 2 + 1) * D], AT[:, c, t * P:(t + 1) * P],
                                            wo[:, c, :], start=(c == 0), stop=(c == 1))
                if t % 2:
                    done.then_inc(out_done, 1)

        @block.scalar
        def _(act):
            norm.scalar(act, core.eps5)
            flip.scalar(act, core.HT)
            act.wait_ge(core.weights_in[6], 16)
            for n in range(4):
                o, half = n // 2, n % 2
                act.wait_ge(q_done, n + 1)
                nc.scalar.activation(QT[:, o, half * 512:(half + 1) * 512], PS[:, n, :], ACT.Identity, bias=bq[:, o:o + 1]).then_inc(q_copied, 1)

            def copy_keys(b, j):
                for o in range(C):
                    act.wait_ge(k_done, 2 * b + (o + 1))
                    done = nc.scalar.activation(kT[j][:, o, :], PS[:, 4 + 2 * o, 0:CTX], ACT.Identity, bias=bk[:, o:o + 1])
                done.then_inc(k_copied, 1)

            def exps(b, j):
                for u in range(U):
                    if u % 2 == 0:
                        act.wait_ge(top_done, 2 * b + (u // 2 + 1))
                    done = nc.scalar.activation(probs[j][:, u, :], PS[:, u, 0:CTX], ACT.Exp, bias=top[j][:, u:u + 1], scale=scale,
                                                accum_out=total[j][:, u:u + 1])
                    if u % 2:
                        done.then_inc(exps_done, 1)

            def copy_probs(b, j):
                act.wait_ge(pt_done, b + 1)
                nc.scalar.copy(probsT[j][:, 0, :], PS[:, 4, :]).then_inc(pt_copied_act, 1)

            def first():
                copy_keys(0, 0)
                copy_keys(1, 1)
                exps(0, 0)

            def turn(b, j):
                copy_probs(b, j)
                exps(b + 1, 1 - j)
                if exists(b + 2):
                    copy_keys(b + 2, j)

            over_batches(act, first, turn, copy_probs)
            norm.load_table(act)

        @block.vector
        def _(dve):
            dve.wait_ge(core.x_in, 16)
            norm.vector(dve, core.X, core.H, rows_done)
            flip.vector(dve, core.HT)
            dve.wait_ge(core.weights_in[6], 16)

            dve.wait_ge(zeros_set, 5)
            dve.wait_ge(last_v_done, 1)
            nc.vector.tensor_tensor(last_rows[:], PS[0:B, 7, 0:D], bv[0:B, :], ALU.add).then_inc(last_rows_done, 1)
            dve.sem_inc(own_done, 1)

            def copy_values(b, j):
                dve.wait_ge(v_done, b + 1)
                at_least(dve, pv_done, b - 1)
                nc.vector.tensor_tensor(V[j][:], PS[:, 5, :].rearrange("p (k d) -> p k d", k=2), bcast(bv, 1, 2), ALU.add).then_inc(v_copied, 1)

            def tops(b, j):
                for n in range(2):
                    dve.wait_ge(sim_done, 2 * b + (n + 1))
                    t = top[j][:, 2 * n:2 * n + 2]
                    dve_step(dve, nc.vector.reduce_max(t, PS[:, 2 * n:2 * n + 2, 0:CTX], AX.X))
                    nc.vector.tensor_scalar(t, t, -scale, None, ALU.mult).then_inc(top_done, 1)

            def weights(b, j):
                for n in range(2):
                    dve.wait_ge(exps_done, 2 * b + (n + 1))
                    t = total[j][:, 2 * n:2 * n + 2]
                    dve_step(dve, nc.vector.reciprocal(t, t))
                    for u in range(2 * n, 2 * n + 2):
                        done = nc.vector.tensor_scalar(probs[j][:, u, :], probs[j][:, u, :], total[j][:, u:u + 1], None, ALU.mult)
                done.then_inc(probs_done, 1)

            def copy_probs(b, j):
                dve.wait_ge(pt_done, b + 1)
                nc.vector.tensor_copy(probsT[j][:, 1, :], PS[:, 5, :])
                nc.vector.tensor_copy(probsT_last[j][0:U], PS[0:U, 6, 3 * P:4 * P]).then_inc(pt_copied_dve, 1)

            def keep_own(b, j):
                dve.wait_ge(pv_done, b + 1)
                nc.vector.tensor_tensor(own_out[:], PS[:, 7, 0:C * P].rearrange("p (c h q) -> p c h q", c=C, q=S),
                                        bcast(bcast(own, 1, C), 3, S), ALU.mult).then_inc(own_done, 1)
                dve.wait_ge(own_done, b + 2)
                nc.vector.reduce_sum(AT[:, :, bass.ds(b * S, S)], own_out[:].rearrange("p c h q -> p c q h"), AX.X).then_inc(at_done, 1)
                dve.wait_ge(at_done, b + 1)

            def first():
                copy_values(0, 0)
                copy_values(1, 1)
                tops(0, 0)
                weights(0, 0)

            def turn(b, j):
                copy_probs(b, j)
                tops(b + 1, 1 - j)
                keep_own(b, j)
                weights(b + 1, 1 - j)
                if exists(b + 2):
                    copy_values(b + 2, j)

            def last(b, j):
                copy_probs(b, j)
                keep_own(b, j)

            over_batches(dve, first, turn, last, lambda i: dve_step.enter(i, 8), dve_step.leave)
            for n in range(NT // 2):
                x = core.X[:, 2 * n:2 * n + 2, :]
                dve_step(dve, nc.vector.tensor_tensor(x, x, bcast(bo, 1, 2), ALU.add))
                dve.wait_ge(out_done, n + 1)
                written = nc.vector.tensor_tensor(x, PS[:, 4 + n, :].rearrange("p (t d) -> p t d", t=2), x, ALU.add)
                norm.take(dve, written, (2 * n, 2 * n + 1))


def l2_self(core, load_next):
    nc, norm, flip, dve_step = core.nc, core.norm, core.flip, core.dve_step
    w = core.arena(7)
    wqk, wv, wo = w.take(C, 2 * D), w.take(C, D), w.take(C, D)
    cos, sin, causal, head_of, batch_of = w.take(8), w.take(8), w.take(S), w.take(8), w.take(TB)
    cap = 50.0
    with ExitStack() as es:
        at = SelfAttention(core, es, "l2a", "capped", cap)
        at.tanh_scale = 16.0 ** -0.5 / cap
        squares = [core.sb(f"l2a_squares{i}", [P, 2 * D], es) for i in range(2)]
        size = core.sb("l2a_size", [P, NT, 32], es)
        rows_done, normed = core.sem("l2a_rows_done"), core.sem("l2a_normed")

        def pairs(rows):
            heads = rows.rearrange("p (h d) -> p h d", h=32)
            return heads[:, :, 0:8], heads[:, :, 8:16]

        rotation = Rotation(core, es, at, pairs, cos, sin, normed)
        block = es.enter_context(nc.Block())

        @block.sync
        def _(sp):
            load_next(sp)

        @block.tensor
        def _(pe):
            pe.wait_ge(core.consts_in, 16)
            pe.wait_ge(core.weights_in[7], 16)
            flip.tensor(pe, core.H, rows_done, 0)
            flip.ready(pe, "pe")
            at.project(pe, core.HT, core.HT, wqk, wv)
            at.flip_tensor(pe)
            flip.ready(pe, "pe")
            at.attend_tensor(pe, wo)

        @block.gpsimd
        def _(pool):
            at.set_zeros(pool)
            pool.wait_ge(core.weights_in[7], 16)
            rotation.gpsimd(pool)
            flip.uses["pool"] = flip.uses["pe"]
            flip.ready(pool, "pool")
            at.spread_keys(pool, head_of)

        @block.scalar
        def _(act):
            norm.scalar(act, core.eps5)
            flip.scalar(act, core.HT)
            at.copy_projections(act, squares, size, bias=core.eps5, scale=1.0 / 16)
            flip.scalar(act, at.QT)
            flip.scalar(act, at.KT)
            at.attend_scalar(act, batch_of)
            norm.load_table(act)

        @block.vector
        def _(dve):
            dve.wait_ge(core.x_in, 16)
            norm.vector(dve, core.X, core.H, rows_done)
            flip.vector(dve, core.HT)
            dve.wait_ge(core.weights_in[7], 16)
            for t in range(NT + 2):
                if t < NT:
                    at.sum_squares(dve, t, squares, size)
                if 1 <= t <= NT:
                    u = t - 1
                    dve.wait_ge(at.rooted, u + 1)
                    dve_step(dve, nc.vector.reciprocal(size[:, u, :], size[:, u, :]))
                    heads = at.QK[:, u, :].rearrange("p (h d) -> p h d", h=32)
                    nc.vector.tensor_tensor(heads, heads, bcast(size[:, u, :], 2, 16), ALU.mult).then_inc(normed, 1)
                    rotation.cosine_products(dve, u)
                if t >= 2:
                    rotation.combine(dve, t - 2)
            flip.vector(dve, at.QT)
            flip.vector(dve, at.KT)
            at.attend_vector(dve, causal)


def l2_feed_forward(core, load_next):
    nc, PS, norm, flip, dve_step = core.nc, core.PS, core.norm, core.flip, core.dve_step
    E = 8
    w = core.arena(8)
    experts, wg, number = w.take(C, E * D), w.take(C, E), w.take(E)
    with ExitStack() as es:
        sb = lambda n, shape: core.sb("l2f_" + n, shape, es)
        scores, gate = sb("scores", [P, NT, E]), sb("gate", [P, NT, E])
        best, place = sb("best", [P, NT]), sb("place", [P, NT])
        rows_done, routed = core.sem("l2f_rows_done"), core.sem("l2f_routed")
        expert_done, summed = core.sem("l2f_expert_done"), core.sem("l2f_summed")
        block = es.enter_context(nc.Block())

        @block.sync
        def _(sp):
            load_next(sp)

        @block.tensor
        def _(pe):
            pe.wait_ge(core.consts_in, 16)
            pe.wait_ge(core.weights_in[8], 16)
            flip.tensor(pe, core.H, rows_done, 0)
            flip.ready(pe, "pe")
            router_tensor(core, pe, core.HT, wg, routed)
            with pe.Fori(0, E // 2) as i:
                for t in range(NT):
                    pe.wait_ge(summed, i * NT + (t + 1))
                    for c in range(C):
                        last = nc.tensor.matmul(PS[:, t % 4, :], core.HT[:, c, t * P:(t + 1) * P],
                                                experts[:, c, bass.ds(i * (2 * D), 2 * D)], start=(c == 0), stop=(c == 1))
                    last.then_inc(expert_done, 1)

        @block.scalar
        def _(act):
            norm.scalar(act, core.eps5)
            flip.scalar(act, core.HT)
            norm.load_table(act)

        @block.vector
        def _(dve):
            dve.sem_inc(summed, 4)
            dve.wait_ge(core.x_in, 16)
            norm.vector(dve, core.X, core.H, rows_done)
            flip.vector(dve, core.HT)
            dve.wait_ge(rows_done, NT)
            nc.vector.tensor_tensor(core.X[:], core.X[:], core.H[:], ALU.add)
            dve.wait_ge(core.weights_in[8], 16)
            dve.wait_ge(routed, 1)
            dve_step(dve, nc.vector.tensor_copy(scores[:], PS[:, 4, 0:NT * E].rearrange("p (t e) -> p t e", e=E)))
            first_best(core, dve, scores, number, best, place, gate)
            with dve.Fori(0, E // 2) as i:
                dve_step.enter(i, 2)
                for half in range(2):
                    for t in range(4 * half, 4 * half + 4):
                        dve.wait_ge(expert_done, i * NT + (t + 1))
                        bank = PS[:, t % 4, :].rearrange("p (e d) -> p e d", e=2)
                        step = nc.vector.scalar_tensor_tensor(core.X[:, t, :], bank[:, 0, :], gate[:, t, bass.ds(2 * i, 1)], core.X[:, t, :], ALU.mult, ALU.add)
                    dve_step(dve, step)
                    for t in range(4 * half, 4 * half + 4):
                        bank = PS[:, t % 4, :].rearrange("p (e d) -> p e d", e=2)
                        nc.vector.scalar_tensor_tensor(core.X[:, t, :], bank[:, 1, :], gate[:, t, bass.ds(2 * i + 1, 1)], core.X[:, t, :],
                                                       ALU.mult, ALU.add).then_inc(summed, 1)
                dve.wait_ge(summed, i * NT + (NT + 4))
                dve_step.leave(E // 2)


def l3_cross(core, load_next):
    nc, PS, norm, flip, cn = core.nc, core.PS, core.norm, core.flip, core.ctx_norm
    dve_step, pool_step = core.dve_step, core.pool_step
    HEADS, DH = 8, 64
    M = HEADS // 2
    KEYS, REST = CTX + S, CTX + S - 2 * P
    w = core.arena(9)
    wq, wkT, wv, wout = w.take(C, M * P), w.take(M, D), w.take(C, M * P), w.take(M, D)
    gm, bm, gl, bl = w.take(C), w.take(C), w.take(C), w.take(C)
    gm_row, bm_row, gl_row, bl_row = w.take(D), w.take(D), w.take(D), w.take(D)
    scale = DH ** 0.5
    with ExitStack() as es:
        sb = lambda n, shape: core.sb("l3x_" + n, shape, es)
        two = lambda n, shape: [sb(f"{n}{i}", shape) for i in range(2)]
        sem = lambda n: core.sem("l3x_" + n)
        QT = OT = sb("QT", [P, M, NT * P])
        QW = sb("QW", [P, C, HEADS, NT * P])
        last_cols, last_rows = sb("last_cols", [P, C, B]), sb("last_rows", [B, D])
        ctx, hat, tokens = two("ctx", [P, 2, D]), two("hat", [P, 2, D]), two("tokens", [P, 2, D])
        keysT, queries = two("keysT", [P, C, KEYS]), two("queries", [P, C, HEADS * S])
        probs, probsT = two("probs", [P, 2, KEYS]), two("probsT", [P, 2, HEADS * S])
        rest, probsT_rest = ([core.H[0:REST, k + j, :] for j in range(2)] for k in (0, 2))
        top, total = two("top", [P, 2]), two("total", [P, 2])
        latents_dram = nc.dram_tensor("latents_dram", (B * S, D), F32).ap()
        last_dram = nc.dram_tensor("last_dram", (B, D), F32).ap()
        normed_done, affine_done, stored = sem("normed_done"), sem("affine_done"), sem("stored")
        q_done, q_copied, qw_done, qw_act, qw_dve = sem("q_done"), sem("q_copied"), sem("qw_done"), sem("qw_act"), sem("qw_dve")
        rest_in = [sem("rest_in0"), sem("rest_in1")]
        last_done, hat_done, ctx_flipped, ctxT_copied = sem("last_done"), sem("hat_done"), sem("ctx_flipped"), sem("ctxT_copied")
        prep_done, tokens_done, sim_done, top_done = sem("prep_done"), sem("tokens_done"), sem("sim_done"), sem("top_done")
        exps_done, probs_done, pt_done, pt_act, pt_dve = (sem(n) for n in ("exps_done", "probs_done", "pt_done", "pt_act", "pt_dve"))
        pv_done, px_copied, out_done, out_act, out_dve, proj_done = (sem(n) for n in ("pv_done", "px_copied", "out_done", "out_act", "out_dve", "proj_done"))
        tile = lambda b: core.dram["ctx"][b, 0:2 * P, :].rearrange("(h p) d -> p h d", p=P)
        before = 16 * cn.loads
        AHEAD = (HEADS * C - 7, HEADS * C - 3)
        block = es.enter_context(nc.Block())

        @block.sync
        def _(sp):
            for j in range(2):
                sp.dma_start(ctx[j][:], tile(j)).then_inc(cn.slot_in[j], 16)
            load_next(sp)
            sp.wait_ge(last_done, 2)
            sp.dma_start(last_dram, last_rows[:]).then_inc(stored, 16)
            sp.wait_ge(affine_done, 1)
            for f in range(TB):
                sp.dma_start(latents_dram.rearrange("(t f q) d -> f q t d", f=TB, q=S)[f],
                             core.H[f * S:(f + 1) * S, :, :]).then_inc(stored, 16)
            sp.wait_ge(stored, 16 * (TB + 1))

            def load_rest(b, j):
                sp.dma_start(rest[j][0:S, :], latents_dram[bass.ds(b * S, S), :]).then_inc(rest_in[j], 16)
                sp.dma_start(rest[j][S:REST, :], last_dram[bass.ds(b, 1), :]).then_inc(rest_in[j], 16)

            def load_context(b, j):
                sp.wait_ge(hat_done, b - 1)
                sp.dma_start(ctx[j][:], tile(b)).then_inc(cn.slot_in[j], 16)

            def turn(b, j):
                if exists(b + 1):
                    load_context(b + 1, 1 - j)
                sp.wait_ge(pv_done, b - 1)
                load_rest(b, j)

            load_rest(0, 0)
            load_rest(1, 1)
            load_context(2, 0)
            with sp.Fori(0, B // 2 - 2) as i:
                turn(2 * i + 2, 0)
                turn(2 * i + 3, 1)
            turn(B - 2, 0)
            turn(B - 1, 1)

        @block.gpsimd
        def _(pool):
            pool.wait_ge(core.weights_in[9], 16)
            pool.wait_ge(last_done, 2)

            def prepare(b, j):
                at_least(pool, sim_done, b - 1)
                nc.gpsimd.tensor_copy(queries[j][:].rearrange("p c (h q) -> p c h q", q=S), QW[:, :, :, bass.ds(b * S, S)])
                nc.gpsimd.tensor_copy(keysT[j][:, :, 2 * P:2 * P + S], core.HT[:, :, bass.ds(b * S, S)])
                nc.gpsimd.tensor_copy(keysT[j][:, :, KEYS - 1:KEYS], last_cols[:, :, bass.ds(b, 1)]).then_inc(prep_done, 1)

            def scale_tokens(b, j):
                pool.wait_ge(hat_done, b + 1)
                at_least(pool, pv_done, b - 1)
                pool_step(pool, nc.gpsimd.tensor_tensor(tokens[j][:], hat[j][:], bcast(gm_row, 1, 2), ALU.mult))
                nc.gpsimd.tensor_tensor(tokens[j][:], tokens[j][:], bcast(bm_row, 1, 2), ALU.add).then_inc(tokens_done, 1)
                pool.wait_ge(tokens_done, b + 1)

            def first():
                scale_tokens(0, 0)
                scale_tokens(1, 1)
                pool.wait_ge(qw_act, HEADS * C)
                pool.wait_ge(qw_dve, HEADS * C)
                prepare(0, 0)
                prepare(1, 1)

            def turn(b, j):
                if exists(b + 2):
                    prepare(b + 2, j)
                    scale_tokens(b + 2, j)

            over_batches(pool, first, turn, lambda b, j: None, lambda i: pool_step.enter(i, 2), pool_step.leave)

        @block.tensor
        def _(pe):
            pe.wait_ge(core.consts_in, 16)
            pe.wait_ge(core.weights_in[9], 16)
            flip.tensor(pe, core.H, normed_done, 0)
            flip.ready(pe, "pe")
            for n in range(2 * M):
                m, half = n // 2, n % 2
                if n >= 4:
                    pe.wait_ge(q_copied, n - 3)
                for c in range(C):
                    done = nc.tensor.matmul(PS[:, 4 + n % 4, :], wq[:, c, m * P:(m + 1) * P], core.HT[:, c, half * 512:(half + 1) * 512],
                                            start=(c == 0), stop=(c == 1))
                done.then_inc(q_done, 1)
            def flip_context(b, j):
                pe.wait_ge(hat_done, b + 1)
                at_least(pe, ctxT_copied, b)
                for c in range(C):
                    for half in range(2):
                        done = nc.tensor.transpose(PS[:, 6, (2 * c + half) * P:(2 * c + half + 1) * P], hat[j][:, half, c * P:(c + 1) * P], core.ident[:])
                done.then_inc(ctx_flipped, 1)

            def sim(b, j):
                pe.wait_ge(ctxT_copied, b + 1)
                pe.wait_ge(prep_done, b + 1)
                for u in range(2):
                    for c in range(C):
                        done = nc.tensor.matmul(PS[:, 2 * j + u, 0:KEYS], queries[j][:, c, u * P:(u + 1) * P], keysT[j][:, c, :],
                                                start=(c == 0), stop=(c == 1))
                done.then_inc(sim_done, 1)

            def flip_probs(b, j):
                pe.wait_ge(probs_done, b + 1)
                for u in range(2):
                    for half in range(2):
                        nc.tensor.transpose(PS[:, 4, half * 2 * P + u * P:half * 2 * P + (u + 1) * P], probs[j][:, u, half * P:(half + 1) * P], core.ident[:])
                    done = nc.tensor.transpose(PS[0:REST, 5, u * P:(u + 1) * P], probs[j][:, u, 2 * P:KEYS], core.ident[:])
                done.then_inc(pt_done, 1)

            def weigh(b, j):
                pe.wait_ge(pt_act, b + 1)
                pe.wait_ge(pt_dve, b + 1)
                pe.wait_ge(tokens_done, b + 1)
                pe.wait_ge(rest_in[j], 16 * b + (32 - 16 * j))
                pe.wait_ge(px_copied, b + 1)
                for c in range(C):
                    out = PS[:, 7, c * 2 * P:(c + 1) * 2 * P]
                    for half in range(2):
                        nc.tensor.matmul(out, tokens[j][:, half, c * P:(c + 1) * P], probsT[j][:, half, :], start=(half == 0), stop=False)
                    done = nc.tensor.matmul(out, rest[j][:, c * P:(c + 1) * P], probsT_rest[j], start=False, stop=True)
                done.then_inc(pv_done, 1)

            def first():
                pe.wait_ge(q_copied, 2 * M)
                for n in range(HEADS * C):
                    m, c, half = n // (2 * C), n // 2 % C, n % 2
                    if n >= 2:
                        pe.wait_ge(qw_act, n - 1)
                        pe.wait_ge(qw_dve, n - 1)
                    for par in range(2):
                        rows = slice(DH * par, DH * (par + 1))
                        nc.tensor.matmul(PS[:, 2 * (n % 2) + par, :], wkT[rows, m, c * P:(c + 1) * P], QT[rows, m, half * 512:(half + 1) * 512],
                                         start=True, stop=True).then_inc(qw_done, 1)
                    if n in AHEAD:
                        flip_context(AHEAD.index(n), AHEAD.index(n))
                pe.wait_ge(qw_act, HEADS * C)
                pe.wait_ge(qw_dve, HEADS * C)
                sim(0, 0)

            def turn(b, j):
                flip_probs(b, j)
                sim(b + 1, 1 - j)
                if exists(b + 2):
                    flip_context(b + 2, j)
                weigh(b, j)

            def last(b, j):
                flip_probs(b, j)
                weigh(b, j)

            over_batches(pe, first, turn, last)
            pe.wait_ge(px_copied, B + 1)
            for n in range(2 * M):
                m, half = n // 2, n % 2
                if n >= 2:
                    pe.wait_ge((out_act, out_dve)[n % 2], n // 2)
                for par in range(2):
                    for c in range(C):
                        at = (2 * m + par) * DH
                        done = nc.tensor.matmul(PS[DH * par:DH * (par + 1), n % 2, :], wv[:, c, at:at + DH], QW[:, c, 2 * m + par, half * 512:(half + 1) * 512],
                                                start=(c == 0), stop=(c == 1))
                done.then_inc(out_done, 1)
            pe.wait_ge(out_act, M)
            pe.wait_ge(out_dve, M)
            for t in range(NT):
                for m in range(M):
                    done = nc.tensor.matmul(PS[:, 4 + t // 2, (t % 2) * D:(t % 2 + 1) * D], OT[:, m, t * P:(t + 1) * P], wout[:, m, :],
                                            start=(m == 0), stop=(m == M - 1))
                if t % 2:
                    done.then_inc(proj_done, 1)

        @block.scalar
        def _(act):
            act.wait_ge(core.weights_in[9], 16)
            norm.scalar_twice(act)
            flip.scalar(act, core.HT, gl, bl)
            for n in range(2 * M):
                act.wait_ge(q_done, n + 1)
                nc.scalar.copy(QT[:, n // 2, (n % 2) * 512:(n % 2 + 1) * 512], PS[:, 4 + n % 4, :]).then_inc(q_copied, 1)
            def normalise(b, j):
                act.wait_ge(cn.slot_in[j], 8 * b + (before + 16 - 8 * j))
                at_least(act, ctx_flipped, b - 1)
                at_least(act, tokens_done, b - 1)
                for h in range(2):
                    done = nc.scalar.activation(hat[j][:, h, :], ctx[j][:, h, :], ACT.Identity, bias=cn.shift[:, b, h:h + 1], scale=cn.rstd[:, b, h:h + 1])
                done.then_inc(hat_done, 1)

            def copy_context(b, j):
                act.wait_ge(ctx_flipped, b + 1)
                at_least(act, sim_done, b - 1)
                for c in range(C):
                    done = nc.scalar.activation(keysT[j][:, c, 0:2 * P], PS[:, 6, c * 2 * P:(c + 1) * 2 * P], ACT.Identity,
                                                bias=bm[:, c:c + 1], scale=gm[:, c:c + 1])
                done.then_inc(ctxT_copied, 1)

            def exps(b, j):
                act.wait_ge(top_done, b + 1)
                for u in range(2):
                    done = nc.scalar.activation(probs[j][:, u, :], PS[:, 2 * j + u, 0:KEYS], ACT.Exp, bias=top[j][:, u:u + 1], scale=scale,
                                                accum_out=total[j][:, u:u + 1])
                done.then_inc(exps_done, 1)

            def copy_probs(b, j):
                act.wait_ge(pt_done, b + 1)
                nc.scalar.copy(probsT[j][:].rearrange("p h e -> p (h e)"), PS[:, 4, :]).then_inc(pt_act, 1)

            def first():
                for n in range(HEADS * C):
                    m, c, half = n // (2 * C), n // 2 % C, n % 2
                    act.wait_ge(qw_done, 2 * n + 1)
                    nc.scalar.copy(QW[:, c, 2 * m, half * 512:(half + 1) * 512], PS[:, 2 * (n % 2), :]).then_inc(qw_act, 1)
                    if n + 4 in AHEAD:
                        normalise(AHEAD.index(n + 4), AHEAD.index(n + 4))
                    if n - 1 in AHEAD:
                        copy_context(AHEAD.index(n - 1), AHEAD.index(n - 1))
                normalise(2, 0)
                exps(0, 0)

            def turn(b, j):
                copy_probs(b, j)
                exps(b + 1, 1 - j)
                if exists(b + 2):
                    copy_context(b + 2, j)
                if exists(b + 3):
                    normalise(b + 3, 1 - j)

            over_batches(act, first, turn, copy_probs)
            for n in range(0, 2 * M, 2):
                act.wait_ge(out_done, n + 1)
                nc.scalar.copy(OT[:, n // 2, 0:512], PS[:, 0, :]).then_inc(out_act, 1)
            norm.load_table(act)

        @block.vector
        def _(dve):
            dve.wait_ge(core.x_in, 16)
            norm.vector(dve, core.X, core.H, normed_done)
            dve.wait_ge(core.weights_in[9], 16)
            flip.vector(dve, core.HT, gl, bl)
            flip.ready(dve, "dve")
            dve.wait_ge(normed_done, NT)
            dve_step(dve, nc.vector.tensor_tensor(core.H[:], core.H[:], bcast(gl_row, 1, NT), ALU.mult))
            nc.vector.tensor_tensor(core.H[:], core.H[:], bcast(bl_row, 1, NT), ALU.add).then_inc(affine_done, 1)
            for c in range(C):
                nc.vector.tensor_scalar(last_cols[:, c, :], cn.lastT[:, c, :], gm[:, c:c + 1], bm[:, c:c + 1], ALU.mult, ALU.add)
            nc.vector.tensor_tensor(last_rows[:], cn.last[:], gm_row[0:B, :], ALU.mult).then_inc(last_done, 1)
            dve.wait_ge(last_done, 1)
            nc.vector.tensor_tensor(last_rows[:], last_rows[:], bm_row[0:B, :], ALU.add).then_inc(last_done, 1)
            for n in range(HEADS * C):
                m, c, half = n // (2 * C), n // 2 % C, n % 2
                dve.wait_ge(qw_done, 2 * n + 2)
                nc.vector.tensor_copy(QW[:, c, 2 * m + 1, half * 512:(half + 1) * 512], PS[:, 1 + 2 * (n % 2), :]).then_inc(qw_dve, 1)
            dve.wait_ge(stored, 16 * (TB + 1))
            dve.sem_inc(px_copied, 1)

            def tops(b, j):
                dve.wait_ge(sim_done, b + 1)
                dve_step(dve, nc.vector.reduce_max(top[j][:], PS[:, 2 * j:2 * j + 2, 0:KEYS], AX.X))
                nc.vector.tensor_scalar(top[j][:], top[j][:], -scale, None, ALU.mult).then_inc(top_done, 1)

            def weights(b, j):
                dve.wait_ge(exps_done, b + 1)
                dve_step(dve, nc.vector.reciprocal(total[j][:], total[j][:]))
                for u in range(2):
                    done = nc.vector.tensor_scalar(probs[j][:, u, :], probs[j][:, u, :], total[j][:, u:u + 1], None, ALU.mult)
                done.then_inc(probs_done, 1)

            def copy_rest(b, j):
                dve.wait_ge(pt_done, b + 1)
                nc.vector.tensor_copy(probsT_rest[j], PS[0:REST, 5, 0:HEADS * S]).then_inc(pt_dve, 1)

            def copy_px(b, j):
                dve.wait_ge(pv_done, b + 1)
                nc.vector.tensor_copy(QW[:, :, :, bass.ds(b * S, S)], PS[:, 7, :].rearrange("p (c h q) -> p c h q", c=C, q=S)).then_inc(px_copied, 1)

            def first():
                tops(0, 0)
                weights(0, 0)

            def turn(b, j):
                copy_rest(b, j)
                tops(b + 1, 1 - j)
                weights(b + 1, 1 - j)
                copy_px(b, j)

            def last(b, j):
                copy_rest(b, j)
                copy_px(b, j)

            over_batches(dve, first, turn, last, lambda i: dve_step.enter(i, 4), dve_step.leave)
            for n in range(1, 2 * M, 2):
                dve.wait_ge(out_done, n + 1)
                nc.vector.tensor_copy(OT[:, n // 2, 512:1024], PS[:, 1, :]).then_inc(out_dve, 1)
            for n in range(NT // 2):
                dve.wait_ge(proj_done, n + 1)
                x = core.X[:, 2 * n:2 * n + 2, :]
                written = nc.vector.tensor_tensor(x, PS[:, 4 + n, :].rearrange("p (t d) -> p t d", t=2), x, ALU.add)
                norm.take(dve, written, (2 * n, 2 * n + 1))


def l3_self(core, load_next):
    nc, norm, flip, dve_step = core.nc, core.norm, core.flip, core.dve_step
    w = core.arena(10)
    wqk, wv, wo = w.take(C, 2 * D), w.take(C, D), w.take(C, D)
    gate = w.take(2, 16)
    bo, ln_w, ln_b, head_of, batch_of = w.take(D), w.take(C), w.take(C), w.take(8), w.take(TB)
    sharp, threshold = 15.0, 0.29514
    with ExitStack() as es:
        at = SelfAttention(core, es, "l3a", "resonance", sharp)
        shift = core.sb("l3a_shift", [P, 1], es)
        at.resonance_bias = shift[:]
        squares = [core.sb(f"l3a_squares{i}", [P, 2 * D], es) for i in range(2)]
        products = [core.sb(f"l3a_products{i}", [P, 2 * D], es) for i in range(2)]
        size = core.sb("l3a_size", [P, NT, 32], es)
        gates = core.sb("l3a_gates", [P, NT, 32], es)
        at.factor = gates[:, :, 0:16]
        rows_done, normed_done, shift_set = core.sem("l3a_rows_done"), core.sem("l3a_normed_done"), core.sem("l3a_shift_set")
        products_done, gates_done, gated = core.sem("l3a_products_done"), core.sem("l3a_gates_done"), core.sem("l3a_gated")
        biased = core.sem("l3a_biased")
        block = es.enter_context(nc.Block())

        @block.sync
        def _(sp):
            load_next(sp)

        @block.tensor
        def _(pe):
            pe.wait_ge(core.consts_in, 16)
            pe.wait_ge(core.weights_in[10], 16)
            flip.tensor(pe, core.H, rows_done, 0)
            flip.tensor(pe, at.Q, normed_done, 0)
            flip.ready(pe, "pe")
            at.project(pe, at.QT, core.HT, wqk, wv)
            at.flip_tensor(pe)
            flip.ready(pe, "pe")
            pe.wait_ge(gated, NT)
            at.attend_tensor(pe, wo)

        @block.gpsimd
        def _(pool):
            at.set_zeros(pool)
            pool.wait_ge(core.weights_in[10], 16)
            pool.wait_ge(normed_done, NT)
            nc.gpsimd.tensor_tensor(core.X[:], core.X[:], bcast(bo, 1, NT), ALU.add).then_inc(biased, 1)
            for t in range(NT):
                pool.wait_ge(at.qk_rows, t + 1)
                if t >= 2:
                    pool.wait_ge(gates_done, t - 1)
                four = lambda m: m.rearrange("p (k h d) -> p k h d", k=2, h=16)
                nc.gpsimd.tensor_tensor(four(products[t % 2][:]), four(at.QK[:, t, :]), bcast(gate, 2, 16), ALU.mult).then_inc(products_done, 1)
            flip.uses["pool"] = flip.uses["pe"]
            flip.ready(pool, "pool")
            at.spread_keys(pool, head_of)

        @block.scalar
        def _(act):
            norm.scalar(act, core.eps5)
            flip.scalar(act, core.HT)
            norm.scalar_twice(act)
            act.wait_ge(core.weights_in[10], 16)
            flip.scalar(act, at.QT, ln_w, ln_b)
            at.copy_projections(act, squares, size)
            flip.scalar(act, at.QT)
            flip.scalar(act, at.KT)
            act.wait_ge(shift_set, 1)
            at.attend_scalar(act, batch_of)
            norm.load_table(act)

        @block.vector
        def _(dve):
            nc.vector.memset(shift[:], -sharp * threshold).then_inc(shift_set, 1)
            dve.wait_ge(core.x_in, 16)
            norm.vector(dve, core.X, core.H, rows_done)
            flip.vector(dve, core.HT)
            norm.vector_again(dve, core.X, at.Q, normed_done)
            dve.wait_ge(core.weights_in[10], 16)
            flip.vector(dve, at.QT, ln_w, ln_b)
            for t in range(NT + 2):
                if t < NT:
                    at.sum_squares(dve, t, squares, size)
                if 1 <= t <= NT:
                    u = t - 1
                    dve.wait_ge(at.rooted, u + 1)
                    dve_step(dve, nc.vector.tensor_scalar(size[:, u, :], size[:, u, :], 1e-12, None, ALU.max))
                    dve_step(dve, nc.vector.reciprocal(size[:, u, :], size[:, u, :]))
                    heads = at.QK[:, u, :].rearrange("p (h d) -> p h d", h=32)
                    nc.vector.tensor_tensor(heads, heads, bcast(size[:, u, :], 2, 16), ALU.mult).then_inc(at.qk_rows, 1)
                if t >= 2:
                    u = t - 2
                    dve.wait_ge(products_done, u + 1)
                    nc.vector.reduce_sum(gates[:, u, :], products[u % 2][:].rearrange("p (h d) -> p h d", d=16), AX.X).then_inc(gates_done, 1)
                    dve.wait_ge(gates_done, u + 1)
                    dve.wait_ge(at.v_copied, u + 1)
                    for side in range(2):
                        values, gate_k = at.values(u, side), gates[:, u, 16:32].rearrange("p (h two) -> p h two", two=2)[:, :, side]
                        done = nc.vector.tensor_tensor(values, values, bcast(gate_k, 2, 16), ALU.mult)
                    done.then_inc(gated, 1)
            flip.vector(dve, at.QT)
            flip.vector(dve, at.KT)
            dve.wait_ge(biased, 1)
            at.attend_vector(dve, None)


def l3_feed_forward(core, load_next):
    nc, PS, norm, flip, dve_step = core.nc, core.PS, core.norm, core.flip, core.dve_step
    E = EXPERTS[11][0]
    w = core.arena(11)
    wg, bg, b2, number = w.take(C, E), w.take(E), w.take(D), w.take(E)
    with ExitStack() as es:
        ex = SortedExperts(core, es, "l3f", 11, "gelu", 2)
        bias = OutputBias(core, es, "l3f", E)
        sb = lambda n, shape: core.sb("l3f_" + n, shape, es)
        logits, gate = sb("logits", [P, NT, E]), sb("gate", [P, NT, E])
        first, second, chosen = sb("first", [P, NT, E]), sb("second", [P, NT, E]), sb("chosen", [P, NT, E])
        best, next_best, place, odds = sb("best", [P, NT]), sb("next_best", [P, NT]), sb("place", [P, NT]), sb("odds", [P, NT])
        rows_done, routed, chosen_done = core.sem("l3f_rows_done"), core.sem("l3f_routed"), core.sem("l3f_chosen_done")
        gap_done, odds_done, weighed = core.sem("l3f_gap_done"), core.sem("l3f_odds_done"), core.sem("l3f_weighed")
        block = es.enter_context(nc.Block())

        @block.sync
        def _(sp):
            load_next(sp)
            ex.load(sp)

        @block.gpsimd
        def _(pool):
            ex.scatter(pool, core.H, rows_done, 0)

        @block.tensor
        def _(pe):
            pe.wait_ge(core.consts_in, 16)
            pe.wait_ge(core.weights_in[11], 16)
            flip.tensor(pe, core.H, rows_done, 0)
            flip.ready(pe, "pe")
            router_tensor(core, pe, core.HT, wg, routed)
            ex.places.tensor(pe, chosen, chosen_done)
            bias.tensor(pe, gate, weighed, b2)
            ex.tensor(pe, core.HT)

        @block.scalar
        def _(act):
            norm.scalar(act, core.eps5)
            flip.scalar(act, core.HT)
            act.wait_ge(gap_done, 1)
            nc.scalar.activation(odds[:], odds[:], ACT.Exp).then_inc(odds_done, 1)
            ex.scalar(act)

        @block.vector
        def _(dve):
            nc.vector.memset(ex.places.ones[:], 1.0)
            dve.wait_ge(core.x_in, 16)
            norm.vector(dve, core.X, core.H, rows_done)
            flip.vector(dve, core.HT)
            dve.wait_ge(core.weights_in[11], 16)
            dve.wait_ge(routed, 1)
            dve_step(dve, nc.vector.tensor_tensor(logits[:], PS[:, 4, 0:NT * E].rearrange("p (t e) -> p t e", e=E), bcast(bg, 1, NT), ALU.add))
            first_best(core, dve, logits, number, best, place, first)
            dve_step(dve, nc.vector.scalar_tensor_tensor(logits[:], first[:], NEG, logits[:], ALU.mult, ALU.add))
            first_best(core, dve, logits, number, next_best, place, second)
            nc.vector.tensor_tensor(odds[:], next_best[:], best[:], ALU.subtract).then_inc(gap_done, 1)
            nc.vector.tensor_tensor(chosen[:], first[:], second[:], ALU.add).then_inc(chosen_done, 1)
            ex.places.vector(dve, (first, second))
            dve.wait_ge(odds_done, 1)
            dve_step(dve, nc.vector.tensor_scalar(best[:], odds[:], 1.0, None, ALU.add))
            dve_step(dve, nc.vector.reciprocal(best[:], best[:]))
            dve_step(dve, nc.vector.tensor_tensor(odds[:], odds[:], best[:], ALU.mult))
            nc.vector.tensor_tensor(gate[:], first[:], bcast(best[:], 2, E), ALU.mult)
            dve_step(dve, nc.vector.tensor_tensor(second[:], second[:], bcast(odds[:], 2, E), ALU.mult))
            nc.vector.tensor_tensor(gate[:], gate[:], second[:], ALU.add).then_inc(weighed, 1)
            dve.wait_ge(weighed, 1)
            bias.vector(dve)
            ex.vector(dve, (best, odds), final=True)


SUBLAYERS = [l0_cross, l0_self, l0_feed_forward, l1_cross, l1_self, l1_feed_forward, l2_cross, l2_self, l2_feed_forward, l3_cross, l3_self, l3_feed_forward]


def begin(core, load_first):
    nc = core.nc
    with nc.Block(no_gpsimd_drain=True) as block:
        @block.sync
        def _(sp):
            sp.dma_start(core.X[:], core.dram["x"].rearrange("(t p) d -> p t d", p=P)).then_inc(core.x_in, 16)
            sp.dma_start(core.consts[:], core.dram["consts"]).then_inc(core.consts_in, 16)
            load_first(sp)

        @block.vector
        def _(dve):
            for i, value in enumerate((1e-5, 1e-10, 1e-6)):
                done = nc.vector.memset(core.eps[:, i:i + 1], value)
            done.then_inc(core.eps_set, 1)


def finish(core):
    nc = core.nc
    stored = core.sem("stored")
    with nc.Block(no_gpsimd_drain=True) as block:
        @block.sync
        def _(sp):
            sp.dma_start(core.dram["out"].rearrange("(t p) d -> p t d", p=P), core.X[:]).then_inc(stored, 16)
            sp.wait_ge(stored, 16)


def program(nc, dram):
    with ExitStack() as es:
        core = Core(nc, es, dram)
        loads = [lambda sp, k=k: load_weights(core, sp, k) for k in LAYERS] + [lambda sp: None]
        begin(core, loads[0])
        for n, k in enumerate(LAYERS):
            SUBLAYERS[k](core, loads[n + 1])
            core.free_sems()
        finish(core)


def by_chunk(w):
    return w.reshape(-1, P, w.shape[1]).transpose(1, 0, 2).reshape(P, -1)


def to_all(v):
    return np.broadcast_to(np.asarray(v).reshape(1, -1), (P, np.asarray(v).size))


def column(v):
    return np.asarray(v).reshape(-1, P).T


def packed(parts):
    return np.ascontiguousarray(np.concatenate([np.asarray(p, np.float32) for p in parts], axis=1))


def constants():
    p = np.arange(P)
    angle = (np.arange(S, dtype=np.float32)[:, None] * (10000.0 ** (-2.0 * np.arange(8, dtype=np.float32) / 16)).astype(np.float32)).astype(np.float32)
    return {
        "cos": np.tile(np.cos(angle), (TB, 1)), "sin": np.tile(np.sin(angle), (TB, 1)),
        "causal": np.tile(np.where(np.tri(S, dtype=bool), 0.0, NEG), (TB, 1)),
        "consts": packed([np.eye(P), p[:, None] < p[None], to_all(np.tri(NT, k=-1)), to_all(P * np.arange(24)), p[:, None]]),
        "batch_of": (p[:, None] // S == np.arange(TB)).astype(np.float32),
        "head_of": (p[:, None] // 16 == np.arange(8)).astype(np.float32),
        "same_head": (p[:, None] // 16 == p // 16).astype(np.float32),
        "order": np.eye(P)[p // 2 % TB * S + p // (2 * TB) * 2 + p % 2],
    }


def layout(a):
    k = constants()
    ctx = a["ctx_1024"]
    ctx_by_feature = ctx.transpose(0, 2, 1).reshape(B, C, P, CTX).transpose(0, 2, 1, 3)
    mask = a["mask_BxS2_ff1"]
    out = {"x": a["x"].reshape(B * S, D), "consts": k["consts"], "ctxT": ctx_by_feature}
    left_col = np.zeros((P, 1), np.float32)
    left_col[0:B, 0] = mask[:, CTX - 1]
    out["pack0"] = packed([
        by_chunk(a["L0_xattn_wq"]),
        by_chunk(np.concatenate([a["L0_xattn_wk"], a["L0_xattn_wv"]], axis=1)),
        by_chunk(a["L0_xattn_dense_w"]), to_all(a["L0_xattn_ln_gamma"]), to_all(a["L0_xattn_ln_beta"]),
        to_all(a["L0_xattn_dense_b"]), k["head_of"], k["same_head"],
        mask[:, 0:2 * P].reshape(B, 2, P).transpose(2, 0, 1).reshape(P, -1), left_col,
        ctx[:, CTX - 1, :].T.reshape(C, P, B).transpose(1, 0, 2).reshape(P, -1), k["order"],
    ])
    first_of = lambda n: to_all(np.arange(n, dtype=np.float32) - n)
    rows = lambda m: np.concatenate([m, np.zeros((P - m.shape[0], m.shape[1]), np.float32)])
    out["pack1"] = packed([
        by_chunk(np.concatenate([a["L0_attn_W_Q"].T, a["L0_attn_W_K"].T], axis=1)),
        by_chunk(a["L0_attn_W_V"].T), by_chunk(a["L0_attn_W_O"].T),
        k["cos"], k["sin"], k["causal"], k["head_of"], k["batch_of"],
    ])
    out["pack2"] = packed([by_chunk(a["L0_ffn_centroids"].T), to_all(a["L0_ffn_scale"]), first_of(8)])
    out["experts2_up"], out["experts2_down"] = (np.stack([by_chunk(w) for w in a[f"L0_ffn_{n}_w"]]) for n in ("up", "down"))
    wkv = a["L1_xattn_Wkv"]
    out["ctx"] = ctx
    out["pack3"] = packed([
        by_chunk(a["L1_xattn_Wq"]), by_chunk(np.concatenate([wkv[:, 0:64], wkv[:, 0:64], wkv[:, 64:128]], axis=1)), by_chunk(a["L1_xattn_Wo"]),
        by_chunk(a["L1_xattn_Wff1"]), by_chunk(a["L1_xattn_Wff2"]), *(column(a[f"L1_xattn_{n}"]) for n in ("ln_g", "ln_b", "cln_g", "cln_b")),
        (np.arange(P)[:, None] // 64 == np.arange(2)[None]).astype(np.float32),
    ])
    w_attn = a["L1_attn_W_attn"].T
    out["pack4"] = packed([
        by_chunk(w_attn[:, 0:1024]), by_chunk(w_attn[:, 1024:1280]), by_chunk(w_attn[:, 1280:1536]), by_chunk(a["L1_attn_W_proj"].T),
        k["causal"], k["head_of"], k["batch_of"],
    ])
    split = lambda m: np.concatenate([m[..., 0::2], m[..., 1::2]], axis=-1)
    with_shared = lambda n: np.concatenate([a[f"L1_ffn_{n}"], a[f"L1_ffn_s{n}"][None]])
    out["pack5"] = packed([by_chunk(a["L1_ffn_gate_w"].T), to_all(a["L1_ffn_gate_b"]), rows(with_shared("b2")), first_of(8)])
    out["experts5_up"], out["experts5_down"] = (np.stack(part) for part in zip(*(
        (packed([by_chunk(split(w1)), by_chunk(split(w3)), column(split(b1)), column(split(b3))]), packed([by_chunk(w2)]))
        for w1, w3, w2, b1, b3 in zip(*map(with_shared, ("w1", "w3", "w2", "b1", "b3"))))))
    out["pack6"] = packed([
        *(by_chunk(a[f"L2_xattn_{n}"]) for n in ("Wq", "Wk", "Wv", "Wo")), column(a["L2_xattn_bq"]), column(a["L2_xattn_bk"]),
        to_all(a["L2_xattn_bv"]), to_all(a["L2_xattn_bo"]), k["head_of"],
        (np.arange(P)[:, None] % 64 // 16 == np.arange(4)[None]).astype(np.float32),
        ctx[:, CTX - 1, :].T.reshape(C, P, B).transpose(1, 0, 2).reshape(P, -1),
    ])
    four = lambda v: np.repeat(np.asarray(v).reshape(D, 4, 16), 4, axis=1).reshape(D, D)
    out["pack7"] = packed([
        by_chunk(np.concatenate([a["L2_attn_w_q"], four(a["L2_attn_w_k"])], axis=1)),
        by_chunk(four(a["L2_attn_w_v"])), by_chunk(a["L2_attn_w_o"]),
        k["cos"], k["sin"], k["causal"], k["head_of"], k["batch_of"],
    ])
    out["pack8"] = packed([by_chunk(a["L2_ffn_expert_w"].transpose(2, 0, 1).reshape(D, -1)), by_chunk(a["L2_ffn_gate_w"].T), first_of(8)])
    wk, wv = a["L3_xattn_Wkv"][:, 0:512], a["L3_xattn_Wkv"][:, 512:1024]
    affine = [a[f"L3_xattn_{n}"] for n in ("gm", "bm", "gl", "bl")]
    out["pack9"] = packed([
        by_chunk(a["L3_xattn_Wq"]), by_chunk(wk.T), by_chunk(wv), by_chunk(a["L3_xattn_Wout"]),
        *(column(v) for v in affine), *(to_all(v) for v in affine),
    ])
    out["pack10"] = packed([
        by_chunk(np.concatenate([a["L3_attn_Wq"], a["L3_attn_Wk"]], axis=1)),
        by_chunk(a["L3_attn_Wv"]), by_chunk(a["L3_attn_Wo"]), to_all(a["L3_attn_gq"]), to_all(a["L3_attn_gk"]),
        to_all(a["L3_attn_bo"]), column(a["L3_attn_ln_w"]), column(a["L3_attn_ln_b"]), k["head_of"], k["batch_of"],
    ])
    out["pack11"] = packed([by_chunk(a["L3_ffn_Wg"]), to_all(a["L3_ffn_bg"]), rows(a["L3_ffn_b2"]), first_of(6)])
    out["experts11_up"] = np.stack([packed([by_chunk(w), column(b)]) for w, b in zip(a["L3_ffn_W1"], a["L3_ffn_b1"])])
    out["experts11_down"] = np.stack([by_chunk(w) for w in a["L3_ffn_W2"]])
    return {n: np.ascontiguousarray(v) for n, v in out.items()}


def kernel(**inputs):
    import concourse.bacc as bacc
    from concourse.bass_utils import run_bass_kernel_spmd

    arrays = layout({n: np.asarray(v) for n, v in inputs.items()})
    nc = bacc.Bacc("TRN2", target_bir_lowering=False, num_devices=1)
    dram = {n: nc.dram_tensor(f"in_{n}_dram", v.shape, F32, kind="ExternalInput").ap() for n, v in arrays.items()}
    dram["out"] = nc.dram_tensor("out_0_dram", (B * S, D), F32, kind="ExternalOutput").ap()
    program(nc, dram)
    got = run_bass_kernel_spmd(nc, [{f"in_{n}_dram": v for n, v in arrays.items()}], core_ids=[0])
    return got.results[0]["out_0_dram"].reshape(B, S, D)
```
